# Optimizing a Trainium2 kernel written in Bass

```python
import numpy as np
import jax
import jax.numpy as jnp

def _softmax(x, axis=-1):
    return jax.nn.softmax(x, axis=axis)

def _gelu(x):
    return jax.nn.gelu(x, approximate=True)

def _silu(x):
    return jax.nn.silu(x)

def _sigmoid(x):
    return jax.nn.sigmoid(x)

def _layernorm(x, axis=-1, eps=1e-05):
    m = jnp.mean(x, axis=axis, keepdims=True)
    v = jnp.var(x, axis=axis, keepdims=True)
    return (x - m) / jnp.sqrt(v + eps)

def _scatter_add(tgt, idx, src, axis=0):
    return tgt.at[idx].add(src)

def _segment_sum(src, seg, n):
    return jax.ops.segment_sum(src, seg, n)
kernel_name = 'mk_adaln_d4_jaxref_r8_059e6a'

def setup_inputs(seed: int=0):
    np.random.seed(seed)
    _w = jnp.asarray

    def _L0_attn_setup():
        import math
        import jax, jax.numpy as jnp
        import numpy as np
        N_EMBD = 128
        N_HEAD = 16
        N_QUERY_SETS = 4
        B, T = (8, 128)
        key = jax.random.key(seed)
        kx, kw1, kw2 = jax.random.split(key, 3)
        C = N_EMBD
        x = jax.random.normal(kx, (B, T, C), dtype=jnp.float32)
        W_attn = jax.random.normal(kw1, ((N_QUERY_SETS + 2) * C, C), dtype=jnp.float32) * (1.0 / math.sqrt(C))
        W_proj = jax.random.normal(kw2, (C, N_QUERY_SETS * C), dtype=jnp.float32) * (1.0 / math.sqrt(N_QUERY_SETS * C))
        return {'x': x, 'W_attn': W_attn, 'W_proj': W_proj}
    _L0_attn_in = _L0_attn_setup()

    def _L0_ffn_setup():
        import jax, jax.numpy as jnp
        import numpy as np
        ALPHA = 1.702
        LIMIT = 7.0
        TOP_K = 2
        key = jax.random.key(seed)
        ks = jax.random.split(key, 4)
        B, S, H, E, I = (2, 128, 128, 8, 256)
        return {'hidden_states': jax.random.normal(ks[0], (B, S, H), jnp.float32), 'router_weight': jax.random.normal(ks[1], (E, H), jnp.float32), 'router_bias': jnp.zeros((E,), jnp.float32), 'gate_up_proj': jax.random.normal(ks[2], (E, H, 2 * I), jnp.float32) * 0.02, 'gate_up_bias': jnp.zeros((E, 2 * I), jnp.float32), 'down_proj': jax.random.normal(ks[3], (E, I, H), jnp.float32) * 0.02, 'down_bias': jnp.zeros((E, H), jnp.float32)}
    _L0_ffn_in = _L0_ffn_setup()
    _L0_c = _w((lambda *s: np.random.randn(*s).astype(np.float32) * 0.05)(16, 128))
    _L0_wmod = _w((lambda *s: np.random.randn(*s).astype(np.float32) * 0.05)(128, 6 * 128) * 128 ** (-0.5))

    def _L1_attn_setup():
        import jax, jax.numpy as jnp
        import numpy as np
        import math
        EMBED_DIM = 128
        NHEAD = 16
        HEAD_DIM = 64
        BATCH = 2
        SEQ = 256
        key = jax.random.key(seed)
        k_in, k_wqkv, k_wo, k_g = jax.random.split(key, 4)
        std = math.sqrt(2.0 / EMBED_DIM)
        inputs = jax.random.normal(k_in, (BATCH, SEQ, EMBED_DIM), dtype=jnp.float32)
        Wqkv_w = jax.random.normal(k_wqkv, (3 * NHEAD * HEAD_DIM, EMBED_DIM), dtype=jnp.float32) * std
        Wqkv_b = jnp.zeros((3 * NHEAD * HEAD_DIM,), dtype=jnp.float32)
        Wo_w = jax.random.normal(k_wo, (EMBED_DIM, NHEAD * HEAD_DIM), dtype=jnp.float32) * std
        Wo_b = jnp.zeros((EMBED_DIM,), dtype=jnp.float32)
        ghost = jax.random.uniform(k_g, (NHEAD,), dtype=jnp.float32) * 0.1
        return {'inputs': inputs, 'Wqkv_w': Wqkv_w, 'Wqkv_b': Wqkv_b, 'Wo_w': Wo_w, 'Wo_b': Wo_b, 'ghost': ghost}
    _L1_attn_in = _L1_attn_setup()

    def _L1_ffn_setup():
        import jax, jax.numpy as jnp
        import numpy as np
        BLOCK = 16
        _GRID = jnp.array([0.0, 0.5, 1.0, 1.5, 2.0, 3.0, 4.0, 6.0], dtype=jnp.float32)
        _MID = jnp.array([0.25, 0.75, 1.25, 1.75, 2.5, 3.5, 5.0], dtype=jnp.float32)

        def fp4_quant_dequant(x):
            shape = x.shape
            xb = x.reshape(shape[:-1] + (shape[-1] // BLOCK, BLOCK))
            scale = jnp.max(jnp.abs(xb), axis=-1, keepdims=True) / 6.0
            scale = jnp.maximum(scale, jnp.float32(1e-12))
            xn = xb / scale
            idx = jnp.searchsorted(_MID, jnp.abs(xn))
            q = _GRID[idx] * jnp.sign(xn) * scale
            return q.reshape(shape)

        def fp4_linear(x, w):
            xq = fp4_quant_dequant(x)
            wq = fp4_quant_dequant(w)
            return jnp.einsum('bsk,nk->bsn', xq, wq)
        key = jax.random.key(seed)
        k1, k2, k3, k4 = jax.random.split(key, 4)
        H, I = (128, 352)
        x = jax.random.normal(k1, (4, 512, H), dtype=jnp.float32)
        w_gate = jax.random.normal(k2, (I, H), dtype=jnp.float32) * 0.02
        w_up = jax.random.normal(k3, (I, H), dtype=jnp.float32) * 0.02
        w_down = jax.random.normal(k4, (H, I), dtype=jnp.float32) * 0.02
        return {'x': x, 'w_gate': w_gate, 'w_up': w_up, 'w_down': w_down}
    _L1_ffn_in = _L1_ffn_setup()
    _L1_c = _w((lambda *s: np.random.randn(*s).astype(np.float32) * 0.05)(16, 128))
    _L1_wmod = _w((lambda *s: np.random.randn(*s).astype(np.float32) * 0.05)(128, 6 * 128) * 128 ** (-0.5))

    def _L2_attn_setup():
        import jax, jax.numpy as jnp
        import numpy as np
        B, S, D = (4, 256, 128)
        KD, VD = (128, 128)
        key = jax.random.key(seed)
        ks = jax.random.split(key, 9)
        sc_in = 1.0 / np.sqrt(D)
        sc_v = 1.0 / np.sqrt(VD)
        return {'x': jax.random.normal(ks[0], (B, S, D), dtype=jnp.float32), 'Wq': jax.random.normal(ks[1], (KD, D), dtype=jnp.float32) * sc_in, 'bq': jax.random.normal(ks[2], (KD,), dtype=jnp.float32) * 0.01, 'Wk': jax.random.normal(ks[3], (KD, D), dtype=jnp.float32) * sc_in, 'bk': jax.random.normal(ks[4], (KD,), dtype=jnp.float32) * 0.01, 'Wv': jax.random.normal(ks[5], (VD, D), dtype=jnp.float32) * sc_in, 'bv': jax.random.normal(ks[6], (VD,), dtype=jnp.float32) * 0.01, 'Wo': jax.random.normal(ks[7], (D, VD), dtype=jnp.float32) * sc_v, 'bo': jax.random.normal(ks[8], (D,), dtype=jnp.float32) * 0.01}
    _L2_attn_in = _L2_attn_setup()

    def _L2_ffn_setup():
        import jax, jax.numpy as jnp
        import numpy as np
        DIM = 128
        DEPTH = 2
        HEADS = 8
        DIM_HEAD = 64
        WINDOW = 64
        INNER = HEADS * DIM_HEAD
        HID = int(DIM * 4 * 2 / 3)
        B, N = (2, 1024)
        QK_SCALE = 8.0

        def shift_token(t):
            t1, t2 = jnp.split(t, 2, axis=-1)
            t2 = jnp.pad(t2, ((0, 0), (1, 0), (0, 0)))[:, :-1]
            return jnp.concatenate([t1, t2], axis=-1)

        def l2norm(t):
            return t / jnp.clip(jnp.linalg.norm(t, axis=-1, keepdims=True), 1e-12)

        def rotate_half(x):
            x1, x2 = jnp.split(x, 2, axis=-1)
            return jnp.concatenate([-x2, x1], axis=-1)

        def rotary_xpos(q, k):
            n = q.shape[-2]
            half_idx = jnp.arange(0, DIM_HEAD, 2, dtype=jnp.float32)
            inv_freq = 1.0 / 10000.0 ** (half_idx / DIM_HEAD)
            t = jnp.arange(n, dtype=jnp.float32)
            freqs = t[:, None] * inv_freq[None, :]
            freqs = jnp.concatenate([freqs, freqs], axis=-1)
            base = (half_idx + 0.4 * DIM_HEAD) / (1.4 * DIM_HEAD)
            power = (t - n // 2) / float(WINDOW // 2)
            scale = base[None, :] ** power[:, None]
            scale = jnp.concatenate([scale, scale], axis=-1)
            cos, sin = (jnp.cos(freqs), jnp.sin(freqs))
            q = q * cos * scale + rotate_half(q) * sin * scale
            k = k * cos / scale + rotate_half(k) * sin / scale
            return (q, k)

        def local_attention(q, k, v):
            b, h, n, d = q.shape
            w = n // WINDOW
            bq = q.reshape(b, h, w, WINDOW, d) * QK_SCALE
            bk = k.reshape(b, h, w, WINDOW, d)
            bv = v.reshape(b, h, w, WINDOW, d)

            def look_around(t):
                p = jnp.pad(t, ((0, 0), (0, 0), (1, 0), (0, 0), (0, 0)))
                return jnp.concatenate([p[:, :, :w], p[:, :, 1:]], axis=3)
            bk, bv = (look_around(bk), look_around(bv))
            bt = jnp.arange(n).reshape(w, WINDOW)
            btp = jnp.pad(bt, ((1, 0), (0, 0)), constant_values=-1)
            btk = jnp.concatenate([btp[:w], btp[1:]], axis=1)
            sim = jnp.einsum('bhwid,bhwjd->bhwij', bq, bk)
            i = bt[:, :, None]
            j = btk[:, None, :]
            mask = (i < j) | (i > j + WINDOW) | (j == -1)
            sim = jnp.where(mask, -jnp.finfo(sim.dtype).max, sim)
            attn = jax.nn.softmax(sim, axis=-1)
            out = jnp.einsum('bhwij,bhwjd->bhwid', attn, bv)
            return out.reshape(b, h, n, d)

        def _layer(x, wqkv, qs, ksc, wo, lg, lb, w1, b1, w2, b2):
            b, n, _ = x.shape
            h = shift_token(x)
            qkv = h @ wqkv
            q, k, v = jnp.split(qkv, 3, axis=-1)
            to_heads = lambda t: t.reshape(b, n, HEADS, DIM_HEAD).transpose(0, 2, 1, 3)
            q, k, v = (to_heads(q), to_heads(k), to_heads(v))
            q = l2norm(q) * qs
            k = l2norm(k) * ksc
            q, k = rotary_xpos(q, k)
            o = local_attention(q, k, v)
            o = o.transpose(0, 2, 1, 3).reshape(b, n, INNER)
            x = x + o @ wo
            h = shift_token(x)
            mu = h.mean(-1, keepdims=True)
            var = h.var(-1, keepdims=True)
            h = (h - mu) / jnp.sqrt(var + 1e-05) * lg + lb
            h = h @ w1 + b1
            a, g = jnp.split(h, 2, axis=-1)
            h = a * jax.nn.gelu(g, approximate=False)
            x = x + h @ w2 + b2
            return x
        key = jax.random.key(seed)
        ks = jax.random.split(key, 6)
        return {'x': jax.random.normal(ks[0], (B, N, DIM), jnp.float32), 'wqkv': jax.random.normal(ks[1], (DEPTH, DIM, 3 * INNER), jnp.float32) * 0.02, 'q_scale': jnp.ones((DEPTH, DIM_HEAD), jnp.float32), 'k_scale': jnp.ones((DEPTH, DIM_HEAD), jnp.float32), 'wo': jax.random.normal(ks[2], (DEPTH, INNER, DIM), jnp.float32) * 0.02, 'ln_g': jnp.ones((DEPTH, DIM), jnp.float32), 'ln_b': jnp.zeros((DEPTH, DIM), jnp.float32), 'w1': jax.random.normal(ks[3], (DEPTH, DIM, 2 * HID), jnp.float32) * 0.02, 'b1': jnp.zeros((DEPTH, 2 * HID), jnp.float32), 'w2': jax.random.normal(ks[4], (DEPTH, HID, DIM), jnp.float32) * 0.02, 'b2': jnp.zeros((DEPTH, DIM), jnp.float32)}
    _L2_ffn_in = _L2_ffn_setup()
    _L2_c = _w((lambda *s: np.random.randn(*s).astype(np.float32) * 0.05)(16, 128))
    _L2_wmod = _w((lambda *s: np.random.randn(*s).astype(np.float32) * 0.05)(128, 6 * 128) * 128 ** (-0.5))

    def _L3_attn_setup():
        import jax, jax.numpy as jnp
        import numpy as np
        B, N, DIM = (2, 256, 128)
        H = 16
        HD = DIM // H
        key = jax.random.key(seed)
        ks = jax.random.split(key, 4)
        x = jax.random.normal(ks[0], (B, N, DIM), dtype=jnp.float32)
        w_qkv = jax.random.normal(ks[1], (DIM, 3 * DIM), dtype=jnp.float32) / np.sqrt(DIM)
        w_proj = jax.random.normal(ks[2], (DIM, DIM), dtype=jnp.float32) / np.sqrt(DIM)
        b_proj = jax.random.normal(ks[3], (DIM,), dtype=jnp.float32) * 0.01
        return {'x': x, 'w_qkv': w_qkv, 'w_proj': w_proj, 'b_proj': b_proj}
    _L3_attn_in = _L3_attn_setup()

    def _L3_ffn_setup():
        import jax, jax.numpy as jnp
        import numpy as np
        DMODEL = 128
        N_EXPERTS = 16
        EXPERT_SIZE = 32
        K = 4
        key = jax.random.key(seed)
        k1, k2, k3, k4 = jax.random.split(key, 4)
        std_sel = 1.0 / np.sqrt(DMODEL)
        std_val = 1.0 / np.sqrt(N_EXPERTS * EXPERT_SIZE)
        return {'x': jax.random.normal(k1, (4, 256, DMODEL), dtype=jnp.float32), 'expert_sel': jax.random.normal(k2, (N_EXPERTS, DMODEL), dtype=jnp.float32) * std_sel, 'keys': jax.random.normal(k3, (N_EXPERTS, DMODEL, EXPERT_SIZE), dtype=jnp.float32) * std_sel, 'values': jax.random.normal(k4, (N_EXPERTS, EXPERT_SIZE, DMODEL), dtype=jnp.float32) * std_val, 'route_scale': jnp.ones((1,), dtype=jnp.float32)}
    _L3_ffn_in = _L3_ffn_setup()
    _L3_c = _w((lambda *s: np.random.randn(*s).astype(np.float32) * 0.05)(16, 128))
    _L3_wmod = _w((lambda *s: np.random.randn(*s).astype(np.float32) * 0.05)(128, 6 * 128) * 128 ** (-0.5))
    _d = {'L0_attn_x': _L0_attn_in['x'], 'L0_attn_W_attn': _L0_attn_in['W_attn'], 'L0_attn_W_proj': _L0_attn_in['W_proj'], 'L0_ffn_router_weight': _L0_ffn_in['router_weight'], 'L0_ffn_router_bias': _L0_ffn_in['router_bias'], 'L0_ffn_gate_up_proj': _L0_ffn_in['gate_up_proj'], 'L0_ffn_gate_up_bias': _L0_ffn_in['gate_up_bias'], 'L0_ffn_down_proj': _L0_ffn_in['down_proj'], 'L0_ffn_down_bias': _L0_ffn_in['down_bias'], 'L0_c': _L0_c, 'L0_wmod': _L0_wmod, 'L1_attn_Wqkv_w': _L1_attn_in['Wqkv_w'], 'L1_attn_Wqkv_b': _L1_attn_in['Wqkv_b'], 'L1_attn_Wo_w': _L1_attn_in['Wo_w'], 'L1_attn_Wo_b': _L1_attn_in['Wo_b'], 'L1_attn_ghost': _L1_attn_in['ghost'], 'L1_ffn_w_gate': _L1_ffn_in['w_gate'], 'L1_ffn_w_up': _L1_ffn_in['w_up'], 'L1_ffn_w_down': _L1_ffn_in['w_down'], 'L1_c': _L1_c, 'L1_wmod': _L1_wmod, 'L2_attn_Wq': _L2_attn_in['Wq'], 'L2_attn_bq': _L2_attn_in['bq'], 'L2_attn_Wk': _L2_attn_in['Wk'], 'L2_attn_bk': _L2_attn_in['bk'], 'L2_attn_Wv': _L2_attn_in['Wv'], 'L2_attn_bv': _L2_attn_in['bv'], 'L2_attn_Wo': _L2_attn_in['Wo'], 'L2_attn_bo': _L2_attn_in['bo'], 'L2_ffn_wqkv': _L2_ffn_in['wqkv'], 'L2_ffn_q_scale': _L2_ffn_in['q_scale'], 'L2_ffn_k_scale': _L2_ffn_in['k_scale'], 'L2_ffn_wo': _L2_ffn_in['wo'], 'L2_ffn_ln_g': _L2_ffn_in['ln_g'], 'L2_ffn_ln_b': _L2_ffn_in['ln_b'], 'L2_ffn_w1': _L2_ffn_in['w1'], 'L2_ffn_b1': _L2_ffn_in['b1'], 'L2_ffn_w2': _L2_ffn_in['w2'], 'L2_ffn_b2': _L2_ffn_in['b2'], 'L2_c': _L2_c, 'L2_wmod': _L2_wmod, 'L3_attn_w_qkv': _L3_attn_in['w_qkv'], 'L3_attn_w_proj': _L3_attn_in['w_proj'], 'L3_attn_b_proj': _L3_attn_in['b_proj'], 'L3_ffn_expert_sel': _L3_ffn_in['expert_sel'], 'L3_ffn_keys': _L3_ffn_in['keys'], 'L3_ffn_values': _L3_ffn_in['values'], 'L3_ffn_route_scale': _L3_ffn_in['route_scale'], 'L3_c': _L3_c, 'L3_wmod': _L3_wmod}
    _x0 = _d['L0_attn_x']
    _d['L0_attn_x'] = jax.random.normal(jax.random.fold_in(jax.random.key(seed), 1), (16, 256, 128), dtype=_x0.dtype)
    del _x0
    return _d

def reference(L0_attn_x, L0_attn_W_attn, L0_attn_W_proj, L0_ffn_router_weight, L0_ffn_router_bias, L0_ffn_gate_up_proj, L0_ffn_gate_up_bias, L0_ffn_down_proj, L0_ffn_down_bias, L0_c, L0_wmod, L1_attn_Wqkv_w, L1_attn_Wqkv_b, L1_attn_Wo_w, L1_attn_Wo_b, L1_attn_ghost, L1_ffn_w_gate, L1_ffn_w_up, L1_ffn_w_down, L1_c, L1_wmod, L2_attn_Wq, L2_attn_bq, L2_attn_Wk, L2_attn_bk, L2_attn_Wv, L2_attn_bv, L2_attn_Wo, L2_attn_bo, L2_ffn_wqkv, L2_ffn_q_scale, L2_ffn_k_scale, L2_ffn_wo, L2_ffn_ln_g, L2_ffn_ln_b, L2_ffn_w1, L2_ffn_b1, L2_ffn_w2, L2_ffn_b2, L2_c, L2_wmod, L3_attn_w_qkv, L3_attn_w_proj, L3_attn_b_proj, L3_ffn_expert_sel, L3_ffn_keys, L3_ffn_values, L3_ffn_route_scale, L3_c, L3_wmod):

    def _L0_attn_ref(x, W_attn, W_proj):
        import math
        import jax, jax.numpy as jnp
        import numpy as np
        N_EMBD = 128
        N_HEAD = 16
        N_QUERY_SETS = 4
        B, T = (8, 128)
        Bz, Tz, C = x.shape
        hd = C // N_HEAD
        scale = 1.0 / math.sqrt(hd)
        qkv = x @ W_attn.T
        parts = jnp.split(qkv, N_QUERY_SETS + 2, axis=-1)
        k = parts[-2].reshape(Bz, Tz, N_HEAD, hd).transpose(0, 2, 1, 3)
        v = parts[-1].reshape(Bz, Tz, N_HEAD, hd).transpose(0, 2, 1, 3)
        causal = jnp.tril(jnp.ones((Tz, Tz), dtype=bool))
        outs = []
        for g in range(N_QUERY_SETS):
            q = parts[g].reshape(Bz, Tz, N_HEAD, hd).transpose(0, 2, 1, 3)
            att = jnp.einsum('bhqd,bhkd->bhqk', q, k) * scale
            att = jnp.where(causal, att, -jnp.inf)
            att = jax.nn.softmax(att, axis=-1)
            y = jnp.einsum('bhqk,bhkd->bhqd', att, v)
            outs.append(y.transpose(0, 2, 1, 3).reshape(Bz, Tz, C))
        combined = jnp.concatenate(outs, axis=-1)
        return combined @ W_proj.T

    def _L0_ffn_ref(hidden_states, router_weight, router_bias, gate_up_proj, gate_up_bias, down_proj, down_bias):
        import jax, jax.numpy as jnp
        import numpy as np
        ALPHA = 1.702
        LIMIT = 7.0
        TOP_K = 2
        B, S, H = hidden_states.shape
        E, _, two_I = gate_up_proj.shape
        I = two_I // 2
        flat = hidden_states.reshape(B * S, H)
        logits = flat @ router_weight.T + router_bias
        scores = jax.nn.softmax(logits, axis=-1)
        topk_w, topk_idx = jax.lax.top_k(scores, TOP_K)
        gu = jnp.einsum('th,ehn->ten', flat, gate_up_proj) + gate_up_bias
        gate = jnp.minimum(gu[..., :I], LIMIT)
        up = jnp.clip(gu[..., I:], -LIMIT, LIMIT)
        glu = gate * jax.nn.sigmoid(gate * ALPHA)
        act = (up + 1.0) * glu
        down = jnp.einsum('tei,eih->teh', act, down_proj) + down_bias
        gathered = jnp.take_along_axis(down, topk_idx[:, :, None], axis=1)
        out = (gathered * topk_w[:, :, None]).sum(axis=1)
        return out.reshape(B, S, H)

    def _L1_attn_ref(inputs, Wqkv_w, Wqkv_b, Wo_w, Wo_b, ghost):
        import jax, jax.numpy as jnp
        import numpy as np
        import math
        EMBED_DIM = 128
        NHEAD = 16
        HEAD_DIM = 64
        BATCH = 2
        SEQ = 256
        b, s, e = inputs.shape
        QKV = inputs @ Wqkv_w.T + Wqkv_b
        QKVh = QKV.reshape(b, s, 3, NHEAD, HEAD_DIM).transpose(0, 3, 2, 1, 4)
        Q, K, V = (QKVh[:, :, 0], QKVh[:, :, 1], QKVh[:, :, 2])
        scores = jnp.einsum('bhqd,bhkd->bhqk', Q, K) / math.sqrt(HEAD_DIM)
        row = jnp.arange(s)
        mask = jnp.where(row[None, :] > row[:, None], -jnp.inf, 0.0).astype(scores.dtype)
        scores = scores + mask[None, None]
        m = jnp.max(scores, axis=-1, keepdims=True)
        z = jnp.exp(scores - m)
        S = z / (jnp.sum(z, axis=-1, keepdims=True) + ghost.reshape(1, -1, 1, 1))
        A = jnp.einsum('bhqk,bhkd->bhqd', S, V)
        A = A.transpose(0, 2, 1, 3).reshape(b, s, NHEAD * HEAD_DIM)
        return A @ Wo_w.T + Wo_b

    def _L1_ffn_ref(x, w_gate, w_up, w_down):
        import jax, jax.numpy as jnp
        import numpy as np
        BLOCK = 16
        _GRID = jnp.array([0.0, 0.5, 1.0, 1.5, 2.0, 3.0, 4.0, 6.0], dtype=jnp.float32)
        _MID = jnp.array([0.25, 0.75, 1.25, 1.75, 2.5, 3.5, 5.0], dtype=jnp.float32)

        def fp4_quant_dequant(x):
            shape = x.shape
            xb = x.reshape(shape[:-1] + (shape[-1] // BLOCK, BLOCK))
            scale = jnp.max(jnp.abs(xb), axis=-1, keepdims=True) / 6.0
            scale = jnp.maximum(scale, jnp.float32(1e-12))
            xn = xb / scale
            idx = jnp.searchsorted(_MID, jnp.abs(xn))
            q = _GRID[idx] * jnp.sign(xn) * scale
            return q.reshape(shape)

        def fp4_linear(x, w):
            xq = fp4_quant_dequant(x)
            wq = fp4_quant_dequant(w)
            return jnp.einsum('bsk,nk->bsn', xq, wq)
        gate = fp4_linear(x, w_gate)
        y = fp4_linear(x, w_up)
        h = jax.nn.silu(gate) * y
        return fp4_linear(h, w_down)

    def _L2_attn_ref(x, Wq, bq, Wk, bk, Wv, bv, Wo, bo):
        import jax, jax.numpy as jnp
        import numpy as np
        B, S, D = (4, 256, 128)
        KD, VD = (128, 128)
        q = jnp.einsum('bsd,kd->bsk', x, Wq) + bq
        k = jnp.einsum('bsd,kd->bsk', x, Wk) + bk
        v = jnp.einsum('bsd,vd->bsv', x, Wv) + bv
        scores = jnp.einsum('bqk,bsk->bqs', q, k) / jnp.sqrt(jnp.float32(KD))
        sign_mask = jnp.sign(scores)
        sign_mask = sign_mask + (sign_mask == 0).astype(jnp.float32)
        seq = scores.shape[-1]
        causal = jnp.tril(jnp.ones((seq, seq), dtype=bool))
        masked = jnp.where(causal, scores * sign_mask, -jnp.inf)
        weights = jax.nn.softmax(masked, axis=2)
        out = jnp.einsum('bqs,bsv->bqv', weights, v)
        return jnp.einsum('bqv,dv->bqd', out, Wo) + bo

    def _L2_ffn_ref(x, wqkv, q_scale, k_scale, wo, ln_g, ln_b, w1, b1, w2, b2):
        import jax, jax.numpy as jnp
        import numpy as np
        DIM = 128
        DEPTH = 2
        HEADS = 8
        DIM_HEAD = 64
        WINDOW = 64
        INNER = HEADS * DIM_HEAD
        HID = int(DIM * 4 * 2 / 3)
        B, N = (2, 1024)
        QK_SCALE = 8.0

        def shift_token(t):
            t1, t2 = jnp.split(t, 2, axis=-1)
            t2 = jnp.pad(t2, ((0, 0), (1, 0), (0, 0)))[:, :-1]
            return jnp.concatenate([t1, t2], axis=-1)

        def l2norm(t):
            return t / jnp.clip(jnp.linalg.norm(t, axis=-1, keepdims=True), 1e-12)

        def rotate_half(x):
            x1, x2 = jnp.split(x, 2, axis=-1)
            return jnp.concatenate([-x2, x1], axis=-1)

        def rotary_xpos(q, k):
            n = q.shape[-2]
            half_idx = jnp.arange(0, DIM_HEAD, 2, dtype=jnp.float32)
            inv_freq = 1.0 / 10000.0 ** (half_idx / DIM_HEAD)
            t = jnp.arange(n, dtype=jnp.float32)
            freqs = t[:, None] * inv_freq[None, :]
            freqs = jnp.concatenate([freqs, freqs], axis=-1)
            base = (half_idx + 0.4 * DIM_HEAD) / (1.4 * DIM_HEAD)
            power = (t - n // 2) / float(WINDOW // 2)
            scale = base[None, :] ** power[:, None]
            scale = jnp.concatenate([scale, scale], axis=-1)
            cos, sin = (jnp.cos(freqs), jnp.sin(freqs))
            q = q * cos * scale + rotate_half(q) * sin * scale
            k = k * cos / scale + rotate_half(k) * sin / scale
            return (q, k)

        def local_attention(q, k, v):
            b, h, n, d = q.shape
            w = n // WINDOW
            bq = q.reshape(b, h, w, WINDOW, d) * QK_SCALE
            bk = k.reshape(b, h, w, WINDOW, d)
            bv = v.reshape(b, h, w, WINDOW, d)

            def look_around(t):
                p = jnp.pad(t, ((0, 0), (0, 0), (1, 0), (0, 0), (0, 0)))
                return jnp.concatenate([p[:, :, :w], p[:, :, 1:]], axis=3)
            bk, bv = (look_around(bk), look_around(bv))
            bt = jnp.arange(n).reshape(w, WINDOW)
            btp = jnp.pad(bt, ((1, 0), (0, 0)), constant_values=-1)
            btk = jnp.concatenate([btp[:w], btp[1:]], axis=1)
            sim = jnp.einsum('bhwid,bhwjd->bhwij', bq, bk)
            i = bt[:, :, None]
            j = btk[:, None, :]
            mask = (i < j) | (i > j + WINDOW) | (j == -1)
            sim = jnp.where(mask, -jnp.finfo(sim.dtype).max, sim)
            attn = jax.nn.softmax(sim, axis=-1)
            out = jnp.einsum('bhwij,bhwjd->bhwid', attn, bv)
            return out.reshape(b, h, n, d)

        def _layer(x, wqkv, qs, ksc, wo, lg, lb, w1, b1, w2, b2):
            b, n, _ = x.shape
            h = shift_token(x)
            qkv = h @ wqkv
            q, k, v = jnp.split(qkv, 3, axis=-1)
            to_heads = lambda t: t.reshape(b, n, HEADS, DIM_HEAD).transpose(0, 2, 1, 3)
            q, k, v = (to_heads(q), to_heads(k), to_heads(v))
            q = l2norm(q) * qs
            k = l2norm(k) * ksc
            q, k = rotary_xpos(q, k)
            o = local_attention(q, k, v)
            o = o.transpose(0, 2, 1, 3).reshape(b, n, INNER)
            x = x + o @ wo
            h = shift_token(x)
            mu = h.mean(-1, keepdims=True)
            var = h.var(-1, keepdims=True)
            h = (h - mu) / jnp.sqrt(var + 1e-05) * lg + lb
            h = h @ w1 + b1
            a, g = jnp.split(h, 2, axis=-1)
            h = a * jax.nn.gelu(g, approximate=False)
            x = x + h @ w2 + b2
            return x
        for l in range(DEPTH):
            x = _layer(x, wqkv[l], q_scale[l], k_scale[l], wo[l], ln_g[l], ln_b[l], w1[l], b1[l], w2[l], b2[l])
        return x

    def _L3_attn_ref(x, w_qkv, w_proj, b_proj):
        import jax, jax.numpy as jnp
        import numpy as np
        B, N, DIM = (2, 256, 128)
        H = 16
        HD = DIM // H
        b, n, c = x.shape
        scale = HD ** (-0.5)
        qkv = jnp.einsum('bnc,cd->bnd', x, w_qkv)
        qkv = qkv.reshape(b, n, 3, H, HD).transpose(2, 0, 3, 1, 4)
        q, k, v = (qkv[0], qkv[1], qkv[2])
        q = q * scale
        attn = jnp.einsum('bhnd,bhmd->bhnm', q, k)
        attn = jax.nn.softmax(attn, axis=-1)
        out = jnp.einsum('bhnm,bhmd->bhnd', attn, v)
        out = out.transpose(0, 2, 1, 3).reshape(b, n, c)
        return jnp.einsum('bnc,cd->bnd', out, w_proj) + b_proj

    def _L3_ffn_ref(x, expert_sel, keys, values, route_scale):
        import jax, jax.numpy as jnp
        import numpy as np
        DMODEL = 128
        N_EXPERTS = 16
        EXPERT_SIZE = 32
        K = 4
        sel_logits = jnp.einsum('btd,ed->bte', x, expert_sel)
        sel_probs = jax.nn.sigmoid(sel_logits)
        _, sel_index = jax.lax.top_k(sel_probs, K)
        sel_val = jnp.take_along_axis(sel_probs, sel_index, axis=-1)
        sel_val = sel_val / jnp.clip(sel_val.sum(-1, keepdims=True), 1e-09)
        sel_val = sel_val * route_scale
        scores_all = jax.nn.relu(jnp.einsum('btd,edh->bteh', x, keys))
        values_all = jnp.einsum('bteh,ehv->btev', scores_all, values)
        sel_idx_exp = sel_index[..., None]
        selected = jnp.take_along_axis(values_all, sel_idx_exp, axis=2)
        out = (selected * sel_val[..., None]).sum(axis=2)
        return out
    x = L0_attn_x
    mod = (_silu(L0_c) @ L0_wmod).reshape(L0_c.shape[0], 6, 1, -1)
    sa, ca, ga, sb, cb, gb = (mod[:, 0], mod[:, 1], mod[:, 2], mod[:, 3], mod[:, 4], mod[:, 5])
    ga = (2 * (ga >= 0) - 1) * jnp.maximum(jnp.abs(ga), 0.25)
    gb = (2 * (gb >= 0) - 1) * jnp.maximum(jnp.abs(gb), 0.25)
    h = _layernorm(x, axis=-1) * (1 + ca) + sa
    x = x + ga * _L0_attn_ref(h, L0_attn_W_attn, L0_attn_W_proj)
    h = _layernorm(x, axis=-1) * (1 + cb) + sb
    x = x + gb * _L0_ffn_ref(h, L0_ffn_router_weight, L0_ffn_router_bias, L0_ffn_gate_up_proj, L0_ffn_gate_up_bias, L0_ffn_down_proj, L0_ffn_down_bias)
    mod = (_silu(L1_c) @ L1_wmod).reshape(L1_c.shape[0], 6, 1, -1)
    sa, ca, ga, sb, cb, gb = (mod[:, 0], mod[:, 1], mod[:, 2], mod[:, 3], mod[:, 4], mod[:, 5])
    ga = (2 * (ga >= 0) - 1) * jnp.maximum(jnp.abs(ga), 0.25)
    gb = (2 * (gb >= 0) - 1) * jnp.maximum(jnp.abs(gb), 0.25)
    h = _layernorm(x, axis=-1) * (1 + ca) + sa
    x = x + ga * _L1_attn_ref(h, L1_attn_Wqkv_w, L1_attn_Wqkv_b, L1_attn_Wo_w, L1_attn_Wo_b, L1_attn_ghost)
    h = _layernorm(x, axis=-1) * (1 + cb) + sb
    x = x + gb * _L1_ffn_ref(h, L1_ffn_w_gate, L1_ffn_w_up, L1_ffn_w_down)
    mod = (_silu(L2_c) @ L2_wmod).reshape(L2_c.shape[0], 6, 1, -1)
    sa, ca, ga, sb, cb, gb = (mod[:, 0], mod[:, 1], mod[:, 2], mod[:, 3], mod[:, 4], mod[:, 5])
    ga = (2 * (ga >= 0) - 1) * jnp.maximum(jnp.abs(ga), 0.25)
    gb = (2 * (gb >= 0) - 1) * jnp.maximum(jnp.abs(gb), 0.25)
    h = _layernorm(x, axis=-1) * (1 + ca) + sa
    x = x + ga * _L2_attn_ref(h, L2_attn_Wq, L2_attn_bq, L2_attn_Wk, L2_attn_bk, L2_attn_Wv, L2_attn_bv, L2_attn_Wo, L2_attn_bo)
    h = _layernorm(x, axis=-1) * (1 + cb) + sb
    x = x + gb * _L2_ffn_ref(h, L2_ffn_wqkv, L2_ffn_q_scale, L2_ffn_k_scale, L2_ffn_wo, L2_ffn_ln_g, L2_ffn_ln_b, L2_ffn_w1, L2_ffn_b1, L2_ffn_w2, L2_ffn_b2)
    mod = (_silu(L3_c) @ L3_wmod).reshape(L3_c.shape[0], 6, 1, -1)
    sa, ca, ga, sb, cb, gb = (mod[:, 0], mod[:, 1], mod[:, 2], mod[:, 3], mod[:, 4], mod[:, 5])
    ga = (2 * (ga >= 0) - 1) * jnp.maximum(jnp.abs(ga), 0.25)
    gb = (2 * (gb >= 0) - 1) * jnp.maximum(jnp.abs(gb), 0.25)
    h = _layernorm(x, axis=-1) * (1 + ca) + sa
    x = x + ga * _L3_attn_ref(h, L3_attn_w_qkv, L3_attn_w_proj, L3_attn_b_proj)
    h = _layernorm(x, axis=-1) * (1 + cb) + sb
    x = x + gb * _L3_ffn_ref(h, L3_ffn_expert_sel, L3_ffn_keys, L3_ffn_values, L3_ffn_route_scale)
    return x

_drawn_inputs = setup_inputs


def setup_inputs(seed=0):
    import zlib

    import numpy as np

    out = dict(_drawn_inputs(seed))
    spreads = {'L0_ffn_router_bias': (0.0, 0.8),
     'L0_ffn_gate_up_bias': (0.0, 0.8),
     'L0_ffn_down_bias': (0.0, 0.1),
     'L1_attn_Wqkv_b': (0.0, 0.1),
     'L1_attn_Wo_b': (0.0, 0.326),
     'L2_ffn_q_scale': (1.0, 0.6),
     'L2_ffn_k_scale': (1.0, 0.6),
     'L2_ffn_ln_g': (1.0, 0.6),
     'L2_ffn_ln_b': (0.0, 0.8),
     'L2_ffn_b1': (0.0, 0.8),
     'L2_ffn_b2': (0.0, 0.944)}
    factors = {'L0_ffn_gate_up_proj': 4.596,
     'L0_ffn_down_proj': 4.174,
     'L1_attn_ghost': 6.401,
     'L1_ffn_w_gate': 8.0,
     'L1_ffn_w_up': 8.0,
     'L1_ffn_w_down': 8.0,
     'L2_attn_bq': 64.0,
     'L2_attn_bk': 64.0,
     'L2_attn_bv': 8.0,
     'L2_attn_bo': 8.0,
     'L2_ffn_wqkv': 6.037,
     'L2_ffn_wo': 6.061,
     'L2_ffn_w1': 8.0,
     'L2_ffn_w2': 8.0,
     'L3_attn_b_proj': 64.0,
     'L3_ffn_expert_sel': 11.493,
     'L3_ffn_keys': 12.436,
     'L3_ffn_values': 8.407,
     'L3_attn_w_qkv': 4.105,
     'L3_attn_w_proj': 4.104}
    for name, (base, spread) in spreads.items():
        noise = np.random.default_rng([zlib.crc32(name.encode()), seed]).standard_normal(out[name].shape)
        drawn = base * np.exp(spread * noise) if base else spread * noise
        out[name] = jnp.asarray(drawn.astype(out[name].dtype))
    for name, factor in factors.items():
        out[name] = (out[name] * factor).astype(out[name].dtype)
    return out
```

```python
from contextlib import ExitStack

import concourse.bass as bass
import numpy as np
from concourse import mybir

ALU = mybir.AluOpType
ACT = mybir.ActivationFunctionType
F32 = mybir.dt.float32
BF16 = mybir.dt.bfloat16
AX_X = mybir.AxisListType.X

P = 128
BATCH = 16
TOK = 256
QT = TOK // P
D = 128
EPS = 1e-5
BIG = -1.0e30
WINDOW = 64


class Chain:

    def __init__(self, eng, sem, turn, per):
        self.eng, self.sem, self.turn, self.per, self.n = eng, sem, turn, per, 0

    def value(self, n):
        return self.turn * self.per + n if self.per else n

    def link(self, ins):
        self.n += 1
        ins.then_inc(self.sem, 1)
        self.eng.wait_ge(self.sem, self.value(self.n))

    def end(self):
        assert self.per in (0, self.n), f"the chain has {self.n} links in a turn, not {self.per}"


class Scope:

    def __init__(self, nc, ctx, name):
        self.nc, self.ctx, self.name, self.sems = nc, ctx, name, []

    def sb(self, name, shape, dt=F32):
        return self.ctx.enter_context(self.nc.sbuf_tensor(f"{self.name}_{name}", list(shape), dt))

    def bank(self, name, dt=F32):
        return self.ctx.enter_context(self.nc.psum_tensor(f"{self.name}_{name}", [P, 512], dt))

    def sem(self, name):
        self.sems.append(self.ctx.enter_context(self.nc.semaphore(f"{self.name}_{name}")))
        return self.sems[-1]

    def block(self):
        self.ctx.callback(self.clear)
        return self.ctx.enter_context(self.nc.Block())

    def clear(self):
        with self.nc.Block() as block:
            @block.gpsimd
            def _(pool):
                for sem in self.sems:
                    pool.sem_clear(sem)


def tiles(x):
    return x.rearrange("p (t q) -> p t q", q=P)


def constants_phase(nc, dram, res):
    with ExitStack() as ctx:
        s = Scope(nc, ctx, "cst")
        loaded = s.sem("loaded")
        narrowed = s.sem("narrowed")
        masks_f = s.sb("masks_f", [P, 6, P])
        head_f = s.sb("head_f", [P, 16, P])
        block = s.block()

        @block.sync
        def _(sp):
            sp.dma_start(res["x"][:, :, :], dram["x"].rearrange("b (t p) d -> p (b t) d", p=P)).then_inc(loaded, 16)
            sp.dma_start(res["ident"][:, :], dram["c_ident"]).then_inc(loaded, 16)
            sp.dma_start(masks_f[:, :, :], dram["c_masks"]).then_inc(loaded, 16)
            sp.dma_start(head_f[:, :, :], dram["c_minus_head"]).then_inc(loaded, 16)
            sp.dma_start(res["head_rows"][:, :], dram["c_head_rows"]).then_inc(loaded, 16)
            sp.wait_ge(loaded, 5 * 16)

        @block.vector
        def _(dve):
            dve.wait_ge(loaded, 5 * 16)
            dve.tensor_copy(res["identb"][:, :], res["ident"][:, :])
            dve.tensor_copy(res["masks"][:, :, :], masks_f[:, :, :])
            dve.tensor_copy(res["minus_head"][:, :, :], head_f[:, :, :]).then_inc(narrowed, 1)
            dve.wait_ge(narrowed, 1)


def modulation_phase(nc, layer, dram, res):
    with ExitStack() as ctx:
        s = Scope(nc, ctx, f"mod{layer}")
        ct = s.sb("ct", [P, BATCH])
        wmod = s.sb("wmod", [P, 6, D])
        e1 = s.sb("e1", [P, BATCH])
        e2 = s.sb("e2", [P, BATCH])
        silu = s.sb("silu", [P, BATCH])
        silu_wide = s.sb("silu_wide", [P, BATCH, P])
        above = s.sb("above", [P, 512])
        below = s.sb("below", [P, 512])
        size = s.sb("size", [P, 512])
        shifts = s.bank("shifts")
        gates = [s.bank(f"gates{n}") for n in range(2)]
        loaded, negexp, widened, products, read, chained = (
            s.sem(x) for x in ("loaded", "negexp", "widened", "products", "read", "chained"))
        block = s.block()

        @block.sync
        def _(sp):
            sp.dma_start(ct[:, :], dram[f"L{layer}_cT"]).then_inc(loaded, 16)
            sp.dma_start(wmod[:, :, :], dram[f"L{layer}_wmod"].rearrange("k (j d) -> k j d", d=D)).then_inc(loaded, 16)

        @block.scalar
        def _(act):
            act.wait_ge(loaded, 32)
            nc.scalar.activation(e1[:, :], ct[:, :], ACT.Exp, scale=-1.0).then_inc(negexp, 1)

        @block.vector
        def _(dve):
            chain = Chain(dve, chained, 0, 0)
            dve.wait_ge(loaded, 32)
            dve.wait_ge(negexp, 1)
            chain.link(dve.tensor_scalar(e2[:, :], e1[:, :], 1.0, None, ALU.add))
            chain.link(dve.reciprocal(e1[:, :], e2[:, :]))
            chain.link(dve.tensor_tensor(silu[:, :], ct[:, :], e1[:, :], ALU.mult))
            dve.tensor_copy(silu_wide[:, :, :], silu[:, :].unsqueeze(2).broadcast_to([P, BATCH, P])).then_inc(widened, 1)
            dve.wait_ge(products, 1)
            for n in range(4):
                dve.tensor_scalar(res["mod"][:, n, :], shifts[:, n * BATCH:(n + 1) * BATCH],
                                  float(n % 2), None, ALU.add)
            for n in range(8):
                dve.wait_ge(products, n + 2)
                g = gates[n % 2][:, :]
                chain.link(dve.tensor_scalar(size[:, :], g, 0.25, None, ALU.max))
                chain.link(dve.scalar_tensor_tensor(out=above[:, :], in0=g, scalar=0.0, in1=size[:, :],
                                                    op0=ALU.is_ge, op1=ALU.mult))
                chain.link(dve.tensor_scalar(size[:, :], g, -0.25, None, ALU.min))
                chain.link(dve.scalar_tensor_tensor(out=below[:, :], in0=g, scalar=0.0, in1=size[:, :],
                                                    op0=ALU.is_lt, op1=ALU.mult))
                out = res["gate"][:, n // 4, 4 * (n % 4):4 * (n % 4) + 4, :]
                dve.tensor_tensor(out.rearrange("p b d -> p (b d)"), above[:, :], below[:, :], ALU.add).then_inc(read, 1)
                dve.wait_ge(read, n + 1)

        @block.tensor
        def _(pe):
            pe.wait_ge(loaded, 32)
            pe.wait_ge(widened, 1)
            for n, j in enumerate((0, 1, 3, 4)):
                mm = pe.matmul(shifts[:, n * BATCH:(n + 1) * BATCH], wmod[:, j, :], silu[:, :],
                               start=(n == 0), stop=True, skip_group_check=True)
            mm.then_inc(products, 1)
            for n in range(8):
                if n >= 2:
                    pe.wait_ge(read, n - 1)
                for k in range(4):
                    mm = pe.matmul(gates[n % 2][:, k * P:(k + 1) * P], silu_wide[:, 4 * (n % 4) + k, :],
                                   wmod[:, (2, 5)[n // 4], :], start=(k == 0), stop=True, skip_group_check=True)
                mm.then_inc(products, 1)


def store_phase(nc, res, out):
    with ExitStack() as ctx:
        s = Scope(nc, ctx, "st")
        stored = s.sem("stored")
        block = s.block()

        @block.sync
        def _(sp):
            sp.dma_start(out.rearrange("b (t p) d -> p (b t) d", p=P), res["x"][:, :, :]).then_inc(stored, 16)
            sp.wait_ge(stored, 16)


class Norm:

    def __init__(self, s, turns_per_loop=1):
        self.stats, self.mv = s.sb("stats", [P, QT, 6]), s.sb("mv", [P, QT, 2])
        self.var, self.power, self.rstd = s.sb("var", [P, QT]), s.sb("power", [P, QT]), s.sb("rstd", [P, QT])
        self.idle = s.sb("idle", [P, 2])
        self.var_ready, self.rstd_ready, self.power_ready = s.sem("var_ready"), s.sem("rstd_ready"), s.sem("power_ready")
        self.per = turns_per_loop

    def start(self, dve):
        dve.memset(self.idle[:, :], 0.0)
        dve.memset(self.power[:, :], -0.5).then_inc(self.power_ready, 1)

    def vector(self, dve, chain, turn, x_at, xhat, ready, nth=0):
        for t in range(QT):
            last = dve.bn_stats(self.stats[:, t, :], x_at(t))
        chain.link(last)
        dve.tensor_copy(self.idle[:, 1:2], self.idle[:, 0:1])
        for t in range(QT):
            last = dve.bn_aggr(self.mv[:, t, :], self.stats[:, t, :])
        chain.link(last)
        dve.tensor_scalar(self.var[:, :], self.mv[:, :, 1], EPS, None, ALU.add).then_inc(self.var_ready, 1)
        dve.wait_ge(self.rstd_ready, turn * self.per + nth + 1)
        for t in range(QT):
            last = dve.tensor_scalar(xhat[:, t, :], x_at(t), self.mv[:, t, 0:1], self.rstd[:, t:t + 1],
                                     ALU.subtract, ALU.mult)
        last.then_inc(ready, 1)

    def gpsimd(self, pool, turn, nth=0):
        pool.wait_ge(self.var_ready, turn * self.per + nth + 1)
        pool.tensor_tensor(self.rstd[:, :], self.var[:, :], self.power[:, :], ALU.pow).then_inc(self.rstd_ready, 1)


class Ring:

    def __init__(self, s, name, banks):
        self.banks = [s.bank(f"{name}_bank{n}") for n in range(banks)]
        self.full, self.free = s.sem(f"{name}_full"), s.sem(f"{name}_free")

    def start(self, reader):
        reader.sem_inc(self.free, len(self.banks))


class Uses:

    def __init__(self, ring, turn, odd, per):
        self.ring, self.turn, self.odd, self.per, self.n = ring, turn, odd, per, 0

    def _bank(self):
        self.n += 1
        return self.ring.banks[(self.odd * self.per + self.n - 1) % len(self.ring.banks)]

    def fill(self, pe):
        pe.wait_ge(self.ring.free, self.turn * self.per + self.n + 1)
        return self._bank()

    def filled(self, mm):
        mm.then_inc(self.ring.full, 1)

    def take(self, reader):
        reader.wait_ge(self.ring.full, self.turn * self.per + self.n + 1)
        return self._bank()

    def emptied(self, ins):
        ins.then_inc(self.ring.free, 1)

    def settled(self, reader):
        reader.wait_ge(self.ring.free, self.turn * self.per + self.n + len(self.ring.banks))

    def end(self):
        assert self.n == self.per, f"{self.ring.full}: {self.n} uses in a batch, not {self.per}"


class Attn:

    def __init__(self, name, sets, heads, hd, kind, packed, scale):
        self.name, self.sets, self.heads, self.hd, self.kind = name, sets, heads, hd, kind
        self.packed, self.scale = packed, scale
        self.units = sets * heads
        self.pairs = self.units // 2
        self.lone = 2 * heads if sets > 1 else heads
        self.by_feature = hd + 1 <= 32
        self.vw = 32 if self.by_feature else hd + 1
        self.width = self.units * hd
        self.per_bank = 16 if self.by_feature else 512 // self.vw
        self.out_banks = -(-self.units // self.per_bank)

    def keys(self, qt):
        return QT if self.kind == "full" else qt + 1

    def mask(self, qt, kb):
        if self.kind == "causal":
            return 0 if qt == kb else None
        if self.kind == "window":
            return 2 if qt == kb else 4
        return None

    def lone_of(self, u):
        return 2 * (u // 4) + u % 2 if self.sets > 1 else u

    def head_of(self, u):
        return u // self.sets

    def max_chunks(self, qt):
        n = 4 // self.keys(qt)
        return [(u, n) for u in range(0, self.units, n)]

    def exp_chunks(self, qt):
        return [(kb, u) for u in range(0, self.units, 4) for kb in range(self.keys(qt))]

    @property
    def n_exp(self):
        return sum(len(self.exp_chunks(qt)) for qt in range(QT))

    @property
    def n_max(self):
        return sum(len(self.max_chunks(qt)) for qt in range(QT)) + QT

    def front(self, project):
        steps = [("norm",), ("hT",)] + project
        first = [("max", 0, j) for j in range(len(self.max_chunks(0)))]
        second = [("max", 1, j) for j in range(len(self.max_chunks(1)))]
        cut = min(2, len(second) - 1)
        return steps + first + [("parts", 0)] + second[:cut] + [("maxT", 0)] + second[cut:] + [("parts", 1), ("maxT", 1)]

    def back(self):
        if self.by_feature:
            at = [(n, n, ("exp", qt, j)) for n, (qt, j) in
                  enumerate((qt, j) for qt in range(QT) for j in range(len(self.exp_chunks(qt))))]
            done = 0
            for qt in range(QT):
                for k in range(self.out_banks):
                    done += len(self.exp_chunks(qt)) // self.out_banks
                    at += [(done + 3, 100 + done, ("drain", qt, k)), (done + 5, 100 + done, ("turn", qt, k))]
                at += [(done + 7, 200, ("outT", qt)), (done + 9, 200, ("out", qt))]
            at.append((self.n_exp + 1, 50, ("heads", 1)))
            return [step for _, _, step in sorted(at)]
        first = [("exp", 0, j) for j in range(len(self.exp_chunks(0)))]
        second = [("exp", 1, j) for j in range(len(self.exp_chunks(1)))]
        c = min(2, len(second) // 2)
        return (first + [("heads", 0)] + second[:c] + [("outT", 0)] + second[c:2 * c] + [("out", 0)] + second[2 * c:]
                + [("heads", 1), ("outT", 1), ("out", 1)])


def merged(front, back):
    out, f, k = [], 0, 0
    while f < len(front) or k < len(back):
        if k >= len(back) or (f < len(front) and f * len(back) <= k * len(front)):
            out.append(("front",) + front[f])
            f += 1
        else:
            out.append(("back",) + back[k])
            k += 1
    return out


def step_lists(a, project):
    both = merged(a.front(project), a.back())
    fronts, backs = [x for x in both if x[0] == "front"], [x for x in both if x[0] == "back"]
    return lambda back_turn, front_turn: fronts if back_turn is None else backs if front_turn is None else both


def pipelined(eng, go):
    go(None, 0, 0, 0)
    with eng.Fori(0, (BATCH - 2) // 2) as pair:
        go(pair * 2, 0, pair * 2 + 1, 1)
        go(pair * 2 + 1, 1, pair * 2 + 2, 0)
    go(BATCH - 2, 0, BATCH - 1, 1)
    go(BATCH - 1, 1, None, 0)


class Attention:

    def __init__(self, s, nc, a, res, front_links, back_links, v_uses, q_uses, v_banks=2, q_banks=1, out_bias=None,
                 ghost=None):
        self.s, self.nc, self.a, self.res = s, nc, a, res
        self.front_links, self.back_links, self.v_uses, self.q_uses = front_links, back_links, v_uses, q_uses
        self.out_bias, self.ghost = out_bias, ghost
        qk = BF16 if a.packed else F32
        self.qT = [s.sb(f"qT{n}", [P, a.pairs, TOK], qk) for n in range(2)]
        self.k_alone = [s.sb(f"k_alone{n}", [P, a.lone, TOK], qk) for n in range(2)]
        self.v = [s.sb(f"v{n}", [P, QT, a.heads, a.vw]) for n in range(2)]
        if a.by_feature:
            self.featured = [s.sb(f"featured{n}", [P, 512]) for n in range(2)]
        self.row_max = s.sb("row_max", [P, QT, a.heads, a.sets])
        self.rest = s.sb("rest", [P, a.heads, a.sets])
        self.max_parts = s.sb("max_parts", [P, QT, a.sets, P], BF16)
        self.maxT = [s.sb(f"maxT{n}", [P, QT, a.sets, P], BF16) for n in range(2)]
        self.probs = [s.sb(f"probs{n}", [P, 512]) for n in range(4)]
        self.inverse = s.sb("inverse", [P, a.units])
        self.denominator = s.sb("denominator", [P, a.units])
        self.heads_out = [s.sb(f"heads_out{n}", [P, a.width]) for n in range(QT if a.by_feature else 1)]
        self.heads_outT = s.sb("heads_outT", [P, a.width // P, P])
        self.w_out = s.sb("w_out", [P, a.width // P, D])
        self.xhat, self.hT, self.scratch = s.sb("xhat", [P, QT, D]), s.sb("hT", [P, TOK]), s.sb("scratch", [P, D])
        self.to_dve = Ring(s, "to_dve", v_banks)
        self.to_act = Ring(s, "to_act", q_banks) if q_banks else None
        self.scores = Ring(s, "scores", 2)
        self.tail = Ring(s, "tail", 1)
        if a.by_feature:
            self.outs = Ring(s, "outs", 2)
        else:
            self.out = [s.bank(f"out{n}") for n in range(a.out_banks)]
        self.xhat_ready, self.hT_ready, self.qkv_ready = s.sem("xhat_ready"), s.sem("hT_ready"), s.sem("qkv_ready")
        self.qT_ready = s.sem("qT_ready") if q_banks else None
        self.parts_ready, self.maxT_ready = s.sem("parts_ready"), s.sem("maxT_ready")
        self.probs_ready = self.scores.free
        self.probs_free = s.sem("probs_free")
        self.heads_ready, self.headsT_ready = s.sem("heads_ready"), s.sem("headsT_ready")
        self.front_chained, self.back_chained = s.sem("front_chained"), s.sem("back_chained")
        self.started, self.loaded = s.sem("started"), s.sem("loaded")

    def begin_vector(self, dve):
        self.to_dve.start(dve)
        self.tail.start(dve)
        dve.sem_inc(self.heads_ready, 1)
        for v in self.v:
            dve.memset(v[:, :, :, self.a.hd:self.a.hd + 1], 1.0)
            if self.a.vw > self.a.hd + 1:
                dve.memset(v[:, :, :, self.a.hd + 1:self.a.vw], 0.0)
        for k in self.k_alone:
            dve.memset(k[:, :, :], 0.0)
        dve.memset(self.max_parts[:, :, :, :], 0.0).then_inc(self.started, 1)

    def begin_scalar(self, act):
        self.scores.start(act)
        act.sem_inc(self.probs_free, 4)
        if self.to_act:
            self.to_act.start(act)
        if self.a.by_feature:
            self.outs.start(act)


    def pe_batch(self, pe, steps, project, bt, bo, ft, fo):
        a = self.a
        front = Uses(self.to_dve, ft, fo, self.v_uses)
        to_act = Uses(self.to_act, ft, fo, self.q_uses) if self.to_act else None
        scores, tail = Uses(self.scores, bt, bo, a.n_exp), Uses(self.tail, bt, bo, self.tail_uses)
        outs = Uses(self.outs, bt, bo, QT * a.out_banks) if a.by_feature else None
        lagging = []
        for half, kind, *at in steps:
            if kind == "norm":
                pass
            elif kind == "hT":
                self.pe_hT(pe, front, ft)
            elif kind == "max":
                self.pe_max(pe, front, at[0], *a.max_chunks(at[0])[at[1]], fo, first=at == [0, 0], turn=ft)
            elif kind == "parts":
                pass
            elif kind == "maxT":
                self.pe_maxT(pe, front, at[0], ft)
            elif kind == "exp":
                self.pe_scores(pe, scores, at[0], *a.exp_chunks(at[0])[at[1]], bo, bt, first=at[1] == 0)
                lagging.append((scores.n - 1, at[0]) + a.exp_chunks(at[0])[at[1]])
                if len(lagging) > 2:
                    self.pe_values(pe, outs, bt, bo, *lagging.pop(0))
            elif kind == "heads":
                while lagging:
                    self.pe_values(pe, outs, bt, bo, *lagging.pop(0))
            elif kind == "turn":
                self.pe_turn(pe, tail, at[0], at[1], bt)
            elif kind == "drain":
                pass
            elif kind == "outT":
                self.pe_outT(pe, tail, at[0], bt)
            elif kind == "out":
                self.pe_out(pe, tail, at[0], bt)
            else:
                project(pe, kind, at, front, to_act, ft, fo)
        if ft is not None:
            front.end()
            if to_act:
                to_act.end()
        if bt is not None:
            scores.end()
            tail.end()

    @property
    def tail_uses(self):
        return QT * (-(-(self.a.width // P) // 4) + 1 + (self.a.out_banks if self.a.by_feature else 0))

    def pe_hT(self, pe, front, turn):
        pe.wait_ge(self.xhat_ready, turn + 1)
        bank = front.fill(pe)
        for t in range(QT):
            mm = pe.transpose(bank[:, t * P:(t + 1) * P], self.xhat[:, t, :], self.res["ident"][:, :])
        front.filled(mm)

    def pe_max(self, pe, front, qt, u0, nu, odd, first, turn):
        a, nk = self.a, self.a.keys(qt)
        if first:
            pe.wait_ge(self.qkv_ready, turn + 1)
            if self.qT_ready:
                pe.wait_ge(self.qT_ready, turn + 1)
        bank = front.fill(pe)
        w = 2 * nk * P
        for n, u in enumerate(range(u0, u0 + nu, 2)):
            lone = a.lone_of(u)
            mm = pe.matmul(bank[:, n * w:(n + 1) * w].rearrange("p (h k) -> p h k", h=2),
                           self.qT[odd][:, u // 2, qt * P:(qt + 1) * P], self.k_alone[odd][:, lone:lone + 2, 0:nk * P],
                           start=(n == 0), stop=True, skip_group_check=True)
        for kb in range(nk):
            mask = a.mask(qt, kb)
            if mask is not None:
                out = bank[:, :].rearrange("p (h k) -> p h k", h=nu)[:, :, kb * P:(kb + 1) * P]
                mm = pe.matmul(out, self.res["identb"][:, :],
                               self.res["masks"][:, mask:mask + 1, :].broadcast_to([P, nu, P]),
                               start=False, stop=True, skip_group_check=True)
        front.filled(mm)

    def pe_maxT(self, pe, front, qt, turn):
        pe.wait_ge(self.parts_ready, turn * QT + qt + 1)
        bank = front.fill(pe)
        for s in range(self.a.sets):
            mm = pe.transpose(bank[:, :].bitcast(BF16)[:, s * P:(s + 1) * P], self.max_parts[:, qt, s, :],
                              self.res["identb"][:, :])
        front.filled(mm)

    def pe_scores(self, pe, scores, qt, kb, u0, odd, turn, first):
        a, res = self.a, self.res
        if first:
            pe.wait_ge(self.maxT_ready, turn * QT + qt + 1)
        bank = scores.fill(pe)
        queries, keys = slice(qt * P, (qt + 1) * P), slice(kb * P, (kb + 1) * P)
        units = bank[:, :].rearrange("p (u q) -> p u q", u=4)
        if a.sets > 1:
            for par in range(2):
                pe.matmul(units.rearrange("p (g two) q -> p g two q", two=2)[:, :, par, :],
                          self.k_alone[odd][:, a.lone_of(u0) + par, keys], self.qT[odd][:, u0 // 2:u0 // 2 + 2, queries],
                          start=(par == 0), stop=False, skip_group_check=True)
            mm = pe.matmul(units, res["minus_head"][:, a.head_of(u0), :], self.maxT[odd][:, qt, :, :],
                           start=False, stop=True, skip_group_check=True)
        else:
            for j in range(4):
                u = u0 + j
                pe.matmul(units[:, j, :], self.k_alone[odd][:, u, keys], self.qT[odd][:, u // 2, queries],
                          start=(j == 0), stop=False, skip_group_check=True)
            for j in range(4):
                mm = pe.matmul(units[:, j, :], res["minus_head"][:, u0 + j, :], self.maxT[odd][:, qt, 0, :],
                               start=False, stop=True, skip_group_check=True)
        mask = a.mask(qt, kb)
        if mask is not None:
            mm = pe.matmul(units, res["identb"][:, :], res["masks"][:, mask + 1:mask + 2, :].broadcast_to([P, 4, P]),
                           start=False, stop=True, skip_group_check=True)
        scores.filled(mm)

    def pe_values(self, pe, outs, turn, odd, n, qt, kb, u0):
        a = self.a
        pe.wait_ge(self.probs_ready, turn * a.n_exp + n + 3)
        if a.by_feature:
            if kb == 0 and u0 % 16 == 0:
                self.out_now = outs.fill(pe)
            probs = self.probs[(odd * a.n_exp + n) % 4]
            c = u0 % 16 // 4
            last = kb == a.keys(qt) - 1
            for j in range(4):
                mm = pe.matmul(self.out_now[32 * j:32 * j + 32, c * P:(c + 1) * P], self.v[odd][:, kb, a.head_of(u0 + j), :],
                               probs[:, j * P:(j + 1) * P], start=(kb == 0), stop=last, skip_group_check=True)
            mm.then_inc(self.probs_free, 1)
            if last and u0 % 16 == 12:
                pe.wait_ge(self.probs_free, turn * a.n_exp + n + 5)
                pe.sem_inc(self.outs.full, 1)
            return
        if kb == 0 and u0 == 0:
            pe.wait_ge(self.heads_ready, turn * QT + qt + 1)
        probs = self.probs[(odd * a.n_exp + n) % 4]
        for u in range(u0, u0 + 4):
            col = (u % a.per_bank) * a.vw
            mm = pe.matmul(self.out[u // a.per_bank][:, col:col + a.vw], probs[:, (u - u0) * P:(u - u0 + 1) * P],
                           self.v[odd][:, kb, a.head_of(u), :], start=(kb == 0 and u % a.per_bank == 0),
                           stop=(kb == a.keys(qt) - 1), skip_group_check=True)
        mm.then_inc(self.probs_free, 1)

    def pe_turn(self, pe, tail, qt, k, turn):
        n = qt * self.a.out_banks + k
        pe.wait_ge(self.outs.free, turn * QT * self.a.out_banks + n + 3)
        bank = tail.fill(pe)
        for c in range(4):
            mm = pe.transpose(bank[:, c * P:(c + 1) * P], self.featured[n % 2][:, c * P:(c + 1) * P], self.res["ident"][:, :])
        tail.filled(mm)

    def pe_outT(self, pe, tail, qt, turn):
        nt = self.a.width // P
        pe.wait_ge(self.heads_ready, turn * QT + qt + 2)
        for t0 in range(0, nt, 4):
            bank = tail.fill(pe)
            for t in range(t0, min(t0 + 4, nt)):
                mm = pe.transpose(bank[:, (t - t0) * P:(t - t0 + 1) * P], self.heads_out[qt % len(self.heads_out)][:, t * P:(t + 1) * P],
                                  self.res["ident"][:, :])
            tail.filled(mm)

    def pe_out(self, pe, tail, qt, turn):
        nt = self.a.width // P
        pe.wait_ge(self.headsT_ready, turn * QT + qt + 1)
        bank = tail.fill(pe)
        for t in range(nt):
            mm = pe.matmul(bank[:, 0:D], self.heads_outT[:, t, :], self.w_out[:, t, :], start=(t == 0), stop=(t == nt - 1))
        tail.filled(mm)


    def act_batch(self, act, steps, project, bt, bo, ft, fo):
        a = self.a
        scores = Uses(self.scores, bt, bo, a.n_exp)
        to_act = Uses(self.to_act, ft, fo, self.q_uses) if self.to_act else None
        outs = Uses(self.outs, bt, bo, QT * a.out_banks) if a.by_feature else None
        for half, kind, *at in steps:
            if kind == "exp":
                n = scores.n
                bank = scores.take(act)
                act.wait_ge(self.probs_free, bt * a.n_exp + n + 1)
                self.nc.scalar.activation(self.probs[(bo * a.n_exp + n) % 4][:, :], bank[:, :], ACT.Exp,
                                          scale=a.scale).then_inc(self.probs_ready, 1)
            elif kind == "drain":
                qt, k = at
                n = qt * a.out_banks + k
                bank = outs.take(act)
                self.nc.scalar.copy(self.featured[n % 2][:, :], bank[:, :]).then_inc(self.outs.free, 1)
            elif half == "front" and project:
                project(act, kind, at, to_act, ft, fo)


    def dve_batch(self, dve, steps, project, norm, modulate, finish, bt, bo, ft, fo):
        front = Uses(self.to_dve, ft, fo, self.v_uses)
        tail = Uses(self.tail, bt, bo, self.tail_uses)
        fchain = Chain(dve, self.front_chained, ft, self.front_links)
        bchain = Chain(dve, self.back_chained, bt, self.back_links)
        for half, kind, *at in steps:
            if kind == "norm":
                norm(dve, fchain, ft)
            elif kind == "hT":
                modulate(dve, front, ft)
            elif kind == "max":
                u0, nu = self.a.max_chunks(at[0])[at[1]]
                bank = front.take(dve)
                front.emptied(dve.tensor_reduce(
                    self.row_max[:, at[0], :, :].rearrange("p h s -> p (h s)")[:, u0:u0 + nu],
                    bank[:, :].rearrange("p (h k) -> p h k", h=nu), AX_X, ALU.max))
            elif kind == "parts":
                self.dve_parts(dve, front, fchain, at[0])
            elif kind == "maxT":
                bank = front.take(dve)
                front.emptied(dve.tensor_copy(self.maxT[fo][:, at[0], :, :].rearrange("p s q -> p (s q)"),
                                              bank[:, :].bitcast(BF16)[:, 0:self.a.sets * P]))
                front.settled(dve)
                dve.sem_inc(self.maxT_ready, 1)
            elif kind == "heads":
                if not self.a.by_feature:
                    self.dve_heads(dve, bchain, at[0], bt)
            elif kind == "turn":
                self.dve_turn(dve, tail, bchain, at[0], at[1])
            elif kind == "drain":
                pass
            elif kind == "outT":
                nt = self.a.width // P
                for t0 in range(0, nt, 4):
                    m = min(4, nt - t0)
                    bank = tail.take(dve)
                    tail.emptied(dve.tensor_copy(self.heads_outT[:, t0:t0 + m, :].rearrange("p t q -> p (t q)"),
                                                 bank[:, 0:m * P]))
                tail.settled(dve)
                dve.sem_inc(self.headsT_ready, 1)
            elif kind == "out":
                bank = tail.take(dve)
                finish(dve, bchain, tail, bt, at[0], bank)
            elif kind != "exp":
                project(dve, kind, at, front, fchain, ft, fo)
        if ft is not None:
            front.end()
            fchain.end()
        if bt is not None:
            tail.end()
            bchain.end()

    def dve_hT(self, dve, front, turn):
        bank = front.take(dve)
        front.emptied(dve.tensor_scalar(self.hT[:, :], bank[:, 0:TOK], self.res["mod"][:, 1, bass.ds(turn, 1)],
                                        self.res["mod"][:, 0, bass.ds(turn, 1)], ALU.mult, ALU.add))
        front.settled(dve)
        dve.sem_inc(self.hT_ready, 1)

    def dve_parts(self, dve, front, chain, qt):
        a = self.a
        front.settled(dve)
        parts = self.max_parts[:, qt, :, 0:48].rearrange("p s (t h) -> p t h s", t=3)[:, :, 0:a.heads, :]
        top = self.row_max[:, qt, :, :]
        chain.link(dve.tensor_copy(parts[:, 0, :, :], top))
        chain.link(dve.tensor_tensor(self.rest[:, :, :], top, parts[:, 0, :, :], ALU.subtract))
        chain.link(dve.tensor_copy(parts[:, 1, :, :], self.rest[:, :, :]))
        dve.tensor_tensor(parts[:, 2, :, :], self.rest[:, :, :], parts[:, 1, :, :],
                          ALU.subtract).then_inc(self.parts_ready, 1)

    def dve_heads(self, dve, chain, qt, turn):
        a = self.a
        done = sum(len(a.exp_chunks(q)) for q in range(qt + 1))
        dve.wait_ge(self.probs_free, turn * a.n_exp + done + 4)
        for ob in range(a.out_banks):
            u0, u1 = ob * a.per_bank, min(a.units, (ob + 1) * a.per_bank)
            o = self.out[ob][:, 0:(u1 - u0) * a.vw].rearrange("p (u w) -> p u w", w=a.vw)
            if self.ghost is None:
                chain.link(dve.reciprocal(self.inverse[:, u0:u1], o[:, :, a.hd]))
            else:
                chain.link(dve.tensor_tensor(self.denominator[:, u0:u1], o[:, :, a.hd], self.ghost[:, u0:u1], ALU.add))
                chain.link(dve.reciprocal(self.inverse[:, u0:u1], self.denominator[:, u0:u1]))
            ins = dve.tensor_tensor(
                self.heads_out[0][:, u0 * a.hd:u1 * a.hd].rearrange("p (u w) -> p u w", w=a.hd), o[:, :, 0:a.hd],
                self.inverse[:, u0:u1].unsqueeze(2).broadcast_to([P, u1 - u0, a.hd]), ALU.mult)
        ins.then_inc(self.heads_ready, 1)

    def dve_turn(self, dve, tail, chain, qt, k):
        a = self.a
        bank = tail.take(dve)
        o = bank[:, :].rearrange("p (u w) -> p u w", w=32)
        chain.link(dve.reciprocal(self.inverse[:, 0:16], o[:, :, a.hd]))
        ins = dve.tensor_tensor(
            self.heads_out[qt][:, 16 * k * a.hd:16 * (k + 1) * a.hd].rearrange("p (u w) -> p u w", w=a.hd), o[:, :, 0:a.hd],
            self.inverse[:, 0:16].unsqueeze(2).broadcast_to([P, 16, a.hd]), ALU.mult)
        tail.emptied(ins)
        if k == a.out_banks - 1:
            tail.settled(dve)
            dve.sem_inc(self.heads_ready, 1)

    def finish_x(self, dve, chain, tail, turn, qt, bank):
        x = x_tile(self.res, turn * QT + qt)
        g = self.res["gate"][:, 0, bass.ds(turn, 1), :].rearrange("p a d -> p (a d)")
        if self.out_bias is None:
            tail.emptied(dve.tensor_tensor(self.scratch[:, :], bank[:, 0:D], g, ALU.mult))
            tail.settled(dve)
        else:
            tail.emptied(dve.tensor_tensor(self.scratch[:, :], bank[:, 0:D], self.out_bias, ALU.add))
            tail.settled(dve)
            chain.link(dve.tensor_tensor(self.scratch[:, :], self.scratch[:, :], g, ALU.mult))
        chain.link(dve.tensor_tensor(x, x, self.scratch[:, :], ALU.add))


def x_tile(res, n):
    return res["x"][:, bass.ds(n, 1), :].rearrange("p a d -> p (a d)")


def load(sp, loaded, pairs):
    for dst, src in pairs:
        sp.dma_start(dst, src).then_inc(loaded, 16)


def row_of(dram, n=P):
    return dram.unsqueeze(0).broadcast_to([n, dram.shape[0]])


def layer0_attention(nc, dram, res):
    small_head_attention(nc, Attn("a0", 4, 16, 8, "causal", True, 8 ** -0.5), dram["L0_w"], dram["L0_wo"], None, res)


def layer3_attention(nc, dram, res):
    small_head_attention(nc, Attn("a3", 1, 16, 8, "full", True, 8 ** -0.5), dram["L3_w"], dram["L3_wo"],
                         dram["L3_attn_b_proj"], res)


def small_head_attention(nc, a, w_dram, wo_dram, bias_dram, res):
    NQ, QW, KW = a.units * 8, a.units * 8, D
    one_bank = QW + 2 * KW <= 512
    nb = 1 if one_bank else 2
    k_tiles = 16 if a.sets > 1 else 8
    v_uses = 1 + QT * nb + QT * (k_tiles // 8) + a.n_max
    q_uses = QT * a.pairs // 8
    n_loaded = 32 if bias_dram is None else 48
    with ExitStack() as ctx:
        s = Scope(nc, ctx, a.name)
        w = s.sb("w", [P, QW + 2 * KW])
        bias = s.sb("bias", [P, D])
        norm = Norm(s)
        at = Attention(s, nc, a, res, 2 + 6 + (3 if a.sets > 1 else 2) * QT, QT * a.out_banks + QT * (1 if bias_dram is None else 2), v_uses,
                       q_uses, out_bias=None if bias_dram is None else bias[:, :])
        packed_q = [s.sb(f"packed_q{t}", [P, a.units, 8, 8], BF16) for t in range(QT)]
        packed_k = [s.sb(f"packed_k{t}", [P, a.heads, 8, 8], BF16) for t in range(QT)]
        twice_k = [s.sb(f"twice_k{t}", [P, a.heads, 2, 64], BF16) for t in range(QT)] if a.sets > 1 else None
        rest_q = [s.sb(f"rest_q{t}", [P, a.units, 8]) for t in range(QT)]
        rest_k = s.sb("rest_k", [P, a.heads, 8])
        high_ready, rest_ready, packed_ready = s.sem("high_ready"), s.sem("rest_ready"), s.sem("packed_ready")
        k_packed_ready, pool_chained, idle = s.sem("k_packed_ready"), s.sem("pool_chained"), s.sem("idle")
        project = [("qkv", t) for t in range(QT)] + [("pack", t) for t in range(QT)]
        steps = step_lists(a, project)
        block = s.block()

        @block.sync
        def _(sp):
            load(sp, at.loaded, [(w[:, :], w_dram), (at.w_out[:, :, :], wo_dram.rearrange("(t p) d -> p t d", p=P))])
            if bias_dram is not None:
                load(sp, at.loaded, [(bias[:, :], row_of(bias_dram))])

        @block.tensor
        def _(pe):
            pe.wait_ge(at.loaded, n_loaded)
            pe.wait_ge(at.started, 1)

            def project(pe, kind, where, front, to_act, turn, odd):
                t, = where
                if kind == "qkv":
                    if t == 0:
                        pe.wait_ge(at.hT_ready, turn + 1)
                    bank = front.fill(pe)
                    cut = QW + 2 * KW if one_bank else QW
                    front.filled(pe.matmul(bank[:, 0:cut], at.hT[:, t * P:(t + 1) * P], w[:, 0:cut], start=True, stop=True))
                    if not one_bank:
                        bank = front.fill(pe)
                        front.filled(pe.matmul(bank[:, 0:2 * KW], at.hT[:, t * P:(t + 1) * P], w[:, QW:QW + 2 * KW],
                                               start=True, stop=True))
                    return
                pe.wait_ge(k_packed_ready, turn * QT + t + 1)
                for n in range(k_tiles // 8):
                    bank = front.fill(pe)
                    for j in range(8):
                        h = n * 8 + j
                        if a.sets > 1:
                            tile = twice_k[t][:, h, :, :].rearrange("p c x -> p (c x)")
                        else:
                            tile = packed_k[t][:, 2 * h:2 * h + 2, :, :].rearrange("p h s d -> p (h s d)")
                        mm = pe.transpose(bank[:, :].bitcast(BF16)[:, j * P:(j + 1) * P], tile, res["identb"][:, :])
                    front.filled(mm)
                pe.wait_ge(packed_ready, turn * QT + t + 1)
                for n in range(a.pairs // 8):
                    bank = to_act.fill(pe)
                    for j in range(8):
                        g = n * 8 + j
                        mm = pe.transpose(bank[:, :].bitcast(BF16)[:, j * P:(j + 1) * P],
                                          packed_q[t][:, 2 * g:2 * g + 2, :, :].rearrange("p u s d -> p (u s d)"),
                                          res["identb"][:, :])
                    to_act.filled(mm)

            pipelined(pe, lambda bt, bo, ft, fo: at.pe_batch(pe, steps(bt, ft), project, bt, bo, ft, fo))

        @block.scalar
        def _(act):
            at.begin_scalar(act)
            act.wait_ge(at.started, 1)

            def project(act, kind, where, to_act, turn, odd):
                if kind == "qkv":
                    t, = where
                    use = 1 + t * nb
                    act.wait_ge(at.to_dve.full, turn * v_uses + use + 1)
                    bank = at.to_dve.banks[(odd * v_uses + use) % 2]
                    nc.scalar.copy(packed_q[t][:, :, 0:3, :],
                                   bank[:, 0:QW].rearrange("p (u d) -> p u d", d=8).unsqueeze(2)
                                   .broadcast_to([P, a.units, 3, 8])).then_inc(high_ready, 1)
                if kind == "pack":
                    t, = where
                    for n in range(a.pairs // 8):
                        bank = to_act.take(act)
                        to_act.emptied(nc.scalar.copy(at.qT[odd][:, 8 * n:8 * n + 8, t * P:(t + 1) * P],
                                                      bank[:, :].bitcast(BF16).rearrange("p (g q) -> p g q", q=P)))
                    if t == QT - 1:
                        to_act.settled(act)
                        act.sem_inc(at.qT_ready, 1)

            pipelined(act, lambda bt, bo, ft, fo: at.act_batch(act, steps(bt, ft), project, bt, bo, ft, fo))

        @block.gpsimd
        def _(pool):
            pool.wait_ge(norm.power_ready, 1)
            pool.wait_ge(at.started, 1)
            with pool.Fori(0, BATCH) as turn:
                norm.gpsimd(pool, turn)
                for t in range(QT):
                    pool.wait_ge(rest_ready, turn * QT + t + 1)
                    pool.sem_inc(idle, 1)
                    pool.tensor_copy(packed_q[t][:, :, 3:5, :],
                                     rest_q[t][:, :, :].unsqueeze(2).broadcast_to([P, a.units, 2, 8])).then_inc(pool_chained, 1)
                    pool.wait_ge(pool_chained, turn * QT + t + 1)
                    pool.tensor_tensor(packed_q[t][:, :, 5, :], rest_q[t][:, :, :], packed_q[t][:, :, 3, :],
                                       ALU.subtract).then_inc(packed_ready, 1)

        @block.vector
        def _(dve):
            norm.start(dve)
            for t in range(QT):
                dve.memset(packed_q[t][:, :, :, :], 0.0)
                dve.memset(packed_k[t][:, :, :, :], 0.0)
            at.begin_vector(dve)
            dve.wait_ge(at.loaded, n_loaded)
            dve.wait_ge(at.started, 1)

            def project(dve, kind, where, front, chain, turn, odd):
                t, = where
                if kind == "qkv":
                    bank = front.take(dve)
                    dve.wait_ge(high_ready, turn * QT + t + 1)
                    ins = dve.tensor_tensor(rest_q[t][:, :, :], bank[:, 0:QW].rearrange("p (u d) -> p u d", d=8),
                                            packed_q[t][:, :, 0, :], ALU.subtract)
                    ins.then_inc(rest_ready, 1)
                    k0 = QW
                    if not one_bank:
                        dve.wait_ge(rest_ready, turn * QT + t + 1)
                        dve.sem_inc(at.to_dve.free, 1)
                        bank, k0 = front.take(dve), 0
                    keys = bank[:, k0:k0 + KW].rearrange("p (h d) -> p h d", d=8)
                    dve.tensor_copy(at.v[odd][:, t, :, 0:8], bank[:, k0 + KW:k0 + 2 * KW].rearrange("p (h d) -> p h d", d=8))
                    odd_slots = packed_k[t][:, :, 0:6, :].rearrange("p h (s two) d -> p h s two d", two=2)[:, :, :, 1, :]
                    even_slots = packed_k[t][:, :, 0:6, :].rearrange("p h (s two) d -> p h s two d", two=2)[:, :, 1:3, 0, :]
                    chain.link(dve.tensor_copy(odd_slots, keys.unsqueeze(2).broadcast_to([P, a.heads, 3, 8])))
                    front.emptied(dve.tensor_tensor(rest_k[:, :, :], keys, packed_k[t][:, :, 1, :], ALU.subtract))
                    front.settled(dve)
                    chain.link(dve.tensor_copy(even_slots, rest_k[:, :, :].unsqueeze(2).broadcast_to([P, a.heads, 2, 8])))
                    ins = dve.tensor_tensor(packed_k[t][:, :, 0, :], rest_k[:, :, :], packed_k[t][:, :, 2, :], ALU.subtract)
                    if a.sets > 1:
                        chain.link(ins)
                        ins = dve.tensor_copy(twice_k[t][:, :, :, :], packed_k[t][:, :, :, :].rearrange("p h s d -> p h (s d)")
                                              .unsqueeze(2).broadcast_to([P, a.heads, 2, 64]))
                    ins.then_inc(k_packed_ready, 1)
                    return
                for n in range(k_tiles // 8):
                    bank = front.take(dve)
                    for half in range(2):
                        r = slice(64 * half, 64 * half + 64)
                        ins = dve.tensor_copy(
                            at.k_alone[odd][r, 16 * n:16 * n + 16, t * P:(t + 1) * P]
                            .rearrange("p (g two) q -> p g two q", two=2)[:, :, half, :],
                            bank[r, :].bitcast(BF16).rearrange("p (g q) -> p g q", q=P))
                    front.emptied(ins)
                if t == QT - 1:
                    front.settled(dve)
                    dve.sem_inc(at.qkv_ready, 1)

            def normalize(dve, chain, turn):
                norm.vector(dve, chain, turn, lambda t: x_tile(res, turn * QT + t), at.xhat, at.xhat_ready)

            pipelined(dve, lambda bt, bo, ft, fo: at.dve_batch(dve, steps(bt, ft), project, normalize, at.dve_hT,
                                                               at.finish_x, bt, bo, ft, fo))


class Turns:

    def __init__(self, b, turn, per, dt16=None):
        self.b, self.turn, self.per, self.n = b, turn, per, 0

    def fill(self, pe):
        if self.n >= 2:
            pe.wait_ge(self.b["vbank_read"], self.turn * self.per + self.n - 1)
        self.n += 1
        return self.b["vbank"][(self.n - 1) % 2]

    def full(self, mm):
        mm.then_inc(self.b["vbank_full"], 1)

    def take(self, dve):
        dve.wait_ge(self.b["vbank_full"], self.turn * self.per + self.n + 1)
        self.n += 1
        return self.b["vbank"][(self.n - 1) % 2]

    def read(self, ins):
        ins.then_inc(self.b["vbank_read"], 1)

    def settled(self, dve):
        dve.wait_ge(self.b["vbank_read"], self.turn * self.per + self.n)

    def end(self):
        assert self.n == self.per, f"{self.n} banks in a turn, not {self.per}"


def pe_norm_transpose(pe, b, turns, res, xhat, turn):
    pe.wait_ge(b["xhat_ready"], turn + 1)
    bank = turns.fill(pe)
    for t in range(QT):
        mm = pe.transpose(bank[:, t * P:(t + 1) * P], xhat[:, t, :], res["ident"][:, :])
    turns.full(mm)


def dve_modulate(dve, b, turns, res, hT, which, turn):
    bank = turns.take(dve)
    ins = dve.tensor_scalar(hT[:, :], bank[:, 0:TOK], res["mod"][:, which + 1, bass.ds(turn, 1)],
                            res["mod"][:, which, bass.ds(turn, 1)], ALU.mult, ALU.add)
    turns.read(ins)
    return ins


def finish_tile(dve, chain, turns, res, gate, turn, qt, bank, scratch, bias=None):
    x = res["x"][:, bass.ds(turn * QT + qt, 1), :].rearrange("p a d -> p (a d)")
    g = res["gate"][:, gate, bass.ds(turn, 1), :].rearrange("p a d -> p (a d)")
    if bias is None:
        ins = dve.tensor_tensor(scratch[:, :], bank[:, 0:D], g, ALU.mult)
        turns.read(ins)
        turns.settled(dve)
    else:
        ins = dve.tensor_tensor(scratch[:, :], bank[:, 0:D], bias, ALU.add)
        turns.read(ins)
        turns.settled(dve)
        chain.link(dve.tensor_tensor(scratch[:, :], scratch[:, :], g, ALU.mult))
    chain.link(dve.tensor_tensor(x, x, scratch[:, :], ALU.add))


def layer1_attention(nc, dram, res):
    a = Attn("a1", 1, 16, 64, "causal", False, 64 ** -0.5)
    nt = a.width // P
    with ExitStack() as ctx:
        s = Scope(nc, ctx, a.name)
        w = s.sb("w", [P, 3 * a.width])
        qk_bias = s.sb("qk_bias", [P, 2 * a.pairs])
        v_bias = s.sb("v_bias", [P, a.heads, a.hd])
        ghost = s.sb("ghost", [P, a.heads])
        bias = s.sb("bias", [P, D])
        norm = Norm(s)
        at = Attention(s, nc, a, res, 2 + 6, QT * (2 * a.out_banks + 2), 1 + 2 * a.pairs + 2 * QT + a.n_max, 0,
                       q_banks=0, out_bias=bias[:, :], ghost=ghost)
        project = ([("q", g) for g in range(a.pairs)] + [("k", g) for g in range(a.pairs)]
                   + [("v", t, c) for t in range(QT) for c in range(2)])
        steps = step_lists(a, project)
        n_loaded = 6 * 16
        block = s.block()

        @block.sync
        def _(sp):
            load(sp, at.loaded, [(w[:, :], dram["L1_w"]),
                                 (at.w_out[:, :, :], dram["L1_wo"].rearrange("(t p) d -> p t d", p=P)),
                                 (qk_bias[:, :], dram["L1_qk_bias"]),
                                 (v_bias[:, :, :].rearrange("p h d -> p (h d)"), row_of(dram["L1_v_bias"])),
                                 (ghost[:, :], row_of(dram["L1_ghost"])),
                                 (bias[:, :], row_of(dram["L1_wo_bias"]))])

        @block.tensor
        def _(pe):
            pe.wait_ge(at.loaded, n_loaded)
            pe.wait_ge(at.started, 1)

            def project(pe, kind, where, front, to_act, turn, odd):
                if kind == "v":
                    t, c = where
                    bank = front.fill(pe)
                    front.filled(pe.matmul(bank[:, :], at.hT[:, t * P:(t + 1) * P],
                                           w[:, 2 * a.width + 512 * c:2 * a.width + 512 * (c + 1)], start=True, stop=True))
                    return
                n = where[0] + (a.pairs if kind == "k" else 0)
                if n == 0:
                    pe.wait_ge(at.hT_ready, turn + 1)
                bank = front.fill(pe)
                front.filled(pe.matmul(bank[:, 0:TOK], w[:, n * P:(n + 1) * P], at.hT[:, :], start=True, stop=True))

            pipelined(pe, lambda bt, bo, ft, fo: at.pe_batch(pe, steps(bt, ft), project, bt, bo, ft, fo))

        @block.scalar
        def _(act):
            at.begin_scalar(act)
            pipelined(act, lambda bt, bo, ft, fo: at.act_batch(act, steps(bt, ft), None, bt, bo, ft, fo))

        @block.gpsimd
        def _(pool):
            pool.wait_ge(norm.power_ready, 1)
            with pool.Fori(0, BATCH) as turn:
                norm.gpsimd(pool, turn)

        @block.vector
        def _(dve):
            norm.start(dve)
            at.begin_vector(dve)
            dve.wait_ge(at.loaded, n_loaded)
            dve.wait_ge(at.started, 1)

            def project(dve, kind, where, front, chain, turn, odd):
                bank = front.take(dve)
                if kind == "q":
                    g, = where
                    ins = dve.tensor_scalar(at.qT[odd][:, g, :], bank[:, 0:TOK], qk_bias[:, g:g + 1], None, ALU.add)
                elif kind == "k":
                    g, = where
                    for half in range(2):
                        r = slice(64 * half, 64 * half + 64)
                        ins = dve.tensor_scalar(at.k_alone[odd][r, 2 * g + half, :], bank[r, 0:TOK],
                                                qk_bias[r, a.pairs + g:a.pairs + g + 1], None, ALU.add)
                else:
                    t, c = where
                    ins = dve.tensor_tensor(at.v[odd][:, t, 8 * c:8 * c + 8, 0:a.hd],
                                            bank[:, :].rearrange("p (h d) -> p h d", d=a.hd),
                                            v_bias[:, 8 * c:8 * c + 8, :], ALU.add)
                front.emptied(ins)
                if kind == "v" and (t, c) == (QT - 1, 1):
                    front.settled(dve)
                    dve.sem_inc(at.qkv_ready, 1)

            def normalize(dve, chain, turn):
                norm.vector(dve, chain, turn, lambda t: x_tile(res, turn * QT + t), at.xhat, at.xhat_ready)

            pipelined(dve, lambda bt, bo, ft, fo: at.dve_batch(dve, steps(bt, ft), project, normalize, at.dve_hT,
                                                               at.finish_x, bt, bo, ft, fo))


def layer2_attention(nc, dram, res):
    scale = float(D) ** -0.5
    banks, links = 5 + 4 * QT, 2 + 5 * QT
    with ExitStack() as ctx:
        s = Scope(nc, ctx, "a2")
        w, wo = s.sb("w", [P, 3 * D]), s.sb("wo", [P, D])
        qk_bias, v_bias, bias = s.sb("qk_bias", [P, 2]), s.sb("v_bias", [P, D]), s.sb("bias", [P, D])
        norm = Norm(s)
        xhat, hT = s.sb("xhat", [P, QT, D]), s.sb("hT", [P, TOK])
        qkT, v = s.sb("qkT", [P, 2, TOK]), s.sb("v", [P, QT, D])
        sizes = [s.sb(f"sizes{n}", [P, TOK]) for n in range(QT)]
        top, shift = s.sb("top", [P, QT]), s.sb("shift", [P, QT])
        probs = [s.sb(f"probs{n}", [P, TOK]) for n in range(QT)]
        total, inverse = s.sb("total", [P, QT]), s.sb("inverse", [P, QT])
        probsT = [s.sb(f"probsT{n}", [P, TOK]) for n in range(QT)]
        mixed = [s.sb(f"mixed{n}", [P, D]) for n in range(QT)]
        mixedT = [s.sb(f"mixedT{n}", [P, P]) for n in range(QT)]
        scratch = s.sb("scratch", [P, D])
        b = {"vbank": [s.bank("vbank0"), s.bank("vbank1")]}
        score_bank = [s.bank(f"scores{n}") for n in range(QT)]
        for name in ("vbank_full", "vbank_read", "xhat_ready", "chained", "hT_ready", "qkv_ready", "loaded",
                     "scores_ready", "sizes_ready", "shift_ready", "probs_ready", "probsT_ready", "mixed_ready",
                     "mixedT_ready"):
            b[name] = s.sem(name)
        n_loaded = 5 * 16
        block = s.block()

        @block.sync
        def _(sp):
            for dst, src in ((w[:, :], dram["L2_w"]), (wo[:, :], dram["L2_wo"]), (qk_bias[:, :], dram["L2_qk_bias"]),
                             (v_bias[:, :], row_of(dram["L2_v_bias"])), (bias[:, :], row_of(dram["L2_wo_bias"]))):
                sp.dma_start(dst, src).then_inc(b["loaded"], 16)

        @block.tensor
        def _(pe):
            pe.wait_ge(b["loaded"], n_loaded)
            with pe.Fori(0, BATCH) as turn:
                turns = Turns(b, turn, banks)
                pe_norm_transpose(pe, b, turns, res, xhat, turn)
                pe.wait_ge(b["hT_ready"], turn + 1)
                for n in range(2):
                    bank = turns.fill(pe)
                    turns.full(pe.matmul(bank[:, 0:TOK], w[:, n * P:(n + 1) * P], hT[:, :], start=True, stop=True))
                for t in range(QT):
                    bank = turns.fill(pe)
                    turns.full(pe.matmul(bank[:, 0:D], hT[:, t * P:(t + 1) * P], w[:, 2 * P:3 * P], start=True, stop=True))
                pe.wait_ge(b["qkv_ready"], turn + 1)
                for qt in range(QT):
                    pe.matmul(score_bank[qt][:, 0:(qt + 1) * P], qkT[:, 0, qt * P:(qt + 1) * P],
                              qkT[:, 1, 0:(qt + 1) * P], start=True, stop=True).then_inc(b["scores_ready"], 1)
                for qt in range(QT):
                    pe.wait_ge(b["probs_ready"], turn * QT + qt + 1)
                    bank = turns.fill(pe)
                    for kb in range(qt + 1):
                        mm = pe.transpose(bank[:, kb * P:(kb + 1) * P], probs[qt][:, kb * P:(kb + 1) * P], res["ident"][:, :])
                    turns.full(mm)
                for qt in range(QT):
                    pe.wait_ge(b["probsT_ready"], turn * QT + qt + 1)
                    bank = turns.fill(pe)
                    for kb in range(qt + 1):
                        mm = pe.matmul(bank[:, 0:D], probsT[qt][:, kb * P:(kb + 1) * P], v[:, kb, :],
                                       start=(kb == 0), stop=(kb == qt))
                    turns.full(mm)
                for qt in range(QT):
                    pe.wait_ge(b["mixed_ready"], turn * QT + qt + 1)
                    bank = turns.fill(pe)
                    turns.full(pe.transpose(bank[:, 0:P], mixed[qt][:, :], res["ident"][:, :]))
                for qt in range(QT):
                    pe.wait_ge(b["mixedT_ready"], turn * QT + qt + 1)
                    bank = turns.fill(pe)
                    turns.full(pe.matmul(bank[:, 0:D], mixedT[qt][:, :], wo[:, :], start=True, stop=True))
                turns.end()

        @block.scalar
        def _(act):
            with act.Fori(0, BATCH) as turn:
                for qt in range(QT):
                    act.wait_ge(b["scores_ready"], turn * QT + qt + 1)
                    nc.scalar.activation(sizes[qt][:, 0:(qt + 1) * P], score_bank[qt][:, 0:(qt + 1) * P],
                                         ACT.Abs).then_inc(b["sizes_ready"], 1)
                for qt in range(QT):
                    act.wait_ge(b["shift_ready"], turn * QT + qt + 1)
                    nc.scalar.activation(probs[qt][:, 0:(qt + 1) * P], sizes[qt][:, 0:(qt + 1) * P], ACT.Exp,
                                         bias=shift[:, qt:qt + 1], scale=scale,
                                         accum_out=total[:, qt:qt + 1]).then_inc(b["probs_ready"], 1)

        @block.gpsimd
        def _(pool):
            pool.wait_ge(norm.power_ready, 1)
            with pool.Fori(0, BATCH) as turn:
                norm.gpsimd(pool, turn)

        @block.vector
        def _(dve):
            norm.start(dve)
            dve.wait_ge(b["loaded"], n_loaded)
            with dve.Fori(0, BATCH) as turn:
                turns = Turns(b, turn, banks)
                chain = Chain(dve, b["chained"], turn, links)
                norm.vector(dve, chain, turn, lambda t: x_tile(res, turn * QT + t), xhat, b["xhat_ready"])
                dve_modulate(dve, b, turns, res, hT, 0, turn)
                turns.settled(dve)
                dve.sem_inc(b["hT_ready"], 1)
                for n in range(2):
                    bank = turns.take(dve)
                    turns.read(dve.tensor_scalar(qkT[:, n, :], bank[:, 0:TOK], qk_bias[:, n:n + 1], None, ALU.add))
                for t in range(QT):
                    bank = turns.take(dve)
                    turns.read(dve.tensor_tensor(v[:, t, :], bank[:, 0:D], v_bias[:, :], ALU.add))
                turns.settled(dve)
                dve.sem_inc(b["qkv_ready"], 1)
                for qt in range(QT):
                    dve.wait_ge(b["sizes_ready"], turn * QT + qt + 1)
                    diagonal = sizes[qt][:, qt * P:(qt + 1) * P]
                    chain.link(dve.tensor_tensor(diagonal, diagonal, res["masks"][:, 0, :], ALU.add))
                    chain.link(dve.tensor_reduce(top[:, qt:qt + 1], sizes[qt][:, 0:(qt + 1) * P], AX_X, ALU.max))
                    dve.tensor_scalar(shift[:, qt:qt + 1], top[:, qt:qt + 1], -scale, None,
                                      ALU.mult).then_inc(b["shift_ready"], 1)
                for qt in range(QT):
                    bank = turns.take(dve)
                    turns.read(dve.tensor_copy(probsT[qt][:, 0:(qt + 1) * P], bank[:, 0:(qt + 1) * P]))
                    turns.settled(dve)
                    dve.sem_inc(b["probsT_ready"], 1)
                for qt in range(QT):
                    bank = turns.take(dve)
                    chain.link(dve.reciprocal(inverse[:, qt:qt + 1], total[:, qt:qt + 1]))
                    turns.read(dve.tensor_scalar(mixed[qt][:, :], bank[:, 0:D], inverse[:, qt:qt + 1], None, ALU.mult))
                    turns.settled(dve)
                    dve.sem_inc(b["mixed_ready"], 1)
                for qt in range(QT):
                    bank = turns.take(dve)
                    turns.read(dve.tensor_copy(mixedT[qt][:, :], bank[:, 0:P]))
                    turns.settled(dve)
                    dve.sem_inc(b["mixedT_ready"], 1)
                for qt in range(QT):
                    bank = turns.take(dve)
                    finish_tile(dve, chain, turns, res, 0, turn, qt, bank, scratch, bias[:, :])
                turns.end()
                chain.end()


class Quant:

    BLOCK = 16

    def __init__(self, s, name, cols, work=None):
        nb = cols // self.BLOCK
        self.work = work or {
            "top": s.sb("q_top", [P, nb]), "inverse": s.sb("q_inverse", [P, nb]), "scale": s.sb("q_scale", [P, nb]),
            "unit": s.sb("q_unit", [P, cols]), "size": s.sb("q_size", [P, cols]), "sign": s.sb("q_sign", [P, cols]),
            "level": s.sb("q_level", [P, cols]), "past": s.sb("q_past", [P, cols])}
        self.top_ready, self.divided, self.parted = (s.sem(f"{name}_{x}") for x in ("top_ready", "divided", "parted"))

    def vector(self, dve, chain, src, dst, cols, n):
        w = self.work
        nb = cols // self.BLOCK
        chain.link(dve.tensor_reduce(w["top"][:, 0:nb], src.rearrange("p (b k) -> p b k", k=self.BLOCK), AX_X,
                                     ALU.max, apply_absolute_value=True))
        chain.link(dve.tensor_scalar(w["scale"][:, 0:nb], w["top"][:, 0:nb], 1.0 / 6.0, 1e-12, ALU.mult, ALU.max))
        dve.reciprocal(w["inverse"][:, 0:nb], w["scale"][:, 0:nb]).then_inc(self.top_ready, 1)
        dve.wait_ge(self.parted, n)
        size, level, past = w["size"][:, 0:cols], w["level"][:, 0:cols], w["past"][:, 0:cols]

        def passed(mid):
            chain.link(dve.scalar_tensor_tensor(out=level, in0=size, scalar=mid, in1=level, op0=ALU.is_gt, op1=ALU.add))

        dve.tensor_scalar(past, size, 1.75, None, ALU.is_gt)
        chain.link(dve.tensor_scalar(level, size, 5.0, 2.0, ALU.is_gt, ALU.mult))
        passed(3.5)
        passed(2.5)
        chain.link(dve.scalar_tensor_tensor(out=level, in0=level, scalar=2.0, in1=past, op0=ALU.mult, op1=ALU.add))
        passed(1.25)
        passed(0.75)
        passed(0.25)
        chain.link(dve.scalar_tensor_tensor(out=level, in0=level, scalar=0.5, in1=w["sign"][:, 0:cols],
                                            op0=ALU.mult, op1=ALU.mult))
        return dve.tensor_tensor(dst.rearrange("p (b k) -> p b k", k=self.BLOCK),
                                 level.rearrange("p (b k) -> p b k", k=self.BLOCK),
                                 w["scale"][:, 0:nb].unsqueeze(2).broadcast_to([P, nb, self.BLOCK]), ALU.mult)

    LINKS = 10

    def gpsimd(self, pool, src, cols, n):
        w = self.work
        nb = cols // self.BLOCK
        pool.wait_ge(self.top_ready, n)
        pool.tensor_tensor(w["unit"][:, 0:cols].rearrange("p (b k) -> p b k", k=self.BLOCK),
                           src.rearrange("p (b k) -> p b k", k=self.BLOCK),
                           w["inverse"][:, 0:nb].unsqueeze(2).broadcast_to([P, nb, self.BLOCK]),
                           ALU.mult).then_inc(self.divided, 1)

    def scalar(self, act, nc, cols, n):
        w = self.work
        act.wait_ge(self.divided, n)
        nc.scalar.activation(w["size"][:, 0:cols], w["unit"][:, 0:cols], ACT.Abs)
        nc.scalar.activation(w["sign"][:, 0:cols], w["unit"][:, 0:cols], ACT.Sign).then_inc(self.parted, 1)


def layer1_ffn(nc, dram, res):
    I = 352
    parts = [(0, P), (P, P), (2 * P, I - 2 * P)]
    banks = 3 + 2 * QT
    links = 2 + 2 * Quant.LINKS + 2 * QT + QT
    with ExitStack() as ctx:
        s = Scope(nc, ctx, "f1")
        raw = [s.sb("raw_gate", [P, 3, D]), s.sb("raw_up", [P, 3, D]), s.sb("raw_down", [P, I])]
        quantized = s.sb("quantized", [P, 3 * D])
        w_in = s.sb("w_in", [P, 2, I])
        w_down = s.sb("w_down", [P, 3, D])
        norm = Norm(s)
        xhat, hT, h = s.sb("xhat", [P, QT, D]), s.sb("hT", [P, TOK]), s.sb("h", [P, TOK])
        hq, hqT = s.sb("hq", [P, TOK]), s.sb("hqT", [P, TOK])
        tanh, gated = s.sb("tanh", [P, QT, I]), s.sb("gated", [P, QT, I])
        hidden, hiddenq = s.sb("hidden", [P, QT, I]), s.sb("hiddenq", [P, QT, I])
        hiddenT = s.sb("hiddenT", [P, QT, 3, P])
        scratch = s.sb("scratch", [P, D])
        first = Quant(s, "qw", QT * I)
        each = Quant(s, "qh", QT * I, first.work)
        b = {"vbank": [s.bank("vbank0"), s.bank("vbank1")]}
        gate_bank = [s.bank(f"gate{n}") for n in range(QT)]
        up_bank = [s.bank(f"up{n}") for n in range(QT)]
        for name in ("vbank_full", "vbank_read", "xhat_ready", "chained", "hT_ready", "loaded", "started",
                     "h_ready", "hq_ready", "hqT_ready", "in_ready", "tanh_ready", "hidden_ready", "hiddenq_ready",
                     "hiddenT_ready"):
            b[name] = s.sem(name)
        b0 = {"vbank": b["vbank"]}
        for name in ("vbank_full", "vbank_read", "chained", "quantized_ready"):
            b0[name] = s.sem("w_" + name)
        block = s.block()

        @block.sync
        def _(sp):
            sp.wait_ge(b["started"], 1)
            for dst, src in ((raw[0], dram["L1_ffn_w_gate"]), (raw[1], dram["L1_ffn_w_up"])):
                sp.dma_start(dst[:, 0:2, :], src[0:2 * P, :].rearrange("(t p) d -> p t d", p=P)).then_inc(b["loaded"], 16)
                sp.dma_start(dst[0:I - 2 * P, 2, :], src[2 * P:I, :]).then_inc(b["loaded"], 16)
            sp.dma_start(raw[2][:, :], dram["L1_ffn_w_down"]).then_inc(b["loaded"], 16)

        weights = [(raw[0][:, :, :].rearrange("p t d -> p (t d)"), 3 * D),
                   (raw[1][:, :, :].rearrange("p t d -> p (t d)"), 3 * D), (raw[2][:, :], I)]

        @block.tensor
        def _(pe):
            turns = Turns(b0, 0, 0)
            for n in range(3):
                pe.wait_ge(b0["quantized_ready"], n + 1)
                bank = turns.fill(pe)
                for t, (r0, rows) in enumerate(parts):
                    if n < 2:
                        mm = pe.transpose(bank[:, r0:r0 + rows], quantized[0:rows, t * D:(t + 1) * D],
                                          res["ident"][0:rows, 0:rows])
                    else:
                        mm = pe.transpose(bank[0:rows, t * P:(t + 1) * P], quantized[:, r0:r0 + rows], res["ident"][:, :])
                turns.full(mm)
            with pe.Fori(0, BATCH) as turn:
                turns = Turns(b, turn, banks)
                pe_norm_transpose(pe, b, turns, res, xhat, turn)
                pe.wait_ge(b["hT_ready"], turn + 1)
                bank = turns.fill(pe)
                for t in range(QT):
                    mm = pe.transpose(bank[:, t * P:(t + 1) * P], hT[:, t * P:(t + 1) * P], res["ident"][:, :])
                turns.full(mm)
                pe.wait_ge(b["hq_ready"], turn + 1)
                bank = turns.fill(pe)
                for t in range(QT):
                    mm = pe.transpose(bank[:, t * P:(t + 1) * P], hq[:, t * P:(t + 1) * P], res["ident"][:, :])
                turns.full(mm)
                pe.wait_ge(b["hqT_ready"], turn + 1)
                for t in range(QT):
                    pe.matmul(gate_bank[t][:, 0:I], hqT[:, t * P:(t + 1) * P], w_in[:, 0, :], start=True, stop=True)
                    pe.matmul(up_bank[t][:, 0:I], hqT[:, t * P:(t + 1) * P], w_in[:, 1, :],
                              start=True, stop=True).then_inc(b["in_ready"], 1)
                pe.wait_ge(b["hiddenq_ready"], turn + 1)
                for t in range(QT):
                    bank = turns.fill(pe)
                    for c, (r0, rows) in enumerate(parts):
                        mm = pe.transpose(bank[0:rows, c * P:(c + 1) * P], hiddenq[:, t, r0:r0 + rows], res["ident"][:, :])
                    turns.full(mm)
                for t in range(QT):
                    pe.wait_ge(b["hiddenT_ready"], turn * QT + t + 1)
                    bank = turns.fill(pe)
                    for c, (r0, rows) in enumerate(parts):
                        mm = pe.matmul(bank[:, 0:D], hiddenT[0:rows, t, c, :], w_down[0:rows, c, :],
                                       start=(c == 0), stop=(c == 2))
                    turns.full(mm)
                turns.end()

        @block.scalar
        def _(act):
            for n in range(3):
                first.scalar(act, nc, weights[n][1], n + 1)
            with act.Fori(0, BATCH) as turn:
                each.scalar(act, nc, TOK, turn * 2 + 1)
                for t in range(QT):
                    act.wait_ge(b["in_ready"], turn * QT + t + 1)
                    nc.scalar.activation(tanh[:, t, :], gate_bank[t][:, 0:I], ACT.Tanh, scale=0.5).then_inc(b["tanh_ready"], 1)
                each.scalar(act, nc, QT * I, turn * 2 + 2)

        @block.gpsimd
        def _(pool):
            pool.wait_ge(norm.power_ready, 1)
            for n in range(3):
                first.gpsimd(pool, weights[n][0], weights[n][1], n + 1)
            with pool.Fori(0, BATCH) as turn:
                norm.gpsimd(pool, turn)
                each.gpsimd(pool, h[:, :], TOK, turn * 2 + 1)
                each.gpsimd(pool, hidden[:, :, :].rearrange("p t i -> p (t i)"), QT * I, turn * 2 + 2)

        @block.vector
        def _(dve):
            dve.memset(raw[0][:, :, :], 0.0)
            norm.start(dve)
            dve.memset(raw[1][:, :, :], 0.0).then_inc(b["started"], 1)
            dve.wait_ge(b["loaded"], 5 * 16)
            turns = Turns(b0, 0, 0)
            chain = Chain(dve, b0["chained"], 0, 0)
            for n in range(3):
                src, cols = weights[n]
                if n:
                    turns.settled(dve)
                first.vector(dve, chain, src, quantized[:, 0:cols], cols, n + 1).then_inc(b0["quantized_ready"], 1)
                bank = turns.take(dve)
                if n < 2:
                    ins = dve.tensor_copy(w_in[:, n, :], bank[:, 0:I])
                else:
                    dve.tensor_copy(w_down[:, 0:2, :].rearrange("p t d -> p (t d)"), bank[:, 0:2 * P])
                    ins = dve.tensor_copy(w_down[0:I - 2 * P, 2, :], bank[0:I - 2 * P, 2 * P:3 * P])
                turns.read(ins)
            turns.settled(dve)
            with dve.Fori(0, BATCH) as turn:
                turns = Turns(b, turn, banks)
                chain = Chain(dve, b["chained"], turn, links)
                norm.vector(dve, chain, turn, lambda t: x_tile(res, turn * QT + t), xhat, b["xhat_ready"])
                dve_modulate(dve, b, turns, res, hT, 2, turn)
                turns.settled(dve)
                dve.sem_inc(b["hT_ready"], 1)
                bank = turns.take(dve)
                turns.read(dve.tensor_copy(h[:, :], bank[:, 0:TOK]))
                turns.settled(dve)
                each.vector(dve, chain, h[:, :], hq[:, :], TOK, turn * 2 + 1).then_inc(b["hq_ready"], 1)
                bank = turns.take(dve)
                turns.read(dve.tensor_copy(hqT[:, :], bank[:, 0:TOK]))
                turns.settled(dve)
                dve.sem_inc(b["hqT_ready"], 1)
                for t in range(QT):
                    dve.wait_ge(b["tanh_ready"], turn * QT + t + 1)
                    chain.link(dve.scalar_tensor_tensor(out=gated[:, t, :], in0=tanh[:, t, :], scalar=1.0,
                                                        in1=gate_bank[t][:, 0:I], op0=ALU.add, op1=ALU.mult))
                    chain.link(dve.tensor_tensor(hidden[:, t, :], up_bank[t][:, 0:I], gated[:, t, :], ALU.mult))
                each.vector(dve, chain, hidden[:, :, :].rearrange("p t i -> p (t i)"),
                            hiddenq[:, :, :].rearrange("p t i -> p (t i)"), QT * I, turn * 2 + 2).then_inc(b["hiddenq_ready"], 1)
                for t in range(QT):
                    bank = turns.take(dve)
                    dve.tensor_copy(hiddenT[:, t, 0:2, :].rearrange("p c q -> p (c q)"), bank[:, 0:2 * P])
                    turns.read(dve.tensor_copy(hiddenT[0:I - 2 * P, t, 2, :], bank[0:I - 2 * P, 2 * P:3 * P]))
                    turns.settled(dve)
                    dve.sem_inc(b["hiddenT_ready"], 1)
                for t in range(QT):
                    bank = turns.take(dve)
                    g = res["gate"][:, 1, bass.ds(turn, 1), :].rearrange("p a d -> p (a d)")
                    turns.read(dve.scalar_tensor_tensor(out=scratch[:, :], in0=bank[:, 0:D], scalar=0.5, in1=g,
                                                        op0=ALU.mult, op1=ALU.mult))
                    turns.settled(dve)
                    x = x_tile(res, turn * QT + t)
                    chain.link(dve.tensor_tensor(x, x, scratch[:, :], ALU.add))
                turns.end()
                chain.end()


def layer3_ffn(nc, dram, res):
    E, ES, K = 16, 32, 4
    NX = E + 8 - K
    banks, links = 1 + 2 * QT, 14 + 1 * QT
    with ExitStack() as ctx:
        s = Scope(nc, ctx, "f3")
        sel, keys, values = s.sb("sel", [P, E]), s.sb("keys", [P, E * ES]), s.sb("values", [P, 4, D])
        route_scale = s.sb("route_scale", [P, 1])
        norm = Norm(s)
        xhat, hT = s.sb("xhat", [P, QT, D]), s.sb("hT", [P, TOK])
        negexp, plus = s.sb("negexp", [P, QT, E]), s.sb("plus", [P, QT, E])
        probs = s.sb("probs", [P, QT, NX])
        best = s.sb("best", [P, QT, 8])
        left = s.sb("left", [P, QT, NX])
        kept, chosen = s.sb("kept", [P, QT, E]), s.sb("chosen", [P, QT, E])
        total, inverse, weight = s.sb("total", [P, QT]), s.sb("inverse", [P, QT]), s.sb("weight", [P, QT, E])
        scores, scoresT = s.sb("scores", [P, QT, E * ES]), s.sb("scoresT", [P, QT, 512])
        scratch = s.sb("scratch", [P, D])
        b = {"vbank": [s.bank("vbank0"), s.bank("vbank1")]}
        score_bank = [s.bank(f"scores{n}") for n in range(QT)]
        for name in ("vbank_full", "vbank_read", "xhat_ready", "chained", "hT_ready", "loaded", "logits_ready",
                     "negexp_ready", "experts_ready", "scores_ready", "scoresT_ready"):
            b[name] = s.sem(name)
        logit_bank = s.bank("logits")
        FILL = 3.0e38
        block = s.block()

        @block.sync
        def _(sp):
            for dst, src in ((sel[:, :], dram["L3_sel"]), (keys[:, :], dram["L3_keys"]),
                             (values[:, :, :], dram["L3_values"].rearrange("(t p) d -> p t d", p=P)),
                             (route_scale[:, :], row_of(dram["L3_ffn_route_scale"]))):
                sp.dma_start(dst, src).then_inc(b["loaded"], 16)

        @block.tensor
        def _(pe):
            pe.wait_ge(b["loaded"], 64)
            with pe.Fori(0, BATCH) as turn:
                turns = Turns(b, turn, banks)
                pe_norm_transpose(pe, b, turns, res, xhat, turn)
                pe.wait_ge(b["hT_ready"], turn + 1)
                for t in range(QT):
                    mm = pe.matmul(logit_bank[:, t * E:(t + 1) * E], hT[:, t * P:(t + 1) * P], sel[:, :],
                                   start=(t == 0), stop=True, skip_group_check=True)
                mm.then_inc(b["logits_ready"], 1)
                for t in range(QT):
                    pe.matmul(score_bank[t][:, :], hT[:, t * P:(t + 1) * P], keys[:, :],
                              start=True, stop=True).then_inc(b["experts_ready"], 1)
                for t in range(QT):
                    pe.wait_ge(b["scores_ready"], turn * QT + t + 1)
                    bank = turns.fill(pe)
                    for c in range(4):
                        mm = pe.transpose(bank[:, c * P:(c + 1) * P], scores[:, t, c * P:(c + 1) * P], res["ident"][:, :])
                    turns.full(mm)
                for t in range(QT):
                    pe.wait_ge(b["scoresT_ready"], turn * QT + t + 1)
                    bank = turns.fill(pe)
                    for c in range(4):
                        mm = pe.matmul(bank[:, 0:D], scoresT[:, t, c * P:(c + 1) * P], values[:, c, :],
                                       start=(c == 0), stop=(c == 3))
                    turns.full(mm)
                turns.end()

        @block.scalar
        def _(act):
            with act.Fori(0, BATCH) as turn:
                act.wait_ge(b["logits_ready"], turn + 1)
                nc.scalar.activation(negexp[:, :, :].rearrange("p t e -> p (t e)"), logit_bank[:, 0:QT * E], ACT.Exp,
                                     scale=-1.0).then_inc(b["negexp_ready"], 1)

        @block.gpsimd
        def _(pool):
            pool.wait_ge(norm.power_ready, 1)
            with pool.Fori(0, BATCH) as turn:
                norm.gpsimd(pool, turn)

        @block.vector
        def _(dve):
            norm.start(dve)
            dve.memset(probs[:, :, :], FILL)
            dve.wait_ge(b["loaded"], 64)
            dve.wait_ge(norm.power_ready, 1)
            with dve.Fori(0, BATCH) as turn:
                turns = Turns(b, turn, banks)
                chain = Chain(dve, b["chained"], turn, links)
                norm.vector(dve, chain, turn, lambda t: x_tile(res, turn * QT + t), xhat, b["xhat_ready"])
                dve_modulate(dve, b, turns, res, hT, 2, turn)
                turns.settled(dve)
                dve.sem_inc(b["hT_ready"], 1)
                dve.wait_ge(b["negexp_ready"], turn + 1)
                chain.link(dve.tensor_scalar(plus[:, :, :], negexp[:, :, :], 1.0, None, ALU.add))
                chain.link(dve.reciprocal(probs[:, :, 0:E], plus[:, :, :]))
                top_places(dve, chain, norm, probs, best, left, E, K, FILL)
                chain.link(dve.tensor_tensor(chosen[:, :, :], probs[:, :, 0:E], left[:, :, 0:E], ALU.not_equal))
                chain.link(dve.tensor_tensor(kept[:, :, :], probs[:, :, 0:E], chosen[:, :, :], ALU.mult))
                chain.link(dve.tensor_reduce(total[:, :], kept[:, :, :], AX_X, ALU.add))
                chain.link(dve.tensor_scalar(total[:, :], total[:, :], 1e-9, None, ALU.max))
                chain.link(dve.reciprocal(inverse[:, :], total[:, :]))
                chain.link(dve.tensor_scalar(inverse[:, :], inverse[:, :], route_scale[:, 0:1], None, ALU.mult))
                chain.link(dve.tensor_tensor(weight[:, :, :], kept[:, :, :],
                                             inverse[:, :].unsqueeze(2).broadcast_to([P, QT, E]), ALU.mult))
                for t in range(QT):
                    dve.wait_ge(b["experts_ready"], turn * QT + t + 1)
                    dve.scalar_tensor_tensor(
                        out=scores[:, t, :].rearrange("p (e k) -> p e k", k=ES),
                        in0=score_bank[t][:, :].rearrange("p (e k) -> p e k", k=ES), scalar=0.0,
                        in1=weight[:, t, :].unsqueeze(2).broadcast_to([P, E, ES]),
                        op0=ALU.max, op1=ALU.mult).then_inc(b["scores_ready"], 1)
                for t in range(QT):
                    bank = turns.take(dve)
                    turns.read(dve.tensor_copy(scoresT[:, t, :], bank[:, :]))
                    turns.settled(dve)
                    dve.sem_inc(b["scoresT_ready"], 1)
                for t in range(QT):
                    bank = turns.take(dve)
                    finish_tile(dve, chain, turns, res, 1, turn, t, bank, scratch)
                turns.end()
                chain.end()


def top_places(dve, chain, norm, values, best, left, width, k, fill):
    carry(dve, norm)
    for t in range(QT):
        last = dve.max(best[:, t, :], values[:, t, 0:width])
    chain.link(last)
    chain.link(dve.memset(best[:, :, k:8], fill))
    carry(dve, norm)
    for t in range(QT):
        last = dve.match_replace(left[:, t, :], in_to_replace=best[:, t, :], in_values=values[:, t, :], imm_value=-1.0e38)
    chain.link(last)


def carry(dve, norm):
    dve.tensor_copy(norm.idle[:, 1:2], norm.idle[:, 0:1])


def layer0_ffn(nc, dram, res):
    E, I, K = 8, 256, 2
    C = I // P
    LIMIT, ALPHA = 7.0, 1.702
    NX = E + 8 - K
    FILL = 3.0e38
    banks, links = 4 + E, 11 + E + QT * 2
    with ExitStack() as ctx:
        s = Scope(nc, ctx, "f0")
        router, router_bias = s.sb("router", [P, E]), s.sb("router_bias", [P, E])
        w_in, b_in = s.sb("w_in", [P, E, 2 * I]), s.sb("b_in", [P, E, 2 * C])
        w_down, b_down = s.sb("w_down", [P, E * C, D]), s.sb("b_down", [E, D])
        norm = Norm(s)
        xhat, hT = s.sb("xhat", [P, QT, D]), s.sb("hT", [P, TOK])
        logits, best, left = s.sb("logits", [P, QT, NX]), s.sb("best", [P, QT, 8]), s.sb("left", [P, QT, NX])
        lowered, exps = s.sb("lowered", [P, QT, E]), s.sb("exps", [P, QT, E])
        total, inverse = s.sb("total", [P, QT]), s.sb("inverse", [P, QT])
        top, chosen = s.sb("top", [P, QT]), s.sb("chosen", [P, QT, E])
        weight, half_weight = s.sb("weight", [P, QT, E]), s.sb("half_weight", [P, QT, E])
        weightT = s.sb("weightT", [E, TOK])
        gate = [s.sb(f"gate{n}", [P, C, TOK]) for n in range(2)]
        up = [s.sb(f"up{n}", [P, C, TOK]) for n in range(2)]
        tanh = [s.sb(f"tanh{n}", [P, C, TOK]) for n in range(2)]
        glu = [s.sb(f"glu{n}", [P, C, TOK]) for n in range(2)]
        hidden = [s.sb(f"hidden{n}", [P, C, TOK]) for n in range(2)]
        mixed = s.sb("mixed", [P, QT, D])
        scratch = s.sb("scratch", [P, D])
        b = {"vbank": [s.bank("vbank0"), s.bank("vbank1")]}
        gate_bank = [s.bank(f"gate_bank{n}") for n in range(2)]
        up_bank = [s.bank(f"up_bank{n}") for n in range(2)]
        for name in ("vbank_full", "vbank_read", "xhat_ready", "chained", "hT_ready", "loaded", "lowered_ready",
                     "exps_ready", "weight_ready", "weightT_ready", "in_ready", "in_read", "gate_ready",
                     "tanh_ready", "glu_ready", "hidden_ready", "down_read"):
            b[name] = s.sem(name)
        n_loaded = 6 * 16
        block = s.block()

        @block.sync
        def _(sp):
            for dst, src in ((router[:, :], dram["L0_router"]), (router_bias[:, :], row_of(dram["L0_router_bias"])),
                             (w_in[:, :, :], dram["L0_gate_up"].rearrange("e h n -> h e n")),
                             (b_in[:, :, :], dram["L0_gate_up_bias"]),
                             (w_down[:, :, :], dram["L0_down"].rearrange("(t p) d -> p t d", p=P)),
                             (b_down[:, :], dram["L0_down_bias"])):
                sp.dma_start(dst, src).then_inc(b["loaded"], 16)

        @block.tensor
        def _(pe):
            pe.wait_ge(b["loaded"], n_loaded)
            with pe.Fori(0, BATCH) as turn:
                turns = Turns(b, turn, banks)
                pe_norm_transpose(pe, b, turns, res, xhat, turn)
                pe.wait_ge(b["hT_ready"], turn + 1)
                bank = turns.fill(pe)
                for t in range(QT):
                    mm = pe.matmul(bank[:, t * E:(t + 1) * E], hT[:, t * P:(t + 1) * P], router[:, :],
                                   start=(t == 0), stop=True, skip_group_check=True)
                turns.full(mm)

                def into(e):
                    if e >= 2:
                        pe.wait_ge(b["in_read"], turn * E + e - 1)
                    for out, first in ((gate_bank[e % 2], 0), (up_bank[e % 2], C)):
                        for c in range(C):
                            mm = pe.matmul(out[:, c * TOK:(c + 1) * TOK], w_in[:, e, (first + c) * P:(first + c + 1) * P],
                                           hT[:, :], start=(c == 0), stop=True, skip_group_check=True)
                    mm.then_inc(b["in_ready"], 1)

                into(0)
                pe.wait_ge(b["weight_ready"], turn + 1)
                bank = turns.fill(pe)
                for t in range(QT):
                    mm = pe.transpose(bank[0:E, t * P:(t + 1) * P], weight[:, t, :], res["ident"][:, :])
                turns.full(mm)
                pe.wait_ge(b["weightT_ready"], turn + 1)
                bank = turns.fill(pe)
                for t in range(QT):
                    mm = pe.matmul(bank[:, t * P:(t + 1) * P], weightT[:, t * P:(t + 1) * P], b_down[:, :],
                                   start=(t == 0), stop=True, skip_group_check=True)
                turns.full(mm)
                for e in range(E):
                    if e + 1 < E:
                        into(e + 1)
                    pe.wait_ge(b["hidden_ready"], turn * E + e + 1)
                    bank = turns.fill(pe)
                    for t in range(QT):
                        for c in range(C):
                            mm = pe.matmul(bank[:, t * P:(t + 1) * P], hidden[e % 2][:, c, t * P:(t + 1) * P],
                                           w_down[:, e * C + c, :], start=(t == 0 and c == 0), stop=(c == C - 1),
                                           skip_group_check=True)
                    turns.full(mm)
                turns.end()

        @block.scalar
        def _(act):
            with act.Fori(0, BATCH) as turn:
                act.wait_ge(b["lowered_ready"], turn + 1)
                nc.scalar.activation(exps[:, :, :], lowered[:, :, :], ACT.Exp).then_inc(b["exps_ready"], 1)
                for e in range(E):
                    act.wait_ge(b["gate_ready"], turn * E + e + 1)
                    nc.scalar.activation(tanh[e % 2][:, :, :], gate[e % 2][:, :, :], ACT.Tanh,
                                         scale=ALPHA / 2).then_inc(b["tanh_ready"], 1)

        @block.gpsimd
        def _(pool):
            pool.wait_ge(norm.power_ready, 1)
            with pool.Fori(0, BATCH) as turn:
                norm.gpsimd(pool, turn)
                for e in range(E):
                    pool.wait_ge(b["glu_ready"], turn * E + e + 1)
                    pool.tensor_tensor(hidden[e % 2][:, :, :], up[e % 2][:, :, :], glu[e % 2][:, :, :],
                                       ALU.mult).then_inc(b["hidden_ready"], 1)

        @block.vector
        def _(dve):
            norm.start(dve)
            dve.memset(logits[:, :, :], FILL)
            dve.wait_ge(b["loaded"], n_loaded)
            dve.wait_ge(norm.power_ready, 1)
            with dve.Fori(0, BATCH) as turn:
                turns = Turns(b, turn, banks)
                chain = Chain(dve, b["chained"], turn, links)
                norm.vector(dve, chain, turn, lambda t: x_tile(res, turn * QT + t), xhat, b["xhat_ready"])
                dve_modulate(dve, b, turns, res, hT, 2, turn)
                turns.settled(dve)
                dve.sem_inc(b["hT_ready"], 1)
                bank = turns.take(dve)
                turns.read(dve.tensor_tensor(logits[:, :, 0:E], bank[:, 0:QT * E].rearrange("p (t e) -> p t e", e=E),
                                             router_bias[:, :].unsqueeze(1).broadcast_to([P, QT, E]), ALU.add))
                turns.settled(dve)
                top_places(dve, chain, norm, logits, best, left, E, K, FILL)
                dve.tensor_tensor(lowered[:, :, :], logits[:, :, 0:E], best[:, :, 0:1].broadcast_to([P, QT, E]),
                                  ALU.subtract).then_inc(b["lowered_ready"], 1)
                chain.link(dve.tensor_tensor(chosen[:, :, :], logits[:, :, 0:E], left[:, :, 0:E], ALU.not_equal))
                dve.wait_ge(b["exps_ready"], turn + 1)
                chain.link(dve.tensor_reduce(total[:, :], exps[:, :, :], AX_X, ALU.add))
                chain.link(dve.reciprocal(inverse[:, :], total[:, :]))
                chain.link(dve.tensor_tensor(weight[:, :, :], exps[:, :, :], chosen[:, :, :], ALU.mult))
                chain.link(dve.tensor_tensor(weight[:, :, :], weight[:, :, :],
                                             inverse[:, :].unsqueeze(2).broadcast_to([P, QT, E]), ALU.mult))
                dve.sem_inc(b["weight_ready"], 1)
                chain.link(dve.tensor_scalar(half_weight[:, :, :], weight[:, :, :], 0.5, None, ALU.mult))

                def biased(e):
                    dve.wait_ge(b["in_ready"], turn * E + e + 1)
                    for c in range(C):
                        dve.tensor_scalar(gate[e % 2][:, c, :], gate_bank[e % 2][:, c * TOK:(c + 1) * TOK],
                                          b_in[:, e, c:c + 1], LIMIT, ALU.add, ALU.min)
                    for c in range(C):
                        ins = dve.tensor_scalar(up[e % 2][:, c, :], up_bank[e % 2][:, c * TOK:(c + 1) * TOK],
                                                b_in[:, e, C + c:C + c + 1], -LIMIT, ALU.add, ALU.max)
                    ins.then_inc(b["in_read"], 1)
                    dve.wait_ge(b["in_read"], turn * E + e + 1)
                    dve.sem_inc(b["gate_ready"], 1)
                    chain.link(dve.tensor_scalar(up[e % 2][:, :, :], up[e % 2][:, :, :], LIMIT, 1.0, ALU.min, ALU.add))

                def combined(e):
                    bank = turns.take(dve)
                    for t in range(QT):
                        ins = dve.scalar_tensor_tensor(out=mixed[:, t, :], in0=bank[:, t * P:(t + 1) * P],
                                                       scalar=half_weight[:, t, e:e + 1], in1=mixed[:, t, :],
                                                       op0=ALU.mult, op1=ALU.add)
                    turns.read(ins)
                    turns.settled(dve)

                biased(0)
                bank = turns.take(dve)
                turns.read(dve.tensor_copy(weightT[:, :], bank[0:E, 0:TOK]))
                turns.settled(dve)
                dve.sem_inc(b["weightT_ready"], 1)
                bank = turns.take(dve)
                turns.read(dve.tensor_copy(mixed[:, :, :].rearrange("p t d -> p (t d)"), bank[:, 0:QT * P]))
                turns.settled(dve)
                for e in range(E):
                    if e + 1 < E:
                        biased(e + 1)
                    dve.wait_ge(b["tanh_ready"], turn * E + e + 1)
                    dve.scalar_tensor_tensor(out=glu[e % 2][:, :, :], in0=tanh[e % 2][:, :, :], scalar=1.0,
                                             in1=gate[e % 2][:, :, :], op0=ALU.add, op1=ALU.mult).then_inc(b["glu_ready"], 1)
                    if e >= 1:
                        combined(e - 1)
                combined(E - 1)
                for t in range(QT):
                    g = res["gate"][:, 1, bass.ds(turn, 1), :].rearrange("p a d -> p (a d)")
                    chain.link(dve.tensor_tensor(scratch[:, :], mixed[:, t, :], g, ALU.mult))
                    x = x_tile(res, turn * QT + t)
                    chain.link(dve.tensor_tensor(x, x, scratch[:, :], ALU.add))
                turns.end()
                chain.end()


def layer2_ffn(nc, dram, res):
    with ExitStack() as ctx:
        s = Scope(nc, ctx, "f2")
        y = s.sb("y", [P, BATCH * QT, D])
        layer2_input(nc, dram, res, y)
        for depth in range(2):
            window_attention(nc, dram, res, y, depth)
            gelu_mlp(nc, dram, res, y, depth)
        layer2_output(nc, res, y)


def y_tile(y, n):
    return y[:, bass.ds(n, 1), :].rearrange("p a d -> p (a d)")


def layer2_input(nc, dram, res, y):
    banks, links = 2, 2
    with ExitStack() as ctx:
        s = Scope(nc, ctx, "i2")
        norm = Norm(s)
        xhat, hT = s.sb("xhat", [P, QT, D]), s.sb("hT", [P, TOK])
        b = {"vbank": [s.bank("vbank0"), s.bank("vbank1")]}
        for name in ("vbank_full", "vbank_read", "xhat_ready", "chained", "hT_ready"):
            b[name] = s.sem(name)
        block = s.block()

        @block.tensor
        def _(pe):
            with pe.Fori(0, BATCH) as turn:
                turns = Turns(b, turn, banks)
                pe_norm_transpose(pe, b, turns, res, xhat, turn)
                pe.wait_ge(b["hT_ready"], turn + 1)
                bank = turns.fill(pe)
                for t in range(QT):
                    mm = pe.transpose(bank[:, t * P:(t + 1) * P], hT[:, t * P:(t + 1) * P], res["ident"][:, :])
                turns.full(mm)
                turns.end()

        @block.gpsimd
        def _(pool):
            pool.wait_ge(norm.power_ready, 1)
            with pool.Fori(0, BATCH) as turn:
                norm.gpsimd(pool, turn)

        @block.vector
        def _(dve):
            norm.start(dve)
            dve.wait_ge(norm.power_ready, 1)
            with dve.Fori(0, BATCH) as turn:
                turns = Turns(b, turn, banks)
                chain = Chain(dve, b["chained"], turn, links)
                norm.vector(dve, chain, turn, lambda t: x_tile(res, turn * QT + t), xhat, b["xhat_ready"])
                dve_modulate(dve, b, turns, res, hT, 2, turn)
                turns.settled(dve)
                dve.sem_inc(b["hT_ready"], 1)
                bank = turns.take(dve)
                turns.read(dve.tensor_copy(y[:, bass.ds(turn * QT, QT), :].rearrange("p t d -> p (t d)"), bank[:, 0:TOK]))
                turns.settled(dve)
                turns.end()
                chain.end()


def layer2_output(nc, res, y):
    with ExitStack() as ctx:
        s = Scope(nc, ctx, "o2")
        scratch = s.sb("scratch", [P, QT, D])
        chained = s.sem("chained")
        block = s.block()

        @block.vector
        def _(dve):
            with dve.Fori(0, BATCH) as turn:
                chain = Chain(dve, chained, turn, 2)
                x = res["x"][:, bass.ds(turn * QT, QT), :]
                chain.link(dve.tensor_tensor(scratch[:, :, :], y[:, bass.ds(turn * QT, QT), :],
                                             res["gate"][:, 1, bass.ds(turn, 1), :].broadcast_to([P, QT, D]), ALU.mult))
                chain.link(dve.tensor_tensor(x, x, scratch[:, :, :], ALU.add))
                chain.end()


def dve_shift(dve, bank, shifted):
    H = D // 2
    dve.tensor_copy(shifted[0:H, :], bank[0:H, 0:TOK])
    return dve.tensor_copy(shifted[H:D, 1:TOK], bank[H:D, 0:TOK - 1])


def window_attention(nc, dram, res, y, depth):
    a = Attn(f"w{depth}", 1, 8, 64, "window", False, 8.0)
    INNER, H = a.width, a.hd // 2
    with ExitStack() as ctx:
        s = Scope(nc, ctx, a.name)
        w = s.sb("w", [P, 3 * INNER])
        scales = s.sb("scales", [P, 2, 64])
        tables = s.sb("tables", [P, 2, 2, QT, 64])
        turned = s.sb("turned", [P, 2, 2, QT, 64])
        power = s.sb("power", [P, 2 * a.heads])

        def each(name, shape):
            return [s.sb(f"{name}{t}", [P, 2] + shape) for t in range(QT)]

        raw, square, unit = each("raw", [8, 64]), each("square", [8, 64]), each("unit", [8, 64])
        by_cos, by_sin, rotated = square, each("by_sin", [8, 64]), each("rotated", [8, 64])
        total, inverse = each("total", [8]), each("inverse", [8])
        at = Attention(s, nc, a, res, 6 + 3 * QT, QT * a.out_banks, 1 + QT + a.n_max, 3 * QT + QT)
        squares_ready, total_ready, inverse_ready = s.sem("squares_ready"), s.sem("total_ready"), s.sem("inverse_ready")
        unit_ready = s.sem("unit_ready")
        by_sin_ready, rotated_ready = s.sem("by_sin_ready"), s.sem("rotated_ready")
        project = ([("qkv", t, c) for t in range(QT) for c in range(3)] + [("total", 0), ("total", 1)]
                   + [("unit", 0), ("unit", 1), ("rotate", 0), ("rotate", 1), ("pack", 0), ("pack", 1)])
        steps = step_lists(a, project)
        n_loaded = 5 * 16
        block = s.block()

        @block.sync
        def _(sp):
            load(sp, at.loaded, [(w[:, :], dram["L2_wqkv"][depth]),
                                 (at.w_out[:, :, :], dram["L2_ffn_wo"][depth].rearrange("(t p) d -> p t d", p=P)),
                                 (scales[:, 0, :], row_of(dram["L2_q_scale"][depth])),
                                 (scales[:, 1, :], row_of(dram["L2_k_scale"][depth])),
                                 (tables[:, :, :, :, :], dram["c_rotary"])])

        @block.tensor
        def _(pe):
            pe.wait_ge(at.loaded, n_loaded)
            pe.wait_ge(at.started, 1)

            def project(pe, kind, where, front, to_act, turn, odd):
                if kind == "qkv":
                    t, c = where
                    if t == 0 and c == 0:
                        pe.wait_ge(at.hT_ready, turn + 1)
                    bank = to_act.fill(pe)
                    to_act.filled(pe.matmul(bank[:, :], at.hT[:, t * P:(t + 1) * P], w[:, c * INNER:(c + 1) * INNER],
                                            start=True, stop=True))
                elif kind == "pack":
                    t, = where
                    pe.wait_ge(rotated_ready, turn * QT + t + 1)
                    for c, ring in enumerate((to_act, front)):
                        bank = ring.fill(pe)
                        for g in range(a.pairs):
                            mm = pe.transpose(bank[:, g * P:(g + 1) * P],
                                              rotated[t][:, c, 2 * g:2 * g + 2, :].rearrange("p h d -> p (h d)"),
                                              res["ident"][:, :])
                        ring.filled(mm)

            pipelined(pe, lambda bt, bo, ft, fo: at.pe_batch(pe, steps(bt, ft), project, bt, bo, ft, fo))

        @block.scalar
        def _(act):
            at.begin_scalar(act)
            act.wait_ge(at.started, 1)

            def project(act, kind, where, to_act, turn, odd):
                if kind == "qkv":
                    t, c = where
                    bank = to_act.take(act)
                    if c == 2:
                        to_act.emptied(nc.scalar.copy(at.v[odd][:, t, :, 0:a.hd],
                                                      bank[:, :].rearrange("p (h d) -> p h d", d=a.hd)))
                        return
                    if c == 0:
                        act.wait_ge(unit_ready, turn * QT + t + 1)
                    nc.scalar.copy(raw[t][:, c, :, :].rearrange("p h d -> p (h d)"), bank[:, :])
                    to_act.emptied(nc.scalar.activation(square[t][:, c, :, :].rearrange("p h d -> p (h d)"), bank[:, :],
                                                        ACT.Square))
                    if c == 1:
                        to_act.settled(act)
                        act.sem_inc(squares_ready, 1)
                elif kind == "pack":
                    t, = where
                    bank = to_act.take(act)
                    to_act.emptied(nc.scalar.copy(at.qT[odd][:, :, t * P:(t + 1) * P],
                                                  bank[:, :].rearrange("p (g q) -> p g q", q=P)))
                    if t == QT - 1:
                        to_act.settled(act)
                        act.sem_inc(at.qT_ready, 1)

            pipelined(act, lambda bt, bo, ft, fo: at.act_batch(act, steps(bt, ft), project, bt, bo, ft, fo))

        @block.gpsimd
        def _(pool):
            pool.wait_ge(at.started, 1)
            with pool.Fori(0, BATCH) as turn:
                for t in range(QT):
                    pool.wait_ge(total_ready, turn * QT + t + 1)
                    pool.tensor_tensor(inverse[t][:, :, :].rearrange("p c h -> p (c h)"),
                                       total[t][:, :, :].rearrange("p c h -> p (c h)"), power[:, :],
                                       ALU.pow).then_inc(inverse_ready, 1)
                for t in range(QT):
                    pool.wait_ge(unit_ready, turn * QT + t + 1 + QT)
                    for half in range(2):
                        here, there = slice(H * half, H * half + H), slice(H - H * half, 2 * H - H * half)
                        last = pool.tensor_tensor(by_sin[t][:, :, :, here], unit[t][:, :, :, there],
                                                  turned[:, :, 1, t, here].unsqueeze(2).broadcast_to([P, 2, 8, H]), ALU.mult)
                    last.then_inc(by_sin_ready, 1)

        @block.vector
        def _(dve):
            dve.memset(power[:, :], -0.5)
            dve.memset(at.hT[:, :], 0.0)
            dve.sem_inc(unit_ready, QT)
            dve.wait_ge(at.loaded, n_loaded)
            for c in range(2):
                for t in range(QT):
                    dve.tensor_tensor(turned[:, c, 0, t, :], tables[:, c, 0, t, :], scales[:, c, :], ALU.mult)
                    dve.tensor_tensor(turned[:, c, 1, t, 0:H], tables[:, c, 1, t, 0:H], scales[:, c, H:2 * H], ALU.mult)
                    dve.tensor_tensor(turned[:, c, 1, t, H:2 * H], tables[:, c, 1, t, H:2 * H],
                                      scales[:, c, 0:H], ALU.mult)
            at.begin_vector(dve)
            dve.wait_ge(at.started, 1)

            def project(dve, kind, where, front, chain, turn, odd):
                if kind == "total":
                    t, = where
                    dve.wait_ge(squares_ready, turn * QT + t + 1)
                    dve.tensor_reduce(total[t][:, :, :], square[t][:, :, :, :], AX_X, ALU.add).then_inc(total_ready, 1)
                elif kind == "unit":
                    t, = where
                    dve.wait_ge(inverse_ready, turn * QT + t + 1)
                    chain.link(dve.tensor_scalar(inverse[t][:, :, :], inverse[t][:, :, :], 1e12, None, ALU.min))
                    chain.link(dve.tensor_tensor(unit[t][:, :, :, :], raw[t][:, :, :, :],
                                                 inverse[t][:, :, :].unsqueeze(3).broadcast_to([P, 2, 8, 64]), ALU.mult))
                    chain.link(dve.tensor_tensor(by_cos[t][:, :, :, :], unit[t][:, :, :, :],
                                                 turned[:, :, 0, t, :].unsqueeze(2).broadcast_to([P, 2, 8, 64]), ALU.mult))
                    dve.sem_inc(unit_ready, 1)
                elif kind == "rotate":
                    t, = where
                    dve.wait_ge(by_sin_ready, turn * QT + t + 1)
                    dve.tensor_tensor(rotated[t][:, :, :, :], by_cos[t][:, :, :, :], by_sin[t][:, :, :, :],
                                      ALU.add).then_inc(rotated_ready, 1)
                elif kind == "pack":
                    t, = where
                    bank = front.take(dve)
                    for half in range(2):
                        r = slice(64 * half, 64 * half + 64)
                        ins = dve.tensor_copy(
                            at.k_alone[odd][r, :, t * P:(t + 1) * P].rearrange("p (g two) q -> p g two q", two=2)[:, :, half, :],
                            bank[r, :].rearrange("p (g q) -> p g q", g=4))
                    front.emptied(ins)
                    if t == QT - 1:
                        front.settled(dve)
                        dve.sem_inc(at.qkv_ready, 1)

            def copy_y(dve, chain, turn):
                dve.tensor_copy(at.xhat[:, :, :], y[:, bass.ds(turn * QT, QT), :]).then_inc(at.xhat_ready, 1)

            def shift(dve, front, turn):
                bank = front.take(dve)
                front.emptied(dve_shift(dve, bank, at.hT))
                front.settled(dve)
                dve.sem_inc(at.hT_ready, 1)

            def add_to_y(dve, chain, tail, turn, qt, bank):
                yt = y_tile(y, turn * QT + qt)
                tail.emptied(dve.tensor_tensor(yt, bank[:, 0:D], yt, ALU.add))
                tail.settled(dve)

            pipelined(dve, lambda bt, bo, ft, fo: at.dve_batch(dve, steps(bt, ft), project, copy_y, shift,
                                                               add_to_y, bt, bo, ft, fo))


def gelu_mlp(nc, dram, res, y, depth):
    HID = 341
    parts = [(0, P), (P, P), (2 * P, HID - 2 * P)]
    banks, links = 3 + 3 + QT, 2 + QT
    with ExitStack() as ctx:
        s = Scope(nc, ctx, f"g{depth}")
        w1, w2 = s.sb("w1", [P, 2 * HID]), s.sb("w2", [P, 3, D])
        b1, b2, affine = s.sb("b1", [P, 2, 3]), s.sb("b2", [P, D]), s.sb("affine", [P, 2])
        norm = Norm(s)
        y_now, shifted, back = s.sb("y_now", [P, QT, D]), s.sb("shifted", [P, TOK]), s.sb("back", [P, QT, D])
        xhat, hT = s.sb("xhat", [P, QT, D]), s.sb("hT", [P, TOK])
        gelu, hidden = s.sb("gelu", [P, 3, TOK]), s.sb("hidden", [P, 3, TOK])
        scratch = s.sb("scratch", [P, D])
        b = {"vbank": [s.bank("vbank0"), s.bank("vbank1")]}
        gelu_bank = [s.bank(f"gelu{n}") for n in range(2)]
        for name in ("vbank_full", "vbank_read", "xhat_ready", "chained", "hT_ready", "loaded", "now_ready",
                     "shifted_ready", "g_ready", "gelu_ready", "hidden_ready"):
            b[name] = s.sem(name)
        block = s.block()
        n_loaded = 6 * 16

        @block.sync
        def _(sp):
            for dst, src in ((w1[:, :], dram["L2_w1"][depth]),
                             (w2[:, 0:2, :], dram["L2_w2"][depth, 0:2 * P, :].rearrange("(t p) d -> p t d", p=P)),
                             (w2[0:HID - 2 * P, 2, :], dram["L2_w2"][depth, 2 * P:HID, :]),
                             (b1[:, :, :], dram["L2_b1"][depth]), (b2[:, :], row_of(dram["L2_b2"][depth])),
                             (affine[:, :], dram["L2_affine"][depth])):
                sp.dma_start(dst, src).then_inc(b["loaded"], 16)

        @block.tensor
        def _(pe):
            pe.wait_ge(b["loaded"], n_loaded)
            with pe.Fori(0, BATCH) as turn:
                turns = Turns(b, turn, banks)

                def turn_over(src, ready):
                    pe.wait_ge(b[ready], turn + 1)
                    bank = turns.fill(pe)
                    for t in range(QT):
                        mm = pe.transpose(bank[:, t * P:(t + 1) * P], src(t), res["ident"][:, :])
                    turns.full(mm)

                turn_over(lambda t: y_now[:, t, :], "now_ready")
                turn_over(lambda t: shifted[:, t * P:(t + 1) * P], "shifted_ready")
                turn_over(lambda t: xhat[:, t, :], "xhat_ready")
                pe.wait_ge(b["hT_ready"], turn + 1)
                for c, (r0, rows) in enumerate(parts):
                    if c == 2:
                        pe.wait_ge(b["gelu_ready"], turn * 3 + 1)
                    pe.matmul(gelu_bank[c % 2][0:rows, 0:TOK], w1[:, HID + r0:HID + r0 + rows], hT[:, :],
                              start=True, stop=True).then_inc(b["g_ready"], 1)
                for c, (r0, rows) in enumerate(parts):
                    bank = turns.fill(pe)
                    turns.full(pe.matmul(bank[0:rows, 0:TOK], w1[:, r0:r0 + rows], hT[:, :], start=True, stop=True))
                pe.wait_ge(b["hidden_ready"], turn + 1)
                for t in range(QT):
                    bank = turns.fill(pe)
                    for c, (r0, rows) in enumerate(parts):
                        mm = pe.matmul(bank[:, 0:D], hidden[0:rows, c, t * P:(t + 1) * P], w2[0:rows, c, :],
                                       start=(c == 0), stop=(c == 2))
                    turns.full(mm)
                turns.end()

        @block.scalar
        def _(act):
            act.wait_ge(b["loaded"], n_loaded)
            with act.Fori(0, BATCH) as turn:
                for c, (r0, rows) in enumerate(parts):
                    act.wait_ge(b["g_ready"], turn * 3 + c + 1)
                    nc.scalar.activation(gelu[0:rows, c, :], gelu_bank[c % 2][0:rows, 0:TOK], ACT.Gelu,
                                         bias=b1[0:rows, 1, c:c + 1]).then_inc(b["gelu_ready"], 1)

        @block.gpsimd
        def _(pool):
            pool.wait_ge(norm.power_ready, 1)
            with pool.Fori(0, BATCH) as turn:
                norm.gpsimd(pool, turn)

        @block.vector
        def _(dve):
            dve.memset(shifted[:, :], 0.0)
            norm.start(dve)
            dve.wait_ge(b["loaded"], n_loaded)
            dve.wait_ge(norm.power_ready, 1)
            with dve.Fori(0, BATCH) as turn:
                turns = Turns(b, turn, banks)
                chain = Chain(dve, b["chained"], turn, links)
                dve.tensor_copy(y_now[:, :, :], y[:, bass.ds(turn * QT, QT), :]).then_inc(b["now_ready"], 1)
                bank = turns.take(dve)
                turns.read(dve_shift(dve, bank, shifted))
                turns.settled(dve)
                dve.sem_inc(b["shifted_ready"], 1)
                bank = turns.take(dve)
                turns.read(dve.tensor_copy(back[:, :, :].rearrange("p t d -> p (t d)"), bank[:, 0:TOK]))
                turns.settled(dve)
                norm.vector(dve, chain, turn, lambda t: back[:, t, :], xhat, b["xhat_ready"])
                bank = turns.take(dve)
                turns.read(dve.tensor_scalar(hT[:, :], bank[:, 0:TOK], affine[:, 0:1], affine[:, 1:2], ALU.mult, ALU.add))
                turns.settled(dve)
                dve.sem_inc(b["hT_ready"], 1)
                for c, (r0, rows) in enumerate(parts):
                    bank = turns.take(dve)
                    dve.wait_ge(b["gelu_ready"], turn * 3 + c + 1)
                    turns.read(dve.scalar_tensor_tensor(out=hidden[0:rows, c, :], in0=bank[0:rows, 0:TOK],
                                                        scalar=b1[0:rows, 0, c:c + 1], in1=gelu[0:rows, c, :],
                                                        op0=ALU.add, op1=ALU.mult))
                turns.settled(dve)
                dve.sem_inc(b["hidden_ready"], 1)
                for t in range(QT):
                    bank = turns.take(dve)
                    turns.read(dve.tensor_tensor(scratch[:, :], bank[:, 0:D], b2[:, :], ALU.add))
                    turns.settled(dve)
                    yt = y_tile(y, turn * QT + t)
                    chain.link(dve.tensor_tensor(yt, yt, scratch[:, :], ALU.add))
                turns.end()
                chain.end()


def lay_out_rest(z):
    t = {}
    t["L1_w"] = z["L1_attn_Wqkv_w"].T
    t["L1_wo"] = z["L1_attn_Wo_w"].T
    t["L1_qk_bias"] = z["L1_attn_Wqkv_b"][:2048].reshape(16, P).T
    t["L1_v_bias"] = z["L1_attn_Wqkv_b"][2048:]
    t["L1_ghost"] = z["L1_attn_ghost"]
    t["L1_wo_bias"] = z["L1_attn_Wo_b"]
    t["L2_w"] = np.concatenate([z["L2_attn_Wq"].T, z["L2_attn_Wk"].T, z["L2_attn_Wv"].T], axis=1)
    t["L2_wo"] = z["L2_attn_Wo"].T
    t["L2_qk_bias"] = np.stack([z["L2_attn_bq"], z["L2_attn_bk"]], axis=1)
    t["L2_v_bias"] = z["L2_attn_bv"]
    t["L2_wo_bias"] = z["L2_attn_bo"]
    for n in ("gate", "up", "down"):
        t[f"L1_ffn_w_{n}"] = z[f"L1_ffn_w_{n}"]
    t["L3_sel"] = z["L3_ffn_expert_sel"].T
    t["L3_keys"] = z["L3_ffn_keys"].transpose(1, 0, 2).reshape(D, 512)
    t["L3_values"] = z["L3_ffn_values"].reshape(512, D)
    t["L3_ffn_route_scale"] = z["L3_ffn_route_scale"]
    t["L0_router"] = z["L0_ffn_router_weight"].T
    t["L0_router_bias"] = z["L0_ffn_router_bias"]
    t["L0_gate_up"] = z["L0_ffn_gate_up_proj"]
    t["L0_gate_up_bias"] = z["L0_ffn_gate_up_bias"].reshape(8, 4, P).transpose(2, 0, 1)
    t["L0_down"] = z["L0_ffn_down_proj"].reshape(8 * 256, D)
    t["L0_down_bias"] = z["L0_ffn_down_bias"]
    t["L2_wqkv"] = z["L2_ffn_wqkv"]
    t["L2_ffn_wo"] = z["L2_ffn_wo"]
    t["L2_q_scale"] = z["L2_ffn_q_scale"]
    t["L2_k_scale"] = z["L2_ffn_k_scale"]
    t["L2_w1"] = z["L2_ffn_w1"]
    t["L2_w2"] = z["L2_ffn_w2"]
    b1 = np.zeros((2, 2, 3 * P), np.float32)
    b1[:, :, 0:341] = z["L2_ffn_b1"].reshape(2, 2, 341)
    t["L2_b1"] = b1.reshape(2, 2, 3, P).transpose(0, 3, 1, 2)
    t["L2_b2"] = z["L2_ffn_b2"]
    t["L2_affine"] = np.stack([z["L2_ffn_ln_g"], z["L2_ffn_ln_b"]], axis=2)
    return t


def shape_constants():
    r = np.arange(P)
    q, k = r[:, None], r[None, :]
    banned = [k > q, (k > q) | (k < q - WINDOW), k < q + P - WINDOW]
    masks = np.zeros((P, 6, P), np.float32)
    for n, m in enumerate(banned):
        masks[:, 2 * n, :] = np.where(m, BIG, 0.0)
        masks[:, 2 * n + 1, :] = np.where(m.T, BIG, 0.0)
    minus_head = np.zeros((P, 16, P), np.float32)
    for part in range(3):
        for h in range(16):
            minus_head[part * 16 + h, h, :] = -1.0
    head_rows = (r[:, None] // 8 == np.arange(16)[None, :]).astype(np.float32)
    half = np.arange(0, 64, 2, dtype=np.float32)
    angle = np.arange(TOK, dtype=np.float32)[:, None] * (1.0 / 10000.0 ** (half / 64))[None, :].astype(np.float32)
    factor = ((half + 25.6) / 89.6)[None, :] ** ((np.arange(TOK) - TOK // 2) / 32.0)[:, None]
    cos, sin = np.cos(angle), np.sin(angle)
    rotary = np.zeros((2, 2, TOK, 64), np.float32)
    for n, f in enumerate((factor, 1.0 / factor)):
        rotary[n, 0] = np.concatenate([cos * f, cos * f], axis=1)
        rotary[n, 1] = np.concatenate([-sin * f, sin * f], axis=1)
    rotary = rotary.reshape(2, 2, QT, P, 64).transpose(3, 0, 1, 2, 4)
    return {"c_rotary": rotary, "c_ident": np.eye(P, dtype=np.float32), "c_masks": masks, "c_minus_head": minus_head,
            "c_head_rows": head_rows}


def lay_out(z):
    t = {"x": z["L0_attn_x"]}
    for n in range(4):
        t[f"L{n}_cT"] = z[f"L{n}_c"].T
        t[f"L{n}_wmod"] = z[f"L{n}_wmod"]
    w = z["L0_attn_W_attn"]
    w_q = w[:512].reshape(4, 16, 8, D).transpose(1, 0, 2, 3).reshape(512, D)
    t["L0_w"] = np.concatenate([w_q, w[512:]], axis=0).T
    t["L0_wo"] = z["L0_attn_W_proj"].reshape(D, 4, 16, 8).transpose(2, 1, 3, 0).reshape(512, D)
    t["L3_w"] = z["L3_attn_w_qkv"]
    t["L3_wo"] = z["L3_attn_w_proj"]
    t["L3_attn_b_proj"] = z["L3_attn_b_proj"]
    t.update(lay_out_rest(z))
    t.update(shape_constants())
    return {k: np.ascontiguousarray(v) for k, v in t.items()}


def resident(s):
    return {
        "x": s.sb("x", [P, BATCH * QT, D]),
        "ident": s.sb("ident", [P, P]),
        "identb": s.sb("identb", [P, P], BF16),
        "masks": s.sb("masks", [P, 6, P], BF16),
        "minus_head": s.sb("minus_head", [P, 16, P], BF16),
        "head_rows": s.sb("head_rows", [P, 16]),
        "mod": s.sb("mod", [P, 4, BATCH]),
        "gate": s.sb("gate", [P, 2, BATCH, D]),
    }


OUT_SHAPE = (BATCH, TOK, D)


def build(nc, dram, out):
    with ExitStack() as ctx:
        res = resident(Scope(nc, ctx, "res"))
        constants_phase(nc, dram, res)
        for layer, (attention, ffn) in enumerate(((layer0_attention, layer0_ffn), (layer1_attention, layer1_ffn),
                                                  (layer2_attention, layer2_ffn), (layer3_attention, layer3_ffn))):
            modulation_phase(nc, layer, dram, res)
            attention(nc, dram, res)
            ffn(nc, dram, res)
        store_phase(nc, res, out)


def kernel(**inputs):
    import concourse.bacc as bacc
    from concourse.bass_utils import run_bass_kernel_spmd

    nc = bacc.Bacc("TRN2", target_bir_lowering=False, num_devices=1)
    arrays = lay_out(inputs)
    dram = {n: nc.dram_tensor(f"in_{n}", a.shape, mybir.dt.from_np(a.dtype), kind="ExternalInput").ap()
            for n, a in arrays.items()}
    out = nc.dram_tensor("out", OUT_SHAPE, F32, kind="ExternalOutput").ap()
    build(nc, dram, out)
    r = run_bass_kernel_spmd(nc, [{f"in_{n}": a for n, a in arrays.items()}], core_ids=[0])
    return r.results[0]["out"]
```

```python
from contextlib import ExitStack

import concourse.bass as bass
import numpy as np
from concourse import mybir

ALU = mybir.AluOpType
ACT = mybir.ActivationFunctionType
F32 = mybir.dt.float32
BF16 = mybir.dt.bfloat16
AX_X = mybir.AxisListType.X

P = 128
BATCH = 16
TOK = 256
QT = TOK // P
D = 128
EPS = 1e-5
BIG = -1.0e30
WINDOW = 64


class Chain:

    def __init__(self, eng, sem, turn, per):
        self.eng, self.sem, self.turn, self.per, self.n = eng, sem, turn, per, 0

    def value(self, n):
        return self.turn * self.per + n if self.per else n

    def link(self, ins):
        self.n += 1
        ins.then_inc(self.sem, 1)
        self.eng.wait_ge(self.sem, self.value(self.n))

    def end(self):
        assert self.per in (0, self.n), f"the chain has {self.n} links in a turn, not {self.per}"


class Scope:

    def __init__(self, nc, ctx, name):
        self.nc, self.ctx, self.name, self.sems = nc, ctx, name, []

    def sb(self, name, shape, dt=F32):
        return self.ctx.enter_context(self.nc.sbuf_tensor(f"{self.name}_{name}", list(shape), dt))

    def bank(self, name, dt=F32):
        return self.ctx.enter_context(self.nc.psum_tensor(f"{self.name}_{name}", [P, 512], dt))

    def sem(self, name):
        self.sems.append(self.ctx.enter_context(self.nc.semaphore(f"{self.name}_{name}")))
        return self.sems[-1]

    def block(self):
        self.ctx.callback(self.clear)
        return self.ctx.enter_context(self.nc.Block())

    def clear(self):
        with self.nc.Block() as block:
            @block.gpsimd
            def _(pool):
                for sem in self.sems:
                    pool.sem_clear(sem)


def tiles(x):
    return x.rearrange("p (t q) -> p t q", q=P)


def constants_phase(nc, dram, res):
    with ExitStack() as ctx:
        s = Scope(nc, ctx, "cst")
        loaded = s.sem("loaded")
        narrowed = s.sem("narrowed")
        masks_f = s.sb("masks_f", [P, 6, P])
        head_f = s.sb("head_f", [P, 16, P])
        block = s.block()

        @block.sync
        def _(sp):
            sp.dma_start(res["x"][:, :, :], dram["x"].rearrange("b (t p) d -> p (b t) d", p=P)).then_inc(loaded, 16)
            sp.dma_start(res["ident"][:, :], dram["c_ident"]).then_inc(loaded, 16)
            sp.dma_start(masks_f[:, :, :], dram["c_masks"]).then_inc(loaded, 16)
            sp.dma_start(head_f[:, :, :], dram["c_minus_head"]).then_inc(loaded, 16)
            sp.dma_start(res["shift"][:, :, :], dram["c_shift"]).then_inc(loaded, 16)
            sp.wait_ge(loaded, 5 * 16)

        @block.vector
        def _(dve):
            dve.wait_ge(loaded, 5 * 16)
            dve.tensor_copy(res["identb"][:, :], res["ident"][:, :])
            dve.tensor_copy(res["masks"][:, :, :], masks_f[:, :, :])
            dve.tensor_copy(res["minus_head"][:, :, :], head_f[:, :, :]).then_inc(narrowed, 1)
            dve.wait_ge(narrowed, 1)


def modulation_phase(nc, layer, dram, res):
    with ExitStack() as ctx:
        s = Scope(nc, ctx, f"mod{layer}")
        ct = s.sb("ct", [P, BATCH])
        wmod = s.sb("wmod", [P, 6, D])
        e1 = s.sb("e1", [P, BATCH])
        e2 = s.sb("e2", [P, BATCH])
        silu = s.sb("silu", [P, BATCH])
        silu_wide = s.sb("silu_wide", [P, BATCH, P])
        above = s.sb("above", [P, 512])
        below = s.sb("below", [P, 512])
        size = s.sb("size", [P, 512])
        shifts = s.bank("shifts")
        gates = [s.bank(f"gates{n}") for n in range(2)]
        loaded, negexp, widened, products, read, chained = (
            s.sem(x) for x in ("loaded", "negexp", "widened", "products", "read", "chained"))
        block = s.block()

        @block.sync
        def _(sp):
            sp.dma_start(ct[:, :], dram[f"L{layer}_cT"]).then_inc(loaded, 16)
            sp.dma_start(wmod[:, :, :], dram[f"L{layer}_wmod"].rearrange("k (j d) -> k j d", d=D)).then_inc(loaded, 16)

        @block.scalar
        def _(act):
            act.wait_ge(loaded, 32)
            nc.scalar.activation(e1[:, :], ct[:, :], ACT.Exp, scale=-1.0).then_inc(negexp, 1)

        @block.vector
        def _(dve):
            chain = Chain(dve, chained, 0, 0)
            dve.wait_ge(loaded, 32)
            dve.wait_ge(negexp, 1)
            chain.link(dve.tensor_scalar(e2[:, :], e1[:, :], 1.0, None, ALU.add))
            chain.link(dve.reciprocal(e1[:, :], e2[:, :]))
            chain.link(dve.tensor_tensor(silu[:, :], ct[:, :], e1[:, :], ALU.mult))
            dve.tensor_copy(silu_wide[:, :, :], silu[:, :].unsqueeze(2).broadcast_to([P, BATCH, P])).then_inc(widened, 1)
            dve.wait_ge(products, 1)
            for n in range(4):
                dve.tensor_scalar(res["mod"][:, n, :], shifts[:, n * BATCH:(n + 1) * BATCH],
                                  float(n % 2), None, ALU.add)
            for n in range(8):
                dve.wait_ge(products, n + 2)
                g = gates[n % 2][:, :]
                chain.link(dve.tensor_scalar(size[:, :], g, 0.25, None, ALU.max))
                chain.link(dve.scalar_tensor_tensor(out=above[:, :], in0=g, scalar=0.0, in1=size[:, :],
                                                    op0=ALU.is_ge, op1=ALU.mult))
                chain.link(dve.tensor_scalar(size[:, :], g, -0.25, None, ALU.min))
                chain.link(dve.scalar_tensor_tensor(out=below[:, :], in0=g, scalar=0.0, in1=size[:, :],
                                                    op0=ALU.is_lt, op1=ALU.mult))
                out = res["gate"][:, n // 4, 4 * (n % 4):4 * (n % 4) + 4, :]
                dve.tensor_tensor(out.rearrange("p b d -> p (b d)"), above[:, :], below[:, :], ALU.add).then_inc(read, 1)
                dve.wait_ge(read, n + 1)

        @block.tensor
        def _(pe):
            pe.wait_ge(loaded, 32)
            pe.wait_ge(widened, 1)
            for n, j in enumerate((0, 1, 3, 4)):
                mm = pe.matmul(shifts[:, n * BATCH:(n + 1) * BATCH], wmod[:, j, :], silu[:, :],
                               start=(n == 0), stop=True, skip_group_check=True)
            mm.then_inc(products, 1)
            for n in range(8):
                if n >= 2:
                    pe.wait_ge(read, n - 1)
                for k in range(4):
                    mm = pe.matmul(gates[n % 2][:, k * P:(k + 1) * P], silu_wide[:, 4 * (n % 4) + k, :],
                                   wmod[:, (2, 5)[n // 4], :], start=(k == 0), stop=True, skip_group_check=True)
                mm.then_inc(products, 1)


def store_phase(nc, res, out):
    with ExitStack() as ctx:
        s = Scope(nc, ctx, "st")
        stored = s.sem("stored")
        block = s.block()

        @block.sync
        def _(sp):
            sp.dma_start(out.rearrange("b (t p) d -> p (b t) d", p=P), res["x"][:, :, :]).then_inc(stored, 16)
            sp.wait_ge(stored, 16)


class Norm:

    def __init__(self, s, turns_per_loop=1):
        self.stats, self.mv = s.sb("stats", [P, QT, 6]), s.sb("mv", [P, QT, 2])
        self.var, self.power, self.rstd = s.sb("var", [P, QT]), s.sb("power", [P, QT]), s.sb("rstd", [P, QT])
        self.idle = s.sb("idle", [P, 2])
        self.var_ready, self.rstd_ready, self.power_ready = s.sem("var_ready"), s.sem("rstd_ready"), s.sem("power_ready")
        self.per = turns_per_loop

    def start(self, dve):
        dve.memset(self.idle[:, :], 0.0)
        dve.memset(self.power[:, :], -0.5).then_inc(self.power_ready, 1)

    def vector(self, dve, chain, turn, x_at, xhat, ready, nth=0):
        for t in range(QT):
            last = dve.bn_stats(self.stats[:, t, :], x_at(t))
        chain.link(last)
        dve.tensor_copy(self.idle[:, 1:2], self.idle[:, 0:1])
        for t in range(QT):
            last = dve.bn_aggr(self.mv[:, t, :], self.stats[:, t, :])
        chain.link(last)
        dve.tensor_scalar(self.var[:, :], self.mv[:, :, 1], EPS, None, ALU.add).then_inc(self.var_ready, 1)
        dve.wait_ge(self.rstd_ready, turn * self.per + nth + 1)
        for t in range(QT):
            last = dve.tensor_scalar(xhat[:, t, :], x_at(t), self.mv[:, t, 0:1], self.rstd[:, t:t + 1],
                                     ALU.subtract, ALU.mult)
        last.then_inc(ready, 1)

    def gpsimd(self, pool, turn, nth=0):
        pool.wait_ge(self.var_ready, turn * self.per + nth + 1)
        pool.tensor_tensor(self.rstd[:, :], self.var[:, :], self.power[:, :], ALU.pow).then_inc(self.rstd_ready, 1)


class Ring:

    def __init__(self, s, name, banks):
        self.banks = [s.bank(f"{name}_bank{n}") for n in range(banks)]
        self.full, self.free = s.sem(f"{name}_full"), s.sem(f"{name}_free")

    def start(self, reader):
        reader.sem_inc(self.free, len(self.banks))


class Uses:

    def __init__(self, ring, turn, odd, per):
        self.ring, self.turn, self.odd, self.per, self.n = ring, turn, odd, per, 0

    def _bank(self):
        self.n += 1
        return self.ring.banks[(self.odd * self.per + self.n - 1) % len(self.ring.banks)]

    def fill(self, pe):
        pe.wait_ge(self.ring.free, self.turn * self.per + self.n + 1)
        return self._bank()

    def filled(self, mm):
        mm.then_inc(self.ring.full, 1)

    def take(self, reader):
        reader.wait_ge(self.ring.full, self.turn * self.per + self.n + 1)
        return self._bank()

    def emptied(self, ins):
        ins.then_inc(self.ring.free, 1)

    def settled(self, reader):
        reader.wait_ge(self.ring.free, self.turn * self.per + self.n + len(self.ring.banks))

    def end(self):
        assert self.n == self.per, f"{self.ring.full}: {self.n} uses in a batch, not {self.per}"


class Attn:

    def __init__(self, name, sets, heads, hd, kind, packed, scale):
        self.name, self.sets, self.heads, self.hd, self.kind = name, sets, heads, hd, kind
        self.packed, self.scale = packed, scale
        self.units = sets * heads
        self.pairs = self.units // 2
        self.lone = 2 * heads if sets > 1 else heads
        self.by_feature = hd + 1 <= 32
        self.vw = 32 if self.by_feature else hd + 1
        self.width = self.units * hd
        self.per_bank = 16 if self.by_feature else 512 // self.vw
        self.out_banks = -(-self.units // self.per_bank)

    def keys(self, qt):
        return QT if self.kind == "full" else qt + 1

    def mask(self, qt, kb):
        if self.kind == "causal":
            return 0 if qt == kb else None
        if self.kind == "window":
            return 2 if qt == kb else 4
        return None

    def lone_of(self, u):
        return 2 * (u // 4) + u % 2 if self.sets > 1 else u

    def head_of(self, u):
        return u // self.sets

    def max_chunks(self, qt):
        n = 4 // self.keys(qt)
        return [(u, n) for u in range(0, self.units, n)]

    def exp_chunks(self, qt):
        return [(kb, u) for u in range(0, self.units, 4) for kb in range(self.keys(qt))]

    @property
    def n_exp(self):
        return sum(len(self.exp_chunks(qt)) for qt in range(QT))

    @property
    def n_max(self):
        return sum(len(self.max_chunks(qt)) for qt in range(QT)) + QT

    def front(self, project):
        steps = [("norm",), ("hT",)] + project
        first = [("max", 0, j) for j in range(len(self.max_chunks(0)))]
        second = [("max", 1, j) for j in range(len(self.max_chunks(1)))]
        cut = min(2, len(second) - 1)
        return steps + first + [("parts", 0)] + second[:cut] + [("maxT", 0)] + second[cut:] + [("parts", 1), ("maxT", 1)]

    def back(self):
        if self.by_feature:
            at = [(n, n, ("exp", qt, j)) for n, (qt, j) in
                  enumerate((qt, j) for qt in range(QT) for j in range(len(self.exp_chunks(qt))))]
            done = 0
            for qt in range(QT):
                for k in range(self.out_banks):
                    done += len(self.exp_chunks(qt)) // self.out_banks
                    at += [(done + 3, 100 + done, ("drain", qt, k)), (done + 5, 100 + done, ("turn", qt, k))]
                at += [(done + 7, 200, ("outT", qt)), (done + 9, 200, ("out", qt))]
            at.append((self.n_exp + 1, 50, ("heads", 1)))
            return [step for _, _, step in sorted(at)]
        first = [("exp", 0, j) for j in range(len(self.exp_chunks(0)))]
        second = [("exp", 1, j) for j in range(len(self.exp_chunks(1)))]
        c = min(2, len(second) // 2)
        return (first + [("heads", 0)] + second[:c] + [("outT", 0)] + second[c:2 * c] + [("out", 0)] + second[2 * c:]
                + [("heads", 1), ("outT", 1), ("out", 1)])


def merged(front, back):
    out, f, k = [], 0, 0
    while f < len(front) or k < len(back):
        if k >= len(back) or (f < len(front) and f * len(back) <= k * len(front)):
            out.append(("front",) + front[f])
            f += 1
        else:
            out.append(("back",) + back[k])
            k += 1
    return out


def step_lists(a, project):
    both = merged(a.front(project), a.back())
    fronts, backs = [x for x in both if x[0] == "front"], [x for x in both if x[0] == "back"]
    return lambda back_turn, front_turn: fronts if back_turn is None else backs if front_turn is None else both


def pipelined(eng, go):
    go(None, 0, 0, 0)
    with eng.Fori(0, (BATCH - 2) // 2) as pair:
        go(pair * 2, 0, pair * 2 + 1, 1)
        go(pair * 2 + 1, 1, pair * 2 + 2, 0)
    go(BATCH - 2, 0, BATCH - 1, 1)
    go(BATCH - 1, 1, None, 0)


class Attention:

    def __init__(self, s, nc, a, res, front_links, back_links, v_uses, q_uses, v_banks=2, q_banks=1, out_bias=None,
                 ghost=None):
        self.s, self.nc, self.a, self.res = s, nc, a, res
        self.front_links, self.back_links, self.v_uses, self.q_uses = front_links, back_links, v_uses, q_uses
        self.out_bias, self.ghost = out_bias, ghost
        qk = BF16 if a.packed else F32
        self.qT = [s.sb(f"qT{n}", [P, a.pairs, TOK], qk) for n in range(2)]
        self.k_alone = [s.sb(f"k_alone{n}", [P, a.lone, TOK], qk) for n in range(2)]
        self.v = [s.sb(f"v{n}", [P, QT, a.heads, a.vw]) for n in range(2)]
        if a.by_feature:
            self.featured = [s.sb(f"featured{n}", [P, 512]) for n in range(2)]
        self.row_max = s.sb("row_max", [P, QT, a.heads, a.sets])
        self.rest = s.sb("rest", [P, a.heads, a.sets])
        self.max_parts = s.sb("max_parts", [P, QT, a.sets, P], BF16)
        self.maxT = [s.sb(f"maxT{n}", [P, QT, a.sets, P], BF16) for n in range(2)]
        self.probs = [s.sb(f"probs{n}", [P, 512]) for n in range(4)]
        self.inverse = s.sb("inverse", [P, a.units])
        self.denominator = s.sb("denominator", [P, a.units])
        self.heads_out = [s.sb(f"heads_out{n}", [P, a.width]) for n in range(QT if a.by_feature else 1)]
        self.heads_outT = s.sb("heads_outT", [P, a.width // P, P])
        self.w_out = s.sb("w_out", [P, a.width // P, D])
        self.xhat, self.hT, self.scratch = s.sb("xhat", [P, QT, D]), s.sb("hT", [P, TOK]), s.sb("scratch", [P, D])
        self.to_dve = Ring(s, "to_dve", v_banks)
        self.to_act = Ring(s, "to_act", q_banks) if q_banks else None
        self.scores = Ring(s, "scores", 2)
        self.tail = Ring(s, "tail", 1)
        if a.by_feature:
            self.outs = Ring(s, "outs", 2)
        else:
            self.out = [s.bank(f"out{n}") for n in range(a.out_banks)]
        self.xhat_ready, self.hT_ready, self.qkv_ready = s.sem("xhat_ready"), s.sem("hT_ready"), s.sem("qkv_ready")
        self.qT_ready = s.sem("qT_ready") if q_banks else None
        self.parts_ready, self.maxT_ready = s.sem("parts_ready"), s.sem("maxT_ready")
        self.probs_ready = self.scores.free
        self.probs_free = s.sem("probs_free")
        self.heads_ready, self.headsT_ready = s.sem("heads_ready"), s.sem("headsT_ready")
        self.front_chained, self.back_chained = s.sem("front_chained"), s.sem("back_chained")
        self.started, self.loaded = s.sem("started"), s.sem("loaded")

    def begin_vector(self, dve):
        self.to_dve.start(dve)
        self.tail.start(dve)
        dve.sem_inc(self.heads_ready, 1)
        for v in self.v:
            dve.memset(v[:, :, :, self.a.hd:self.a.hd + 1], 1.0)
            if self.a.vw > self.a.hd + 1:
                dve.memset(v[:, :, :, self.a.hd + 1:self.a.vw], 0.0)
        for k in self.k_alone:
            dve.memset(k[:, :, :], 0.0)
        dve.memset(self.max_parts[:, :, :, :], 0.0).then_inc(self.started, 1)

    def begin_scalar(self, act):
        self.scores.start(act)
        act.sem_inc(self.probs_free, 4)
        if self.to_act:
            self.to_act.start(act)
        if self.a.by_feature:
            self.outs.start(act)


    def pe_batch(self, pe, steps, project, bt, bo, ft, fo):
        a = self.a
        front = Uses(self.to_dve, ft, fo, self.v_uses)
        to_act = Uses(self.to_act, ft, fo, self.q_uses) if self.to_act else None
        scores, tail = Uses(self.scores, bt, bo, a.n_exp), Uses(self.tail, bt, bo, self.tail_uses)
        outs = Uses(self.outs, bt, bo, QT * a.out_banks) if a.by_feature else None
        lagging = []
        for half, kind, *at in steps:
            if kind == "norm":
                pass
            elif kind == "hT":
                self.pe_hT(pe, front, ft)
            elif kind == "max":
                self.pe_max(pe, front, at[0], *a.max_chunks(at[0])[at[1]], fo, first=at == [0, 0], turn=ft)
            elif kind == "parts":
                pass
            elif kind == "maxT":
                self.pe_maxT(pe, front, at[0], ft)
            elif kind == "exp":
                self.pe_scores(pe, scores, at[0], *a.exp_chunks(at[0])[at[1]], bo, bt, first=at[1] == 0)
                lagging.append((scores.n - 1, at[0]) + a.exp_chunks(at[0])[at[1]])
                if len(lagging) > 2:
                    self.pe_values(pe, outs, bt, bo, *lagging.pop(0))
            elif kind == "heads":
                while lagging:
                    self.pe_values(pe, outs, bt, bo, *lagging.pop(0))
            elif kind == "turn":
                self.pe_turn(pe, tail, at[0], at[1], bt)
            elif kind == "drain":
                pass
            elif kind == "outT":
                self.pe_outT(pe, tail, at[0], bt)
            elif kind == "out":
                self.pe_out(pe, tail, at[0], bt)
            else:
                project(pe, kind, at, front, to_act, ft, fo)
        if ft is not None:
            front.end()
            if to_act:
                to_act.end()
        if bt is not None:
            scores.end()
            tail.end()

    @property
    def tail_uses(self):
        return QT * (-(-(self.a.width // P) // 4) + 1 + (self.a.out_banks if self.a.by_feature else 0))

    def pe_hT(self, pe, front, turn):
        pe.wait_ge(self.xhat_ready, turn + 1)
        bank = front.fill(pe)
        for t in range(QT):
            mm = pe.transpose(bank[:, t * P:(t + 1) * P], self.xhat[:, t, :], self.res["ident"][:, :])
        front.filled(mm)

    def pe_max(self, pe, front, qt, u0, nu, odd, first, turn):
        a, nk = self.a, self.a.keys(qt)
        if first:
            pe.wait_ge(self.qkv_ready, turn + 1)
            if self.qT_ready:
                pe.wait_ge(self.qT_ready, turn + 1)
        bank = front.fill(pe)
        w = 2 * nk * P
        for n, u in enumerate(range(u0, u0 + nu, 2)):
            lone = a.lone_of(u)
            mm = pe.matmul(bank[:, n * w:(n + 1) * w].rearrange("p (h k) -> p h k", h=2),
                           self.qT[odd][:, u // 2, qt * P:(qt + 1) * P], self.k_alone[odd][:, lone:lone + 2, 0:nk * P],
                           start=(n == 0), stop=True, skip_group_check=True)
        for kb in range(nk):
            mask = a.mask(qt, kb)
            if mask is not None:
                out = bank[:, :].rearrange("p (h k) -> p h k", h=nu)[:, :, kb * P:(kb + 1) * P]
                mm = pe.matmul(out, self.res["identb"][:, :],
                               self.res["masks"][:, mask:mask + 1, :].broadcast_to([P, nu, P]),
                               start=False, stop=True, skip_group_check=True)
        front.filled(mm)

    def pe_maxT(self, pe, front, qt, turn):
        pe.wait_ge(self.parts_ready, turn * QT + qt + 1)
        bank = front.fill(pe)
        for s in range(self.a.sets):
            mm = pe.transpose(bank[:, :].bitcast(BF16)[:, s * P:(s + 1) * P], self.max_parts[:, qt, s, :],
                              self.res["identb"][:, :])
        front.filled(mm)

    def pe_scores(self, pe, scores, qt, kb, u0, odd, turn, first):
        a, res = self.a, self.res
        if first:
            pe.wait_ge(self.maxT_ready, turn * QT + qt + 1)
        bank = scores.fill(pe)
        queries, keys = slice(qt * P, (qt + 1) * P), slice(kb * P, (kb + 1) * P)
        units = bank[:, :].rearrange("p (u q) -> p u q", u=4)
        if a.sets > 1:
            for par in range(2):
                pe.matmul(units.rearrange("p (g two) q -> p g two q", two=2)[:, :, par, :],
                          self.k_alone[odd][:, a.lone_of(u0) + par, keys], self.qT[odd][:, u0 // 2:u0 // 2 + 2, queries],
                          start=(par == 0), stop=False, skip_group_check=True)
            mm = pe.matmul(units, res["minus_head"][:, a.head_of(u0), :], self.maxT[odd][:, qt, :, :],
                           start=False, stop=True, skip_group_check=True)
        else:
            for j in range(4):
                u = u0 + j
                pe.matmul(units[:, j, :], self.k_alone[odd][:, u, keys], self.qT[odd][:, u // 2, queries],
                          start=(j == 0), stop=False, skip_group_check=True)
            for j in range(4):
                mm = pe.matmul(units[:, j, :], res["minus_head"][:, u0 + j, :], self.maxT[odd][:, qt, 0, :],
                               start=False, stop=True, skip_group_check=True)
        mask = a.mask(qt, kb)
        if mask is not None:
            mm = pe.matmul(units, res["identb"][:, :], res["masks"][:, mask + 1:mask + 2, :].broadcast_to([P, 4, P]),
                           start=False, stop=True, skip_group_check=True)
        scores.filled(mm)

    def pe_values(self, pe, outs, turn, odd, n, qt, kb, u0):
        a = self.a
        pe.wait_ge(self.probs_ready, turn * a.n_exp + n + 3)
        if a.by_feature:
            if kb == 0 and u0 % 16 == 0:
                self.out_now = outs.fill(pe)
            probs = self.probs[(odd * a.n_exp + n) % 4]
            c = u0 % 16 // 4
            last = kb == a.keys(qt) - 1
            for j in range(4):
                mm = pe.matmul(self.out_now[32 * j:32 * j + 32, c * P:(c + 1) * P], self.v[odd][:, kb, a.head_of(u0 + j), :],
                               probs[:, j * P:(j + 1) * P], start=(kb == 0), stop=last, skip_group_check=True)
            mm.then_inc(self.probs_free, 1)
            if last and u0 % 16 == 12:
                pe.wait_ge(self.probs_free, turn * a.n_exp + n + 5)
                pe.sem_inc(self.outs.full, 1)
            return
        if kb == 0 and u0 == 0:
            pe.wait_ge(self.heads_ready, turn * QT + qt + 1)
        probs = self.probs[(odd * a.n_exp + n) % 4]
        for u in range(u0, u0 + 4):
            col = (u % a.per_bank) * a.vw
            mm = pe.matmul(self.out[u // a.per_bank][:, col:col + a.vw], probs[:, (u - u0) * P:(u - u0 + 1) * P],
                           self.v[odd][:, kb, a.head_of(u), :], start=(kb == 0 and u % a.per_bank == 0),
                           stop=(kb == a.keys(qt) - 1), skip_group_check=True)
        mm.then_inc(self.probs_free, 1)

    def pe_turn(self, pe, tail, qt, k, turn):
        n = qt * self.a.out_banks + k
        pe.wait_ge(self.outs.free, turn * QT * self.a.out_banks + n + 3)
        bank = tail.fill(pe)
        for c in range(4):
            mm = pe.transpose(bank[:, c * P:(c + 1) * P], self.featured[n % 2][:, c * P:(c + 1) * P], self.res["ident"][:, :])
        tail.filled(mm)

    def pe_outT(self, pe, tail, qt, turn):
        nt = self.a.width // P
        pe.wait_ge(self.heads_ready, turn * QT + qt + 2)
        for t0 in range(0, nt, 4):
            bank = tail.fill(pe)
            for t in range(t0, min(t0 + 4, nt)):
                mm = pe.transpose(bank[:, (t - t0) * P:(t - t0 + 1) * P], self.heads_out[qt % len(self.heads_out)][:, t * P:(t + 1) * P],
                                  self.res["ident"][:, :])
            tail.filled(mm)

    def pe_out(self, pe, tail, qt, turn):
        nt = self.a.width // P
        pe.wait_ge(self.headsT_ready, turn * QT + qt + 1)
        bank = tail.fill(pe)
        for t in range(nt):
            mm = pe.matmul(bank[:, 0:D], self.heads_outT[:, t, :], self.w_out[:, t, :], start=(t == 0), stop=(t == nt - 1))
        tail.filled(mm)


    def act_batch(self, act, steps, project, bt, bo, ft, fo):
        a = self.a
        scores = Uses(self.scores, bt, bo, a.n_exp)
        to_act = Uses(self.to_act, ft, fo, self.q_uses) if self.to_act else None
        outs = Uses(self.outs, bt, bo, QT * a.out_banks) if a.by_feature else None
        for half, kind, *at in steps:
            if kind == "exp":
                n = scores.n
                bank = scores.take(act)
                act.wait_ge(self.probs_free, bt * a.n_exp + n + 1)
                self.nc.scalar.activation(self.probs[(bo * a.n_exp + n) % 4][:, :], bank[:, :], ACT.Exp,
                                          scale=a.scale).then_inc(self.probs_ready, 1)
            elif kind == "drain":
                qt, k = at
                n = qt * a.out_banks + k
                bank = outs.take(act)
                self.nc.scalar.copy(self.featured[n % 2][:, :], bank[:, :]).then_inc(self.outs.free, 1)
            elif half == "front" and project:
                project(act, kind, at, to_act, ft, fo)


    def dve_batch(self, dve, steps, project, norm, modulate, finish, bt, bo, ft, fo):
        front = Uses(self.to_dve, ft, fo, self.v_uses)
        tail = Uses(self.tail, bt, bo, self.tail_uses)
        fchain = Chain(dve, self.front_chained, ft, self.front_links)
        bchain = Chain(dve, self.back_chained, bt, self.back_links)
        for half, kind, *at in steps:
            if kind == "norm":
                norm(dve, fchain, ft)
            elif kind == "hT":
                modulate(dve, front, ft)
            elif kind == "max":
                u0, nu = self.a.max_chunks(at[0])[at[1]]
                bank = front.take(dve)
                front.emptied(dve.tensor_reduce(
                    self.row_max[:, at[0], :, :].rearrange("p h s -> p (h s)")[:, u0:u0 + nu],
                    bank[:, :].rearrange("p (h k) -> p h k", h=nu), AX_X, ALU.max))
            elif kind == "parts":
                self.dve_parts(dve, front, fchain, at[0])
            elif kind == "maxT":
                bank = front.take(dve)
                front.emptied(dve.tensor_copy(self.maxT[fo][:, at[0], :, :].rearrange("p s q -> p (s q)"),
                                              bank[:, :].bitcast(BF16)[:, 0:self.a.sets * P]))
                front.settled(dve)
                dve.sem_inc(self.maxT_ready, 1)
            elif kind == "heads":
                if not self.a.by_feature:
                    self.dve_heads(dve, bchain, at[0], bt)
            elif kind == "turn":
                self.dve_turn(dve, tail, bchain, at[0], at[1])
            elif kind == "drain":
                pass
            elif kind == "outT":
                nt = self.a.width // P
                for t0 in range(0, nt, 4):
                    m = min(4, nt - t0)
                    bank = tail.take(dve)
                    tail.emptied(dve.tensor_copy(self.heads_outT[:, t0:t0 + m, :].rearrange("p t q -> p (t q)"),
                                                 bank[:, 0:m * P]))
                tail.settled(dve)
                dve.sem_inc(self.headsT_ready, 1)
            elif kind == "out":
                bank = tail.take(dve)
                finish(dve, bchain, tail, bt, at[0], bank)
            elif kind != "exp":
                project(dve, kind, at, front, fchain, ft, fo)
        if ft is not None:
            front.end()
            fchain.end()
        if bt is not None:
            tail.end()
            bchain.end()

    def dve_hT(self, dve, front, turn):
        bank = front.take(dve)
        front.emptied(dve.tensor_scalar(self.hT[:, :], bank[:, 0:TOK], self.res["mod"][:, 1, bass.ds(turn, 1)],
                                        self.res["mod"][:, 0, bass.ds(turn, 1)], ALU.mult, ALU.add))
        front.settled(dve)
        dve.sem_inc(self.hT_ready, 1)

    def dve_parts(self, dve, front, chain, qt):
        a = self.a
        front.settled(dve)
        parts = self.max_parts[:, qt, :, 0:48].rearrange("p s (t h) -> p t h s", t=3)[:, :, 0:a.heads, :]
        top = self.row_max[:, qt, :, :]
        chain.link(dve.tensor_copy(parts[:, 0, :, :], top))
        chain.link(dve.tensor_tensor(self.rest[:, :, :], top, parts[:, 0, :, :], ALU.subtract))
        chain.link(dve.tensor_copy(parts[:, 1, :, :], self.rest[:, :, :]))
        dve.tensor_tensor(parts[:, 2, :, :], self.rest[:, :, :], parts[:, 1, :, :],
                          ALU.subtract).then_inc(self.parts_ready, 1)

    def dve_heads(self, dve, chain, qt, turn):
        a = self.a
        done = sum(len(a.exp_chunks(q)) for q in range(qt + 1))
        dve.wait_ge(self.probs_free, turn * a.n_exp + done + 4)
        for ob in range(a.out_banks):
            u0, u1 = ob * a.per_bank, min(a.units, (ob + 1) * a.per_bank)
            o = self.out[ob][:, 0:(u1 - u0) * a.vw].rearrange("p (u w) -> p u w", w=a.vw)
            if self.ghost is None:
                chain.link(dve.reciprocal(self.inverse[:, u0:u1], o[:, :, a.hd]))
            else:
                chain.link(dve.tensor_tensor(self.denominator[:, u0:u1], o[:, :, a.hd], self.ghost[:, u0:u1], ALU.add))
                chain.link(dve.reciprocal(self.inverse[:, u0:u1], self.denominator[:, u0:u1]))
            ins = dve.tensor_tensor(
                self.heads_out[0][:, u0 * a.hd:u1 * a.hd].rearrange("p (u w) -> p u w", w=a.hd), o[:, :, 0:a.hd],
                self.inverse[:, u0:u1].unsqueeze(2).broadcast_to([P, u1 - u0, a.hd]), ALU.mult)
        ins.then_inc(self.heads_ready, 1)

    def dve_turn(self, dve, tail, chain, qt, k):
        a = self.a
        bank = tail.take(dve)
        o = bank[:, :].rearrange("p (u w) -> p u w", w=32)
        chain.link(dve.reciprocal(self.inverse[:, 0:16], o[:, :, a.hd]))
        ins = dve.tensor_tensor(
            self.heads_out[qt][:, 16 * k * a.hd:16 * (k + 1) * a.hd].rearrange("p (u w) -> p u w", w=a.hd), o[:, :, 0:a.hd],
            self.inverse[:, 0:16].unsqueeze(2).broadcast_to([P, 16, a.hd]), ALU.mult)
        tail.emptied(ins)
        if k == a.out_banks - 1:
            tail.settled(dve)
            dve.sem_inc(self.heads_ready, 1)

    def finish_x(self, dve, chain, tail, turn, qt, bank):
        x = x_tile(self.res, turn * QT + qt)
        g = self.res["gate"][:, 0, bass.ds(turn, 1), :].rearrange("p a d -> p (a d)")
        if self.out_bias is None:
            tail.emptied(dve.tensor_tensor(self.scratch[:, :], bank[:, 0:D], g, ALU.mult))
            tail.settled(dve)
        else:
            tail.emptied(dve.tensor_tensor(self.scratch[:, :], bank[:, 0:D], self.out_bias, ALU.add))
            tail.settled(dve)
            chain.link(dve.tensor_tensor(self.scratch[:, :], self.scratch[:, :], g, ALU.mult))
        chain.link(dve.tensor_tensor(x, x, self.scratch[:, :], ALU.add))


def x_tile(res, n):
    return res["x"][:, bass.ds(n, 1), :].rearrange("p a d -> p (a d)")


def load(sp, loaded, pairs):
    for dst, src in pairs:
        sp.dma_start(dst, src).then_inc(loaded, 16)


def row_of(dram, n=P):
    return dram.unsqueeze(0).broadcast_to([n, dram.shape[0]])


def layer0_attention(nc, dram, res):
    small_head_attention(nc, Attn("a0", 4, 16, 8, "causal", True, 8 ** -0.5), dram["L0_w"], dram["L0_wo"], None, res)


def layer3_attention(nc, dram, res):
    small_head_attention(nc, Attn("a3", 1, 16, 8, "full", True, 8 ** -0.5), dram["L3_w"], dram["L3_wo"],
                         dram["L3_attn_b_proj"], res)


def small_head_attention(nc, a, w_dram, wo_dram, bias_dram, res):
    NQ, QW, KW = a.units * 8, a.units * 8, D
    one_bank = QW + 2 * KW <= 512
    nb = 1 if one_bank else 2
    k_tiles = 16 if a.sets > 1 else 8
    v_uses = 1 + QT * nb + QT * (k_tiles // 8) + a.n_max
    q_uses = QT * a.pairs // 8
    n_loaded = 32 if bias_dram is None else 48
    with ExitStack() as ctx:
        s = Scope(nc, ctx, a.name)
        w = s.sb("w", [P, QW + 2 * KW])
        bias = s.sb("bias", [P, D])
        norm = Norm(s)
        at = Attention(s, nc, a, res, 2 + 6 + (3 if a.sets > 1 else 2) * QT, QT * a.out_banks + QT * (1 if bias_dram is None else 2), v_uses,
                       q_uses, out_bias=None if bias_dram is None else bias[:, :])
        packed_q = [s.sb(f"packed_q{t}", [P, a.units, 8, 8], BF16) for t in range(QT)]
        packed_k = [s.sb(f"packed_k{t}", [P, a.heads, 8, 8], BF16) for t in range(QT)]
        twice_k = [s.sb(f"twice_k{t}", [P, a.heads, 2, 64], BF16) for t in range(QT)] if a.sets > 1 else None
        rest_q = [s.sb(f"rest_q{t}", [P, a.units, 8]) for t in range(QT)]
        rest_k = s.sb("rest_k", [P, a.heads, 8])
        high_ready, rest_ready, packed_ready = s.sem("high_ready"), s.sem("rest_ready"), s.sem("packed_ready")
        k_packed_ready, pool_chained, idle = s.sem("k_packed_ready"), s.sem("pool_chained"), s.sem("idle")
        project = [("qkv", t) for t in range(QT)] + [("pack", t) for t in range(QT)]
        steps = step_lists(a, project)
        block = s.block()

        @block.sync
        def _(sp):
            load(sp, at.loaded, [(w[:, :], w_dram), (at.w_out[:, :, :], wo_dram.rearrange("(t p) d -> p t d", p=P))])
            if bias_dram is not None:
                load(sp, at.loaded, [(bias[:, :], row_of(bias_dram))])

        @block.tensor
        def _(pe):
            pe.wait_ge(at.loaded, n_loaded)
            pe.wait_ge(at.started, 1)

            def project(pe, kind, where, front, to_act, turn, odd):
                t, = where
                if kind == "qkv":
                    if t == 0:
                        pe.wait_ge(at.hT_ready, turn + 1)
                    bank = front.fill(pe)
                    cut = QW + 2 * KW if one_bank else QW
                    front.filled(pe.matmul(bank[:, 0:cut], at.hT[:, t * P:(t + 1) * P], w[:, 0:cut], start=True, stop=True))
                    if not one_bank:
                        bank = front.fill(pe)
                        front.filled(pe.matmul(bank[:, 0:2 * KW], at.hT[:, t * P:(t + 1) * P], w[:, QW:QW + 2 * KW],
                                               start=True, stop=True))
                    return
                pe.wait_ge(k_packed_ready, turn * QT + t + 1)
                for n in range(k_tiles // 8):
                    bank = front.fill(pe)
                    for j in range(8):
                        h = n * 8 + j
                        if a.sets > 1:
                            tile = twice_k[t][:, h, :, :].rearrange("p c x -> p (c x)")
                        else:
                            tile = packed_k[t][:, 2 * h:2 * h + 2, :, :].rearrange("p h s d -> p (h s d)")
                        mm = pe.transpose(bank[:, :].bitcast(BF16)[:, j * P:(j + 1) * P], tile, res["identb"][:, :])
                    front.filled(mm)
                pe.wait_ge(packed_ready, turn * QT + t + 1)
                for n in range(a.pairs // 8):
                    bank = to_act.fill(pe)
                    for j in range(8):
                        g = n * 8 + j
                        mm = pe.transpose(bank[:, :].bitcast(BF16)[:, j * P:(j + 1) * P],
                                          packed_q[t][:, 2 * g:2 * g + 2, :, :].rearrange("p u s d -> p (u s d)"),
                                          res["identb"][:, :])
                    to_act.filled(mm)

            pipelined(pe, lambda bt, bo, ft, fo: at.pe_batch(pe, steps(bt, ft), project, bt, bo, ft, fo))

        @block.scalar
        def _(act):
            at.begin_scalar(act)
            act.wait_ge(at.started, 1)

            def project(act, kind, where, to_act, turn, odd):
                if kind == "qkv":
                    t, = where
                    use = 1 + t * nb
                    act.wait_ge(at.to_dve.full, turn * v_uses + use + 1)
                    bank = at.to_dve.banks[(odd * v_uses + use) % 2]
                    nc.scalar.copy(packed_q[t][:, :, 0:3, :],
                                   bank[:, 0:QW].rearrange("p (u d) -> p u d", d=8).unsqueeze(2)
                                   .broadcast_to([P, a.units, 3, 8])).then_inc(high_ready, 1)
                if kind == "pack":
                    t, = where
                    for n in range(a.pairs // 8):
                        bank = to_act.take(act)
                        to_act.emptied(nc.scalar.copy(at.qT[odd][:, 8 * n:8 * n + 8, t * P:(t + 1) * P],
                                                      bank[:, :].bitcast(BF16).rearrange("p (g q) -> p g q", q=P)))
                    if t == QT - 1:
                        to_act.settled(act)
                        act.sem_inc(at.qT_ready, 1)

            pipelined(act, lambda bt, bo, ft, fo: at.act_batch(act, steps(bt, ft), project, bt, bo, ft, fo))

        @block.gpsimd
        def _(pool):
            pool.wait_ge(norm.power_ready, 1)
            pool.wait_ge(at.started, 1)
            with pool.Fori(0, BATCH) as turn:
                norm.gpsimd(pool, turn)
                for t in range(QT):
                    pool.wait_ge(rest_ready, turn * QT + t + 1)
                    pool.sem_inc(idle, 1)
                    pool.tensor_copy(packed_q[t][:, :, 3:5, :],
                                     rest_q[t][:, :, :].unsqueeze(2).broadcast_to([P, a.units, 2, 8])).then_inc(pool_chained, 1)
                    pool.wait_ge(pool_chained, turn * QT + t + 1)
                    pool.tensor_tensor(packed_q[t][:, :, 5, :], rest_q[t][:, :, :], packed_q[t][:, :, 3, :],
                                       ALU.subtract).then_inc(packed_ready, 1)

        @block.vector
        def _(dve):
            norm.start(dve)
            for t in range(QT):
                dve.memset(packed_q[t][:, :, :, :], 0.0)
                dve.memset(packed_k[t][:, :, :, :], 0.0)
            at.begin_vector(dve)
            dve.wait_ge(at.loaded, n_loaded)
            dve.wait_ge(at.started, 1)

            def project(dve, kind, where, front, chain, turn, odd):
                t, = where
                if kind == "qkv":
                    bank = front.take(dve)
                    dve.wait_ge(high_ready, turn * QT + t + 1)
                    ins = dve.tensor_tensor(rest_q[t][:, :, :], bank[:, 0:QW].rearrange("p (u d) -> p u d", d=8),
                                            packed_q[t][:, :, 0, :], ALU.subtract)
                    ins.then_inc(rest_ready, 1)
                    k0 = QW
                    if not one_bank:
                        dve.wait_ge(rest_ready, turn * QT + t + 1)
                        dve.sem_inc(at.to_dve.free, 1)
                        bank, k0 = front.take(dve), 0
                    keys = bank[:, k0:k0 + KW].rearrange("p (h d) -> p h d", d=8)
                    dve.tensor_copy(at.v[odd][:, t, :, 0:8], bank[:, k0 + KW:k0 + 2 * KW].rearrange("p (h d) -> p h d", d=8))
                    odd_slots = packed_k[t][:, :, 0:6, :].rearrange("p h (s two) d -> p h s two d", two=2)[:, :, :, 1, :]
                    even_slots = packed_k[t][:, :, 0:6, :].rearrange("p h (s two) d -> p h s two d", two=2)[:, :, 1:3, 0, :]
                    chain.link(dve.tensor_copy(odd_slots, keys.unsqueeze(2).broadcast_to([P, a.heads, 3, 8])))
                    front.emptied(dve.tensor_tensor(rest_k[:, :, :], keys, packed_k[t][:, :, 1, :], ALU.subtract))
                    front.settled(dve)
                    chain.link(dve.tensor_copy(even_slots, rest_k[:, :, :].unsqueeze(2).broadcast_to([P, a.heads, 2, 8])))
                    ins = dve.tensor_tensor(packed_k[t][:, :, 0, :], rest_k[:, :, :], packed_k[t][:, :, 2, :], ALU.subtract)
                    if a.sets > 1:
                        chain.link(ins)
                        ins = dve.tensor_copy(twice_k[t][:, :, :, :], packed_k[t][:, :, :, :].rearrange("p h s d -> p h (s d)")
                                              .unsqueeze(2).broadcast_to([P, a.heads, 2, 64]))
                    ins.then_inc(k_packed_ready, 1)
                    return
                for n in range(k_tiles // 8):
                    bank = front.take(dve)
                    for half in range(2):
                        r = slice(64 * half, 64 * half + 64)
                        ins = dve.tensor_copy(
                            at.k_alone[odd][r, 16 * n:16 * n + 16, t * P:(t + 1) * P]
                            .rearrange("p (g two) q -> p g two q", two=2)[:, :, half, :],
                            bank[r, :].bitcast(BF16).rearrange("p (g q) -> p g q", q=P))
                    front.emptied(ins)
                if t == QT - 1:
                    front.settled(dve)
                    dve.sem_inc(at.qkv_ready, 1)

            def normalize(dve, chain, turn):
                norm.vector(dve, chain, turn, lambda t: x_tile(res, turn * QT + t), at.xhat, at.xhat_ready)

            pipelined(dve, lambda bt, bo, ft, fo: at.dve_batch(dve, steps(bt, ft), project, normalize, at.dve_hT,
                                                               at.finish_x, bt, bo, ft, fo))


class Turns:

    def __init__(self, b, turn, per, dt16=None):
        self.b, self.turn, self.per, self.n = b, turn, per, 0

    def fill(self, pe):
        if self.n >= 2:
            pe.wait_ge(self.b["vbank_read"], self.turn * self.per + self.n - 1)
        self.n += 1
        return self.b["vbank"][(self.n - 1) % 2]

    def full(self, mm):
        mm.then_inc(self.b["vbank_full"], 1)

    def take(self, dve):
        dve.wait_ge(self.b["vbank_full"], self.turn * self.per + self.n + 1)
        self.n += 1
        return self.b["vbank"][(self.n - 1) % 2]

    def read(self, ins):
        ins.then_inc(self.b["vbank_read"], 1)

    def settled(self, dve):
        dve.wait_ge(self.b["vbank_read"], self.turn * self.per + self.n)

    def end(self):
        assert self.n == self.per, f"{self.n} banks in a turn, not {self.per}"


def pe_norm_transpose(pe, b, turns, res, xhat, turn):
    pe.wait_ge(b["xhat_ready"], turn + 1)
    bank = turns.fill(pe)
    for t in range(QT):
        mm = pe.transpose(bank[:, t * P:(t + 1) * P], xhat[:, t, :], res["ident"][:, :])
    turns.full(mm)


def dve_modulate(dve, b, turns, res, hT, which, turn):
    bank = turns.take(dve)
    ins = dve.tensor_scalar(hT[:, :], bank[:, 0:TOK], res["mod"][:, which + 1, bass.ds(turn, 1)],
                            res["mod"][:, which, bass.ds(turn, 1)], ALU.mult, ALU.add)
    turns.read(ins)
    return ins


def finish_tile(dve, chain, turns, res, gate, turn, qt, bank, scratch, bias=None):
    x = res["x"][:, bass.ds(turn * QT + qt, 1), :].rearrange("p a d -> p (a d)")
    g = res["gate"][:, gate, bass.ds(turn, 1), :].rearrange("p a d -> p (a d)")
    if bias is None:
        ins = dve.tensor_tensor(scratch[:, :], bank[:, 0:D], g, ALU.mult)
        turns.read(ins)
        turns.settled(dve)
    else:
        ins = dve.tensor_tensor(scratch[:, :], bank[:, 0:D], bias, ALU.add)
        turns.read(ins)
        turns.settled(dve)
        chain.link(dve.tensor_tensor(scratch[:, :], scratch[:, :], g, ALU.mult))
    chain.link(dve.tensor_tensor(x, x, scratch[:, :], ALU.add))


def layer1_attention(nc, dram, res):
    a = Attn("a1", 1, 16, 64, "causal", False, 64 ** -0.5)
    nt = a.width // P
    with ExitStack() as ctx:
        s = Scope(nc, ctx, a.name)
        w = s.sb("w", [P, 3 * a.width])
        qk_bias = s.sb("qk_bias", [P, 2 * a.pairs])
        v_bias = s.sb("v_bias", [P, a.heads, a.hd])
        ghost = s.sb("ghost", [P, a.heads])
        bias = s.sb("bias", [P, D])
        norm = Norm(s)
        at = Attention(s, nc, a, res, 2 + 6, QT * (2 * a.out_banks + 2), 1 + 2 * a.pairs + 2 * QT + a.n_max, 0,
                       q_banks=0, out_bias=bias[:, :], ghost=ghost)
        project = ([("q", g) for g in range(a.pairs)] + [("k", g) for g in range(a.pairs)]
                   + [("v", t, c) for t in range(QT) for c in range(2)])
        steps = step_lists(a, project)
        n_loaded = 6 * 16
        block = s.block()

        @block.sync
        def _(sp):
            load(sp, at.loaded, [(w[:, :], dram["L1_w"]),
                                 (at.w_out[:, :, :], dram["L1_wo"].rearrange("(t p) d -> p t d", p=P)),
                                 (qk_bias[:, :], dram["L1_qk_bias"]),
                                 (v_bias[:, :, :].rearrange("p h d -> p (h d)"), row_of(dram["L1_v_bias"])),
                                 (ghost[:, :], row_of(dram["L1_ghost"])),
                                 (bias[:, :], row_of(dram["L1_wo_bias"]))])

        @block.tensor
        def _(pe):
            pe.wait_ge(at.loaded, n_loaded)
            pe.wait_ge(at.started, 1)

            def project(pe, kind, where, front, to_act, turn, odd):
                if kind == "v":
                    t, c = where
                    bank = front.fill(pe)
                    front.filled(pe.matmul(bank[:, :], at.hT[:, t * P:(t + 1) * P],
                                           w[:, 2 * a.width + 512 * c:2 * a.width + 512 * (c + 1)], start=True, stop=True))
                    return
                n = where[0] + (a.pairs if kind == "k" else 0)
                if n == 0:
                    pe.wait_ge(at.hT_ready, turn + 1)
                bank = front.fill(pe)
                front.filled(pe.matmul(bank[:, 0:TOK], w[:, n * P:(n + 1) * P], at.hT[:, :], start=True, stop=True))

            pipelined(pe, lambda bt, bo, ft, fo: at.pe_batch(pe, steps(bt, ft), project, bt, bo, ft, fo))

        @block.scalar
        def _(act):
            at.begin_scalar(act)
            pipelined(act, lambda bt, bo, ft, fo: at.act_batch(act, steps(bt, ft), None, bt, bo, ft, fo))

        @block.gpsimd
        def _(pool):
            pool.wait_ge(norm.power_ready, 1)
            with pool.Fori(0, BATCH) as turn:
                norm.gpsimd(pool, turn)

        @block.vector
        def _(dve):
            norm.start(dve)
            at.begin_vector(dve)
            dve.wait_ge(at.loaded, n_loaded)
            dve.wait_ge(at.started, 1)

            def project(dve, kind, where, front, chain, turn, odd):
                bank = front.take(dve)
                if kind == "q":
                    g, = where
                    ins = dve.tensor_scalar(at.qT[odd][:, g, :], bank[:, 0:TOK], qk_bias[:, g:g + 1], None, ALU.add)
                elif kind == "k":
                    g, = where
                    for half in range(2):
                        r = slice(64 * half, 64 * half + 64)
                        ins = dve.tensor_scalar(at.k_alone[odd][r, 2 * g + half, :], bank[r, 0:TOK],
                                                qk_bias[r, a.pairs + g:a.pairs + g + 1], None, ALU.add)
                else:
                    t, c = where
                    ins = dve.tensor_tensor(at.v[odd][:, t, 8 * c:8 * c + 8, 0:a.hd],
                                            bank[:, :].rearrange("p (h d) -> p h d", d=a.hd),
                                            v_bias[:, 8 * c:8 * c + 8, :], ALU.add)
                front.emptied(ins)
                if kind == "v" and (t, c) == (QT - 1, 1):
                    front.settled(dve)
                    dve.sem_inc(at.qkv_ready, 1)

            def normalize(dve, chain, turn):
                norm.vector(dve, chain, turn, lambda t: x_tile(res, turn * QT + t), at.xhat, at.xhat_ready)

            pipelined(dve, lambda bt, bo, ft, fo: at.dve_batch(dve, steps(bt, ft), project, normalize, at.dve_hT,
                                                               at.finish_x, bt, bo, ft, fo))


def layer2_attention(nc, dram, res):
    scale = float(D) ** -0.5
    with ExitStack() as ctx:
        s = Scope(nc, ctx, "a2")
        w, wo = s.sb("w", [P, 3 * D]), s.sb("wo", [P, D])
        qk_bias, v_bias, bias = s.sb("qk_bias", [P, 2]), s.sb("v_bias", [P, D]), s.sb("bias", [P, D])
        qkT = [s.sb(f"qkT{n}", [P, 2, TOK]) for n in range(2)]
        v = [s.sb(f"v{n}", [P, QT, D]) for n in range(2)]
        sizes = [s.sb(f"sizes{n}", [P, TOK]) for n in range(QT)]
        top, shift = s.sb("top", [P, QT]), s.sb("shift", [P, QT])
        total, inverse = s.sb("total", [P, QT]), s.sb("inverse", [P, QT])
        BLOCKS = QT * (QT + 1) // 2
        probs, probsT = s.sb("probs", [P, BLOCKS * P]), s.sb("probsT", [P, BLOCKS * P])
        mixed, mixedT = s.sb("mixed", [P, QT, D]), s.sb("mixedT", [P, TOK])
        scratch = s.sb("scratch", [P, QT, D])
        fronts, scores, turned, outs = Ring(s, "fronts", 2), Ring(s, "scores", 2), Ring(s, "turned", 1), Ring(s, "outs", 1)
        m = Modulated(s, nc, res, 0, fronts)
        loaded, front_chained, back_chained, qkv_ready, shift_ready, probs_ready, mixed_ready = (s.sem(name) for name in (
            "loaded", "front_chained", "back_chained", "qkv_ready", "shift_ready", "probs_ready", "mixed_ready"))
        front = [("norm",), ("hT",), ("qk",), ("v",)]
        back = [("scores", 0), ("scores", 1), ("max", 0), ("max", 1), ("probsT",), ("mix",), ("mixedT",), ("out",)]
        block = s.block()

        def block_of(qt, kb):
            n = qt * (qt + 1) // 2 + kb
            return slice(n * P, (n + 1) * P)

        @block.sync
        def _(sp):
            load(sp, loaded, [(w[:, :], dram["L2_w"]), (wo[:, :], dram["L2_wo"]), (qk_bias[:, :], dram["L2_qk_bias"]),
                              (v_bias[:, :], row_of(dram["L2_v_bias"])), (bias[:, :], row_of(dram["L2_wo_bias"]))])

        @block.tensor
        def _(pe):
            pe.wait_ge(loaded, 5 * 16)

            def go(steps, bt, bo, ft, fo):
                front, score, turn, out = (Uses(fronts, ft, fo, 3), Uses(scores, bt, bo, QT), Uses(turned, bt, bo, 2),
                                           Uses(outs, bt, bo, 2))
                for half, kind, *at in steps:
                    m.pe(pe, kind, front, ft)
                    if kind == "qk":
                        pe.wait_ge(m.hT_ready, ft + 1)
                        bank = front.fill(pe)
                        for n in range(2):
                            mm = pe.matmul(bank[:, n * TOK:(n + 1) * TOK], w[:, n * P:(n + 1) * P], m.hT[fo][:, :],
                                           start=(n == 0), stop=True, skip_group_check=True)
                        front.filled(mm)
                    elif kind == "v":
                        bank = front.fill(pe)
                        for t in range(QT):
                            mm = pe.matmul(bank[:, t * D:(t + 1) * D], m.hT[fo][:, t * P:(t + 1) * P], w[:, 2 * P:3 * P],
                                           start=(t == 0), stop=True, skip_group_check=True)
                        front.filled(mm)
                    elif kind == "scores":
                        qt, = at
                        pe.wait_ge(qkv_ready, bt + 1)
                        bank = score.fill(pe)
                        score.filled(pe.matmul(bank[:, 0:(qt + 1) * P], qkT[bo][:, 0, qt * P:(qt + 1) * P],
                                               qkT[bo][:, 1, 0:(qt + 1) * P], start=True, stop=True))
                    elif kind == "probsT":
                        pe.wait_ge(probs_ready, bt * QT + QT)
                        bank = turn.fill(pe)
                        for n in range(BLOCKS):
                            mm = pe.transpose(bank[:, n * P:(n + 1) * P], probs[:, n * P:(n + 1) * P], res["ident"][:, :])
                        turn.filled(mm)
                    elif kind == "mix":
                        pe.wait_ge(turned.free, bt * 2 + 1 + 1)
                        bank = out.fill(pe)
                        for qt in range(QT):
                            for kb in range(qt + 1):
                                mm = pe.matmul(bank[:, qt * D:(qt + 1) * D], probsT[:, block_of(qt, kb)], v[bo][:, kb, :],
                                               start=(qt == 0), stop=(kb == qt), skip_group_check=True)
                        out.filled(mm)
                    elif kind == "mixedT":
                        pe.wait_ge(mixed_ready, bt + 1)
                        bank = turn.fill(pe)
                        for qt in range(QT):
                            mm = pe.transpose(bank[:, qt * P:(qt + 1) * P], mixed[:, qt, :], res["ident"][:, :])
                        turn.filled(mm)
                    elif kind == "out":
                        pe.wait_ge(turned.free, bt * 2 + 2 + 1)
                        bank = out.fill(pe)
                        for qt in range(QT):
                            mm = pe.matmul(bank[:, qt * D:(qt + 1) * D], mixedT[:, qt * P:(qt + 1) * P], wo[:, :],
                                           start=(qt == 0), stop=True, skip_group_check=True)
                        out.filled(mm)

            walk(pe, front, back, go)

        @block.scalar
        def _(act):
            scores.start(act)
            turned.start(act)

            def go(steps, bt, bo, ft, fo):
                score, turn = Uses(scores, bt, bo, QT), Uses(turned, bt, bo, 2)
                for half, kind, *at in steps:
                    if kind == "scores":
                        qt, = at
                        bank = score.take(act)
                        score.emptied(nc.scalar.activation(sizes[qt][:, 0:(qt + 1) * P], bank[:, 0:(qt + 1) * P], ACT.Abs))
                    elif kind == "max":
                        qt, = at
                        act.wait_ge(shift_ready, bt * QT + qt + 1)
                        first = block_of(qt, 0).start
                        nc.scalar.activation(probs[:, first:first + (qt + 1) * P], sizes[qt][:, 0:(qt + 1) * P], ACT.Exp,
                                             bias=shift[:, qt:qt + 1], scale=scale,
                                             accum_out=total[:, qt:qt + 1]).then_inc(probs_ready, 1)
                    elif kind == "probsT":
                        bank = turn.take(act)
                        turn.emptied(nc.scalar.copy(probsT[:, :], bank[:, 0:BLOCKS * P]))
                    elif kind == "mixedT":
                        bank = turn.take(act)
                        turn.emptied(nc.scalar.copy(mixedT[:, :], bank[:, 0:TOK]))

            walk(act, front, back, go)

        @block.gpsimd
        def _(pool):
            pool.wait_ge(m.norm.power_ready, 1)
            with pool.Fori(0, BATCH) as turn:
                m.norm.gpsimd(pool, turn)

        @block.vector
        def _(dve):
            m.norm.start(dve)
            fronts.start(dve)
            outs.start(dve)
            dve.wait_ge(loaded, 5 * 16)

            def go(steps, bt, bo, ft, fo):
                front, out = Uses(fronts, ft, fo, 3), Uses(outs, bt, bo, 2)
                chain, back_chain = Chain(dve, front_chained, ft, m.LINKS), Chain(dve, back_chained, bt, 2 * QT + 1 + 2)
                for half, kind, *at in steps:
                    m.dve(dve, kind, front, chain, ft, fo)
                    if kind == "qk":
                        bank = front.take(dve)
                        for n in range(2):
                            ins = dve.tensor_scalar(qkT[fo][:, n, :], bank[:, n * TOK:(n + 1) * TOK], qk_bias[:, n:n + 1], None,
                                                    ALU.add)
                        front.emptied(ins)
                    elif kind == "v":
                        bank = front.take(dve)
                        front.emptied(dve.tensor_tensor(v[fo][:, :, :], bank[:, 0:QT * D].rearrange("p (t d) -> p t d", d=D),
                                                        v_bias[:, :].unsqueeze(1).broadcast_to([P, QT, D]), ALU.add))
                        front.settled(dve)
                        dve.sem_inc(qkv_ready, 1)
                    elif kind == "max":
                        qt, = at
                        dve.wait_ge(scores.free, bt * QT + qt + 1 + 2)
                        diagonal = sizes[qt][:, qt * P:(qt + 1) * P]
                        back_chain.link(dve.tensor_tensor(diagonal, diagonal, res["masks"][:, 0, :], ALU.add))
                        back_chain.link(dve.tensor_reduce(top[:, qt:qt + 1], sizes[qt][:, 0:(qt + 1) * P], AX_X, ALU.max))
                        dve.tensor_scalar(shift[:, qt:qt + 1], top[:, qt:qt + 1], -scale, None,
                                          ALU.mult).then_inc(shift_ready, 1)
                    elif kind == "mix":
                        bank = out.take(dve)
                        back_chain.link(dve.reciprocal(inverse[:, :], total[:, :]))
                        out.emptied(dve.tensor_tensor(mixed[:, :, :], bank[:, 0:QT * D].rearrange("p (t d) -> p t d", d=D),
                                                      inverse[:, :].unsqueeze(2).broadcast_to([P, QT, D]), ALU.mult))
                        out.settled(dve)
                        dve.sem_inc(mixed_ready, 1)
                    elif kind == "out":
                        bank = out.take(dve)
                        out.emptied(dve.tensor_tensor(scratch[:, :, :], bank[:, 0:QT * D].rearrange("p (t d) -> p t d", d=D),
                                                      bias[:, :].unsqueeze(1).broadcast_to([P, QT, D]), ALU.add))
                        out.settled(dve)
                        add_gated(dve, res, back_chain, bt, scratch[:, :, :], scratch, gate=0)

            walk(dve, front, back, go)


class Quant:

    BLOCK = 16

    def __init__(self, s, name, cols, work=None):
        nb = cols // self.BLOCK
        self.work = work or {
            "top": s.sb(name + "_top", [P, nb]), "inverse": s.sb(name + "_inverse", [P, nb]), "scale": s.sb(name + "_scale", [P, nb]),
            "unit": s.sb(name + "_unit", [P, cols]), "size": s.sb(name + "_size", [P, cols]), "sign": s.sb(name + "_sign", [P, cols]),
            "level": s.sb(name + "_level", [P, cols]), "past": s.sb(name + "_past", [P, cols])}
        self.top_ready, self.divided, self.parted = (s.sem(f"{name}_{x}") for x in ("top_ready", "divided", "parted"))

    def vector(self, dve, chain, src, dst, cols, n):
        self.vector_scale(dve, chain, src, cols)
        return self.vector_levels(dve, chain, dst, cols, n)

    def vector_scale(self, dve, chain, src, cols):
        w = self.work
        nb = cols // self.BLOCK
        chain.link(dve.tensor_reduce(w["top"][:, 0:nb], src.rearrange("p (b k) -> p b k", k=self.BLOCK), AX_X,
                                     ALU.max, apply_absolute_value=True))
        chain.link(dve.tensor_scalar(w["scale"][:, 0:nb], w["top"][:, 0:nb], 1.0 / 6.0, 1e-12, ALU.mult, ALU.max))
        dve.reciprocal(w["inverse"][:, 0:nb], w["scale"][:, 0:nb]).then_inc(self.top_ready, 1)

    def vector_levels(self, dve, chain, dst, cols, n):
        w = self.work
        nb = cols // self.BLOCK
        dve.wait_ge(self.parted, n)
        size, level, past = w["size"][:, 0:cols], w["level"][:, 0:cols], w["past"][:, 0:cols]

        def passed(mid):
            chain.link(dve.scalar_tensor_tensor(out=level, in0=size, scalar=mid, in1=level, op0=ALU.is_gt, op1=ALU.add))

        dve.tensor_scalar(past, size, 1.75, None, ALU.is_gt)
        chain.link(dve.tensor_scalar(level, size, 5.0, 2.0, ALU.is_gt, ALU.mult))
        passed(3.5)
        passed(2.5)
        chain.link(dve.scalar_tensor_tensor(out=level, in0=level, scalar=2.0, in1=past, op0=ALU.mult, op1=ALU.add))
        passed(1.25)
        passed(0.75)
        passed(0.25)
        chain.link(dve.scalar_tensor_tensor(out=level, in0=level, scalar=0.5, in1=w["sign"][:, 0:cols],
                                            op0=ALU.mult, op1=ALU.mult))
        return dve.tensor_tensor(dst.rearrange("p (b k) -> p b k", k=self.BLOCK),
                                 level.rearrange("p (b k) -> p b k", k=self.BLOCK),
                                 w["scale"][:, 0:nb].unsqueeze(2).broadcast_to([P, nb, self.BLOCK]), ALU.mult)

    LINKS = 10

    def gpsimd(self, pool, src, cols, n):
        w = self.work
        nb = cols // self.BLOCK
        pool.wait_ge(self.top_ready, n)
        pool.tensor_tensor(w["unit"][:, 0:cols].rearrange("p (b k) -> p b k", k=self.BLOCK),
                           src.rearrange("p (b k) -> p b k", k=self.BLOCK),
                           w["inverse"][:, 0:nb].unsqueeze(2).broadcast_to([P, nb, self.BLOCK]),
                           ALU.mult).then_inc(self.divided, 1)

    def scalar(self, act, nc, cols, n):
        w = self.work
        act.wait_ge(self.divided, n)
        nc.scalar.activation(w["size"][:, 0:cols], w["unit"][:, 0:cols], ACT.Abs)
        nc.scalar.activation(w["sign"][:, 0:cols], w["unit"][:, 0:cols], ACT.Sign).then_inc(self.parted, 1)


def layer1_ffn(nc, dram, res):
    I = 352
    parts = [(0, P), (P, P), (2 * P, I - 2 * P)]
    with ExitStack() as ctx:
        s = Scope(nc, ctx, "f1")
        raw = [s.sb("raw_gate", [P, 3, D]), s.sb("raw_up", [P, 3, D]), s.sb("raw_down", [P, I])]
        quantized = s.sb("quantized", [P, 3 * D])
        w_in = s.sb("w_in", [P, 2, I])
        w_down = s.sb("w_down", [P, 3, D])
        h, hq = s.sb("h", [P, TOK]), s.sb("hq", [P, TOK])
        hqT = [s.sb(f"hqT{n}", [P, TOK]) for n in range(2)]
        tanh, gated = s.sb("tanh", [P, QT, I]), s.sb("gated", [P, QT, I])
        hidden, hiddenq = s.sb("hidden", [P, QT, I]), s.sb("hiddenq", [P, QT, I])
        hiddenT = s.sb("hiddenT", [P, QT, 3, P])
        scratch = s.sb("scratch", [P, QT, D])
        quant_h, quant_hidden = Quant(s, "qh", TOK), Quant(s, "qi", QT * I)
        quant_w = Quant(s, "qw", QT * I, quant_hidden.work)
        fronts, front_copies, back_copies, outs = (Ring(s, name, 1) for name in ("fronts", "front_copies", "back_copies", "outs"))
        gates, ups = Ring(s, "gates", 2), Ring(s, "ups", 2)
        m = Modulated(s, nc, res, 2, fronts)
        loaded, started, front_chained, back_chained, tanh_ready, h_ready, hq_ready, hiddenq_ready = (
            s.sem(name) for name in ("loaded", "started", "front_chained", "back_chained", "tanh_ready", "h_ready",
                                     "hq_ready", "hiddenq_ready"))
        b0 = {"vbank": [fronts.banks[0], outs.banks[0]]}
        for name in ("vbank_full", "vbank_read", "chained", "quantized_ready"):
            b0[name] = s.sem("w_" + name)
        front = [("norm",), ("hT",), ("by_token",), ("h_scale",), ("h_levels",), ("hqT",)]
        back = [("in", 0), ("in", 1), ("hidden", 0), ("hidden", 1), ("scale",), ("levels",), ("hiddenT", 0), ("hiddenT", 1),
                ("out",), ("finish",)]
        block = s.block()

        @block.sync
        def _(sp):
            sp.wait_ge(started, 1)
            for dst, src in ((raw[0], dram["L1_ffn_w_gate"]), (raw[1], dram["L1_ffn_w_up"])):
                load(sp, loaded, [(dst[:, 0:2, :], src[0:2 * P, :].rearrange("(t p) d -> p t d", p=P)),
                                  (dst[0:I - 2 * P, 2, :], src[2 * P:I, :])])
            load(sp, loaded, [(raw[2][:, :], dram["L1_ffn_w_down"])])

        weights = [(raw[0][:, :, :].rearrange("p t d -> p (t d)"), 3 * D),
                   (raw[1][:, :, :].rearrange("p t d -> p (t d)"), 3 * D), (raw[2][:, :], I)]

        @block.tensor
        def _(pe):
            turns = Turns(b0, 0, 0)
            for n in range(3):
                pe.wait_ge(b0["quantized_ready"], n + 1)
                bank = turns.fill(pe)
                for t, (r0, rows) in enumerate(parts):
                    if n < 2:
                        mm = pe.transpose(bank[:, r0:r0 + rows], quantized[0:rows, t * D:(t + 1) * D],
                                          res["ident"][0:rows, 0:rows])
                    else:
                        mm = pe.transpose(bank[0:rows, t * P:(t + 1) * P], quantized[:, r0:r0 + rows], res["ident"][:, :])
                turns.full(mm)

            def go(steps, bt, bo, ft, fo):
                front, copies = Uses(fronts, ft, fo, 1), Uses(front_copies, ft, fo, 2)
                gate_in, up_in = Uses(gates, bt, bo, QT), Uses(ups, bt, bo, QT)
                back, out = Uses(back_copies, bt, bo, QT), Uses(outs, bt, bo, 1)
                for half, kind, *at in steps:
                    m.pe(pe, kind, front, ft)
                    if kind == "by_token":
                        pe.wait_ge(m.hT_ready, ft + 1)
                        bank = copies.fill(pe)
                        for t in range(QT):
                            mm = pe.transpose(bank[:, t * P:(t + 1) * P], m.hT[fo][:, t * P:(t + 1) * P], res["ident"][:, :])
                        copies.filled(mm)
                    elif kind == "hqT":
                        pe.wait_ge(hq_ready, ft + 1)
                        bank = copies.fill(pe)
                        for t in range(QT):
                            mm = pe.transpose(bank[:, t * P:(t + 1) * P], hq[:, t * P:(t + 1) * P], res["ident"][:, :])
                        copies.filled(mm)
                    elif kind == "in":
                        t, = at
                        pe.wait_ge(front_copies.free, bt * 2 + 2 + 1)
                        for n, ring in enumerate((gate_in, up_in)):
                            bank = ring.fill(pe)
                            ring.filled(pe.matmul(bank[:, 0:I], hqT[bo][:, t * P:(t + 1) * P], w_in[:, n, :],
                                                  start=True, stop=True))
                    elif kind == "hiddenT":
                        t, = at
                        pe.wait_ge(hiddenq_ready, bt + 1)
                        bank = back.fill(pe)
                        for c, (r0, rows) in enumerate(parts):
                            mm = pe.transpose(bank[0:rows, c * P:(c + 1) * P], hiddenq[:, t, r0:r0 + rows], res["ident"][:, :])
                        back.filled(mm)
                    elif kind == "out":
                        pe.wait_ge(back_copies.free, bt * QT + QT + 1)
                        bank = out.fill(pe)
                        for t in range(QT):
                            for c in range(3):
                                mm = pe.matmul(bank[:, t * P:(t + 1) * P], hiddenT[:, t, c, :], w_down[:, c, :],
                                               start=(t == 0 and c == 0), stop=(c == 2), skip_group_check=True)
                        out.filled(mm)

            walk(pe, front, back, go)

        @block.scalar
        def _(act):
            for n in range(3):
                quant_w.scalar(act, nc, weights[n][1], n + 1)
            for ring in (front_copies, back_copies):
                ring.start(act)

            def go(steps, bt, bo, ft, fo):
                copies, back = Uses(front_copies, ft, fo, 2), Uses(back_copies, bt, bo, QT)
                for half, kind, *at in steps:
                    if kind == "by_token":
                        bank = copies.take(act)
                        copies.emptied(nc.scalar.copy(h[:, :], bank[:, 0:TOK]))
                    elif kind == "h_scale":
                        quant_h.scalar(act, nc, TOK, ft + 1)
                    elif kind == "hqT":
                        bank = copies.take(act)
                        copies.emptied(nc.scalar.copy(hqT[fo][:, :], bank[:, 0:TOK]))
                    elif kind == "hidden":
                        t, = at
                        act.wait_ge(gates.full, bt * QT + t + 1)
                        nc.scalar.activation(tanh[:, t, :], gates.banks[t][:, 0:I], ACT.Tanh, scale=0.5).then_inc(tanh_ready, 1)
                    elif kind == "scale":
                        quant_hidden.scalar(act, nc, QT * I, bt + 1)
                    elif kind == "hiddenT":
                        t, = at
                        bank = back.take(act)
                        nc.scalar.copy(hiddenT[:, t, 0:2, :].rearrange("p c q -> p (c q)"), bank[:, 0:2 * P])
                        back.emptied(nc.scalar.copy(hiddenT[0:I - 2 * P, t, 2, :], bank[0:I - 2 * P, 2 * P:3 * P]))

            walk(act, front, back, go)

        @block.gpsimd
        def _(pool):
            pool.wait_ge(m.norm.power_ready, 1)
            for n in range(3):
                quant_w.gpsimd(pool, weights[n][0], weights[n][1], n + 1)

            def go(steps, bt, bo, ft, fo):
                for half, kind, *at in steps:
                    m.gpsimd(pool, kind, ft)
                    if kind == "h_scale":
                        quant_h.gpsimd(pool, h[:, :], TOK, ft + 1)
                    elif kind == "scale":
                        quant_hidden.gpsimd(pool, hidden[:, :, :].rearrange("p t i -> p (t i)"), QT * I, bt + 1)

            walk(pool, front, back, go)

        @block.vector
        def _(dve):
            dve.memset(raw[0][:, :, :], 0.0)
            dve.memset(hiddenT[:, :, 2, :], 0.0)
            dve.memset(w_down[:, 2, :], 0.0)
            m.norm.start(dve)
            dve.memset(raw[1][:, :, :], 0.0).then_inc(started, 1)
            dve.wait_ge(loaded, 5 * 16)
            turns = Turns(b0, 0, 0)
            chain = Chain(dve, b0["chained"], 0, 0)
            for n in range(3):
                src, cols = weights[n]
                if n:
                    turns.settled(dve)
                quant_w.vector(dve, chain, src, quantized[:, 0:cols], cols, n + 1).then_inc(b0["quantized_ready"], 1)
                bank = turns.take(dve)
                if n < 2:
                    ins = dve.tensor_copy(w_in[:, n, :], bank[:, 0:I])
                else:
                    dve.tensor_copy(w_down[:, 0:2, :].rearrange("p t d -> p (t d)"), bank[:, 0:2 * P])
                    ins = dve.tensor_copy(w_down[0:I - 2 * P, 2, :], bank[0:I - 2 * P, 2 * P:3 * P])
                turns.read(ins)
            turns.settled(dve)
            for ring in (fronts, gates, ups, outs):
                ring.start(dve)

            def go(steps, bt, bo, ft, fo):
                front = Uses(fronts, ft, fo, 1)
                gate_in, up_in, out = Uses(gates, bt, bo, QT), Uses(ups, bt, bo, QT), Uses(outs, bt, bo, 1)
                chain = Chain(dve, front_chained, ft, m.LINKS + Quant.LINKS)
                back_chain = Chain(dve, back_chained, bt, Quant.LINKS + 1)
                for half, kind, *at in steps:
                    m.dve(dve, kind, front, chain, ft, fo)
                    if kind == "h_scale":
                        dve.wait_ge(front_copies.free, ft * 2 + 1 + 1)
                        quant_h.vector_scale(dve, chain, h[:, :], TOK)
                    elif kind == "h_levels":
                        quant_h.vector_levels(dve, chain, hq[:, :], TOK, ft + 1).then_inc(hq_ready, 1)
                    elif kind == "hidden":
                        t, = at
                        bank = gate_in.take(dve)
                        dve.wait_ge(tanh_ready, bt * QT + t + 1)
                        gate_in.emptied(dve.scalar_tensor_tensor(out=gated[:, t, :], in0=tanh[:, t, :], scalar=1.0,
                                                                 in1=bank[:, 0:I], op0=ALU.add, op1=ALU.mult))
                        gate_in.settled(dve)
                        bank = up_in.take(dve)
                        ins = dve.tensor_tensor(hidden[:, t, :], bank[:, 0:I], gated[:, t, :], ALU.mult)
                        up_in.emptied(ins)
                        if t == QT - 1:
                            up_in.settled(dve)
                    elif kind == "scale":
                        quant_hidden.vector_scale(dve, back_chain, hidden[:, :, :].rearrange("p t i -> p (t i)"), QT * I)
                    elif kind == "levels":
                        quant_hidden.vector_levels(dve, back_chain, hiddenq[:, :, :].rearrange("p t i -> p (t i)"), QT * I,
                                                   bt + 1).then_inc(hiddenq_ready, 1)
                    elif kind == "out":
                        bank = out.take(dve)
                        g = res["gate"][:, 1, bass.ds(bt, 1), :].rearrange("p a d -> p (a d)")
                        for t in range(QT):
                            ins = dve.scalar_tensor_tensor(out=scratch[:, t, :], in0=bank[:, t * P:(t + 1) * P], scalar=0.5,
                                                           in1=g, op0=ALU.mult, op1=ALU.mult)
                        out.emptied(ins)
                        out.settled(dve)
                    elif kind == "finish":
                        x = res["x"][:, bass.ds(bt * QT, QT), :]
                        back_chain.link(dve.tensor_tensor(x, x, scratch[:, :, :], ALU.add))

            walk(dve, front, back, go)


def layer3_ffn(nc, dram, res):
    E, ES, K = 16, 32, 4
    NX = E + 8 - K
    with ExitStack() as ctx:
        s = Scope(nc, ctx, "f3")
        sel, keys, values = s.sb("sel", [P, E]), s.sb("keys", [P, E * ES]), s.sb("values", [P, 4, D])
        route_scale = s.sb("route_scale", [P, 1])
        negexp, plus = s.sb("negexp", [P, QT, E]), s.sb("plus", [P, QT, E])
        probs = s.sb("probs", [P, QT, NX])
        best, left = s.sb("best", [P, QT, 8]), s.sb("left", [P, QT, NX])
        kept, chosen = s.sb("kept", [P, QT, E]), s.sb("chosen", [P, QT, E])
        total, inverse = s.sb("total", [P, QT]), s.sb("inverse", [P, QT])
        weight = [s.sb(f"weight{n}", [P, QT, E]) for n in range(2)]
        scores, scoresT = s.sb("scores", [P, QT, E * ES]), s.sb("scoresT", [P, QT, 512])
        scratch = s.sb("scratch", [P, QT, D])
        fronts, logits, experts, turned, outs = (Ring(s, name, n) for name, n in (
            ("fronts", 1), ("logits", 1), ("experts", 2), ("turned", 2), ("outs", 1)))
        m = Modulated(s, nc, res, 2, fronts)
        loaded, front_chained, back_chained = s.sem("loaded"), s.sem("front_chained"), s.sem("back_chained")
        FILL = 3.0e38
        front = [("norm",), ("hT",), ("logits",), ("places",), ("weight",)]
        back = [("experts", 0), ("experts", 1), ("turn", 0), ("turn", 1), ("out",)]
        block = s.block()

        @block.sync
        def _(sp):
            load(sp, loaded, [(sel[:, :], dram["L3_sel"]), (keys[:, :], dram["L3_keys"]),
                              (values[:, :, :], dram["L3_values"].rearrange("(t p) d -> p t d", p=P)),
                              (route_scale[:, :], row_of(dram["L3_ffn_route_scale"]))])

        @block.tensor
        def _(pe):
            pe.wait_ge(loaded, 64)

            def go(steps, bt, bo, ft, fo):
                front, logit = Uses(fronts, ft, fo, 1), Uses(logits, ft, fo, 1)
                expert, turn, out = Uses(experts, bt, bo, QT), Uses(turned, bt, bo, QT), Uses(outs, bt, bo, 1)
                for half, kind, *at in steps:
                    m.pe(pe, kind, front, ft)
                    if kind == "logits":
                        pe.wait_ge(m.hT_ready, ft + 1)
                        bank = logit.fill(pe)
                        for t in range(QT):
                            mm = pe.matmul(bank[:, t * E:(t + 1) * E], m.hT[fo][:, t * P:(t + 1) * P], sel[:, :],
                                           start=(t == 0), stop=True, skip_group_check=True)
                        logit.filled(mm)
                    elif kind == "experts":
                        t, = at
                        bank = expert.fill(pe)
                        expert.filled(pe.matmul(bank[:, :], m.hT[bo][:, t * P:(t + 1) * P], keys[:, :], start=True, stop=True))
                    elif kind == "turn":
                        t, = at
                        pe.wait_ge(experts.free, bt * QT + t + 1 + 2)
                        bank = turn.fill(pe)
                        for c in range(4):
                            mm = pe.transpose(bank[:, c * P:(c + 1) * P], scores[:, t, c * P:(c + 1) * P], res["ident"][:, :])
                        turn.filled(mm)
                    elif kind == "out":
                        bank = out.fill(pe)
                        for t in range(QT):
                            pe.wait_ge(turned.free, bt * QT + t + 1 + 2)
                            for c in range(4):
                                mm = pe.matmul(bank[:, t * D:(t + 1) * D], scoresT[:, t, c * P:(c + 1) * P], values[:, c, :],
                                               start=(t == 0 and c == 0), stop=(c == 3), skip_group_check=True)
                        out.filled(mm)

            walk(pe, front, back, go)

        @block.scalar
        def _(act):
            logits.start(act)
            turned.start(act)

            def go(steps, bt, bo, ft, fo):
                logit, turn = Uses(logits, ft, fo, 1), Uses(turned, bt, bo, QT)
                for half, kind, *at in steps:
                    if kind == "logits":
                        bank = logit.take(act)
                        logit.emptied(nc.scalar.activation(negexp[:, :, :].rearrange("p t e -> p (t e)"), bank[:, 0:QT * E],
                                                           ACT.Exp, scale=-1.0))
                    elif kind == "turn":
                        t, = at
                        bank = turn.take(act)
                        turn.emptied(nc.scalar.copy(scoresT[:, t, :], bank[:, :]))

            walk(act, front, back, go)

        @block.gpsimd
        def _(pool):
            pool.wait_ge(m.norm.power_ready, 1)
            with pool.Fori(0, BATCH) as turn:
                m.norm.gpsimd(pool, turn)

        @block.vector
        def _(dve):
            m.norm.start(dve)
            for ring in (fronts, experts, outs):
                ring.start(dve)
            dve.memset(probs[:, :, :], FILL)
            dve.wait_ge(loaded, 64)
            dve.wait_ge(m.norm.power_ready, 1)

            def go(steps, bt, bo, ft, fo):
                front, expert, out = Uses(fronts, ft, fo, 1), Uses(experts, bt, bo, QT), Uses(outs, bt, bo, 1)
                chain, back_chain = Chain(dve, front_chained, ft, m.LINKS + 12), Chain(dve, back_chained, bt, 1)
                for half, kind, *at in steps:
                    m.dve(dve, kind, front, chain, ft, fo)
                    if kind == "places":
                        dve.wait_ge(logits.free, ft + 1 + 1)
                        chain.link(dve.tensor_scalar(plus[:, :, :], negexp[:, :, :], 1.0, None, ALU.add))
                        chain.link(dve.reciprocal(probs[:, :, 0:E], plus[:, :, :]))
                        top_places(dve, chain, m.norm, probs, best, left, E, K, FILL)
                    elif kind == "weight":
                        chain.link(dve.tensor_tensor(chosen[:, :, :], probs[:, :, 0:E], left[:, :, 0:E], ALU.not_equal))
                        chain.link(dve.tensor_tensor(kept[:, :, :], probs[:, :, 0:E], chosen[:, :, :], ALU.mult))
                        chain.link(dve.tensor_reduce(total[:, :], kept[:, :, :], AX_X, ALU.add))
                        chain.link(dve.tensor_scalar(total[:, :], total[:, :], 1e-9, None, ALU.max))
                        chain.link(dve.reciprocal(inverse[:, :], total[:, :]))
                        chain.link(dve.tensor_scalar(inverse[:, :], inverse[:, :], route_scale[:, 0:1], None, ALU.mult))
                        chain.link(dve.tensor_tensor(weight[fo][:, :, :], kept[:, :, :],
                                                     inverse[:, :].unsqueeze(2).broadcast_to([P, QT, E]), ALU.mult))
                    elif kind == "experts":
                        t, = at
                        bank = expert.take(dve)
                        expert.emptied(dve.scalar_tensor_tensor(
                            out=scores[:, t, :].rearrange("p (e k) -> p e k", k=ES),
                            in0=bank[:, :].rearrange("p (e k) -> p e k", k=ES), scalar=0.0,
                            in1=weight[bo][:, t, :].unsqueeze(2).broadcast_to([P, E, ES]), op0=ALU.max, op1=ALU.mult))
                    elif kind == "out":
                        bank = out.take(dve)
                        g = res["gate"][:, 1, bass.ds(bt, 1), :].broadcast_to([P, QT, D])
                        out.emptied(dve.tensor_tensor(scratch[:, :, :], bank[:, 0:QT * D].rearrange("p (t d) -> p t d", d=D),
                                                      g, ALU.mult))
                        out.settled(dve)
                        x = res["x"][:, bass.ds(bt * QT, QT), :]
                        back_chain.link(dve.tensor_tensor(x, x, scratch[:, :, :], ALU.add))

            walk(dve, front, back, go)


def top_places(dve, chain, norm, values, best, left, width, k, fill):
    carry(dve, norm)
    for t in range(QT):
        last = dve.max(best[:, t, :], values[:, t, 0:width])
    chain.link(last)
    chain.link(dve.memset(best[:, :, k:8], fill))
    carry(dve, norm)
    for t in range(QT):
        last = dve.match_replace(left[:, t, :], in_to_replace=best[:, t, :], in_values=values[:, t, :], imm_value=-1.0e38)
    chain.link(last)


def carry(dve, norm):
    dve.tensor_copy(norm.idle[:, 1:2], norm.idle[:, 0:1])


def walk(eng, front, back, do):
    both = merged(front, back)
    fronts, backs = [x for x in both if x[0] == "front"], [x for x in both if x[0] == "back"]
    pipelined(eng, lambda bt, bo, ft, fo: do(fronts if bt is None else backs if ft is None else both, bt, bo, ft, fo))


class Modulated:

    def __init__(self, s, nc, res, which, ring):
        self.nc, self.res, self.which, self.ring = nc, res, which, ring
        self.norm = Norm(s)
        self.xhat = s.sb("xhat", [P, QT, D])
        self.hT = [s.sb(f"hT{n}", [P, TOK]) for n in range(2)]
        self.xhat_ready, self.hT_ready = s.sem("xhat_ready"), s.sem("hT_ready")

    LINKS = 2

    def pe(self, pe, kind, front, turn):
        if kind == "hT":
            pe.wait_ge(self.xhat_ready, turn + 1)
            bank = front.fill(pe)
            for t in range(QT):
                mm = pe.transpose(bank[:, t * P:(t + 1) * P], self.xhat[:, t, :], self.res["ident"][:, :])
            front.filled(mm)

    def dve(self, dve, kind, front, chain, turn, odd):
        if kind == "norm":
            self.norm.vector(dve, chain, turn, lambda t: x_tile(self.res, turn * QT + t), self.xhat, self.xhat_ready)
        elif kind == "hT":
            bank = front.take(dve)
            front.emptied(dve.tensor_scalar(self.hT[odd][:, :], bank[:, 0:TOK],
                                            self.res["mod"][:, self.which + 1, bass.ds(turn, 1)],
                                            self.res["mod"][:, self.which, bass.ds(turn, 1)], ALU.mult, ALU.add))
            front.settled(dve)
            dve.sem_inc(self.hT_ready, 1)

    def gpsimd(self, pool, kind, turn):
        if kind == "norm":
            self.norm.gpsimd(pool, turn)


def add_gated(dve, res, chain, turn, y, scratch, gate=1):
    x = res["x"][:, bass.ds(turn * QT, QT), :]
    chain.link(dve.tensor_tensor(scratch[:, :, :], y, res["gate"][:, gate, bass.ds(turn, 1), :].broadcast_to([P, QT, D]),
                                 ALU.mult))
    chain.link(dve.tensor_tensor(x, x, scratch[:, :, :], ALU.add))


def layer0_ffn(nc, dram, res):
    E, I, K = 8, 256, 2
    C = I // P
    LIMIT, ALPHA = 7.0, 1.702
    NX = E + 8 - K
    FILL = 3.0e38
    with ExitStack() as ctx:
        s = Scope(nc, ctx, "f0")
        router, router_bias = s.sb("router", [P, E]), s.sb("router_bias", [P, E])
        w_in, b_in = s.sb("w_in", [P, E, 2 * I]), s.sb("b_in", [P, E, 2 * C])
        b_up = s.sb("b_up", [P, E, C])
        w_down, b_down = s.sb("w_down", [P, E * C, D]), s.sb("b_down", [E, D])
        logits, best, left = s.sb("logits", [P, QT, NX]), s.sb("best", [P, QT, 8]), s.sb("left", [P, QT, NX])
        lowered, exps = s.sb("lowered", [P, QT, E]), s.sb("exps", [P, QT, E])
        total, inverse = s.sb("total", [P, QT]), s.sb("inverse", [P, QT])
        chosen, weight = s.sb("chosen", [P, QT, E]), s.sb("weight", [P, QT, E])
        half_weight = [s.sb(f"half_weight{n}", [P, QT, E]) for n in range(2)]
        weightT = s.sb("weightT", [E, TOK])
        mixed = [s.sb(f"mixed{n}", [P, QT, D]) for n in range(2)]
        gate, up_raw, tanh, glu, up, hidden = ([s.sb(f"{name}{n}", [P, C, TOK]) for n in range(4)]
                                               for name in ("gate", "up_raw", "tanh", "glu", "up", "hidden"))
        scratch = s.sb("scratch", [P, QT, D])
        fronts, gates, ups, downs = Ring(s, "fronts", 1), Ring(s, "gates", 2), Ring(s, "ups", 2), Ring(s, "downs", 2)
        h = Modulated(s, nc, res, 2, fronts)
        (loaded, started, front_chained, back_chained, lowered_ready, exps_ready, weight_ready, weightT_ready, gate_ready,
         tanh_ready, glu_ready, hidden_ready) = (s.sem(name) for name in (
             "loaded", "started", "front_chained", "back_chained", "lowered_ready", "exps_ready", "weight_ready",
             "weightT_ready", "gate_ready", "tanh_ready", "glu_ready", "hidden_ready"))
        n_loaded = 6 * 16
        front = [("norm",), ("hT",), ("logits",), ("places",), ("weight",), ("weightT",), ("biases",)]
        back = []
        for n in range(-1, E + 3):
            back += [(kind, n - lag) for kind, lag in (("into", -1), ("bias", 0), ("down", 2), ("combine", 3), ("glu", 1))
                     if 0 <= n - lag < E]
        back.append(("finish",))
        block = s.block()

        @block.sync
        def _(sp):
            load(sp, loaded, [(router[:, :], dram["L0_router"]), (router_bias[:, :], row_of(dram["L0_router_bias"])),
                              (w_in[:, :, :], dram["L0_gate_up"].rearrange("e h n -> h e n")),
                              (b_in[:, :, :], dram["L0_gate_up_bias"]),
                              (w_down[:, :, :], dram["L0_down"].rearrange("(t p) d -> p t d", p=P)),
                              (b_down[:, :], dram["L0_down_bias"])])

        @block.tensor
        def _(pe):
            pe.wait_ge(loaded, n_loaded)

            def go(steps, bt, bo, ft, fo):
                front, gate_in, up_in = Uses(fronts, ft, fo, 4), Uses(gates, bt, bo, E), Uses(ups, bt, bo, E)
                out = Uses(downs, bt, bo, E)
                for half, kind, *at in steps:
                    h.pe(pe, kind, front, ft)
                    if kind == "logits":
                        pe.wait_ge(h.hT_ready, ft + 1)
                        bank = front.fill(pe)
                        for t in range(QT):
                            mm = pe.matmul(bank[:, t * E:(t + 1) * E], h.hT[fo][:, t * P:(t + 1) * P], router[:, :],
                                           start=(t == 0), stop=True, skip_group_check=True)
                        front.filled(mm)
                    elif kind == "weightT":
                        pe.wait_ge(weight_ready, ft + 1)
                        bank = front.fill(pe)
                        for t in range(QT):
                            mm = pe.transpose(bank[0:E, t * P:(t + 1) * P], weight[:, t, :], res["ident"][:, :])
                        front.filled(mm)
                    elif kind == "biases":
                        pe.wait_ge(weightT_ready, ft + 1)
                        bank = front.fill(pe)
                        for t in range(QT):
                            mm = pe.matmul(bank[:, t * P:(t + 1) * P], weightT[:, t * P:(t + 1) * P], b_down[:, :],
                                           start=(t == 0), stop=True, skip_group_check=True)
                        front.filled(mm)
                    elif kind == "into":
                        e, = at
                        for ring, first in ((gate_in, 0), (up_in, C)):
                            bank = ring.fill(pe)
                            for c in range(C):
                                mm = pe.matmul(bank[:, c * TOK:(c + 1) * TOK],
                                               w_in[:, e, (first + c) * P:(first + c + 1) * P], h.hT[bo][:, :],
                                               start=(c == 0), stop=True, skip_group_check=True)
                            ring.filled(mm)
                    elif kind == "down":
                        e, = at
                        pe.wait_ge(hidden_ready, bt * E + e + 1)
                        bank = out.fill(pe)
                        for t in range(QT):
                            for c in range(C):
                                mm = pe.matmul(bank[:, t * P:(t + 1) * P], hidden[e % 4][:, c, t * P:(t + 1) * P],
                                               w_down[:, e * C + c, :], start=(t == 0 and c == 0), stop=(c == C - 1),
                                               skip_group_check=True)
                        out.filled(mm)

            walk(pe, front, back, go)

        @block.scalar
        def _(act):
            ups.start(act)
            act.wait_ge(started, 1)

            def go(steps, bt, bo, ft, fo):
                up_in = Uses(ups, bt, bo, E)
                for half, kind, *at in steps:
                    if kind == "places":
                        act.wait_ge(lowered_ready, ft + 1)
                        nc.scalar.activation(exps[:, :, :], lowered[:, :, :], ACT.Exp).then_inc(exps_ready, 1)
                    elif kind == "bias":
                        e, = at
                        bank = up_in.take(act)
                        for c in range(C):
                            ins = nc.scalar.activation(up_raw[e % 4][:, c, :], bank[:, c * TOK:(c + 1) * TOK], ACT.Identity,
                                                       bias=b_up[:, e, c:c + 1])
                        up_in.emptied(ins)
                        act.wait_ge(gate_ready, bt * E + e + 1)
                        nc.scalar.activation(tanh[e % 4][:, :, :], gate[e % 4][:, :, :], ACT.Tanh,
                                             scale=ALPHA / 2).then_inc(tanh_ready, 1)

            walk(act, front, back, go)

        @block.gpsimd
        def _(pool):
            pool.wait_ge(h.norm.power_ready, 1)

            def go(steps, bt, bo, ft, fo):
                for half, kind, *at in steps:
                    h.gpsimd(pool, kind, ft)
                    if kind == "glu":
                        e, = at
                        pool.wait_ge(glu_ready, bt * E + e + 1)
                        pool.tensor_tensor(hidden[e % 4][:, :, :], up[e % 4][:, :, :], glu[e % 4][:, :, :],
                                           ALU.mult).then_inc(hidden_ready, 1)

            walk(pool, front, back, go)

        @block.vector
        def _(dve):
            h.norm.start(dve)
            for ring in (fronts, gates, downs):
                ring.start(dve)
            dve.memset(logits[:, :, :], FILL)
            dve.wait_ge(loaded, n_loaded)
            dve.tensor_scalar(b_up[:, :, :], b_in[:, :, C:2 * C], 1.0, None, ALU.add).then_inc(started, 1)
            dve.wait_ge(started, 1)

            def go(steps, bt, bo, ft, fo):
                front, gate_in, out = Uses(fronts, ft, fo, 4), Uses(gates, bt, bo, E), Uses(downs, bt, bo, E)
                chain, back_chain = Chain(dve, front_chained, ft, h.LINKS + 9), Chain(dve, back_chained, bt, 2)
                for half, kind, *at in steps:
                    h.dve(dve, kind, front, chain, ft, fo)
                    if kind == "logits":
                        bank = front.take(dve)
                        front.emptied(dve.tensor_tensor(logits[:, :, 0:E], bank[:, 0:QT * E].rearrange("p (t e) -> p t e", e=E),
                                                        router_bias[:, :].unsqueeze(1).broadcast_to([P, QT, E]), ALU.add))
                        front.settled(dve)
                    elif kind == "places":
                        top_places(dve, chain, h.norm, logits, best, left, E, K, FILL)
                        dve.tensor_tensor(lowered[:, :, :], logits[:, :, 0:E], best[:, :, 0:1].broadcast_to([P, QT, E]),
                                          ALU.subtract).then_inc(lowered_ready, 1)
                        chain.link(dve.tensor_tensor(chosen[:, :, :], logits[:, :, 0:E], left[:, :, 0:E], ALU.not_equal))
                    elif kind == "weight":
                        dve.wait_ge(exps_ready, ft + 1)
                        chain.link(dve.tensor_reduce(total[:, :], exps[:, :, :], AX_X, ALU.add))
                        chain.link(dve.reciprocal(inverse[:, :], total[:, :]))
                        chain.link(dve.tensor_tensor(weight[:, :, :], exps[:, :, :], chosen[:, :, :], ALU.mult))
                        chain.link(dve.tensor_tensor(weight[:, :, :], weight[:, :, :],
                                                     inverse[:, :].unsqueeze(2).broadcast_to([P, QT, E]), ALU.mult))
                        dve.sem_inc(weight_ready, 1)
                        chain.link(dve.tensor_scalar(half_weight[fo][:, :, :], weight[:, :, :], 0.5, None, ALU.mult))
                    elif kind == "weightT":
                        bank = front.take(dve)
                        front.emptied(dve.tensor_copy(weightT[:, :], bank[0:E, 0:TOK]))
                        front.settled(dve)
                        dve.sem_inc(weightT_ready, 1)
                    elif kind == "biases":
                        bank = front.take(dve)
                        front.emptied(dve.tensor_copy(mixed[fo][:, :, :].rearrange("p t d -> p (t d)"), bank[:, 0:QT * P]))
                        front.settled(dve)
                    elif kind == "bias":
                        e, = at
                        bank = gate_in.take(dve)
                        for c in range(C):
                            ins = dve.tensor_scalar(gate[e % 4][:, c, :], bank[:, c * TOK:(c + 1) * TOK],
                                                    b_in[:, e, c:c + 1], LIMIT, ALU.add, ALU.min)
                        gate_in.emptied(ins)
                        gate_in.settled(dve)
                        dve.sem_inc(gate_ready, 1)
                        dve.wait_ge(ups.free, bt * E + e + 3)
                        dve.tensor_scalar(up[e % 4][:, :, :], up_raw[e % 4][:, :, :], 1.0 - LIMIT, 1.0 + LIMIT,
                                          ALU.max, ALU.min)
                    elif kind == "combine":
                        e, = at
                        if e:
                            out.settled(dve)
                        bank = out.take(dve)
                        for t in range(QT):
                            ins = dve.scalar_tensor_tensor(out=mixed[bo][:, t, :], in0=bank[:, t * P:(t + 1) * P],
                                                           scalar=half_weight[bo][:, t, e:e + 1], in1=mixed[bo][:, t, :],
                                                           op0=ALU.mult, op1=ALU.add)
                        out.emptied(ins)
                    elif kind == "glu":
                        e, = at
                        dve.wait_ge(tanh_ready, bt * E + e + 1)
                        dve.scalar_tensor_tensor(out=glu[e % 4][:, :, :], in0=tanh[e % 4][:, :, :], scalar=1.0,
                                                 in1=gate[e % 4][:, :, :], op0=ALU.add, op1=ALU.mult).then_inc(glu_ready, 1)
                    elif kind == "finish":
                        out.settled(dve)
                        add_gated(dve, res, back_chain, bt, mixed[bo][:, :, :], scratch)

            walk(dve, front, back, go)


def layer2_ffn(nc, dram, res):
    with ExitStack() as ctx:
        s = Scope(nc, ctx, "f2")
        y = s.sb("y", [P, BATCH * QT, D])
        layer2_input(nc, dram, res, y)
        for depth in range(2):
            window_attention(nc, dram, res, y, depth)
            gelu_mlp(nc, dram, res, y, depth)
        layer2_output(nc, res, y)


def y_tile(y, n):
    return y[:, bass.ds(n, 1), :].rearrange("p a d -> p (a d)")


def layer2_input(nc, dram, res, y):
    banks, links = 2, 2
    with ExitStack() as ctx:
        s = Scope(nc, ctx, "i2")
        norm = Norm(s)
        xhat, hT = s.sb("xhat", [P, QT, D]), s.sb("hT", [P, TOK])
        b = {"vbank": [s.bank("vbank0"), s.bank("vbank1")]}
        for name in ("vbank_full", "vbank_read", "xhat_ready", "chained", "hT_ready"):
            b[name] = s.sem(name)
        block = s.block()

        @block.tensor
        def _(pe):
            with pe.Fori(0, BATCH) as turn:
                turns = Turns(b, turn, banks)
                pe_norm_transpose(pe, b, turns, res, xhat, turn)
                pe.wait_ge(b["hT_ready"], turn + 1)
                bank = turns.fill(pe)
                for t in range(QT):
                    mm = pe.transpose(bank[:, t * P:(t + 1) * P], hT[:, t * P:(t + 1) * P], res["ident"][:, :])
                turns.full(mm)
                turns.end()

        @block.gpsimd
        def _(pool):
            pool.wait_ge(norm.power_ready, 1)
            with pool.Fori(0, BATCH) as turn:
                norm.gpsimd(pool, turn)

        @block.vector
        def _(dve):
            norm.start(dve)
            dve.wait_ge(norm.power_ready, 1)
            with dve.Fori(0, BATCH) as turn:
                turns = Turns(b, turn, banks)
                chain = Chain(dve, b["chained"], turn, links)
                norm.vector(dve, chain, turn, lambda t: x_tile(res, turn * QT + t), xhat, b["xhat_ready"])
                dve_modulate(dve, b, turns, res, hT, 2, turn)
                turns.settled(dve)
                dve.sem_inc(b["hT_ready"], 1)
                bank = turns.take(dve)
                turns.read(dve.tensor_copy(y[:, bass.ds(turn * QT, QT), :].rearrange("p t d -> p (t d)"), bank[:, 0:TOK]))
                turns.settled(dve)
                turns.end()
                chain.end()


def layer2_output(nc, res, y):
    with ExitStack() as ctx:
        s = Scope(nc, ctx, "o2")
        scratch = s.sb("scratch", [P, QT, D])
        chained = s.sem("chained")
        block = s.block()

        @block.vector
        def _(dve):
            with dve.Fori(0, BATCH) as turn:
                chain = Chain(dve, chained, turn, 2)
                x = res["x"][:, bass.ds(turn * QT, QT), :]
                chain.link(dve.tensor_tensor(scratch[:, :, :], y[:, bass.ds(turn * QT, QT), :],
                                             res["gate"][:, 1, bass.ds(turn, 1), :].broadcast_to([P, QT, D]), ALU.mult))
                chain.link(dve.tensor_tensor(x, x, scratch[:, :, :], ALU.add))
                chain.end()


def dve_shift(dve, bank, shifted):
    H = D // 2
    dve.tensor_copy(shifted[0:H, :], bank[0:H, 0:TOK])
    return dve.tensor_copy(shifted[H:D, 1:TOK], bank[H:D, 0:TOK - 1])


def window_attention(nc, dram, res, y, depth):
    a = Attn(f"w{depth}", 1, 8, 64, "window", False, 8.0)
    INNER, H = a.width, a.hd // 2
    with ExitStack() as ctx:
        s = Scope(nc, ctx, a.name)
        w = s.sb("w", [P, 3 * INNER])
        scales = s.sb("scales", [P, 2, 64])
        tables = s.sb("tables", [P, 2, 2, QT, 64])
        turned = s.sb("turned", [P, 2, 2, QT, 64])
        power = s.sb("power", [P, 2 * a.heads])

        def each(name, shape):
            return [s.sb(f"{name}{t}", [P, 2] + shape) for t in range(QT)]

        raw, square, unit = each("raw", [8, 64]), each("square", [8, 64]), each("unit", [8, 64])
        by_cos, by_sin, rotated = square, each("by_sin", [8, 64]), each("rotated", [8, 64])
        total, inverse = each("total", [8]), each("inverse", [8])
        at = Attention(s, nc, a, res, 6 + 3 * QT, QT * a.out_banks, 1 + QT + a.n_max, 3 * QT + QT)
        squares_ready, total_ready, inverse_ready = s.sem("squares_ready"), s.sem("total_ready"), s.sem("inverse_ready")
        unit_ready = s.sem("unit_ready")
        by_sin_ready, rotated_ready = s.sem("by_sin_ready"), s.sem("rotated_ready")
        project = ([("qkv", t, c) for t in range(QT) for c in range(3)] + [("total", 0), ("total", 1)]
                   + [("unit", 0), ("unit", 1), ("rotate", 0), ("rotate", 1), ("pack", 0), ("pack", 1)])
        steps = step_lists(a, project)
        n_loaded = 5 * 16
        block = s.block()

        @block.sync
        def _(sp):
            load(sp, at.loaded, [(w[:, :], dram["L2_wqkv"][depth]),
                                 (at.w_out[:, :, :], dram["L2_ffn_wo"][depth].rearrange("(t p) d -> p t d", p=P)),
                                 (scales[:, 0, :], row_of(dram["L2_q_scale"][depth])),
                                 (scales[:, 1, :], row_of(dram["L2_k_scale"][depth])),
                                 (tables[:, :, :, :, :], dram["c_rotary"])])

        @block.tensor
        def _(pe):
            pe.wait_ge(at.loaded, n_loaded)
            pe.wait_ge(at.started, 1)

            def project(pe, kind, where, front, to_act, turn, odd):
                if kind == "qkv":
                    t, c = where
                    if t == 0 and c == 0:
                        pe.wait_ge(at.hT_ready, turn + 1)
                    bank = to_act.fill(pe)
                    to_act.filled(pe.matmul(bank[:, :], at.hT[:, t * P:(t + 1) * P], w[:, c * INNER:(c + 1) * INNER],
                                            start=True, stop=True))
                elif kind == "pack":
                    t, = where
                    pe.wait_ge(rotated_ready, turn * QT + t + 1)
                    for c, ring in enumerate((to_act, front)):
                        bank = ring.fill(pe)
                        for g in range(a.pairs):
                            mm = pe.transpose(bank[:, g * P:(g + 1) * P],
                                              rotated[t][:, c, 2 * g:2 * g + 2, :].rearrange("p h d -> p (h d)"),
                                              res["ident"][:, :])
                        ring.filled(mm)

            pipelined(pe, lambda bt, bo, ft, fo: at.pe_batch(pe, steps(bt, ft), project, bt, bo, ft, fo))

        @block.scalar
        def _(act):
            at.begin_scalar(act)
            act.wait_ge(at.started, 1)

            def project(act, kind, where, to_act, turn, odd):
                if kind == "qkv":
                    t, c = where
                    bank = to_act.take(act)
                    if c == 2:
                        to_act.emptied(nc.scalar.copy(at.v[odd][:, t, :, 0:a.hd],
                                                      bank[:, :].rearrange("p (h d) -> p h d", d=a.hd)))
                        return
                    if c == 0:
                        act.wait_ge(unit_ready, turn * QT + t + 1)
                    nc.scalar.copy(raw[t][:, c, :, :].rearrange("p h d -> p (h d)"), bank[:, :])
                    to_act.emptied(nc.scalar.activation(square[t][:, c, :, :].rearrange("p h d -> p (h d)"), bank[:, :],
                                                        ACT.Square))
                    if c == 1:
                        to_act.settled(act)
                        act.sem_inc(squares_ready, 1)
                elif kind == "pack":
                    t, = where
                    bank = to_act.take(act)
                    to_act.emptied(nc.scalar.copy(at.qT[odd][:, :, t * P:(t + 1) * P],
                                                  bank[:, :].rearrange("p (g q) -> p g q", q=P)))
                    if t == QT - 1:
                        to_act.settled(act)
                        act.sem_inc(at.qT_ready, 1)

            pipelined(act, lambda bt, bo, ft, fo: at.act_batch(act, steps(bt, ft), project, bt, bo, ft, fo))

        @block.gpsimd
        def _(pool):
            pool.wait_ge(at.started, 1)
            with pool.Fori(0, BATCH) as turn:
                for t in range(QT):
                    pool.wait_ge(total_ready, turn * QT + t + 1)
                    pool.tensor_tensor(inverse[t][:, :, :].rearrange("p c h -> p (c h)"),
                                       total[t][:, :, :].rearrange("p c h -> p (c h)"), power[:, :],
                                       ALU.pow).then_inc(inverse_ready, 1)
                for t in range(QT):
                    pool.wait_ge(unit_ready, turn * QT + t + 1 + QT)
                    for half in range(2):
                        here, there = slice(H * half, H * half + H), slice(H - H * half, 2 * H - H * half)
                        last = pool.tensor_tensor(by_sin[t][:, :, :, here], unit[t][:, :, :, there],
                                                  turned[:, :, 1, t, here].unsqueeze(2).broadcast_to([P, 2, 8, H]), ALU.mult)
                    last.then_inc(by_sin_ready, 1)

        @block.vector
        def _(dve):
            dve.memset(power[:, :], -0.5)
            dve.memset(at.hT[:, :], 0.0)
            dve.sem_inc(unit_ready, QT)
            dve.wait_ge(at.loaded, n_loaded)
            for c in range(2):
                for t in range(QT):
                    dve.tensor_tensor(turned[:, c, 0, t, :], tables[:, c, 0, t, :], scales[:, c, :], ALU.mult)
                    dve.tensor_tensor(turned[:, c, 1, t, 0:H], tables[:, c, 1, t, 0:H], scales[:, c, H:2 * H], ALU.mult)
                    dve.tensor_tensor(turned[:, c, 1, t, H:2 * H], tables[:, c, 1, t, H:2 * H],
                                      scales[:, c, 0:H], ALU.mult)
            at.begin_vector(dve)
            dve.wait_ge(at.started, 1)

            def project(dve, kind, where, front, chain, turn, odd):
                if kind == "total":
                    t, = where
                    dve.wait_ge(squares_ready, turn * QT + t + 1)
                    dve.tensor_reduce(total[t][:, :, :], square[t][:, :, :, :], AX_X, ALU.add).then_inc(total_ready, 1)
                elif kind == "unit":
                    t, = where
                    dve.wait_ge(inverse_ready, turn * QT + t + 1)
                    chain.link(dve.tensor_scalar(inverse[t][:, :, :], inverse[t][:, :, :], 1e12, None, ALU.min))
                    chain.link(dve.tensor_tensor(unit[t][:, :, :, :], raw[t][:, :, :, :],
                                                 inverse[t][:, :, :].unsqueeze(3).broadcast_to([P, 2, 8, 64]), ALU.mult))
                    chain.link(dve.tensor_tensor(by_cos[t][:, :, :, :], unit[t][:, :, :, :],
                                                 turned[:, :, 0, t, :].unsqueeze(2).broadcast_to([P, 2, 8, 64]), ALU.mult))
                    dve.sem_inc(unit_ready, 1)
                elif kind == "rotate":
                    t, = where
                    dve.wait_ge(by_sin_ready, turn * QT + t + 1)
                    dve.tensor_tensor(rotated[t][:, :, :, :], by_cos[t][:, :, :, :], by_sin[t][:, :, :, :],
                                      ALU.add).then_inc(rotated_ready, 1)
                elif kind == "pack":
                    t, = where
                    bank = front.take(dve)
                    for half in range(2):
                        r = slice(64 * half, 64 * half + 64)
                        ins = dve.tensor_copy(
                            at.k_alone[odd][r, :, t * P:(t + 1) * P].rearrange("p (g two) q -> p g two q", two=2)[:, :, half, :],
                            bank[r, :].rearrange("p (g q) -> p g q", g=4))
                    front.emptied(ins)
                    if t == QT - 1:
                        front.settled(dve)
                        dve.sem_inc(at.qkv_ready, 1)

            def copy_y(dve, chain, turn):
                dve.tensor_copy(at.xhat[:, :, :], y[:, bass.ds(turn * QT, QT), :]).then_inc(at.xhat_ready, 1)

            def shift(dve, front, turn):
                bank = front.take(dve)
                front.emptied(dve_shift(dve, bank, at.hT))
                front.settled(dve)
                dve.sem_inc(at.hT_ready, 1)

            def add_to_y(dve, chain, tail, turn, qt, bank):
                yt = y_tile(y, turn * QT + qt)
                tail.emptied(dve.tensor_tensor(yt, bank[:, 0:D], yt, ALU.add))
                tail.settled(dve)

            pipelined(dve, lambda bt, bo, ft, fo: at.dve_batch(dve, steps(bt, ft), project, copy_y, shift,
                                                               add_to_y, bt, bo, ft, fo))


def gelu_mlp(nc, dram, res, y, depth):
    HID, H = 341, D // 2
    parts = [(0, P), (P, P), (2 * P, HID - 2 * P)]
    with ExitStack() as ctx:
        s = Scope(nc, ctx, f"g{depth}")
        w1, w2 = s.sb("w1", [P, 2 * HID]), s.sb("w2", [P, 3, D])
        b1, b2, affine = s.sb("b1", [P, 2, 3]), s.sb("b2", [P, D]), s.sb("affine", [P, 2])
        norm = Norm(s)
        upper = s.sb("upper", [P, QT, H])
        shifted, xhat = s.sb("shifted", [P, QT, D]), s.sb("xhat", [P, QT, D])
        hT = [s.sb(f"hT{n}", [P, TOK]) for n in range(2)]
        gelu, hidden = s.sb("gelu", [P, 3, TOK]), s.sb("hidden", [P, 3, TOK])
        scratch = s.sb("scratch", [P, QT, D])
        fronts, gs, linears, outs = Ring(s, "fronts", 1), Ring(s, "gs", 2), Ring(s, "linears", 2), Ring(s, "outs", 1)
        loaded, started, front_chained, back_chained, upper_ready, xhat_ready, hT_ready = (s.sem(name) for name in (
            "loaded", "started", "front_chained", "back_chained", "upper_ready", "xhat_ready", "hT_ready"))
        front = [("take",), ("shift",), ("norm",), ("hT",)]
        back = [("g", 0), ("g", 1), ("linear", 0), ("g", 2), ("linear", 1), ("linear", 2), ("out",)]
        block = s.block()
        n_loaded = 6 * 16

        @block.sync
        def _(sp):
            sp.wait_ge(started, 1)
            load(sp, loaded, [(w1[:, :], dram["L2_w1"][depth]),
                              (w2[:, 0:2, :], dram["L2_w2"][depth, 0:2 * P, :].rearrange("(t p) d -> p t d", p=P)),
                              (w2[0:HID - 2 * P, 2, :], dram["L2_w2"][depth, 2 * P:HID, :]),
                              (b1[:, :, :], dram["L2_b1"][depth]), (b2[:, :], row_of(dram["L2_b2"][depth])),
                              (affine[:, :], dram["L2_affine"][depth])])

        @block.tensor
        def _(pe):
            pe.wait_ge(loaded, n_loaded)

            def go(steps, bt, bo, ft, fo):
                front, g_in, linear_in = Uses(fronts, ft, fo, 2), Uses(gs, bt, bo, 3), Uses(linears, bt, bo, 3)
                out = Uses(outs, bt, bo, 1)
                for half, kind, *at in steps:
                    if kind == "shift":
                        pe.wait_ge(upper_ready, ft + 1)
                        bank = front.fill(pe)
                        for t in range(QT):
                            mm = pe.matmul(bank[:, t * H:(t + 1) * H], res["shift"][:, 0, :], upper[:, t, :],
                                           start=(t == 0), stop=(t == 0), skip_group_check=True)
                            if t:
                                mm = pe.matmul(bank[:, t * H:(t + 1) * H], res["shift"][:, 1, :], upper[:, t - 1, :],
                                               start=False, stop=True, skip_group_check=True)
                        front.filled(mm)
                    elif kind == "hT":
                        pe.wait_ge(xhat_ready, ft + 1)
                        bank = front.fill(pe)
                        for t in range(QT):
                            mm = pe.transpose(bank[:, t * P:(t + 1) * P], xhat[:, t, :], res["ident"][:, :])
                        front.filled(mm)
                    elif kind in ("g", "linear"):
                        c, = at
                        if (kind, c) == ("g", 0):
                            pe.wait_ge(hT_ready, bt + 1)
                        r0, rows = parts[c]
                        ring = g_in if kind == "g" else linear_in
                        w0 = r0 + (HID if kind == "g" else 0)
                        bank = ring.fill(pe)
                        ring.filled(pe.matmul(bank[0:rows, 0:TOK], w1[:, w0:w0 + rows], hT[bo][:, :], start=True, stop=True))
                    elif kind == "out":
                        pe.wait_ge(linears.free, bt * 3 + 3 + 2)
                        bank = out.fill(pe)
                        for t in range(QT):
                            for c in range(3):
                                mm = pe.matmul(bank[:, t * P:(t + 1) * P], hidden[:, c, t * P:(t + 1) * P], w2[:, c, :],
                                               start=(t == 0 and c == 0), stop=(c == 2), skip_group_check=True)
                        out.filled(mm)

            walk(pe, front, back, go)

        @block.scalar
        def _(act):
            gs.start(act)
            act.wait_ge(loaded, n_loaded)

            def go(steps, bt, bo, ft, fo):
                g_in = Uses(gs, bt, bo, 3)
                for half, kind, *at in steps:
                    if kind == "g":
                        c, = at
                        rows = parts[c][1]
                        bank = g_in.take(act)
                        g_in.emptied(nc.scalar.activation(gelu[0:rows, c, :], bank[0:rows, 0:TOK], ACT.Gelu,
                                                          bias=b1[0:rows, 1, c:c + 1]))

            walk(act, front, back, go)

        @block.gpsimd
        def _(pool):
            pool.wait_ge(norm.power_ready, 1)
            with pool.Fori(0, BATCH) as turn:
                norm.gpsimd(pool, turn)

        @block.vector
        def _(dve):
            for ring in (fronts, linears, outs):
                ring.start(dve)
            dve.memset(w2[:, 2, :], 0.0)
            dve.memset(hidden[:, 2, :], 0.0).then_inc(started, 1)
            norm.start(dve)
            dve.wait_ge(loaded, n_loaded)
            dve.wait_ge(norm.power_ready, 1)

            def go(steps, bt, bo, ft, fo):
                front, linear_in, out = Uses(fronts, ft, fo, 2), Uses(linears, bt, bo, 3), Uses(outs, bt, bo, 1)
                chain, back_chain = Chain(dve, front_chained, ft, 2), Chain(dve, back_chained, bt, 1)
                for half, kind, *at in steps:
                    if kind == "take":
                        now = y[:, bass.ds(ft * QT, QT), :]
                        dve.tensor_copy(upper[:, :, :], now[:, :, H:D]).then_inc(upper_ready, 1)
                        dve.tensor_copy(shifted[:, :, 0:H], now[:, :, 0:H])
                    elif kind == "shift":
                        bank = front.take(dve)
                        front.emptied(dve.tensor_copy(shifted[:, :, H:D], bank[:, 0:QT * H].rearrange("p (t d) -> p t d", d=H)))
                        front.settled(dve)
                    elif kind == "norm":
                        norm.vector(dve, chain, ft, lambda t: shifted[:, t, :], xhat, xhat_ready)
                    elif kind == "hT":
                        bank = front.take(dve)
                        front.emptied(dve.tensor_scalar(hT[fo][:, :], bank[:, 0:TOK], affine[:, 0:1], affine[:, 1:2],
                                                        ALU.mult, ALU.add))
                        front.settled(dve)
                        dve.sem_inc(hT_ready, 1)
                    elif kind == "linear":
                        c, = at
                        rows = parts[c][1]
                        bank = linear_in.take(dve)
                        dve.wait_ge(gs.free, bt * 3 + c + 1 + 2)
                        linear_in.emptied(dve.scalar_tensor_tensor(out=hidden[0:rows, c, :], in0=bank[0:rows, 0:TOK],
                                                                   scalar=b1[0:rows, 0, c:c + 1], in1=gelu[0:rows, c, :],
                                                                   op0=ALU.add, op1=ALU.mult))
                    elif kind == "out":
                        bank = out.take(dve)
                        out.emptied(dve.tensor_tensor(scratch[:, :, :], bank[:, 0:QT * D].rearrange("p (t d) -> p t d", d=D),
                                                      b2[:, :].unsqueeze(1).broadcast_to([P, QT, D]), ALU.add))
                        out.settled(dve)
                        now = y[:, bass.ds(bt * QT, QT), :]
                        back_chain.link(dve.tensor_tensor(now, now, scratch[:, :, :], ALU.add))

            walk(dve, front, back, go)


def shape_constants():
    r = np.arange(P)
    q, k = r[:, None], r[None, :]
    banned = [k > q, (k > q) | (k < q - WINDOW), k < q + P - WINDOW]
    masks = np.zeros((P, 6, P), np.float32)
    for n, m in enumerate(banned):
        masks[:, 2 * n, :] = np.where(m, BIG, 0.0)
        masks[:, 2 * n + 1, :] = np.where(m.T, BIG, 0.0)
    minus_head = np.zeros((P, 16, P), np.float32)
    for part in range(3):
        for h in range(16):
            minus_head[part * 16 + h, h, :] = -1.0
    shift = np.zeros((P, 2, P), np.float32)
    shift[r[:-1], 0, r[1:]] = 1.0
    shift[P - 1, 1, 0] = 1.0
    half = np.arange(0, 64, 2, dtype=np.float32)
    angle = np.arange(TOK, dtype=np.float32)[:, None] * (1.0 / 10000.0 ** (half / 64))[None, :].astype(np.float32)
    factor = ((half + 25.6) / 89.6)[None, :] ** ((np.arange(TOK) - TOK // 2) / 32.0)[:, None]
    cos, sin = np.cos(angle), np.sin(angle)
    rotary = np.zeros((2, 2, TOK, 64), np.float32)
    for n, f in enumerate((factor, 1.0 / factor)):
        rotary[n, 0] = np.concatenate([cos * f, cos * f], axis=1)
        rotary[n, 1] = np.concatenate([-sin * f, sin * f], axis=1)
    rotary = rotary.reshape(2, 2, QT, P, 64).transpose(3, 0, 1, 2, 4)
    return {"c_rotary": rotary, "c_ident": np.eye(P, dtype=np.float32), "c_masks": masks, "c_minus_head": minus_head,
            "c_shift": shift}


def lay_out(z):
    t = {"x": z["L0_attn_x"]}
    for n in range(4):
        t[f"L{n}_cT"] = z[f"L{n}_c"].T
        t[f"L{n}_wmod"] = z[f"L{n}_wmod"]
    w = z["L0_attn_W_attn"]
    w_q = w[:512].reshape(4, 16, 8, D).transpose(1, 0, 2, 3).reshape(512, D)
    t["L0_w"] = np.concatenate([w_q, w[512:]], axis=0).T
    t["L0_wo"] = z["L0_attn_W_proj"].reshape(D, 4, 16, 8).transpose(2, 1, 3, 0).reshape(512, D)
    t["L3_w"] = z["L3_attn_w_qkv"]
    t["L3_wo"] = z["L3_attn_w_proj"]
    t["L3_attn_b_proj"] = z["L3_attn_b_proj"]
    t.update(lay_out_rest(z))
    t.update(shape_constants())
    return {k: np.ascontiguousarray(v) for k, v in t.items()}


def resident(s):
    return {
        "x": s.sb("x", [P, BATCH * QT, D]),
        "ident": s.sb("ident", [P, P]),
        "identb": s.sb("identb", [P, P], BF16),
        "masks": s.sb("masks", [P, 6, P], BF16),
        "minus_head": s.sb("minus_head", [P, 16, P], BF16),
        "shift": s.sb("shift", [P, 2, P]),
        "mod": s.sb("mod", [P, 4, BATCH]),
        "gate": s.sb("gate", [P, 2, BATCH, D]),
    }


def lay_out_rest(z):
    t = {}
    t["L1_w"] = z["L1_attn_Wqkv_w"].T
    t["L1_wo"] = z["L1_attn_Wo_w"].T
    t["L1_qk_bias"] = z["L1_attn_Wqkv_b"][:2048].reshape(16, P).T
    t["L1_v_bias"] = z["L1_attn_Wqkv_b"][2048:]
    t["L1_ghost"] = z["L1_attn_ghost"]
    t["L1_wo_bias"] = z["L1_attn_Wo_b"]
    t["L2_w"] = np.concatenate([z["L2_attn_Wq"].T, z["L2_attn_Wk"].T, z["L2_attn_Wv"].T], axis=1)
    t["L2_wo"] = z["L2_attn_Wo"].T
    t["L2_qk_bias"] = np.stack([z["L2_attn_bq"], z["L2_attn_bk"]], axis=1)
    t["L2_v_bias"] = z["L2_attn_bv"]
    t["L2_wo_bias"] = z["L2_attn_bo"]
    for n in ("gate", "up", "down"):
        t[f"L1_ffn_w_{n}"] = z[f"L1_ffn_w_{n}"]
    t["L3_sel"] = z["L3_ffn_expert_sel"].T
    t["L3_keys"] = z["L3_ffn_keys"].transpose(1, 0, 2).reshape(D, 512)
    t["L3_values"] = z["L3_ffn_values"].reshape(512, D)
    t["L3_ffn_route_scale"] = z["L3_ffn_route_scale"]
    t["L0_router"] = z["L0_ffn_router_weight"].T
    t["L0_router_bias"] = z["L0_ffn_router_bias"]
    t["L0_gate_up"] = z["L0_ffn_gate_up_proj"]
    t["L0_gate_up_bias"] = z["L0_ffn_gate_up_bias"].reshape(8, 4, P).transpose(2, 0, 1)
    t["L0_down"] = z["L0_ffn_down_proj"].reshape(8 * 256, D)
    t["L0_down_bias"] = z["L0_ffn_down_bias"]
    t["L2_wqkv"] = z["L2_ffn_wqkv"]
    t["L2_ffn_wo"] = z["L2_ffn_wo"]
    t["L2_q_scale"] = z["L2_ffn_q_scale"]
    t["L2_k_scale"] = z["L2_ffn_k_scale"]
    t["L2_w1"] = z["L2_ffn_w1"]
    t["L2_w2"] = z["L2_ffn_w2"]
    b1 = np.zeros((2, 2, 3 * P), np.float32)
    b1[:, :, 0:341] = z["L2_ffn_b1"].reshape(2, 2, 341)
    t["L2_b1"] = b1.reshape(2, 2, 3, P).transpose(0, 3, 1, 2)
    t["L2_b2"] = z["L2_ffn_b2"]
    t["L2_affine"] = np.stack([z["L2_ffn_ln_g"], z["L2_ffn_ln_b"]], axis=2)
    return t


OUT_SHAPE = (BATCH, TOK, D)


def build(nc, dram, out):
    with ExitStack() as ctx:
        res = resident(Scope(nc, ctx, "res"))
        constants_phase(nc, dram, res)
        for layer, (attention, ffn) in enumerate(((layer0_attention, layer0_ffn), (layer1_attention, layer1_ffn),
                                                  (layer2_attention, layer2_ffn), (layer3_attention, layer3_ffn))):
            modulation_phase(nc, layer, dram, res)
            attention(nc, dram, res)
            ffn(nc, dram, res)
        store_phase(nc, res, out)


def kernel(**inputs):
    import concourse.bacc as bacc
    from concourse.bass_utils import run_bass_kernel_spmd

    nc = bacc.Bacc("TRN2", target_bir_lowering=False, num_devices=1)
    arrays = lay_out(inputs)
    dram = {n: nc.dram_tensor(f"in_{n}", a.shape, mybir.dt.from_np(a.dtype), kind="ExternalInput").ap()
            for n, a in arrays.items()}
    out = nc.dram_tensor("out", OUT_SHAPE, F32, kind="ExternalOutput").ap()
    build(nc, dram, out)
    r = run_bass_kernel_spmd(nc, [{f"in_{n}": a for n, a in arrays.items()}], core_ids=[0])
    return r.results[0]["out"]
```

```python
from contextlib import ExitStack

import concourse.bass as bass
import numpy as np
from concourse import mybir

ALU = mybir.AluOpType
ACT = mybir.ActivationFunctionType
F32 = mybir.dt.float32
BF16 = mybir.dt.bfloat16
AX_X = mybir.AxisListType.X

P = 128
BATCH = 16
TOK = 256
QT = TOK // P
D = 128
EPS = 1e-5
BIG = -1.0e30
WINDOW = 64
LAYERS = 4


class Chain:

    def __init__(self, eng, sem, turn, per):
        self.eng, self.sem, self.turn, self.per, self.n = eng, sem, turn, per, 0

    def value(self, n):
        return self.turn * self.per + n if self.per else n

    def link(self, ins):
        self.n += 1
        ins.then_inc(self.sem, 1)
        self.eng.wait_ge(self.sem, self.value(self.n))

    def end(self):
        assert self.per in (0, self.n), f"the chain has {self.n} links in a turn, not {self.per}"


class Scope:

    def __init__(self, nc, ctx, name):
        self.nc, self.ctx, self.name, self.sems = nc, ctx, name, []

    def sb(self, name, shape, dt=F32):
        return self.ctx.enter_context(self.nc.sbuf_tensor(f"{self.name}_{name}", list(shape), dt))

    def bank(self, name, dt=F32):
        return self.ctx.enter_context(self.nc.psum_tensor(f"{self.name}_{name}", [P, 512], dt))

    def sem(self, name):
        self.sems.append(self.ctx.enter_context(self.nc.semaphore(f"{self.name}_{name}")))
        return self.sems[-1]

    def block(self):
        self.ctx.callback(self.clear)
        return self.ctx.enter_context(self.nc.Block())

    def clear(self):
        with self.nc.Block() as block:
            @block.gpsimd
            def _(pool):
                for sem in self.sems:
                    pool.sem_clear(sem)


def tiles(x):
    return x.rearrange("p (t q) -> p t q", q=P)


def constants_phase(nc, dram, res):
    L = LAYERS
    with ExitStack() as ctx:
        s = Scope(nc, ctx, "cst")
        masks_f, head_f = s.sb("masks_f", [P, 6, P]), s.sb("head_f", [P, 16, P])
        ct, wmod = s.sb("ct", [P, L, BATCH]), s.sb("wmod", [P, L, 6, D])
        e1, e2 = s.sb("e1", [P, L, BATCH]), s.sb("e2", [P, L, BATCH])
        silu = s.sb("silu", [P, L, P])
        above, below, size = s.sb("above", [P, 512]), s.sb("below", [P, 512]), s.sb("size", [P, 512])
        shifts = s.bank("shifts")
        gates = [s.bank(f"gates{n}") for n in range(2)]
        conditions, weights, constants, loaded = (s.sem(x) for x in ("conditions", "weights", "constants", "loaded"))
        negexp, silu_ready, products, chained = (s.sem(x) for x in ("negexp", "silu_ready", "products", "chained"))
        block = s.block()

        @block.sync
        def _(sp):
            for layer in range(L):
                sp.dma_start(ct[:, layer, :], dram[f"L{layer}_cT"]).then_inc(conditions, 16)
            sp.dma_start(res["ident"][:, :], dram["c_ident"]).then_inc(constants, 16)
            for layer in range(L):
                sp.dma_start(wmod[:, layer, :, :],
                             dram[f"L{layer}_wmod"].rearrange("k (j d) -> k j d", d=D)).then_inc(weights, 16)
            sp.dma_start(masks_f[:, :, :], dram["c_masks"]).then_inc(constants, 16)
            sp.dma_start(head_f[:, :, :], dram["c_minus_head"]).then_inc(constants, 16)
            sp.dma_start(res["shift"][:, :, :], dram["c_shift"]).then_inc(loaded, 16)
            sp.dma_start(res["x"][:, :, :], dram["x"].rearrange("b (t p) d -> p (b t) d", p=P)).then_inc(loaded, 16)
            sp.wait_ge(loaded, 2 * 16)

        @block.scalar
        def _(act):
            act.wait_ge(conditions, L * 16)
            nc.scalar.activation(e1[:, :, :], ct[:, :, :], ACT.Exp, scale=-1.0).then_inc(negexp, 1)

        @block.vector
        def _(dve):
            chain = Chain(dve, chained, 0, 0)
            chain.link(dve.memset(silu[:, :, :], 0.0))
            dve.wait_ge(conditions, L * 16)
            dve.wait_ge(negexp, 1)
            chain.link(dve.tensor_scalar(e2[:, :, :], e1[:, :, :], 1.0, None, ALU.add))
            chain.link(dve.reciprocal(e1[:, :, :], e2[:, :, :]))
            dve.tensor_tensor(silu[:, :, 0:BATCH], ct[:, :, :], e1[:, :, :], ALU.mult).then_inc(silu_ready, 1)
            dve.wait_ge(constants, 3 * 16)
            dve.tensor_copy(res["one_hot"][:, :, :], res["ident"][:, 0:BATCH].unsqueeze(2).broadcast_to([P, BATCH, P]))
            dve.tensor_copy(res["identb"][:, :], res["ident"][:, :])
            dve.tensor_copy(res["masks"][:, :, :], masks_f[:, :, :])
            dve.tensor_copy(res["minus_head"][:, :, :], head_f[:, :, :])
            for n in range(2):
                dve.wait_ge(products, n + 1)
                g = gates[n][:, :]
                chain.link(dve.tensor_scalar(size[:, :], g, 0.25, None, ALU.max))
                chain.link(dve.scalar_tensor_tensor(out=above[:, :], in0=g, scalar=0.0, in1=size[:, :],
                                                    op0=ALU.is_ge, op1=ALU.mult))
                chain.link(dve.tensor_scalar(size[:, :], g, -0.25, None, ALU.min))
                chain.link(dve.scalar_tensor_tensor(out=below[:, :], in0=g, scalar=0.0, in1=size[:, :],
                                                    op0=ALU.is_lt, op1=ALU.mult))
                chain.link(dve.tensor_tensor(res["gate_rows"][:, 2 * n:2 * n + 2, :].rearrange("p l d -> p (l d)"),
                                             above[:, :], below[:, :], ALU.add))
            dve.wait_ge(products, 3)
            for layer in range(L):
                for n in range(2):
                    last = dve.tensor_scalar(
                        res["mods"][layer][:, n::2, :],
                        shifts[:, 4 * layer * BATCH:4 * (layer + 1) * BATCH].rearrange("p (n b) -> p n b", b=BATCH)[:, n::2, :],
                        float(n), None, ALU.add)
            chain.link(last)

        @block.tensor
        def _(pe):
            pe.wait_ge(weights, L * 16)
            pe.wait_ge(silu_ready, 1)
            for n in range(2):
                for k in range(2):
                    mm = pe.matmul(gates[n][:, k * 2 * D:(k + 1) * 2 * D], silu[:, 2 * n + k, :],
                                   wmod[:, 2 * n + k, 2::3, :], start=(k == 0), stop=True, skip_group_check=True)
                mm.then_inc(products, 1)
            for layer in range(L):
                for n, j in enumerate((0, 1, 3, 4)):
                    c = (4 * layer + n) * BATCH
                    mm = pe.matmul(shifts[:, c:c + BATCH], wmod[:, layer, j, :], silu[:, layer, 0:BATCH],
                                   start=(c == 0), stop=True, skip_group_check=True)
            mm.then_inc(products, 1)


def gates_phase(nc, layer, res):
    with ExitStack() as ctx:
        s = Scope(nc, ctx, f"gt{layer}")
        banks = [s.bank(f"rows{n}") for n in range(BATCH // 2)]
        picked, copied = s.sem("picked"), s.sem("copied")
        block = s.block()

        def copied_to(n):
            return res["gate"][:, :, 2 * n:2 * n + 2, :].rearrange("p g b d -> p b g d")

        @block.tensor
        def _(pe):
            for n in range(BATCH // 2):
                for k in range(2):
                    mm = pe.matmul(banks[n][:, k * 2 * D:(k + 1) * 2 * D], res["one_hot"][:, 2 * n + k, :],
                                   res["gate_rows"][:, layer, :], start=(k == 0), stop=True, skip_group_check=True)
                mm.then_inc(picked, 1)

        @block.scalar
        def _(act):
            for n in range(0, BATCH // 2, 2):
                act.wait_ge(picked, n + 1)
                nc.scalar.copy(copied_to(n), banks[n][:, :].rearrange("p (b g d) -> p b g d", b=2, g=2)).then_inc(copied, 1)

        @block.vector
        def _(dve):
            for n in range(1, BATCH // 2, 2):
                dve.wait_ge(picked, n + 1)
                dve.tensor_copy(copied_to(n), banks[n][:, :].rearrange("p (b g d) -> p b g d", b=2, g=2)).then_inc(copied, 1)
            dve.wait_ge(copied, BATCH // 2)


def store_phase(nc, res, out):
    with ExitStack() as ctx:
        s = Scope(nc, ctx, "st")
        stored = s.sem("stored")
        block = s.block()

        @block.sync
        def _(sp):
            sp.dma_start(out.rearrange("b (t p) d -> p (b t) d", p=P), res["x"][:, :, :]).then_inc(stored, 16)
            sp.wait_ge(stored, 16)


class Norm:

    def __init__(self, s, turns_per_loop=1):
        self.stats, self.mv = s.sb("stats", [P, QT, 6]), s.sb("mv", [P, QT, 2])
        self.var, self.power, self.rstd = s.sb("var", [P, QT]), s.sb("power", [P, QT]), s.sb("rstd", [P, QT])
        self.idle = s.sb("idle", [P, 2])
        self.var_ready, self.rstd_ready, self.power_ready = s.sem("var_ready"), s.sem("rstd_ready"), s.sem("power_ready")
        self.per = turns_per_loop

    def start(self, dve):
        dve.memset(self.idle[:, :], 0.0)
        dve.memset(self.power[:, :], -0.5).then_inc(self.power_ready, 1)

    def vector(self, dve, chain, turn, x_at, xhat, ready, nth=0):
        for t in range(QT):
            last = dve.bn_stats(self.stats[:, t, :], x_at(t))
        chain.link(last)
        dve.tensor_copy(self.idle[:, 1:2], self.idle[:, 0:1])
        for t in range(QT):
            last = dve.bn_aggr(self.mv[:, t, :], self.stats[:, t, :])
        chain.link(last)
        dve.tensor_scalar(self.var[:, :], self.mv[:, :, 1], EPS, None, ALU.add).then_inc(self.var_ready, 1)
        dve.wait_ge(self.rstd_ready, turn * self.per + nth + 1)
        for t in range(QT):
            last = dve.tensor_scalar(xhat[:, t, :], x_at(t), self.mv[:, t, 0:1], self.rstd[:, t:t + 1],
                                     ALU.subtract, ALU.mult)
        last.then_inc(ready, 1)

    def gpsimd(self, pool, turn, nth=0):
        pool.wait_ge(self.var_ready, turn * self.per + nth + 1)
        pool.tensor_tensor(self.rstd[:, :], self.var[:, :], self.power[:, :], ALU.pow).then_inc(self.rstd_ready, 1)


class Ring:

    def __init__(self, s, name, banks):
        self.banks = [s.bank(f"{name}_bank{n}") for n in range(banks)]
        self.full, self.free = s.sem(f"{name}_full"), s.sem(f"{name}_free")

    def start(self, reader):
        reader.sem_inc(self.free, len(self.banks))


class Uses:

    def __init__(self, ring, turn, odd, per):
        self.ring, self.turn, self.odd, self.per, self.n = ring, turn, odd, per, 0

    def _bank(self):
        self.n += 1
        return self.ring.banks[(self.odd * self.per + self.n - 1) % len(self.ring.banks)]

    def fill(self, pe):
        pe.wait_ge(self.ring.free, self.turn * self.per + self.n + 1)
        return self._bank()

    def filled(self, mm):
        mm.then_inc(self.ring.full, 1)

    def take(self, reader):
        reader.wait_ge(self.ring.full, self.turn * self.per + self.n + 1)
        return self._bank()

    def emptied(self, ins):
        ins.then_inc(self.ring.free, 1)

    def settled(self, reader):
        reader.wait_ge(self.ring.free, self.turn * self.per + self.n + len(self.ring.banks))

    def end(self):
        assert self.n == self.per, f"{self.ring.full}: {self.n} uses in a batch, not {self.per}"


class Attn:

    def __init__(self, name, sets, heads, hd, kind, scale):
        self.name, self.sets, self.heads, self.hd, self.kind = name, sets, heads, hd, kind
        self.scale = scale
        self.units = sets * heads
        self.pairs = self.units // 2
        self.lone = 2 * heads if sets > 1 else heads
        self.narrow = hd + 1 <= 32
        self.vw = 32
        self.width = self.units * hd
        self.per_bank = 16 if self.narrow else 512 // hd
        self.out_banks = -(-self.units // self.per_bank)
        self.chunks = [(qt, u, nu) for qt in range(QT) for u, nu in self.max_chunks(qt)]
        self.n_chunks = len(self.chunks)

    def keys(self, qt):
        return QT if self.kind == "full" else qt + 1

    def mask(self, qt, kb):
        if self.kind == "causal":
            return 0 if qt == kb else None
        if self.kind == "window":
            return 2 if qt == kb else 4
        return None

    def lone_of(self, u):
        return 2 * (u // 4) + u % 2 if self.sets > 1 else u

    def head_of(self, u):
        return u // self.sets

    def max_chunks(self, qt):
        n = 4 // self.keys(qt)
        return [(u, n) for u in range(0, self.units, n)]

    def exp_chunks(self, qt):
        return [(kb, u) for u in range(0, self.units, 4) for kb in range(self.keys(qt))]

    @property
    def n_exp(self):
        return sum(len(self.exp_chunks(qt)) for qt in range(QT))

    @property
    def n_max(self):
        return sum(len(self.max_chunks(qt)) for qt in range(QT)) + QT

    def front(self, project):
        steps = [("norm",), ("hT",)] + project
        if not self.narrow:
            return steps
        first = [("max", 0, j) for j in range(len(self.max_chunks(0)))]
        second = [("max", 1, j) for j in range(len(self.max_chunks(1)))]
        cut = min(2, len(second) - 1)
        return steps + first + [("parts", 0)] + second[:cut] + [("maxT", 0)] + second[cut:] + [("parts", 1), ("maxT", 1)]

    def back(self):
        if self.narrow:
            at = [(n, n, ("exp", qt, j)) for n, (qt, j) in
                  enumerate((qt, j) for qt in range(QT) for j in range(len(self.exp_chunks(qt))))]
            done = 0
            for qt in range(QT):
                for k in range(self.out_banks):
                    done += len(self.exp_chunks(qt)) // self.out_banks
                    at += [(done + 3, 100 + done, ("drain", qt, k)), (done + 5, 100 + done, ("turn", qt, k))]
                at += [(done + 7, 200, ("outT", qt)), (done + 9, 200, ("out", qt))]
            at.append((self.n_exp + 1, 50, ("heads", 1)))
            return [step for _, _, step in sorted(at)]
        steps, last = [], {}
        for n, (qt, _, _) in enumerate(self.chunks):
            last[qt] = n
        for n in range(self.n_chunks + 2):
            steps += [(kind, n - lag) for kind, lag in (("score", 0), ("turn", 1), ("values", 2)) if 0 <= n - lag < self.n_chunks]
            for qt in range(QT):
                steps += [(kind, qt) for kind, lag in (("heads", 2), ("outT", 3), ("out", 4))
                          if n - lag == last[qt] and qt < QT - 1]
        return steps + [("heads", QT - 1), ("outT", QT - 1), ("out", QT - 1)]


WEIGHTS = {
    "a0": {"middle": 2, "hT": 2, "turn": 0.3, "out": 1.6, "exp": 1.25, "exp0": 0.8, "norm": 3, "qkv": 6, "pack": 4, "heads": 1.4, "max0": 0.8},
    "a1": {"values": 0.3, "q": 1.5, "norm": 1.75, "v": 1.25, "lead": 1.6, "heads": 1.25},
    "a3": {"exp0": 0.4, "heads": 5, "max": 1.25, "lead": 0.4, "norm": 2, "hT": 2, "qkv": 2, "middle": 2, "pack": 2},
    "w": {"norm": 0.7, "total": 0.8, "out": 0.6, "qkv": 1.25},
    "f0": {"trail": 7, "hT": 1.6, "norm": 1.6, "into": 0.8},
    "f1": {"hidden0": 0.2, "lead": 0.6, "hiddenT": 2, "hqT": 4, "in": 0.5, "scale": 0.2, "finish": 2},
    "a2": {"mixedT": 1.4, "hT": 1.4, "scores": 0.5, "v": 1.6, "lead": 1.6, "qk": 0.6},
    "f3": {"logits": 3, "weight": 1.6, "experts": 1.25},
    "i": {},
    "g": {"norm": 0.7, "out": 0.6},
}


def merged(front, back, weight):
    def spread(half, steps):
        weights = [weight.get("".join(map(str, step[:2])), weight.get(step[0], 1.0)) for step in steps]
        lead = weight.get("lead", 0.0) if half == "front" else 0.0
        ends = lead + np.cumsum(weights)
        total = ends[-1] + (weight.get("trail", 0.0) if half == "front" else 0.0)
        return [((end - w / 2) / total, half, step) for end, w, step in zip(ends, weights, steps)]

    both = sorted(spread("back", back) + spread("front", front), key=lambda x: x[0])
    return [(half,) + step for _, half, step in both]


def step_lists(a, project):
    both = merged(a.front(project), a.back(), WEIGHTS[a.name.rstrip("01") if a.kind == "window" else a.name])
    fronts, backs = [x for x in both if x[0] == "front"], [x for x in both if x[0] == "back"]
    return lambda back_turn, front_turn: fronts if back_turn is None else backs if front_turn is None else both


def pipelined(eng, go):
    go(None, 0, 0, 0)
    with eng.Fori(0, (BATCH - 2) // 2) as pair:
        go(pair * 2, 0, pair * 2 + 1, 1)
        go(pair * 2 + 1, 1, pair * 2 + 2, 0)
    go(BATCH - 2, 0, BATCH - 1, 1)
    go(BATCH - 1, 1, None, 0)


class Attention:

    def pe_hT(self, pe, front, turn):
        pe.wait_ge(self.xhat_ready, turn + 1)
        bank = front.fill(pe)
        for t in range(QT):
            mm = pe.transpose(bank[:, t * P:(t + 1) * P], self.xhat[:, t, :], self.res["ident"][:, :])
        front.filled(mm)

    def pe_outT(self, pe, tail, qt, turn):
        nt = self.a.width // P
        pe.wait_ge(self.heads_ready, turn * QT + qt + 2)
        for t0 in range(0, nt, 4):
            bank = tail.fill(pe)
            for t in range(t0, min(t0 + 4, nt)):
                mm = pe.transpose(bank[:, (t - t0) * P:(t - t0 + 1) * P], self.heads_out[qt % len(self.heads_out)][:, t * P:(t + 1) * P],
                                  self.res["ident"][:, :])
            tail.filled(mm)

    def pe_out(self, pe, tail, qt, turn):
        nt = self.a.width // P
        pe.wait_ge(self.headsT_ready, turn * QT + qt + 1)
        bank = tail.fill(pe)
        for t in range(nt):
            mm = pe.matmul(bank[:, 0:D], self.heads_outT[:, t, :], self.w_out[:, t, :], start=(t == 0), stop=(t == nt - 1))
        tail.filled(mm)

    def dve_outT(self, dve, tail):
        nt = self.a.width // P
        for t0 in range(0, nt, 4):
            m = min(4, nt - t0)
            bank = tail.take(dve)
            tail.emptied(dve.tensor_copy(self.heads_outT[:, t0:t0 + m, :].rearrange("p t q -> p (t q)"), bank[:, 0:m * P]))
        tail.settled(dve)
        dve.sem_inc(self.headsT_ready, 1)

    def dve_hT(self, dve, front, turn):
        bank = front.take(dve)
        front.emptied(dve.tensor_scalar(self.hT[:, :], bank[:, 0:TOK], self.res["mod"][:, 1, bass.ds(turn, 1)],
                                        self.res["mod"][:, 0, bass.ds(turn, 1)], ALU.mult, ALU.add))
        front.settled(dve)
        dve.sem_inc(self.hT_ready, 1)

    def finish_x(self, dve, chain, tail, turn, qt, bank):
        x = x_tile(self.res, turn * QT + qt)
        g = self.res["gate"][:, 0, bass.ds(turn, 1), :].rearrange("p a d -> p (a d)")
        if self.out_bias is None:
            tail.emptied(dve.tensor_tensor(self.scratch[:, :], bank[:, 0:D], g, ALU.mult))
            tail.settled(dve)
        else:
            tail.emptied(dve.tensor_tensor(self.scratch[:, :], bank[:, 0:D], self.out_bias, ALU.add))
            tail.settled(dve)
            chain.link(dve.tensor_tensor(self.scratch[:, :], self.scratch[:, :], g, ALU.mult))
        chain.link(dve.tensor_tensor(x, x, self.scratch[:, :], ALU.add))


class NarrowAttention(Attention):

    def __init__(self, s, nc, a, res, front_links, back_links, v_uses, q_uses, out_bias=None):
        self.s, self.nc, self.a, self.res = s, nc, a, res
        self.front_links, self.back_links, self.v_uses, self.q_uses = front_links, back_links, v_uses, q_uses
        self.out_bias = out_bias
        self.qT = [s.sb(f"qT{n}", [P, a.pairs, TOK], BF16) for n in range(2)]
        self.k_alone = [s.sb(f"k_alone{n}", [P, a.lone, TOK], BF16) for n in range(2)]
        self.v = [s.sb(f"v{n}", [P, QT, a.heads, a.vw]) for n in range(2)]
        self.featured = [s.sb(f"featured{n}", [P, 512]) for n in range(2)]
        self.row_max = s.sb("row_max", [P, QT, a.heads, a.sets])
        self.rest = s.sb("rest", [P, a.heads, a.sets])
        self.max_parts = s.sb("max_parts", [P, QT, a.sets, P], BF16)
        self.maxT = [s.sb(f"maxT{n}", [P, QT, a.sets, P], BF16) for n in range(2)]
        self.probs = [s.sb(f"probs{n}", [P, 512]) for n in range(4)]
        self.inverse = s.sb("inverse", [P, a.units])
        self.heads_out = [s.sb(f"heads_out{n}", [P, a.width]) for n in range(QT)]
        self.heads_outT = s.sb("heads_outT", [P, a.width // P, P])
        self.w_out = s.sb("w_out", [P, a.width // P, D])
        self.xhat, self.hT, self.scratch = s.sb("xhat", [P, QT, D]), s.sb("hT", [P, TOK]), s.sb("scratch", [P, D])
        self.to_dve = Ring(s, "to_dve", 2)
        self.to_act = Ring(s, "to_act", 1)
        self.scores = Ring(s, "scores", 2)
        self.tail = Ring(s, "tail", 1)
        self.outs = Ring(s, "outs", 2)
        self.xhat_ready, self.hT_ready, self.qkv_ready = s.sem("xhat_ready"), s.sem("hT_ready"), s.sem("qkv_ready")
        self.qT_ready = s.sem("qT_ready")
        self.parts_ready, self.maxT_ready = s.sem("parts_ready"), s.sem("maxT_ready")
        self.probs_ready = self.scores.free
        self.probs_free = s.sem("probs_free")
        self.heads_ready, self.headsT_ready = s.sem("heads_ready"), s.sem("headsT_ready")
        self.front_chained, self.back_chained = s.sem("front_chained"), s.sem("back_chained")
        self.started, self.loaded = s.sem("started"), s.sem("loaded")

    def begin_vector(self, dve):
        self.to_dve.start(dve)
        self.tail.start(dve)
        dve.sem_inc(self.heads_ready, 1)
        for v in self.v:
            dve.memset(v[:, :, :, self.a.hd:self.a.hd + 1], 1.0)
            dve.memset(v[:, :, :, self.a.hd + 1:self.a.vw], 0.0)
        for k in self.k_alone:
            dve.memset(k[:, :, :], 0.0)
        dve.memset(self.max_parts[:, :, :, :], 0.0).then_inc(self.started, 1)

    def begin_scalar(self, act):
        self.scores.start(act)
        act.sem_inc(self.probs_free, 4)
        self.to_act.start(act)
        self.outs.start(act)


    def pe_batch(self, pe, steps, project, bt, bo, ft, fo):
        a = self.a
        front = Uses(self.to_dve, ft, fo, self.v_uses)
        to_act = Uses(self.to_act, ft, fo, self.q_uses)
        scores, tail = Uses(self.scores, bt, bo, a.n_exp), Uses(self.tail, bt, bo, self.tail_uses)
        outs = Uses(self.outs, bt, bo, QT * a.out_banks)
        lagging = []
        for half, kind, *at in steps:
            if kind == "norm":
                pass
            elif kind == "hT":
                self.pe_hT(pe, front, ft)
            elif kind == "max":
                self.pe_max(pe, front, at[0], *a.max_chunks(at[0])[at[1]], fo, first=at == [0, 0], turn=ft)
            elif kind == "parts":
                pass
            elif kind == "maxT":
                self.pe_maxT(pe, front, at[0], ft)
            elif kind == "exp":
                self.pe_scores(pe, scores, at[0], *a.exp_chunks(at[0])[at[1]], bo, bt, first=at[1] == 0)
                lagging.append((scores.n - 1, at[0]) + a.exp_chunks(at[0])[at[1]])
                if len(lagging) > 2:
                    self.pe_values(pe, outs, bt, bo, *lagging.pop(0))
            elif kind == "heads":
                while lagging:
                    self.pe_values(pe, outs, bt, bo, *lagging.pop(0))
            elif kind == "turn":
                self.pe_turn(pe, tail, at[0], at[1], bt)
            elif kind == "drain":
                pass
            elif kind == "outT":
                self.pe_outT(pe, tail, at[0], bt)
            elif kind == "out":
                self.pe_out(pe, tail, at[0], bt)
            else:
                project(pe, kind, at, front, to_act, ft, fo)
        if ft is not None:
            front.end()
            to_act.end()
        if bt is not None:
            scores.end()
            tail.end()

    @property
    def tail_uses(self):
        return QT * (-(-(self.a.width // P) // 4) + 1 + self.a.out_banks)

    def pe_max(self, pe, front, qt, u0, nu, odd, first, turn):
        a, nk = self.a, self.a.keys(qt)
        if first:
            pe.wait_ge(self.qkv_ready, turn + 1)
            pe.wait_ge(self.qT_ready, turn + 1)
        bank = front.fill(pe)
        w = 2 * nk * P
        for n, u in enumerate(range(u0, u0 + nu, 2)):
            lone = a.lone_of(u)
            mm = pe.matmul(bank[:, n * w:(n + 1) * w].rearrange("p (h k) -> p h k", h=2),
                           self.qT[odd][:, u // 2, qt * P:(qt + 1) * P], self.k_alone[odd][:, lone:lone + 2, 0:nk * P],
                           start=(n == 0), stop=True, skip_group_check=True)
        for kb in range(nk):
            mask = a.mask(qt, kb)
            if mask is not None:
                out = bank[:, :].rearrange("p (h k) -> p h k", h=nu)[:, :, kb * P:(kb + 1) * P]
                mm = pe.matmul(out, self.res["identb"][:, :],
                               self.res["masks"][:, mask:mask + 1, :].broadcast_to([P, nu, P]),
                               start=False, stop=True, skip_group_check=True)
        front.filled(mm)

    def pe_maxT(self, pe, front, qt, turn):
        pe.wait_ge(self.parts_ready, turn * QT + qt + 1)
        bank = front.fill(pe)
        for s in range(self.a.sets):
            mm = pe.transpose(bank[:, :].bitcast(BF16)[:, s * P:(s + 1) * P], self.max_parts[:, qt, s, :],
                              self.res["identb"][:, :])
        front.filled(mm)

    def pe_scores(self, pe, scores, qt, kb, u0, odd, turn, first):
        a, res = self.a, self.res
        if first:
            pe.wait_ge(self.maxT_ready, turn * QT + qt + 1)
        bank = scores.fill(pe)
        queries, keys = slice(qt * P, (qt + 1) * P), slice(kb * P, (kb + 1) * P)
        units = bank[:, :].rearrange("p (u q) -> p u q", u=4)
        if a.sets > 1:
            for par in range(2):
                pe.matmul(units.rearrange("p (g two) q -> p g two q", two=2)[:, :, par, :],
                          self.k_alone[odd][:, a.lone_of(u0) + par, keys], self.qT[odd][:, u0 // 2:u0 // 2 + 2, queries],
                          start=(par == 0), stop=False, skip_group_check=True)
            mm = pe.matmul(units, res["minus_head"][:, a.head_of(u0), :], self.maxT[odd][:, qt, :, :],
                           start=False, stop=True, skip_group_check=True)
        else:
            for j in range(4):
                u = u0 + j
                pe.matmul(units[:, j, :], self.k_alone[odd][:, u, keys], self.qT[odd][:, u // 2, queries],
                          start=(j == 0), stop=False, skip_group_check=True)
            for j in range(4):
                mm = pe.matmul(units[:, j, :], res["minus_head"][:, u0 + j, :], self.maxT[odd][:, qt, 0, :],
                               start=False, stop=True, skip_group_check=True)
        mask = a.mask(qt, kb)
        if mask is not None:
            mm = pe.matmul(units, res["identb"][:, :], res["masks"][:, mask + 1:mask + 2, :].broadcast_to([P, 4, P]),
                           start=False, stop=True, skip_group_check=True)
        scores.filled(mm)

    def pe_values(self, pe, outs, turn, odd, n, qt, kb, u0):
        a = self.a
        pe.wait_ge(self.probs_ready, turn * a.n_exp + n + 3)
        if kb == 0 and u0 % 16 == 0:
            self.out_now = outs.fill(pe)
        probs = self.probs[(odd * a.n_exp + n) % 4]
        c = u0 % 16 // 4
        last = kb == a.keys(qt) - 1
        for j in range(4):
            mm = pe.matmul(self.out_now[32 * j:32 * j + 32, c * P:(c + 1) * P], self.v[odd][:, kb, a.head_of(u0 + j), :],
                           probs[:, j * P:(j + 1) * P], start=(kb == 0), stop=last, skip_group_check=True)
        mm.then_inc(self.probs_free, 1)
        if last and u0 % 16 == 12:
            pe.wait_ge(self.probs_free, turn * a.n_exp + n + 5)
            pe.sem_inc(self.outs.full, 1)

    def pe_turn(self, pe, tail, qt, k, turn):
        n = qt * self.a.out_banks + k
        pe.wait_ge(self.outs.free, turn * QT * self.a.out_banks + n + 3)
        bank = tail.fill(pe)
        for c in range(4):
            mm = pe.transpose(bank[:, c * P:(c + 1) * P], self.featured[n % 2][:, c * P:(c + 1) * P], self.res["ident"][:, :])
        tail.filled(mm)


    def act_batch(self, act, steps, project, bt, bo, ft, fo):
        a = self.a
        scores = Uses(self.scores, bt, bo, a.n_exp)
        to_act = Uses(self.to_act, ft, fo, self.q_uses)
        outs = Uses(self.outs, bt, bo, QT * a.out_banks)
        for half, kind, *at in steps:
            if kind == "exp":
                n = scores.n
                bank = scores.take(act)
                act.wait_ge(self.probs_free, bt * a.n_exp + n + 1)
                self.nc.scalar.activation(self.probs[(bo * a.n_exp + n) % 4][:, :], bank[:, :], ACT.Exp,
                                          scale=a.scale).then_inc(self.probs_ready, 1)
            elif kind == "drain":
                qt, k = at
                n = qt * a.out_banks + k
                bank = outs.take(act)
                self.nc.scalar.copy(self.featured[n % 2][:, :], bank[:, :]).then_inc(self.outs.free, 1)
            elif half == "front":
                project(act, kind, at, to_act, ft, fo)


    def dve_batch(self, dve, steps, project, norm, modulate, finish, bt, bo, ft, fo):
        front = Uses(self.to_dve, ft, fo, self.v_uses)
        tail = Uses(self.tail, bt, bo, self.tail_uses)
        fchain = Chain(dve, self.front_chained, ft, self.front_links)
        bchain = Chain(dve, self.back_chained, bt, self.back_links)
        for half, kind, *at in steps:
            if kind == "norm":
                norm(dve, fchain, ft)
            elif kind == "hT":
                modulate(dve, front, ft)
            elif kind == "max":
                u0, nu = self.a.max_chunks(at[0])[at[1]]
                bank = front.take(dve)
                front.emptied(dve.tensor_reduce(
                    self.row_max[:, at[0], :, :].rearrange("p h s -> p (h s)")[:, u0:u0 + nu],
                    bank[:, :].rearrange("p (h k) -> p h k", h=nu), AX_X, ALU.max))
            elif kind == "parts":
                self.dve_parts(dve, front, fchain, at[0])
            elif kind == "maxT":
                bank = front.take(dve)
                front.emptied(dve.tensor_copy(self.maxT[fo][:, at[0], :, :].rearrange("p s q -> p (s q)"),
                                              bank[:, :].bitcast(BF16)[:, 0:self.a.sets * P]))
                front.settled(dve)
                dve.sem_inc(self.maxT_ready, 1)
            elif kind == "turn":
                self.dve_turn(dve, tail, bchain, at[0], at[1])
            elif kind == "outT":
                self.dve_outT(dve, tail)
            elif kind == "out":
                bank = tail.take(dve)
                finish(dve, bchain, tail, bt, at[0], bank)
            elif kind not in ("exp", "heads", "drain"):
                project(dve, kind, at, front, fchain, ft, fo)
        if ft is not None:
            front.end()
            fchain.end()
        if bt is not None:
            tail.end()
            bchain.end()

    def dve_parts(self, dve, front, chain, qt):
        a = self.a
        front.settled(dve)
        parts = self.max_parts[:, qt, :, 0:48].rearrange("p s (t h) -> p t h s", t=3)[:, :, 0:a.heads, :]
        top = self.row_max[:, qt, :, :]
        chain.link(dve.tensor_copy(parts[:, 0, :, :], top))
        chain.link(dve.tensor_tensor(self.rest[:, :, :], top, parts[:, 0, :, :], ALU.subtract))
        chain.link(dve.tensor_copy(parts[:, 1, :, :], self.rest[:, :, :]))
        dve.tensor_tensor(parts[:, 2, :, :], self.rest[:, :, :], parts[:, 1, :, :],
                          ALU.subtract).then_inc(self.parts_ready, 1)

    def dve_turn(self, dve, tail, chain, qt, k):
        a = self.a
        bank = tail.take(dve)
        o = bank[:, :].rearrange("p (u w) -> p u w", w=32)
        chain.link(dve.reciprocal(self.inverse[:, 0:16], o[:, :, a.hd]))
        ins = dve.tensor_tensor(
            self.heads_out[qt][:, 16 * k * a.hd:16 * (k + 1) * a.hd].rearrange("p (u w) -> p u w", w=a.hd), o[:, :, 0:a.hd],
            self.inverse[:, 0:16].unsqueeze(2).broadcast_to([P, 16, a.hd]), ALU.mult)
        tail.emptied(ins)
        if k == a.out_banks - 1:
            tail.settled(dve)
            dve.sem_inc(self.heads_ready, 1)


class WideAttention(Attention):

    def __init__(self, s, nc, a, res, front_links, v_uses, q_uses, q_banks=1, out_bias=None, ghost=None):
        self.s, self.nc, self.a, self.res = s, nc, a, res
        self.front_links, self.v_uses, self.q_uses = front_links, v_uses, q_uses
        self.back_links = (a.n_chunks + QT * a.out_banks * (1 if ghost is None else 2)
                           + QT * (0 if out_bias is None else 2))
        self.out_bias, self.ghost = out_bias, ghost
        self.qT = [s.sb(f"qT{n}", [P, a.pairs, TOK]) for n in range(2)]
        self.k_alone = [s.sb(f"k_alone{n}", [P, a.lone, TOK]) for n in range(2)]
        self.v = [s.sb(f"v{n}", [P, QT, a.heads, a.hd]) for n in range(2)]
        self.row_max, self.shift = s.sb("row_max", [P, QT, a.units]), s.sb("shift", [P, QT, a.units])
        self.total, self.denominator = s.sb("total", [P, QT, a.units]), s.sb("denominator", [P, a.units])
        self.inverse = s.sb("inverse", [P, a.units])
        self.probs = [s.sb(f"probs{n}", [P, 512]) for n in range(2)]
        self.probsT = [s.sb(f"probsT{n}", [P, 512]) for n in range(2)]
        self.heads_out = [s.sb("heads_out", [P, a.width])]
        self.heads_outT = s.sb("heads_outT", [P, a.width // P, P])
        self.w_out = s.sb("w_out", [P, a.width // P, D])
        self.xhat, self.hT, self.scratch = s.sb("xhat", [P, QT, D]), s.sb("hT", [P, TOK]), s.sb("scratch", [P, D])
        self.to_dve = Ring(s, "to_dve", 2)
        self.to_act = Ring(s, "to_act", q_banks) if q_banks else None
        self.scores, self.turned = Ring(s, "scores", 2), Ring(s, "turned", 1)
        self.tail = Ring(s, "tail", 1)
        self.out = [s.bank(f"out{n}") for n in range(a.out_banks)]
        self.xhat_ready, self.hT_ready, self.qkv_ready = s.sem("xhat_ready"), s.sem("hT_ready"), s.sem("qkv_ready")
        self.qT_ready = s.sem("qT_ready") if q_banks else None
        self.shift_ready = s.sem("shift_ready")
        self.probs_free = s.sem("probs_free")
        self.heads_ready, self.headsT_ready = s.sem("heads_ready"), s.sem("headsT_ready")
        self.front_chained, self.back_chained = s.sem("front_chained"), s.sem("back_chained")
        self.started, self.loaded = s.sem("started"), s.sem("loaded")

    @property
    def tail_uses(self):
        return QT * (-(-(self.a.width // P) // 4) + 1)

    def begin_vector(self, dve):
        self.to_dve.start(dve)
        self.tail.start(dve)
        dve.sem_inc(self.heads_ready, 1)
        for k in self.k_alone:
            ins = dve.memset(k[:, :, :], 0.0)
        ins.then_inc(self.started, 1)

    def begin_scalar(self, act):
        self.scores.start(act)
        self.turned.start(act)
        act.sem_inc(self.probs_free, 2)
        if self.to_act:
            self.to_act.start(act)


    def pe_batch(self, pe, steps, project, bt, bo, ft, fo):
        a = self.a
        front = Uses(self.to_dve, ft, fo, self.v_uses)
        to_act = Uses(self.to_act, ft, fo, self.q_uses) if self.to_act else None
        scores, turned = Uses(self.scores, bt, bo, a.n_chunks), Uses(self.turned, bt, bo, a.n_chunks)
        tail = Uses(self.tail, bt, bo, self.tail_uses)
        for half, kind, *at in steps:
            if kind in ("norm", "heads"):
                pass
            elif kind == "hT":
                self.pe_hT(pe, front, ft)
            elif kind == "score":
                self.pe_score(pe, scores, at[0], bt, bo)
            elif kind == "turn":
                self.pe_turn(pe, turned, at[0], bt)
            elif kind == "values":
                self.pe_values(pe, at[0], bt, bo)
            elif kind == "outT":
                self.pe_outT(pe, tail, at[0], bt)
            elif kind == "out":
                self.pe_out(pe, tail, at[0], bt)
            else:
                project(pe, kind, at, front, to_act, ft, fo)
        if ft is not None:
            front.end()
            if to_act:
                to_act.end()
        if bt is not None:
            scores.end()
            turned.end()
            tail.end()

    def pe_score(self, pe, scores, n, turn, odd):
        a = self.a
        qt, u0, nu = a.chunks[n]
        nk = a.keys(qt)
        if n == 0:
            pe.wait_ge(self.qkv_ready, turn + 1)
            if self.qT_ready:
                pe.wait_ge(self.qT_ready, turn + 1)
        bank = scores.fill(pe)
        w = 2 * nk * P
        for i, u in enumerate(range(u0, u0 + nu, 2)):
            mm = pe.matmul(bank[:, i * w:(i + 1) * w].rearrange("p (h k) -> p h k", h=2),
                           self.qT[odd][:, u // 2, qt * P:(qt + 1) * P], self.k_alone[odd][:, u:u + 2, 0:nk * P],
                           start=(i == 0), stop=True, skip_group_check=True)
        for kb in range(nk):
            mask = a.mask(qt, kb)
            if mask is not None:
                out = bank[:, :].rearrange("p (h k) -> p h k", h=nu)[:, :, kb * P:(kb + 1) * P]
                mm = pe.matmul(out, self.res["identb"][:, :],
                               self.res["masks"][:, mask:mask + 1, :].broadcast_to([P, nu, P]),
                               start=False, stop=True, skip_group_check=True)
        scores.filled(mm)

    def pe_turn(self, pe, turned, n, turn):
        pe.wait_ge(self.scores.free, turn * self.a.n_chunks + n + 1 + 2)
        bank = turned.fill(pe)
        for j in range(4):
            mm = pe.transpose(bank[:, j * P:(j + 1) * P], self.probs[n % 2][:, j * P:(j + 1) * P], self.res["ident"][:, :])
        turned.filled(mm)

    def pe_values(self, pe, n, turn, odd):
        a = self.a
        qt, u0, nu = a.chunks[n]
        nk = a.keys(qt)
        pe.wait_ge(self.turned.free, turn * a.n_chunks + n + 1 + 1)
        if u0 == 0:
            pe.wait_ge(self.heads_ready, turn * QT + qt + 1)
        for i in range(nu):
            u = u0 + i
            col = (u % a.per_bank) * a.hd
            for kb in range(nk):
                j = i * nk + kb
                mm = pe.matmul(self.out[u // a.per_bank][:, col:col + a.hd], self.probsT[n % 2][:, j * P:(j + 1) * P],
                               self.v[odd][:, kb, u, :], start=(kb == 0 and u % a.per_bank == 0), stop=(kb == nk - 1),
                               skip_group_check=True)
        mm.then_inc(self.probs_free, 1)


    def act_batch(self, act, steps, project, bt, bo, ft, fo):
        a = self.a
        scores, turned = Uses(self.scores, bt, bo, a.n_chunks), Uses(self.turned, bt, bo, a.n_chunks)
        to_act = Uses(self.to_act, ft, fo, self.q_uses) if self.to_act else None
        for half, kind, *at in steps:
            if kind == "score":
                n, = at
                qt, u0, nu = a.chunks[n]
                w = a.keys(qt) * P
                bank = scores.take(act)
                act.wait_ge(self.shift_ready, bt * a.n_chunks + n + 1)
                for i in range(nu):
                    u = u0 + i
                    ins = self.nc.scalar.activation(self.probs[n % 2][:, i * w:(i + 1) * w], bank[:, i * w:(i + 1) * w],
                                                    ACT.Exp, bias=self.shift[:, qt, u:u + 1], scale=a.scale,
                                                    accum_out=self.total[:, qt, u:u + 1])
                scores.emptied(ins)
            elif kind == "turn":
                n, = at
                bank = turned.take(act)
                act.wait_ge(self.probs_free, bt * a.n_chunks + n + 1)
                turned.emptied(self.nc.scalar.copy(self.probsT[n % 2][:, :], bank[:, :]))
            elif half == "front" and project:
                project(act, kind, at, to_act, ft, fo)


    def dve_batch(self, dve, steps, project, norm, modulate, finish, bt, bo, ft, fo):
        a = self.a
        front, tail = Uses(self.to_dve, ft, fo, self.v_uses), Uses(self.tail, bt, bo, self.tail_uses)
        fchain = Chain(dve, self.front_chained, ft, self.front_links)
        bchain = Chain(dve, self.back_chained, bt, self.back_links)
        for half, kind, *at in steps:
            if kind == "norm":
                norm(dve, fchain, ft)
            elif kind == "hT":
                modulate(dve, front, ft)
            elif kind == "score":
                n, = at
                qt, u0, nu = a.chunks[n]
                dve.wait_ge(self.scores.full, bt * a.n_chunks + n + 1)
                bank = self.scores.banks[n % 2]
                bchain.link(dve.tensor_reduce(self.row_max[:, qt, u0:u0 + nu],
                                              bank[:, :].rearrange("p (h k) -> p h k", h=nu), AX_X, ALU.max))
                dve.tensor_scalar(self.shift[:, qt, u0:u0 + nu], self.row_max[:, qt, u0:u0 + nu], -a.scale, None,
                                  ALU.mult).then_inc(self.shift_ready, 1)
            elif kind in ("turn", "values"):
                pass
            elif kind == "heads":
                self.dve_heads(dve, bchain, at[0], bt)
            elif kind == "outT":
                self.dve_outT(dve, tail)
            elif kind == "out":
                bank = tail.take(dve)
                finish(dve, bchain, tail, bt, at[0], bank)
            else:
                project(dve, kind, at, front, fchain, ft, fo)
        if ft is not None:
            front.end()
            fchain.end()
        if bt is not None:
            tail.end()
            bchain.end()

    def dve_heads(self, dve, chain, qt, turn):
        a = self.a
        done = sum(c[0] <= qt for c in a.chunks)
        dve.wait_ge(self.probs_free, turn * a.n_chunks + done + 2)
        for ob in range(a.out_banks):
            u0, u1 = ob * a.per_bank, min(a.units, (ob + 1) * a.per_bank)
            o = self.out[ob][:, 0:(u1 - u0) * a.hd].rearrange("p (u w) -> p u w", w=a.hd)
            sums = self.total[:, qt, u0:u1]
            if self.ghost is not None:
                chain.link(dve.tensor_tensor(self.denominator[:, u0:u1], sums, self.ghost[:, u0:u1], ALU.add))
                sums = self.denominator[:, u0:u1]
            chain.link(dve.reciprocal(self.inverse[:, u0:u1], sums))
            ins = dve.tensor_tensor(
                self.heads_out[0][:, u0 * a.hd:u1 * a.hd].rearrange("p (u w) -> p u w", w=a.hd), o,
                self.inverse[:, u0:u1].unsqueeze(2).broadcast_to([P, u1 - u0, a.hd]), ALU.mult)
        ins.then_inc(self.heads_ready, 1)


def x_tile(res, n):
    return res["x"][:, bass.ds(n, 1), :].rearrange("p a d -> p (a d)")


def load(sp, loaded, pairs):
    for dst, src in pairs:
        sp.dma_start(dst, src).then_inc(loaded, 16)


def row_of(dram, n=P):
    return dram.unsqueeze(0).broadcast_to([n, dram.shape[0]])


def layer0_attention(nc, dram, res):
    small_head_attention(nc, Attn("a0", 4, 16, 8, "causal", 8 ** -0.5), dram["L0_w"], dram["L0_wo"], None, res)


def layer3_attention(nc, dram, res):
    small_head_attention(nc, Attn("a3", 1, 16, 8, "full", 8 ** -0.5), dram["L3_w"], dram["L3_wo"],
                         dram["L3_attn_b_proj"], res)


def small_head_attention(nc, a, w_dram, wo_dram, bias_dram, res):
    QW, KW = a.units * 8, D
    one_bank = QW + 2 * KW <= 512
    nb = 1 if one_bank else 2
    k_tiles = 16 if a.sets > 1 else 8
    v_uses = 1 + QT * nb + QT * (k_tiles // 8) + a.n_max
    q_uses = QT * a.pairs // 8
    n_loaded = 32 if bias_dram is None else 48
    with ExitStack() as ctx:
        s = Scope(nc, ctx, a.name)
        w = s.sb("w", [P, QW + 2 * KW])
        bias = s.sb("bias", [P, D])
        norm = Norm(s)
        at = NarrowAttention(s, nc, a, res, 2 + 6 + (3 if a.sets > 1 else 2) * QT, QT * a.out_banks + QT * (1 if bias_dram is None else 2), v_uses,
                       q_uses, out_bias=None if bias_dram is None else bias[:, :])
        packed_q = [s.sb(f"packed_q{t}", [P, a.units, 8, 8], BF16) for t in range(QT)]
        packed_k = [s.sb(f"packed_k{t}", [P, a.heads, 8, 8], BF16) for t in range(QT)]
        twice_k = [s.sb(f"twice_k{t}", [P, a.heads, 2, 64], BF16) for t in range(QT)] if a.sets > 1 else None
        rest_q = [s.sb(f"rest_q{t}", [P, a.units, 8]) for t in range(QT)]
        rest_k = s.sb("rest_k", [P, a.heads, 8])
        high_ready, rest_ready, packed_ready = s.sem("high_ready"), s.sem("rest_ready"), s.sem("packed_ready")
        k_packed_ready, middle_ready = s.sem("k_packed_ready"), s.sem("middle_ready")
        project = [(kind, t) for kind in ("qkv", "middle", "pack") for t in range(QT)]
        steps = step_lists(a, project)
        block = s.block()

        @block.sync
        def _(sp):
            load(sp, at.loaded, [(w[:, :], w_dram), (at.w_out[:, :, :], wo_dram.rearrange("(t p) d -> p t d", p=P))])
            if bias_dram is not None:
                load(sp, at.loaded, [(bias[:, :], row_of(bias_dram))])

        @block.tensor
        def _(pe):
            pe.wait_ge(at.loaded, n_loaded)
            pe.wait_ge(at.started, 1)

            def project(pe, kind, where, front, to_act, turn, odd):
                t, = where
                if kind == "middle":
                    return
                if kind == "qkv":
                    if t == 0:
                        pe.wait_ge(at.hT_ready, turn + 1)
                    bank = front.fill(pe)
                    cut = QW + 2 * KW if one_bank else QW
                    front.filled(pe.matmul(bank[:, 0:cut], at.hT[:, t * P:(t + 1) * P], w[:, 0:cut], start=True, stop=True))
                    if not one_bank:
                        bank = front.fill(pe)
                        front.filled(pe.matmul(bank[:, 0:2 * KW], at.hT[:, t * P:(t + 1) * P], w[:, QW:QW + 2 * KW],
                                               start=True, stop=True))
                    return
                pe.wait_ge(k_packed_ready, turn * QT + t + 1)
                for n in range(k_tiles // 8):
                    bank = front.fill(pe)
                    for j in range(8):
                        h = n * 8 + j
                        if a.sets > 1:
                            tile = twice_k[t][:, h, :, :].rearrange("p c x -> p (c x)")
                        else:
                            tile = packed_k[t][:, 2 * h:2 * h + 2, :, :].rearrange("p h s d -> p (h s d)")
                        mm = pe.transpose(bank[:, :].bitcast(BF16)[:, j * P:(j + 1) * P], tile, res["identb"][:, :])
                    front.filled(mm)
                pe.wait_ge(packed_ready, turn * QT + t + 1)
                for n in range(a.pairs // 8):
                    bank = to_act.fill(pe)
                    for j in range(8):
                        g = n * 8 + j
                        mm = pe.transpose(bank[:, :].bitcast(BF16)[:, j * P:(j + 1) * P],
                                          packed_q[t][:, 2 * g:2 * g + 2, :, :].rearrange("p u s d -> p (u s d)"),
                                          res["identb"][:, :])
                    to_act.filled(mm)

            pipelined(pe, lambda bt, bo, ft, fo: at.pe_batch(pe, steps(bt, ft), project, bt, bo, ft, fo))

        @block.scalar
        def _(act):
            at.begin_scalar(act)
            act.wait_ge(at.started, 1)

            def project(act, kind, where, to_act, turn, odd):
                if kind == "qkv":
                    t, = where
                    use = 1 + t * nb
                    act.wait_ge(at.to_dve.full, turn * v_uses + use + 1)
                    bank = at.to_dve.banks[(odd * v_uses + use) % 2]
                    nc.scalar.copy(packed_q[t][:, :, 0:3, :],
                                   bank[:, 0:QW].rearrange("p (u d) -> p u d", d=8).unsqueeze(2)
                                   .broadcast_to([P, a.units, 3, 8])).then_inc(high_ready, 1)
                if kind == "middle":
                    t, = where
                    act.wait_ge(rest_ready, turn * QT + t + 1)
                    nc.scalar.copy(packed_q[t][:, :, 3:5, :], rest_q[t][:, :, :].unsqueeze(2)
                                   .broadcast_to([P, a.units, 2, 8])).then_inc(middle_ready, 1)
                if kind == "pack":
                    t, = where
                    for n in range(a.pairs // 8):
                        bank = to_act.take(act)
                        to_act.emptied(nc.scalar.copy(at.qT[odd][:, 8 * n:8 * n + 8, t * P:(t + 1) * P],
                                                      bank[:, :].bitcast(BF16).rearrange("p (g q) -> p g q", q=P)))
                    if t == QT - 1:
                        to_act.settled(act)
                        act.sem_inc(at.qT_ready, 1)

            pipelined(act, lambda bt, bo, ft, fo: at.act_batch(act, steps(bt, ft), project, bt, bo, ft, fo))

        @block.gpsimd
        def _(pool):
            pool.wait_ge(norm.power_ready, 1)
            pool.wait_ge(at.started, 1)
            with pool.Fori(0, BATCH) as turn:
                norm.gpsimd(pool, turn)
                for t in range(QT):
                    pool.wait_ge(middle_ready, turn * QT + t + 1)
                    pool.tensor_tensor(packed_q[t][:, :, 5, :], rest_q[t][:, :, :], packed_q[t][:, :, 3, :],
                                       ALU.subtract).then_inc(packed_ready, 1)

        @block.vector
        def _(dve):
            norm.start(dve)
            for t in range(QT):
                dve.memset(packed_q[t][:, :, :, :], 0.0)
                dve.memset(packed_k[t][:, :, :, :], 0.0)
            at.begin_vector(dve)
            dve.wait_ge(at.started, 1)

            def project(dve, kind, where, front, chain, turn, odd):
                t, = where
                if kind == "middle":
                    return
                if kind == "qkv":
                    bank = front.take(dve)
                    dve.wait_ge(high_ready, turn * QT + t + 1)
                    ins = dve.tensor_tensor(rest_q[t][:, :, :], bank[:, 0:QW].rearrange("p (u d) -> p u d", d=8),
                                            packed_q[t][:, :, 0, :], ALU.subtract)
                    ins.then_inc(rest_ready, 1)
                    k0 = QW
                    if not one_bank:
                        dve.wait_ge(rest_ready, turn * QT + t + 1)
                        dve.sem_inc(at.to_dve.free, 1)
                        bank, k0 = front.take(dve), 0
                    keys = bank[:, k0:k0 + KW].rearrange("p (h d) -> p h d", d=8)
                    dve.tensor_copy(at.v[odd][:, t, :, 0:8], bank[:, k0 + KW:k0 + 2 * KW].rearrange("p (h d) -> p h d", d=8))
                    odd_slots = packed_k[t][:, :, 0:6, :].rearrange("p h (s two) d -> p h s two d", two=2)[:, :, :, 1, :]
                    even_slots = packed_k[t][:, :, 0:6, :].rearrange("p h (s two) d -> p h s two d", two=2)[:, :, 1:3, 0, :]
                    chain.link(dve.tensor_copy(odd_slots, keys.unsqueeze(2).broadcast_to([P, a.heads, 3, 8])))
                    front.emptied(dve.tensor_tensor(rest_k[:, :, :], keys, packed_k[t][:, :, 1, :], ALU.subtract))
                    front.settled(dve)
                    chain.link(dve.tensor_copy(even_slots, rest_k[:, :, :].unsqueeze(2).broadcast_to([P, a.heads, 2, 8])))
                    ins = dve.tensor_tensor(packed_k[t][:, :, 0, :], rest_k[:, :, :], packed_k[t][:, :, 2, :], ALU.subtract)
                    if a.sets > 1:
                        chain.link(ins)
                        ins = dve.tensor_copy(twice_k[t][:, :, :, :], packed_k[t][:, :, :, :].rearrange("p h s d -> p h (s d)")
                                              .unsqueeze(2).broadcast_to([P, a.heads, 2, 64]))
                    ins.then_inc(k_packed_ready, 1)
                    return
                for n in range(k_tiles // 8):
                    bank = front.take(dve)
                    for half in range(2):
                        r = slice(64 * half, 64 * half + 64)
                        ins = dve.tensor_copy(
                            at.k_alone[odd][r, 16 * n:16 * n + 16, t * P:(t + 1) * P]
                            .rearrange("p (g two) q -> p g two q", two=2)[:, :, half, :],
                            bank[r, :].bitcast(BF16).rearrange("p (g q) -> p g q", q=P))
                    front.emptied(ins)
                if t == QT - 1:
                    front.settled(dve)
                    dve.sem_inc(at.qkv_ready, 1)

            def normalize(dve, chain, turn):
                norm.vector(dve, chain, turn, lambda t: x_tile(res, turn * QT + t), at.xhat, at.xhat_ready)

            pipelined(dve, lambda bt, bo, ft, fo: at.dve_batch(dve, steps(bt, ft), project, normalize, at.dve_hT,
                                                               at.finish_x, bt, bo, ft, fo))


class Turns:

    def __init__(self, b):
        self.b, self.n = b, 0

    def fill(self, pe):
        if self.n >= 2:
            pe.wait_ge(self.b["vbank_read"], self.n - 1)
        self.n += 1
        return self.b["vbank"][(self.n - 1) % 2]

    def full(self, mm):
        mm.then_inc(self.b["vbank_full"], 1)

    def take(self, dve):
        dve.wait_ge(self.b["vbank_full"], self.n + 1)
        self.n += 1
        return self.b["vbank"][(self.n - 1) % 2]

    def read(self, ins):
        ins.then_inc(self.b["vbank_read"], 1)

    def settled(self, dve):
        dve.wait_ge(self.b["vbank_read"], self.n)


def layer1_attention(nc, dram, res):
    a = Attn("a1", 1, 16, 64, "causal", 64 ** -0.5)
    with ExitStack() as ctx:
        s = Scope(nc, ctx, a.name)
        w = s.sb("w", [P, 3 * a.width])
        qk_bias = s.sb("qk_bias", [P, 2 * a.pairs])
        v_bias = s.sb("v_bias", [P, a.heads, a.hd])
        ghost = s.sb("ghost", [P, a.heads])
        bias = s.sb("bias", [P, D])
        norm = Norm(s)
        at = WideAttention(s, nc, a, res, 2, 1 + 2 * a.pairs + 2 * QT, 0, q_banks=0, out_bias=bias[:, :], ghost=ghost)
        project = ([("q", g) for g in range(a.pairs)] + [("k", g) for g in range(a.pairs)]
                   + [("v", t, c) for t in range(QT) for c in range(2)])
        steps = step_lists(a, project)
        n_loaded = 6 * 16
        block = s.block()

        @block.sync
        def _(sp):
            load(sp, at.loaded, [(w[:, :], dram["L1_w"]),
                                 (at.w_out[:, :, :], dram["L1_wo"].rearrange("(t p) d -> p t d", p=P)),
                                 (qk_bias[:, :], dram["L1_qk_bias"]),
                                 (v_bias[:, :, :].rearrange("p h d -> p (h d)"), row_of(dram["L1_v_bias"])),
                                 (ghost[:, :], row_of(dram["L1_ghost"])),
                                 (bias[:, :], row_of(dram["L1_wo_bias"]))])

        @block.tensor
        def _(pe):
            pe.wait_ge(at.loaded, n_loaded)
            pe.wait_ge(at.started, 1)

            def project(pe, kind, where, front, to_act, turn, odd):
                if kind == "v":
                    t, c = where
                    bank = front.fill(pe)
                    front.filled(pe.matmul(bank[:, :], at.hT[:, t * P:(t + 1) * P],
                                           w[:, 2 * a.width + 512 * c:2 * a.width + 512 * (c + 1)], start=True, stop=True))
                    return
                n = where[0] + (a.pairs if kind == "k" else 0)
                if n == 0:
                    pe.wait_ge(at.hT_ready, turn + 1)
                bank = front.fill(pe)
                front.filled(pe.matmul(bank[:, 0:TOK], w[:, n * P:(n + 1) * P], at.hT[:, :], start=True, stop=True))

            pipelined(pe, lambda bt, bo, ft, fo: at.pe_batch(pe, steps(bt, ft), project, bt, bo, ft, fo))

        @block.scalar
        def _(act):
            at.begin_scalar(act)
            pipelined(act, lambda bt, bo, ft, fo: at.act_batch(act, steps(bt, ft), None, bt, bo, ft, fo))

        @block.gpsimd
        def _(pool):
            pool.wait_ge(norm.power_ready, 1)
            with pool.Fori(0, BATCH) as turn:
                norm.gpsimd(pool, turn)

        @block.vector
        def _(dve):
            norm.start(dve)
            at.begin_vector(dve)
            dve.wait_ge(at.started, 1)

            def project(dve, kind, where, front, chain, turn, odd):
                bank = front.take(dve)
                if kind == "q":
                    g, = where
                    ins = dve.tensor_scalar(at.qT[odd][:, g, :], bank[:, 0:TOK], qk_bias[:, g:g + 1], None, ALU.add)
                elif kind == "k":
                    g, = where
                    for half in range(2):
                        r = slice(64 * half, 64 * half + 64)
                        ins = dve.tensor_scalar(at.k_alone[odd][r, 2 * g + half, :], bank[r, 0:TOK],
                                                qk_bias[r, a.pairs + g:a.pairs + g + 1], None, ALU.add)
                else:
                    t, c = where
                    ins = dve.tensor_tensor(at.v[odd][:, t, 8 * c:8 * c + 8, 0:a.hd],
                                            bank[:, :].rearrange("p (h d) -> p h d", d=a.hd),
                                            v_bias[:, 8 * c:8 * c + 8, :], ALU.add)
                front.emptied(ins)
                if kind == "v" and (t, c) == (QT - 1, 1):
                    front.settled(dve)
                    dve.sem_inc(at.qkv_ready, 1)

            def normalize(dve, chain, turn):
                norm.vector(dve, chain, turn, lambda t: x_tile(res, turn * QT + t), at.xhat, at.xhat_ready)

            pipelined(dve, lambda bt, bo, ft, fo: at.dve_batch(dve, steps(bt, ft), project, normalize, at.dve_hT,
                                                               at.finish_x, bt, bo, ft, fo))


def layer2_attention(nc, dram, res):
    scale = float(D) ** -0.5
    with ExitStack() as ctx:
        s = Scope(nc, ctx, "a2")
        w, wo = s.sb("w", [P, 3 * D]), s.sb("wo", [P, D])
        qk_bias, v_bias, bias = s.sb("qk_bias", [P, 2]), s.sb("v_bias", [P, D]), s.sb("bias", [P, D])
        qkT = [s.sb(f"qkT{n}", [P, 2, TOK]) for n in range(2)]
        v = [s.sb(f"v{n}", [P, QT, D]) for n in range(2)]
        sizes = [s.sb(f"sizes{n}", [P, TOK]) for n in range(QT)]
        top, shift = s.sb("top", [P, QT]), s.sb("shift", [P, QT])
        total, inverse = s.sb("total", [P, QT]), s.sb("inverse", [P, QT])
        BLOCKS = QT * (QT + 1) // 2
        probs, probsT = s.sb("probs", [P, BLOCKS * P]), s.sb("probsT", [P, BLOCKS * P])
        mixed, mixedT = s.sb("mixed", [P, QT, D]), s.sb("mixedT", [P, TOK])
        scratch = s.sb("scratch", [P, QT, D])
        fronts, scores, turned, outs = Ring(s, "fronts", 2), Ring(s, "scores", 2), Ring(s, "turned", 1), Ring(s, "outs", 1)
        m = Modulated(s, nc, res, 0, fronts)
        loaded, front_chained, back_chained, qkv_ready, shift_ready, probs_ready, mixed_ready = (s.sem(name) for name in (
            "loaded", "front_chained", "back_chained", "qkv_ready", "shift_ready", "probs_ready", "mixed_ready"))
        front = [("norm",), ("hT",), ("qk",), ("v",)]
        back = [("scores", 0), ("scores", 1), ("max", 0), ("max", 1), ("probsT",), ("mix",), ("mixedT",), ("out",)]
        block = s.block()

        def block_of(qt, kb):
            n = qt * (qt + 1) // 2 + kb
            return slice(n * P, (n + 1) * P)

        @block.sync
        def _(sp):
            load(sp, loaded, [(w[:, :], dram["L2_w"]), (wo[:, :], dram["L2_wo"]), (qk_bias[:, :], dram["L2_qk_bias"]),
                              (v_bias[:, :], row_of(dram["L2_v_bias"])), (bias[:, :], row_of(dram["L2_wo_bias"]))])

        @block.tensor
        def _(pe):
            pe.wait_ge(loaded, 5 * 16)

            def go(steps, bt, bo, ft, fo):
                front, score, turn, out = (Uses(fronts, ft, fo, 3), Uses(scores, bt, bo, QT), Uses(turned, bt, bo, 2),
                                           Uses(outs, bt, bo, 2))
                for half, kind, *at in steps:
                    m.pe(pe, kind, front, ft)
                    if kind == "qk":
                        pe.wait_ge(m.hT_ready, ft + 1)
                        bank = front.fill(pe)
                        for n in range(2):
                            mm = pe.matmul(bank[:, n * TOK:(n + 1) * TOK], w[:, n * P:(n + 1) * P], m.hT[fo][:, :],
                                           start=(n == 0), stop=True, skip_group_check=True)
                        front.filled(mm)
                    elif kind == "v":
                        bank = front.fill(pe)
                        for t in range(QT):
                            mm = pe.matmul(bank[:, t * D:(t + 1) * D], m.hT[fo][:, t * P:(t + 1) * P], w[:, 2 * P:3 * P],
                                           start=(t == 0), stop=True, skip_group_check=True)
                        front.filled(mm)
                    elif kind == "scores":
                        qt, = at
                        pe.wait_ge(qkv_ready, bt + 1)
                        bank = score.fill(pe)
                        score.filled(pe.matmul(bank[:, 0:(qt + 1) * P], qkT[bo][:, 0, qt * P:(qt + 1) * P],
                                               qkT[bo][:, 1, 0:(qt + 1) * P], start=True, stop=True))
                    elif kind == "probsT":
                        pe.wait_ge(probs_ready, bt * QT + QT)
                        bank = turn.fill(pe)
                        for n in range(BLOCKS):
                            mm = pe.transpose(bank[:, n * P:(n + 1) * P], probs[:, n * P:(n + 1) * P], res["ident"][:, :])
                        turn.filled(mm)
                    elif kind == "mix":
                        pe.wait_ge(turned.free, bt * 2 + 1 + 1)
                        bank = out.fill(pe)
                        for qt in range(QT):
                            for kb in range(qt + 1):
                                mm = pe.matmul(bank[:, qt * D:(qt + 1) * D], probsT[:, block_of(qt, kb)], v[bo][:, kb, :],
                                               start=(qt == 0), stop=(kb == qt), skip_group_check=True)
                        out.filled(mm)
                    elif kind == "mixedT":
                        pe.wait_ge(mixed_ready, bt + 1)
                        bank = turn.fill(pe)
                        for qt in range(QT):
                            mm = pe.transpose(bank[:, qt * P:(qt + 1) * P], mixed[:, qt, :], res["ident"][:, :])
                        turn.filled(mm)
                    elif kind == "out":
                        pe.wait_ge(turned.free, bt * 2 + 2 + 1)
                        bank = out.fill(pe)
                        for qt in range(QT):
                            mm = pe.matmul(bank[:, qt * D:(qt + 1) * D], mixedT[:, qt * P:(qt + 1) * P], wo[:, :],
                                           start=(qt == 0), stop=True, skip_group_check=True)
                        out.filled(mm)

            walk(pe, WEIGHTS["a2"], front, back, go)

        @block.scalar
        def _(act):
            scores.start(act)
            turned.start(act)

            def go(steps, bt, bo, ft, fo):
                score, turn = Uses(scores, bt, bo, QT), Uses(turned, bt, bo, 2)
                for half, kind, *at in steps:
                    if kind == "scores":
                        qt, = at
                        bank = score.take(act)
                        score.emptied(nc.scalar.activation(sizes[qt][:, 0:(qt + 1) * P], bank[:, 0:(qt + 1) * P], ACT.Abs))
                    elif kind == "max":
                        qt, = at
                        act.wait_ge(shift_ready, bt * QT + qt + 1)
                        first = block_of(qt, 0).start
                        nc.scalar.activation(probs[:, first:first + (qt + 1) * P], sizes[qt][:, 0:(qt + 1) * P], ACT.Exp,
                                             bias=shift[:, qt:qt + 1], scale=scale,
                                             accum_out=total[:, qt:qt + 1]).then_inc(probs_ready, 1)
                    elif kind == "probsT":
                        bank = turn.take(act)
                        turn.emptied(nc.scalar.copy(probsT[:, :], bank[:, 0:BLOCKS * P]))
                    elif kind == "mixedT":
                        bank = turn.take(act)
                        turn.emptied(nc.scalar.copy(mixedT[:, :], bank[:, 0:TOK]))

            walk(act, WEIGHTS["a2"], front, back, go)

        @block.gpsimd
        def _(pool):
            pool.wait_ge(m.norm.power_ready, 1)
            with pool.Fori(0, BATCH) as turn:
                m.norm.gpsimd(pool, turn)

        @block.vector
        def _(dve):
            m.norm.start(dve)
            fronts.start(dve)
            outs.start(dve)

            def go(steps, bt, bo, ft, fo):
                front, out = Uses(fronts, ft, fo, 3), Uses(outs, bt, bo, 2)
                chain, back_chain = Chain(dve, front_chained, ft, m.LINKS), Chain(dve, back_chained, bt, 2 * QT + 1 + 2)
                for half, kind, *at in steps:
                    m.dve(dve, kind, front, chain, ft, fo)
                    if kind == "qk":
                        bank = front.take(dve)
                        for n in range(2):
                            ins = dve.tensor_scalar(qkT[fo][:, n, :], bank[:, n * TOK:(n + 1) * TOK], qk_bias[:, n:n + 1], None,
                                                    ALU.add)
                        front.emptied(ins)
                    elif kind == "v":
                        bank = front.take(dve)
                        front.emptied(dve.tensor_tensor(v[fo][:, :, :], bank[:, 0:QT * D].rearrange("p (t d) -> p t d", d=D),
                                                        v_bias[:, :].unsqueeze(1).broadcast_to([P, QT, D]), ALU.add))
                        front.settled(dve)
                        dve.sem_inc(qkv_ready, 1)
                    elif kind == "max":
                        qt, = at
                        dve.wait_ge(scores.free, bt * QT + qt + 1 + 2)
                        diagonal = sizes[qt][:, qt * P:(qt + 1) * P]
                        back_chain.link(dve.tensor_tensor(diagonal, diagonal, res["masks"][:, 0, :], ALU.add))
                        back_chain.link(dve.tensor_reduce(top[:, qt:qt + 1], sizes[qt][:, 0:(qt + 1) * P], AX_X, ALU.max))
                        dve.tensor_scalar(shift[:, qt:qt + 1], top[:, qt:qt + 1], -scale, None,
                                          ALU.mult).then_inc(shift_ready, 1)
                    elif kind == "mix":
                        bank = out.take(dve)
                        back_chain.link(dve.reciprocal(inverse[:, :], total[:, :]))
                        out.emptied(dve.tensor_tensor(mixed[:, :, :], bank[:, 0:QT * D].rearrange("p (t d) -> p t d", d=D),
                                                      inverse[:, :].unsqueeze(2).broadcast_to([P, QT, D]), ALU.mult))
                        out.settled(dve)
                        dve.sem_inc(mixed_ready, 1)
                    elif kind == "out":
                        bank = out.take(dve)
                        out.emptied(dve.tensor_tensor(scratch[:, :, :], bank[:, 0:QT * D].rearrange("p (t d) -> p t d", d=D),
                                                      bias[:, :].unsqueeze(1).broadcast_to([P, QT, D]), ALU.add))
                        out.settled(dve)
                        add_gated(dve, res, back_chain, bt, scratch[:, :, :], scratch, gate=0)

            walk(dve, WEIGHTS["a2"], front, back, go)


class Quant:

    BLOCK = 16

    def __init__(self, s, name, cols, work=None):
        nb = cols // self.BLOCK
        self.work = work or {
            "top": s.sb(name + "_top", [P, nb]), "inverse": s.sb(name + "_inverse", [P, nb]), "scale": s.sb(name + "_scale", [P, nb]),
            "unit": s.sb(name + "_unit", [P, cols]), "size": s.sb(name + "_size", [P, cols]), "sign": s.sb(name + "_sign", [P, cols]),
            "level": s.sb(name + "_level", [P, cols]), "past": s.sb(name + "_past", [P, cols])}
        self.top_ready, self.divided, self.parted = (s.sem(f"{name}_{x}") for x in ("top_ready", "divided", "parted"))

    def vector(self, dve, chain, src, dst, cols, n):
        self.vector_scale(dve, chain, src, cols)
        return self.vector_levels(dve, chain, dst, cols, n)

    def vector_scale(self, dve, chain, src, cols):
        w = self.work
        nb = cols // self.BLOCK
        chain.link(dve.tensor_reduce(w["top"][:, 0:nb], src.rearrange("p (b k) -> p b k", k=self.BLOCK), AX_X,
                                     ALU.max, apply_absolute_value=True))
        chain.link(dve.tensor_scalar(w["scale"][:, 0:nb], w["top"][:, 0:nb], 1.0 / 6.0, 1e-12, ALU.mult, ALU.max))
        dve.reciprocal(w["inverse"][:, 0:nb], w["scale"][:, 0:nb]).then_inc(self.top_ready, 1)

    def vector_levels(self, dve, chain, dst, cols, n):
        w = self.work
        nb = cols // self.BLOCK
        dve.wait_ge(self.parted, n)
        size, level, past = w["size"][:, 0:cols], w["level"][:, 0:cols], w["past"][:, 0:cols]

        def passed(mid):
            chain.link(dve.scalar_tensor_tensor(out=level, in0=size, scalar=mid, in1=level, op0=ALU.is_gt, op1=ALU.add))

        dve.tensor_scalar(past, size, 1.75, None, ALU.is_gt)
        chain.link(dve.tensor_scalar(level, size, 5.0, 2.0, ALU.is_gt, ALU.mult))
        passed(3.5)
        passed(2.5)
        chain.link(dve.scalar_tensor_tensor(out=level, in0=level, scalar=2.0, in1=past, op0=ALU.mult, op1=ALU.add))
        passed(1.25)
        passed(0.75)
        passed(0.25)
        chain.link(dve.scalar_tensor_tensor(out=level, in0=level, scalar=0.5, in1=w["sign"][:, 0:cols],
                                            op0=ALU.mult, op1=ALU.mult))
        return dve.tensor_tensor(dst.rearrange("p (b k) -> p b k", k=self.BLOCK),
                                 level.rearrange("p (b k) -> p b k", k=self.BLOCK),
                                 w["scale"][:, 0:nb].unsqueeze(2).broadcast_to([P, nb, self.BLOCK]), ALU.mult)

    LINKS = 10

    def gpsimd(self, pool, src, cols, n):
        w = self.work
        nb = cols // self.BLOCK
        pool.wait_ge(self.top_ready, n)
        pool.tensor_tensor(w["unit"][:, 0:cols].rearrange("p (b k) -> p b k", k=self.BLOCK),
                           src.rearrange("p (b k) -> p b k", k=self.BLOCK),
                           w["inverse"][:, 0:nb].unsqueeze(2).broadcast_to([P, nb, self.BLOCK]),
                           ALU.mult).then_inc(self.divided, 1)

    def scalar(self, act, nc, cols, n):
        w = self.work
        act.wait_ge(self.divided, n)
        nc.scalar.activation(w["size"][:, 0:cols], w["unit"][:, 0:cols], ACT.Abs)
        nc.scalar.activation(w["sign"][:, 0:cols], w["unit"][:, 0:cols], ACT.Sign).then_inc(self.parted, 1)


def layer1_ffn(nc, dram, res):
    I = 352
    parts = [(0, P), (P, P), (2 * P, I - 2 * P)]
    with ExitStack() as ctx:
        s = Scope(nc, ctx, "f1")
        raw = [s.sb("raw_gate", [P, 3, D]), s.sb("raw_up", [P, 3, D]), s.sb("raw_down", [P, I])]
        quantized = s.sb("quantized", [P, 3 * D])
        w_in = s.sb("w_in", [P, 2, I])
        w_down = s.sb("w_down", [P, 3, D])
        h, hq = s.sb("h", [P, TOK]), s.sb("hq", [P, TOK])
        hqT = [s.sb(f"hqT{n}", [P, TOK]) for n in range(2)]
        tanh, gated = s.sb("tanh", [P, QT, I]), s.sb("gated", [P, QT, I])
        hidden, hiddenq = s.sb("hidden", [P, QT, I]), s.sb("hiddenq", [P, QT, I])
        hiddenT = s.sb("hiddenT", [P, QT, 3, P])
        scratch = s.sb("scratch", [P, QT, D])
        quant_h, quant_hidden = Quant(s, "qh", TOK), [Quant(s, f"qi{t}", I) for t in range(QT)]
        quant_w = Quant(s, "qw", 3 * D)
        fronts, front_copies, back_copies, outs = (Ring(s, name, 1) for name in ("fronts", "front_copies", "back_copies", "outs"))
        gates, ups = Ring(s, "gates", 2), Ring(s, "ups", 2)
        m = Modulated(s, nc, res, 2, fronts)
        loaded, started, front_chained, back_chained, tanh_ready, hq_ready, hiddenq_ready = (
            s.sem(name) for name in ("loaded", "started", "front_chained", "back_chained", "tanh_ready",
                                     "hq_ready", "hiddenq_ready"))
        b0 = {"vbank": [fronts.banks[0], outs.banks[0]]}
        for name in ("vbank_full", "vbank_read", "chained", "quantized_ready"):
            b0[name] = s.sem("w_" + name)
        front = [("norm",), ("hT",), ("by_token",), ("h_scale",), ("h_levels",), ("hqT",)]
        back = [("in", 0), ("in", 1), ("hidden", 0), ("scale", 0), ("hidden", 1), ("scale", 1), ("levels", 0), ("hiddenT", 0),
                ("levels", 1), ("hiddenT", 1), ("out",), ("finish",)]
        block = s.block()

        @block.sync
        def _(sp):
            sp.wait_ge(started, 1)
            for dst, src in ((raw[0], dram["L1_ffn_w_gate"]), (raw[1], dram["L1_ffn_w_up"])):
                load(sp, loaded, [(dst[:, 0:2, :], src[0:2 * P, :].rearrange("(t p) d -> p t d", p=P)),
                                  (dst[0:I - 2 * P, 2, :], src[2 * P:I, :])])
            load(sp, loaded, [(raw[2][:, :], dram["L1_ffn_w_down"])])

        weights = [(raw[0][:, :, :].rearrange("p t d -> p (t d)"), 3 * D),
                   (raw[1][:, :, :].rearrange("p t d -> p (t d)"), 3 * D), (raw[2][:, :], I)]

        @block.tensor
        def _(pe):
            turns = Turns(b0)
            for n in range(3):
                pe.wait_ge(b0["quantized_ready"], n + 1)
                bank = turns.fill(pe)
                for t, (r0, rows) in enumerate(parts):
                    if n < 2:
                        mm = pe.transpose(bank[:, r0:r0 + rows], quantized[0:rows, t * D:(t + 1) * D],
                                          res["ident"][0:rows, 0:rows])
                    else:
                        mm = pe.transpose(bank[0:rows, t * P:(t + 1) * P], quantized[:, r0:r0 + rows], res["ident"][:, :])
                turns.full(mm)

            def go(steps, bt, bo, ft, fo):
                front, copies = Uses(fronts, ft, fo, 1), Uses(front_copies, ft, fo, 2)
                gate_in, up_in = Uses(gates, bt, bo, QT), Uses(ups, bt, bo, QT)
                back, out = Uses(back_copies, bt, bo, QT), Uses(outs, bt, bo, 1)
                for half, kind, *at in steps:
                    m.pe(pe, kind, front, ft)
                    if kind == "by_token":
                        pe.wait_ge(m.hT_ready, ft + 1)
                        bank = copies.fill(pe)
                        for t in range(QT):
                            mm = pe.transpose(bank[:, t * P:(t + 1) * P], m.hT[fo][:, t * P:(t + 1) * P], res["ident"][:, :])
                        copies.filled(mm)
                    elif kind == "hqT":
                        pe.wait_ge(hq_ready, ft + 1)
                        bank = copies.fill(pe)
                        for t in range(QT):
                            mm = pe.transpose(bank[:, t * P:(t + 1) * P], hq[:, t * P:(t + 1) * P], res["ident"][:, :])
                        copies.filled(mm)
                    elif kind == "in":
                        t, = at
                        pe.wait_ge(front_copies.free, bt * 2 + 2 + 1)
                        for n, ring in enumerate((gate_in, up_in)):
                            bank = ring.fill(pe)
                            ring.filled(pe.matmul(bank[:, 0:I], hqT[bo][:, t * P:(t + 1) * P], w_in[:, n, :],
                                                  start=True, stop=True))
                    elif kind == "hiddenT":
                        t, = at
                        pe.wait_ge(hiddenq_ready, bt * QT + t + 1)
                        bank = back.fill(pe)
                        for c, (r0, rows) in enumerate(parts):
                            mm = pe.transpose(bank[0:rows, c * P:(c + 1) * P], hiddenq[:, t, r0:r0 + rows], res["ident"][:, :])
                        back.filled(mm)
                    elif kind == "out":
                        pe.wait_ge(back_copies.free, bt * QT + QT + 1)
                        bank = out.fill(pe)
                        for t in range(QT):
                            for c in range(3):
                                mm = pe.matmul(bank[:, t * P:(t + 1) * P], hiddenT[:, t, c, :], w_down[:, c, :],
                                               start=(t == 0 and c == 0), stop=(c == 2), skip_group_check=True)
                        out.filled(mm)

            walk(pe, WEIGHTS["f1"], front, back, go)

        @block.scalar
        def _(act):
            for n in range(3):
                quant_w.scalar(act, nc, weights[n][1], n + 1)
            for ring in (front_copies, back_copies):
                ring.start(act)

            def go(steps, bt, bo, ft, fo):
                copies, back = Uses(front_copies, ft, fo, 2), Uses(back_copies, bt, bo, QT)
                for half, kind, *at in steps:
                    if kind == "by_token":
                        bank = copies.take(act)
                        copies.emptied(nc.scalar.copy(h[:, :], bank[:, 0:TOK]))
                    elif kind == "h_scale":
                        quant_h.scalar(act, nc, TOK, ft + 1)
                    elif kind == "hqT":
                        bank = copies.take(act)
                        copies.emptied(nc.scalar.copy(hqT[fo][:, :], bank[:, 0:TOK]))
                    elif kind == "hidden":
                        t, = at
                        act.wait_ge(gates.full, bt * QT + t + 1)
                        nc.scalar.activation(tanh[:, t, :], gates.banks[t][:, 0:I], ACT.Tanh, scale=0.5).then_inc(tanh_ready, 1)
                    elif kind == "scale":
                        quant_hidden[at[0]].scalar(act, nc, I, bt + 1)
                    elif kind == "hiddenT":
                        t, = at
                        bank = back.take(act)
                        nc.scalar.copy(hiddenT[:, t, 0:2, :].rearrange("p c q -> p (c q)"), bank[:, 0:2 * P])
                        back.emptied(nc.scalar.copy(hiddenT[0:I - 2 * P, t, 2, :], bank[0:I - 2 * P, 2 * P:3 * P]))

            walk(act, WEIGHTS["f1"], front, back, go)

        @block.gpsimd
        def _(pool):
            pool.wait_ge(m.norm.power_ready, 1)
            for n in range(3):
                quant_w.gpsimd(pool, weights[n][0], weights[n][1], n + 1)

            def go(steps, bt, bo, ft, fo):
                for half, kind, *at in steps:
                    m.gpsimd(pool, kind, ft)
                    if kind == "h_scale":
                        quant_h.gpsimd(pool, h[:, :], TOK, ft + 1)
                    elif kind == "scale":
                        quant_hidden[at[0]].gpsimd(pool, hidden[:, at[0], :], I, bt + 1)

            walk(pool, WEIGHTS["f1"], front, back, go)

        @block.vector
        def _(dve):
            dve.memset(raw[0][:, :, :], 0.0)
            dve.memset(hiddenT[:, :, 2, :], 0.0)
            dve.memset(w_down[:, 2, :], 0.0)
            m.norm.start(dve)
            dve.memset(raw[1][:, :, :], 0.0).then_inc(started, 1)
            dve.wait_ge(loaded, 5 * 16)
            turns = Turns(b0)
            chain = Chain(dve, b0["chained"], 0, 0)
            for n in range(3):
                src, cols = weights[n]
                if n:
                    turns.settled(dve)
                quant_w.vector(dve, chain, src, quantized[:, 0:cols], cols, n + 1).then_inc(b0["quantized_ready"], 1)
                bank = turns.take(dve)
                if n < 2:
                    ins = dve.tensor_copy(w_in[:, n, :], bank[:, 0:I])
                else:
                    dve.tensor_copy(w_down[:, 0:2, :].rearrange("p t d -> p (t d)"), bank[:, 0:2 * P])
                    ins = dve.tensor_copy(w_down[0:I - 2 * P, 2, :], bank[0:I - 2 * P, 2 * P:3 * P])
                turns.read(ins)
            turns.settled(dve)
            for ring in (fronts, gates, ups, outs):
                ring.start(dve)

            def go(steps, bt, bo, ft, fo):
                front = Uses(fronts, ft, fo, 1)
                gate_in, up_in, out = Uses(gates, bt, bo, QT), Uses(ups, bt, bo, QT), Uses(outs, bt, bo, 1)
                chain = Chain(dve, front_chained, ft, m.LINKS + Quant.LINKS)
                back_chain = Chain(dve, back_chained, bt, QT * Quant.LINKS + 1)
                for half, kind, *at in steps:
                    m.dve(dve, kind, front, chain, ft, fo)
                    if kind == "h_scale":
                        dve.wait_ge(front_copies.free, ft * 2 + 1 + 1)
                        quant_h.vector_scale(dve, chain, h[:, :], TOK)
                    elif kind == "h_levels":
                        quant_h.vector_levels(dve, chain, hq[:, :], TOK, ft + 1).then_inc(hq_ready, 1)
                    elif kind == "hidden":
                        t, = at
                        bank = gate_in.take(dve)
                        dve.wait_ge(tanh_ready, bt * QT + t + 1)
                        gate_in.emptied(dve.scalar_tensor_tensor(out=gated[:, t, :], in0=tanh[:, t, :], scalar=1.0,
                                                                 in1=bank[:, 0:I], op0=ALU.add, op1=ALU.mult))
                        gate_in.settled(dve)
                        bank = up_in.take(dve)
                        ins = dve.tensor_tensor(hidden[:, t, :], bank[:, 0:I], gated[:, t, :], ALU.mult)
                        up_in.emptied(ins)
                        up_in.settled(dve)
                    elif kind == "scale":
                        quant_hidden[at[0]].vector_scale(dve, back_chain, hidden[:, at[0], :], I)
                    elif kind == "levels":
                        t, = at
                        quant_hidden[t].vector_levels(dve, back_chain, hiddenq[:, t, :], I, bt + 1).then_inc(hiddenq_ready, 1)
                    elif kind == "out":
                        bank = out.take(dve)
                        g = res["gate"][:, 1, bass.ds(bt, 1), :].rearrange("p a d -> p (a d)")
                        for t in range(QT):
                            ins = dve.scalar_tensor_tensor(out=scratch[:, t, :], in0=bank[:, t * P:(t + 1) * P], scalar=0.5,
                                                           in1=g, op0=ALU.mult, op1=ALU.mult)
                        out.emptied(ins)
                        out.settled(dve)
                    elif kind == "finish":
                        x = res["x"][:, bass.ds(bt * QT, QT), :]
                        back_chain.link(dve.tensor_tensor(x, x, scratch[:, :, :], ALU.add))

            walk(dve, WEIGHTS["f1"], front, back, go)


def layer3_ffn(nc, dram, res):
    E, ES, K = 16, 32, 4
    NX = E + 8 - K
    with ExitStack() as ctx:
        s = Scope(nc, ctx, "f3")
        sel, keys, values = s.sb("sel", [P, E]), s.sb("keys", [P, E * ES]), s.sb("values", [P, 4, D])
        route_scale = s.sb("route_scale", [P, 1])
        negexp, plus = s.sb("negexp", [P, QT, E]), s.sb("plus", [P, QT, E])
        probs = s.sb("probs", [P, QT, NX])
        best, left = s.sb("best", [P, QT, 8]), s.sb("left", [P, QT, NX])
        kept, chosen = s.sb("kept", [P, QT, E]), s.sb("chosen", [P, QT, E])
        total, inverse = s.sb("total", [P, QT]), s.sb("inverse", [P, QT])
        weight = [s.sb(f"weight{n}", [P, QT, E]) for n in range(2)]
        scores, scoresT = s.sb("scores", [P, QT, E * ES]), s.sb("scoresT", [P, QT, 512])
        scratch = s.sb("scratch", [P, QT, D])
        fronts, logits, experts, turned, outs = (Ring(s, name, n) for name, n in (
            ("fronts", 1), ("logits", 1), ("experts", 2), ("turned", 2), ("outs", 1)))
        m = Modulated(s, nc, res, 2, fronts)
        loaded, front_chained, back_chained = s.sem("loaded"), s.sem("front_chained"), s.sem("back_chained")
        FILL = 3.0e38
        front = [("norm",), ("hT",), ("logits",), ("places",), ("weight",)]
        back = [("experts", 0), ("experts", 1), ("turn", 0), ("turn", 1), ("out",)]
        block = s.block()

        @block.sync
        def _(sp):
            load(sp, loaded, [(sel[:, :], dram["L3_sel"]), (keys[:, :], dram["L3_keys"]),
                              (values[:, :, :], dram["L3_values"].rearrange("(t p) d -> p t d", p=P)),
                              (route_scale[:, :], row_of(dram["L3_ffn_route_scale"]))])

        @block.tensor
        def _(pe):
            pe.wait_ge(loaded, 64)

            def go(steps, bt, bo, ft, fo):
                front, logit = Uses(fronts, ft, fo, 1), Uses(logits, ft, fo, 1)
                expert, turn, out = Uses(experts, bt, bo, QT), Uses(turned, bt, bo, QT), Uses(outs, bt, bo, 1)
                for half, kind, *at in steps:
                    m.pe(pe, kind, front, ft)
                    if kind == "logits":
                        pe.wait_ge(m.hT_ready, ft + 1)
                        bank = logit.fill(pe)
                        for t in range(QT):
                            mm = pe.matmul(bank[:, t * E:(t + 1) * E], m.hT[fo][:, t * P:(t + 1) * P], sel[:, :],
                                           start=(t == 0), stop=True, skip_group_check=True)
                        logit.filled(mm)
                    elif kind == "experts":
                        t, = at
                        bank = expert.fill(pe)
                        expert.filled(pe.matmul(bank[:, :], m.hT[bo][:, t * P:(t + 1) * P], keys[:, :], start=True, stop=True))
                    elif kind == "turn":
                        t, = at
                        pe.wait_ge(experts.free, bt * QT + t + 1 + 2)
                        bank = turn.fill(pe)
                        for c in range(4):
                            mm = pe.transpose(bank[:, c * P:(c + 1) * P], scores[:, t, c * P:(c + 1) * P], res["ident"][:, :])
                        turn.filled(mm)
                    elif kind == "out":
                        bank = out.fill(pe)
                        for t in range(QT):
                            pe.wait_ge(turned.free, bt * QT + t + 1 + 2)
                            for c in range(4):
                                mm = pe.matmul(bank[:, t * D:(t + 1) * D], scoresT[:, t, c * P:(c + 1) * P], values[:, c, :],
                                               start=(t == 0 and c == 0), stop=(c == 3), skip_group_check=True)
                        out.filled(mm)

            walk(pe, WEIGHTS["f3"], front, back, go)

        @block.scalar
        def _(act):
            logits.start(act)
            turned.start(act)

            def go(steps, bt, bo, ft, fo):
                logit, turn = Uses(logits, ft, fo, 1), Uses(turned, bt, bo, QT)
                for half, kind, *at in steps:
                    if kind == "logits":
                        bank = logit.take(act)
                        logit.emptied(nc.scalar.activation(negexp[:, :, :].rearrange("p t e -> p (t e)"), bank[:, 0:QT * E],
                                                           ACT.Exp, scale=-1.0))
                    elif kind == "turn":
                        t, = at
                        bank = turn.take(act)
                        turn.emptied(nc.scalar.copy(scoresT[:, t, :], bank[:, :]))

            walk(act, WEIGHTS["f3"], front, back, go)

        @block.gpsimd
        def _(pool):
            pool.wait_ge(m.norm.power_ready, 1)
            with pool.Fori(0, BATCH) as turn:
                m.norm.gpsimd(pool, turn)

        @block.vector
        def _(dve):
            m.norm.start(dve)
            for ring in (fronts, experts, outs):
                ring.start(dve)
            dve.memset(probs[:, :, :], FILL)
            dve.wait_ge(m.norm.power_ready, 1)

            def go(steps, bt, bo, ft, fo):
                front, expert, out = Uses(fronts, ft, fo, 1), Uses(experts, bt, bo, QT), Uses(outs, bt, bo, 1)
                chain, back_chain = Chain(dve, front_chained, ft, m.LINKS + 12), Chain(dve, back_chained, bt, 1)
                for half, kind, *at in steps:
                    m.dve(dve, kind, front, chain, ft, fo)
                    if kind == "places":
                        dve.wait_ge(logits.free, ft + 1 + 1)
                        chain.link(dve.tensor_scalar(plus[:, :, :], negexp[:, :, :], 1.0, None, ALU.add))
                        chain.link(dve.reciprocal(probs[:, :, 0:E], plus[:, :, :]))
                        top_places(dve, chain, m.norm, probs, best, left, E, K, FILL)
                    elif kind == "weight":
                        chain.link(dve.tensor_tensor(chosen[:, :, :], probs[:, :, 0:E], left[:, :, 0:E], ALU.not_equal))
                        chain.link(dve.tensor_tensor(kept[:, :, :], probs[:, :, 0:E], chosen[:, :, :], ALU.mult))
                        chain.link(dve.tensor_reduce(total[:, :], kept[:, :, :], AX_X, ALU.add))
                        chain.link(dve.tensor_scalar(total[:, :], total[:, :], 1e-9, None, ALU.max))
                        chain.link(dve.reciprocal(inverse[:, :], total[:, :]))
                        chain.link(dve.tensor_scalar(inverse[:, :], inverse[:, :], route_scale[:, 0:1], None, ALU.mult))
                        chain.link(dve.tensor_tensor(weight[fo][:, :, :], kept[:, :, :],
                                                     inverse[:, :].unsqueeze(2).broadcast_to([P, QT, E]), ALU.mult))
                    elif kind == "experts":
                        t, = at
                        bank = expert.take(dve)
                        expert.emptied(dve.scalar_tensor_tensor(
                            out=scores[:, t, :].rearrange("p (e k) -> p e k", k=ES),
                            in0=bank[:, :].rearrange("p (e k) -> p e k", k=ES), scalar=0.0,
                            in1=weight[bo][:, t, :].unsqueeze(2).broadcast_to([P, E, ES]), op0=ALU.max, op1=ALU.mult))
                    elif kind == "out":
                        bank = out.take(dve)
                        g = res["gate"][:, 1, bass.ds(bt, 1), :].broadcast_to([P, QT, D])
                        out.emptied(dve.tensor_tensor(scratch[:, :, :], bank[:, 0:QT * D].rearrange("p (t d) -> p t d", d=D),
                                                      g, ALU.mult))
                        out.settled(dve)
                        x = res["x"][:, bass.ds(bt * QT, QT), :]
                        back_chain.link(dve.tensor_tensor(x, x, scratch[:, :, :], ALU.add))

            walk(dve, WEIGHTS["f3"], front, back, go)


def top_places(dve, chain, norm, values, best, left, width, k, fill):
    carry(dve, norm)
    for t in range(QT):
        last = dve.max(best[:, t, :], values[:, t, 0:width])
    chain.link(last)
    chain.link(dve.memset(best[:, :, k:8], fill))
    carry(dve, norm)
    for t in range(QT):
        last = dve.match_replace(left[:, t, :], in_to_replace=best[:, t, :], in_values=values[:, t, :], imm_value=-1.0e38)
    chain.link(last)


def carry(dve, norm):
    dve.tensor_copy(norm.idle[:, 1:2], norm.idle[:, 0:1])


def walk(eng, weight, front, back, do):
    both = merged(front, back, weight)
    fronts, backs = [x for x in both if x[0] == "front"], [x for x in both if x[0] == "back"]
    pipelined(eng, lambda bt, bo, ft, fo: do(fronts if bt is None else backs if ft is None else both, bt, bo, ft, fo))


class Modulated:

    def __init__(self, s, nc, res, which, ring):
        self.nc, self.res, self.which, self.ring = nc, res, which, ring
        self.norm = Norm(s)
        self.xhat = s.sb("xhat", [P, QT, D])
        self.hT = [s.sb(f"hT{n}", [P, TOK]) for n in range(2)]
        self.xhat_ready, self.hT_ready = s.sem("xhat_ready"), s.sem("hT_ready")

    LINKS = 2

    def pe(self, pe, kind, front, turn):
        if kind == "hT":
            pe.wait_ge(self.xhat_ready, turn + 1)
            bank = front.fill(pe)
            for t in range(QT):
                mm = pe.transpose(bank[:, t * P:(t + 1) * P], self.xhat[:, t, :], self.res["ident"][:, :])
            front.filled(mm)

    def dve(self, dve, kind, front, chain, turn, odd):
        if kind == "norm":
            self.norm.vector(dve, chain, turn, lambda t: x_tile(self.res, turn * QT + t), self.xhat, self.xhat_ready)
        elif kind == "hT":
            bank = front.take(dve)
            front.emptied(dve.tensor_scalar(self.hT[odd][:, :], bank[:, 0:TOK],
                                            self.res["mod"][:, self.which + 1, bass.ds(turn, 1)],
                                            self.res["mod"][:, self.which, bass.ds(turn, 1)], ALU.mult, ALU.add))
            front.settled(dve)
            dve.sem_inc(self.hT_ready, 1)

    def gpsimd(self, pool, kind, turn):
        if kind == "norm":
            self.norm.gpsimd(pool, turn)


def add_gated(dve, res, chain, turn, y, scratch, gate=1):
    x = res["x"][:, bass.ds(turn * QT, QT), :]
    chain.link(dve.tensor_tensor(scratch[:, :, :], y, res["gate"][:, gate, bass.ds(turn, 1), :].broadcast_to([P, QT, D]),
                                 ALU.mult))
    chain.link(dve.tensor_tensor(x, x, scratch[:, :, :], ALU.add))


def layer0_ffn(nc, dram, res):
    E, I, K = 8, 256, 2
    C = I // P
    LIMIT, ALPHA = 7.0, 1.702
    NX = E + 8 - K
    FILL = 3.0e38
    with ExitStack() as ctx:
        s = Scope(nc, ctx, "f0")
        router, router_bias = s.sb("router", [P, E]), s.sb("router_bias", [P, E])
        w_in, b_in = s.sb("w_in", [P, E, 2 * I]), s.sb("b_in", [P, E, 2 * C])
        b_up = s.sb("b_up", [P, E, C])
        w_down, b_down = s.sb("w_down", [P, E * C, D]), s.sb("b_down", [E, D])
        logits, best, left = s.sb("logits", [P, QT, NX]), s.sb("best", [P, QT, 8]), s.sb("left", [P, QT, NX])
        lowered, exps = s.sb("lowered", [P, QT, E]), s.sb("exps", [P, QT, E])
        total, inverse = s.sb("total", [P, QT]), s.sb("inverse", [P, QT])
        chosen, weight = s.sb("chosen", [P, QT, E]), s.sb("weight", [P, QT, E])
        half_weight = [s.sb(f"half_weight{n}", [P, QT, E]) for n in range(2)]
        weightT = s.sb("weightT", [E, TOK])
        mixed = [s.sb(f"mixed{n}", [P, QT, D]) for n in range(2)]
        gate, up_raw, tanh, glu, up, hidden = ([s.sb(f"{name}{n}", [P, C, TOK]) for n in range(4)]
                                               for name in ("gate", "up_raw", "tanh", "glu", "up", "hidden"))
        scratch = s.sb("scratch", [P, QT, D])
        fronts, gates, ups, downs = Ring(s, "fronts", 1), Ring(s, "gates", 2), Ring(s, "ups", 2), Ring(s, "downs", 2)
        h = Modulated(s, nc, res, 2, fronts)
        (loaded, started, front_chained, back_chained, lowered_ready, exps_ready, weight_ready, weightT_ready, gate_ready,
         tanh_ready, glu_ready, hidden_ready) = (s.sem(name) for name in (
             "loaded", "started", "front_chained", "back_chained", "lowered_ready", "exps_ready", "weight_ready",
             "weightT_ready", "gate_ready", "tanh_ready", "glu_ready", "hidden_ready"))
        n_loaded = 6 * 16
        front = [("norm",), ("hT",), ("logits",), ("places",), ("weight",), ("weightT",), ("biases",)]
        back = []
        for n in range(-1, E + 3):
            back += [(kind, n - lag) for kind, lag in (("bias", 0), ("into", -1), ("glu", 1), ("combine", 3), ("down", 2))
                     if 0 <= n - lag < E]
        back.append(("finish",))
        block = s.block()

        @block.sync
        def _(sp):
            load(sp, loaded, [(router[:, :], dram["L0_router"]), (router_bias[:, :], row_of(dram["L0_router_bias"])),
                              (w_in[:, :, :], dram["L0_gate_up"].rearrange("e h n -> h e n")),
                              (b_in[:, :, :], dram["L0_gate_up_bias"]),
                              (w_down[:, :, :], dram["L0_down"].rearrange("(t p) d -> p t d", p=P)),
                              (b_down[:, :], dram["L0_down_bias"])])

        @block.tensor
        def _(pe):
            pe.wait_ge(loaded, n_loaded)

            def go(steps, bt, bo, ft, fo):
                front, gate_in, up_in = Uses(fronts, ft, fo, 4), Uses(gates, bt, bo, E), Uses(ups, bt, bo, E)
                out = Uses(downs, bt, bo, E)
                for half, kind, *at in steps:
                    h.pe(pe, kind, front, ft)
                    if kind == "logits":
                        pe.wait_ge(h.hT_ready, ft + 1)
                        bank = front.fill(pe)
                        for t in range(QT):
                            mm = pe.matmul(bank[:, t * E:(t + 1) * E], h.hT[fo][:, t * P:(t + 1) * P], router[:, :],
                                           start=(t == 0), stop=True, skip_group_check=True)
                        front.filled(mm)
                    elif kind == "weightT":
                        pe.wait_ge(weight_ready, ft + 1)
                        bank = front.fill(pe)
                        for t in range(QT):
                            mm = pe.transpose(bank[0:E, t * P:(t + 1) * P], weight[:, t, :], res["ident"][:, :])
                        front.filled(mm)
                    elif kind == "biases":
                        pe.wait_ge(weightT_ready, ft + 1)
                        bank = front.fill(pe)
                        for t in range(QT):
                            mm = pe.matmul(bank[:, t * P:(t + 1) * P], weightT[:, t * P:(t + 1) * P], b_down[:, :],
                                           start=(t == 0), stop=True, skip_group_check=True)
                        front.filled(mm)
                    elif kind == "into":
                        e, = at
                        for ring, first in ((gate_in, 0), (up_in, C)):
                            bank = ring.fill(pe)
                            for c in range(C):
                                mm = pe.matmul(bank[:, c * TOK:(c + 1) * TOK],
                                               w_in[:, e, (first + c) * P:(first + c + 1) * P], h.hT[bo][:, :],
                                               start=(c == 0), stop=True, skip_group_check=True)
                            ring.filled(mm)
                    elif kind == "down":
                        e, = at
                        pe.wait_ge(hidden_ready, bt * E + e + 1)
                        bank = out.fill(pe)
                        for t in range(QT):
                            for c in range(C):
                                mm = pe.matmul(bank[:, t * P:(t + 1) * P], hidden[e % 4][:, c, t * P:(t + 1) * P],
                                               w_down[:, e * C + c, :], start=(t == 0 and c == 0), stop=(c == C - 1),
                                               skip_group_check=True)
                        out.filled(mm)

            walk(pe, WEIGHTS["f0"], front, back, go)

        @block.scalar
        def _(act):
            ups.start(act)
            act.wait_ge(started, 1)

            def go(steps, bt, bo, ft, fo):
                up_in = Uses(ups, bt, bo, E)
                for half, kind, *at in steps:
                    if kind == "places":
                        act.wait_ge(lowered_ready, ft + 1)
                        nc.scalar.activation(exps[:, :, :], lowered[:, :, :], ACT.Exp).then_inc(exps_ready, 1)
                    elif kind == "bias":
                        e, = at
                        bank = up_in.take(act)
                        for c in range(C):
                            ins = nc.scalar.activation(up_raw[e % 4][:, c, :], bank[:, c * TOK:(c + 1) * TOK], ACT.Identity,
                                                       bias=b_up[:, e, c:c + 1])
                        up_in.emptied(ins)
                        act.wait_ge(gate_ready, bt * E + e + 1)
                        nc.scalar.activation(tanh[e % 4][:, :, :], gate[e % 4][:, :, :], ACT.Tanh,
                                             scale=ALPHA / 2).then_inc(tanh_ready, 1)

            walk(act, WEIGHTS["f0"], front, back, go)

        @block.gpsimd
        def _(pool):
            pool.wait_ge(h.norm.power_ready, 1)

            def go(steps, bt, bo, ft, fo):
                for half, kind, *at in steps:
                    h.gpsimd(pool, kind, ft)
                    if kind == "glu":
                        e, = at
                        pool.wait_ge(glu_ready, bt * E + e + 1)
                        pool.tensor_tensor(hidden[e % 4][:, :, :], up[e % 4][:, :, :], glu[e % 4][:, :, :],
                                           ALU.mult).then_inc(hidden_ready, 1)

            walk(pool, WEIGHTS["f0"], front, back, go)

        @block.vector
        def _(dve):
            h.norm.start(dve)
            for ring in (fronts, gates, downs):
                ring.start(dve)
            dve.memset(logits[:, :, :], FILL)
            dve.wait_ge(loaded, n_loaded)
            dve.tensor_scalar(b_up[:, :, :], b_in[:, :, C:2 * C], 1.0, None, ALU.add).then_inc(started, 1)
            dve.wait_ge(started, 1)

            def go(steps, bt, bo, ft, fo):
                front, gate_in, out = Uses(fronts, ft, fo, 4), Uses(gates, bt, bo, E), Uses(downs, bt, bo, E)
                chain, back_chain = Chain(dve, front_chained, ft, h.LINKS + 9), Chain(dve, back_chained, bt, 2)
                for half, kind, *at in steps:
                    h.dve(dve, kind, front, chain, ft, fo)
                    if kind == "logits":
                        bank = front.take(dve)
                        front.emptied(dve.tensor_tensor(logits[:, :, 0:E], bank[:, 0:QT * E].rearrange("p (t e) -> p t e", e=E),
                                                        router_bias[:, :].unsqueeze(1).broadcast_to([P, QT, E]), ALU.add))
                        front.settled(dve)
                    elif kind == "places":
                        top_places(dve, chain, h.norm, logits, best, left, E, K, FILL)
                        dve.tensor_tensor(lowered[:, :, :], logits[:, :, 0:E], best[:, :, 0:1].broadcast_to([P, QT, E]),
                                          ALU.subtract).then_inc(lowered_ready, 1)
                        chain.link(dve.tensor_tensor(chosen[:, :, :], logits[:, :, 0:E], left[:, :, 0:E], ALU.not_equal))
                    elif kind == "weight":
                        dve.wait_ge(exps_ready, ft + 1)
                        chain.link(dve.tensor_reduce(total[:, :], exps[:, :, :], AX_X, ALU.add))
                        chain.link(dve.reciprocal(inverse[:, :], total[:, :]))
                        chain.link(dve.tensor_tensor(weight[:, :, :], exps[:, :, :], chosen[:, :, :], ALU.mult))
                        chain.link(dve.tensor_tensor(weight[:, :, :], weight[:, :, :],
                                                     inverse[:, :].unsqueeze(2).broadcast_to([P, QT, E]), ALU.mult))
                        dve.sem_inc(weight_ready, 1)
                        chain.link(dve.tensor_scalar(half_weight[fo][:, :, :], weight[:, :, :], 0.5, None, ALU.mult))
                    elif kind == "weightT":
                        bank = front.take(dve)
                        front.emptied(dve.tensor_copy(weightT[:, :], bank[0:E, 0:TOK]))
                        front.settled(dve)
                        dve.sem_inc(weightT_ready, 1)
                    elif kind == "biases":
                        bank = front.take(dve)
                        front.emptied(dve.tensor_copy(mixed[fo][:, :, :].rearrange("p t d -> p (t d)"), bank[:, 0:QT * P]))
                        front.settled(dve)
                    elif kind == "bias":
                        e, = at
                        bank = gate_in.take(dve)
                        for c in range(C):
                            ins = dve.tensor_scalar(gate[e % 4][:, c, :], bank[:, c * TOK:(c + 1) * TOK],
                                                    b_in[:, e, c:c + 1], LIMIT, ALU.add, ALU.min)
                        gate_in.emptied(ins)
                        gate_in.settled(dve)
                        dve.sem_inc(gate_ready, 1)
                    elif kind == "combine":
                        e, = at
                        if e:
                            out.settled(dve)
                        bank = out.take(dve)
                        for t in range(QT):
                            ins = dve.scalar_tensor_tensor(out=mixed[bo][:, t, :], in0=bank[:, t * P:(t + 1) * P],
                                                           scalar=half_weight[bo][:, t, e:e + 1], in1=mixed[bo][:, t, :],
                                                           op0=ALU.mult, op1=ALU.add)
                        out.emptied(ins)
                    elif kind == "glu":
                        e, = at
                        dve.wait_ge(ups.free, bt * E + e + 3)
                        dve.tensor_scalar(up[e % 4][:, :, :], up_raw[e % 4][:, :, :], 1.0 - LIMIT, 1.0 + LIMIT,
                                          ALU.max, ALU.min)
                        dve.wait_ge(tanh_ready, bt * E + e + 1)
                        dve.scalar_tensor_tensor(out=glu[e % 4][:, :, :], in0=tanh[e % 4][:, :, :], scalar=1.0,
                                                 in1=gate[e % 4][:, :, :], op0=ALU.add, op1=ALU.mult).then_inc(glu_ready, 1)
                    elif kind == "finish":
                        out.settled(dve)
                        add_gated(dve, res, back_chain, bt, mixed[bo][:, :, :], scratch)

            walk(dve, WEIGHTS["f0"], front, back, go)


def layer2_ffn(nc, dram, res):
    with ExitStack() as ctx:
        s = Scope(nc, ctx, "f2")
        y = s.sb("y", [P, BATCH * QT, D])
        layer2_input(nc, res, y)
        for depth in range(2):
            window_attention(nc, dram, res, y, depth)
            gelu_mlp(nc, dram, res, y, depth)
        layer2_output(nc, res, y)


def y_tile(y, n):
    return y[:, bass.ds(n, 1), :].rearrange("p a d -> p (a d)")


def layer2_input(nc, res, y):
    with ExitStack() as ctx:
        s = Scope(nc, ctx, "i2")
        fronts, outs = Ring(s, "fronts", 1), Ring(s, "outs", 1)
        m = Modulated(s, nc, res, 2, fronts)
        chained = s.sem("chained")
        front, back = [("norm",), ("hT",)], [("by_token",)]
        block = s.block()

        @block.tensor
        def _(pe):
            def go(steps, bt, bo, ft, fo):
                front, out = Uses(fronts, ft, fo, 1), Uses(outs, bt, bo, 1)
                for _, kind in steps:
                    m.pe(pe, kind, front, ft)
                    if kind == "by_token":
                        pe.wait_ge(m.hT_ready, bt + 1)
                        bank = out.fill(pe)
                        for t in range(QT):
                            mm = pe.transpose(bank[:, t * P:(t + 1) * P], m.hT[bo][:, t * P:(t + 1) * P], res["ident"][:, :])
                        out.filled(mm)

            walk(pe, WEIGHTS["i"], front, back, go)

        @block.gpsimd
        def _(pool):
            pool.wait_ge(m.norm.power_ready, 1)
            with pool.Fori(0, BATCH) as turn:
                m.norm.gpsimd(pool, turn)

        @block.vector
        def _(dve):
            m.norm.start(dve)
            fronts.start(dve)
            outs.start(dve)

            def go(steps, bt, bo, ft, fo):
                front, out = Uses(fronts, ft, fo, 1), Uses(outs, bt, bo, 1)
                chain = Chain(dve, chained, ft, m.LINKS)
                for _, kind in steps:
                    m.dve(dve, kind, front, chain, ft, fo)
                    if kind == "by_token":
                        bank = out.take(dve)
                        out.emptied(dve.tensor_copy(y[:, bass.ds(bt * QT, QT), :].rearrange("p t d -> p (t d)"),
                                                    bank[:, 0:TOK]))

            walk(dve, WEIGHTS["i"], front, back, go)


def layer2_output(nc, res, y):
    with ExitStack() as ctx:
        s = Scope(nc, ctx, "o2")
        scratch = s.sb("scratch", [P, QT, D])
        chained = s.sem("chained")
        block = s.block()

        @block.vector
        def _(dve):
            with dve.Fori(0, BATCH) as turn:
                chain = Chain(dve, chained, turn, 2)
                x = res["x"][:, bass.ds(turn * QT, QT), :]
                chain.link(dve.tensor_tensor(scratch[:, :, :], y[:, bass.ds(turn * QT, QT), :],
                                             res["gate"][:, 1, bass.ds(turn, 1), :].broadcast_to([P, QT, D]), ALU.mult))
                chain.link(dve.tensor_tensor(x, x, scratch[:, :, :], ALU.add))
                chain.end()


def dve_shift(dve, bank, shifted):
    H = D // 2
    dve.tensor_copy(shifted[0:H, :], bank[0:H, 0:TOK])
    return dve.tensor_copy(shifted[H:D, 1:TOK], bank[H:D, 0:TOK - 1])


def window_attention(nc, dram, res, y, depth):
    a = Attn(f"w{depth}", 1, 8, 64, "window", 8.0)
    INNER, H = a.width, a.hd // 2
    with ExitStack() as ctx:
        s = Scope(nc, ctx, a.name)
        w = s.sb("w", [P, 3 * INNER])
        scales = s.sb("scales", [P, 2, 64])
        tables = s.sb("tables", [P, 2, 2, QT, 64])
        turned = s.sb("turned", [P, 2, 2, QT, 64])
        power = s.sb("power", [P, 2 * a.heads])

        def each(name, shape):
            return [s.sb(f"{name}{t}", [P, 2] + shape) for t in range(QT)]

        raw, square, unit = each("raw", [8, 64]), each("square", [8, 64]), each("unit", [8, 64])
        by_cos, by_sin, rotated = square, each("by_sin", [8, 64]), each("rotated", [8, 64])
        total, inverse = each("total", [8]), each("inverse", [8])
        at = WideAttention(s, nc, a, res, 3 * QT, 1 + QT, 3 * QT + QT)
        squares_ready, total_ready, inverse_ready = s.sem("squares_ready"), s.sem("total_ready"), s.sem("inverse_ready")
        unit_ready = s.sem("unit_ready")
        by_sin_ready, rotated_ready = s.sem("by_sin_ready"), s.sem("rotated_ready")
        project = ([("qkv", t, c) for t in range(QT) for c in range(3)] + [("total", 0), ("total", 1)]
                   + [("unit", 0), ("unit", 1), ("rotate", 0), ("rotate", 1), ("pack", 0), ("pack", 1)])
        steps = step_lists(a, project)
        n_loaded = 5 * 16
        block = s.block()

        @block.sync
        def _(sp):
            load(sp, at.loaded, [(w[:, :], dram["L2_wqkv"][depth]),
                                 (at.w_out[:, :, :], dram["L2_ffn_wo"][depth].rearrange("(t p) d -> p t d", p=P)),
                                 (scales[:, 0, :], row_of(dram["L2_q_scale"][depth])),
                                 (scales[:, 1, :], row_of(dram["L2_k_scale"][depth])),
                                 (tables[:, :, :, :, :], dram["c_rotary"])])

        @block.tensor
        def _(pe):
            pe.wait_ge(at.loaded, n_loaded)
            pe.wait_ge(at.started, 1)

            def project(pe, kind, where, front, to_act, turn, odd):
                if kind == "qkv":
                    t, c = where
                    if t == 0 and c == 0:
                        pe.wait_ge(at.hT_ready, turn + 1)
                    bank = to_act.fill(pe)
                    to_act.filled(pe.matmul(bank[:, :], at.hT[:, t * P:(t + 1) * P], w[:, c * INNER:(c + 1) * INNER],
                                            start=True, stop=True))
                elif kind == "pack":
                    t, = where
                    pe.wait_ge(rotated_ready, turn * QT + t + 1)
                    for c, ring in enumerate((to_act, front)):
                        bank = ring.fill(pe)
                        for g in range(a.pairs):
                            mm = pe.transpose(bank[:, g * P:(g + 1) * P],
                                              rotated[t][:, c, 2 * g:2 * g + 2, :].rearrange("p h d -> p (h d)"),
                                              res["ident"][:, :])
                        ring.filled(mm)

            pipelined(pe, lambda bt, bo, ft, fo: at.pe_batch(pe, steps(bt, ft), project, bt, bo, ft, fo))

        @block.scalar
        def _(act):
            at.begin_scalar(act)
            act.wait_ge(at.started, 1)

            def project(act, kind, where, to_act, turn, odd):
                if kind == "qkv":
                    t, c = where
                    bank = to_act.take(act)
                    if c == 2:
                        to_act.emptied(nc.scalar.copy(at.v[odd][:, t, :, 0:a.hd],
                                                      bank[:, :].rearrange("p (h d) -> p h d", d=a.hd)))
                        return
                    if c == 0:
                        act.wait_ge(unit_ready, turn * QT + t + 1)
                    nc.scalar.copy(raw[t][:, c, :, :].rearrange("p h d -> p (h d)"), bank[:, :])
                    to_act.emptied(nc.scalar.activation(square[t][:, c, :, :].rearrange("p h d -> p (h d)"), bank[:, :],
                                                        ACT.Square))
                    if c == 1:
                        to_act.settled(act)
                        act.sem_inc(squares_ready, 1)
                elif kind == "pack":
                    t, = where
                    bank = to_act.take(act)
                    to_act.emptied(nc.scalar.copy(at.qT[odd][:, :, t * P:(t + 1) * P],
                                                  bank[:, :].rearrange("p (g q) -> p g q", q=P)))
                    if t == QT - 1:
                        to_act.settled(act)
                        act.sem_inc(at.qT_ready, 1)

            pipelined(act, lambda bt, bo, ft, fo: at.act_batch(act, steps(bt, ft), project, bt, bo, ft, fo))

        @block.gpsimd
        def _(pool):
            pool.wait_ge(at.started, 1)
            with pool.Fori(0, BATCH) as turn:
                for t in range(QT):
                    pool.wait_ge(total_ready, turn * QT + t + 1)
                    pool.tensor_tensor(inverse[t][:, :, :].rearrange("p c h -> p (c h)"),
                                       total[t][:, :, :].rearrange("p c h -> p (c h)"), power[:, :],
                                       ALU.pow).then_inc(inverse_ready, 1)
                for t in range(QT):
                    pool.wait_ge(unit_ready, turn * QT + t + 1 + QT)
                    for half in range(2):
                        here, there = slice(H * half, H * half + H), slice(H - H * half, 2 * H - H * half)
                        last = pool.tensor_tensor(by_sin[t][:, :, :, here], unit[t][:, :, :, there],
                                                  turned[:, :, 1, t, here].unsqueeze(2).broadcast_to([P, 2, 8, H]), ALU.mult)
                    last.then_inc(by_sin_ready, 1)

        @block.vector
        def _(dve):
            dve.memset(power[:, :], -0.5)
            dve.memset(at.hT[:, :], 0.0)
            dve.sem_inc(unit_ready, QT)
            dve.wait_ge(at.loaded, n_loaded)
            for c in range(2):
                for t in range(QT):
                    dve.tensor_tensor(turned[:, c, 0, t, :], tables[:, c, 0, t, :], scales[:, c, :], ALU.mult)
                    dve.tensor_tensor(turned[:, c, 1, t, 0:H], tables[:, c, 1, t, 0:H], scales[:, c, H:2 * H], ALU.mult)
                    dve.tensor_tensor(turned[:, c, 1, t, H:2 * H], tables[:, c, 1, t, H:2 * H],
                                      scales[:, c, 0:H], ALU.mult)
            at.begin_vector(dve)
            dve.wait_ge(at.started, 1)

            def project(dve, kind, where, front, chain, turn, odd):
                if kind == "total":
                    t, = where
                    dve.wait_ge(squares_ready, turn * QT + t + 1)
                    dve.tensor_reduce(total[t][:, :, :], square[t][:, :, :, :], AX_X, ALU.add).then_inc(total_ready, 1)
                elif kind == "unit":
                    t, = where
                    dve.wait_ge(inverse_ready, turn * QT + t + 1)
                    chain.link(dve.tensor_scalar(inverse[t][:, :, :], inverse[t][:, :, :], 1e12, None, ALU.min))
                    chain.link(dve.tensor_tensor(unit[t][:, :, :, :], raw[t][:, :, :, :],
                                                 inverse[t][:, :, :].unsqueeze(3).broadcast_to([P, 2, 8, 64]), ALU.mult))
                    chain.link(dve.tensor_tensor(by_cos[t][:, :, :, :], unit[t][:, :, :, :],
                                                 turned[:, :, 0, t, :].unsqueeze(2).broadcast_to([P, 2, 8, 64]), ALU.mult))
                    dve.sem_inc(unit_ready, 1)
                elif kind == "rotate":
                    t, = where
                    dve.wait_ge(by_sin_ready, turn * QT + t + 1)
                    dve.tensor_tensor(rotated[t][:, :, :, :], by_cos[t][:, :, :, :], by_sin[t][:, :, :, :],
                                      ALU.add).then_inc(rotated_ready, 1)
                elif kind == "pack":
                    t, = where
                    bank = front.take(dve)
                    for half in range(2):
                        r = slice(64 * half, 64 * half + 64)
                        ins = dve.tensor_copy(
                            at.k_alone[odd][r, :, t * P:(t + 1) * P].rearrange("p (g two) q -> p g two q", two=2)[:, :, half, :],
                            bank[r, :].rearrange("p (g q) -> p g q", g=4))
                    front.emptied(ins)
                    if t == QT - 1:
                        front.settled(dve)
                        dve.sem_inc(at.qkv_ready, 1)

            def copy_y(dve, chain, turn):
                dve.tensor_copy(at.xhat[:, :, :], y[:, bass.ds(turn * QT, QT), :]).then_inc(at.xhat_ready, 1)

            def shift(dve, front, turn):
                bank = front.take(dve)
                front.emptied(dve_shift(dve, bank, at.hT))
                front.settled(dve)
                dve.sem_inc(at.hT_ready, 1)

            def add_to_y(dve, chain, tail, turn, qt, bank):
                yt = y_tile(y, turn * QT + qt)
                tail.emptied(dve.tensor_tensor(yt, bank[:, 0:D], yt, ALU.add))
                tail.settled(dve)

            pipelined(dve, lambda bt, bo, ft, fo: at.dve_batch(dve, steps(bt, ft), project, copy_y, shift,
                                                               add_to_y, bt, bo, ft, fo))


def gelu_mlp(nc, dram, res, y, depth):
    HID, H = 341, D // 2
    parts = [(0, P), (P, P), (2 * P, HID - 2 * P)]
    with ExitStack() as ctx:
        s = Scope(nc, ctx, f"g{depth}")
        w1, w2 = s.sb("w1", [P, 2 * HID]), s.sb("w2", [P, 3, D])
        b1, b2, affine = s.sb("b1", [P, 2, 3]), s.sb("b2", [P, D]), s.sb("affine", [P, 2])
        norm = Norm(s)
        upper = s.sb("upper", [P, QT, H])
        shifted, xhat = s.sb("shifted", [P, QT, D]), s.sb("xhat", [P, QT, D])
        hT = [s.sb(f"hT{n}", [P, TOK]) for n in range(2)]
        gelu, hidden = s.sb("gelu", [P, 3, TOK]), s.sb("hidden", [P, 3, TOK])
        scratch = s.sb("scratch", [P, QT, D])
        fronts, gs, linears, outs = Ring(s, "fronts", 1), Ring(s, "gs", 2), Ring(s, "linears", 2), Ring(s, "outs", 1)
        loaded, started, front_chained, back_chained, upper_ready, xhat_ready, hT_ready = (s.sem(name) for name in (
            "loaded", "started", "front_chained", "back_chained", "upper_ready", "xhat_ready", "hT_ready"))
        front = [("take",), ("shift",), ("norm",), ("hT",)]
        back = [("g", 0), ("g", 1), ("linear", 0), ("g", 2), ("linear", 1), ("linear", 2), ("out",)]
        block = s.block()
        n_loaded = 6 * 16

        @block.sync
        def _(sp):
            sp.wait_ge(started, 1)
            load(sp, loaded, [(w1[:, :], dram["L2_w1"][depth]),
                              (w2[:, 0:2, :], dram["L2_w2"][depth, 0:2 * P, :].rearrange("(t p) d -> p t d", p=P)),
                              (w2[0:HID - 2 * P, 2, :], dram["L2_w2"][depth, 2 * P:HID, :]),
                              (b1[:, :, :], dram["L2_b1"][depth]), (b2[:, :], row_of(dram["L2_b2"][depth])),
                              (affine[:, :], dram["L2_affine"][depth])])

        @block.tensor
        def _(pe):
            pe.wait_ge(loaded, n_loaded)

            def go(steps, bt, bo, ft, fo):
                front, g_in, linear_in = Uses(fronts, ft, fo, 2), Uses(gs, bt, bo, 3), Uses(linears, bt, bo, 3)
                out = Uses(outs, bt, bo, 1)
                for half, kind, *at in steps:
                    if kind == "shift":
                        pe.wait_ge(upper_ready, ft + 1)
                        bank = front.fill(pe)
                        for t in range(QT):
                            mm = pe.matmul(bank[:, t * H:(t + 1) * H], res["shift"][:, 0, :], upper[:, t, :],
                                           start=(t == 0), stop=(t == 0), skip_group_check=True)
                            if t:
                                mm = pe.matmul(bank[:, t * H:(t + 1) * H], res["shift"][:, 1, :], upper[:, t - 1, :],
                                               start=False, stop=True, skip_group_check=True)
                        front.filled(mm)
                    elif kind == "hT":
                        pe.wait_ge(xhat_ready, ft + 1)
                        bank = front.fill(pe)
                        for t in range(QT):
                            mm = pe.transpose(bank[:, t * P:(t + 1) * P], xhat[:, t, :], res["ident"][:, :])
                        front.filled(mm)
                    elif kind in ("g", "linear"):
                        c, = at
                        if (kind, c) == ("g", 0):
                            pe.wait_ge(hT_ready, bt + 1)
                        r0, rows = parts[c]
                        ring = g_in if kind == "g" else linear_in
                        w0 = r0 + (HID if kind == "g" else 0)
                        bank = ring.fill(pe)
                        ring.filled(pe.matmul(bank[0:rows, 0:TOK], w1[:, w0:w0 + rows], hT[bo][:, :], start=True, stop=True))
                    elif kind == "out":
                        pe.wait_ge(linears.free, bt * 3 + 3 + 2)
                        bank = out.fill(pe)
                        for t in range(QT):
                            for c in range(3):
                                mm = pe.matmul(bank[:, t * P:(t + 1) * P], hidden[:, c, t * P:(t + 1) * P], w2[:, c, :],
                                               start=(t == 0 and c == 0), stop=(c == 2), skip_group_check=True)
                        out.filled(mm)

            walk(pe, WEIGHTS["g"], front, back, go)

        @block.scalar
        def _(act):
            gs.start(act)
            act.wait_ge(loaded, n_loaded)

            def go(steps, bt, bo, ft, fo):
                g_in = Uses(gs, bt, bo, 3)
                for half, kind, *at in steps:
                    if kind == "g":
                        c, = at
                        rows = parts[c][1]
                        bank = g_in.take(act)
                        g_in.emptied(nc.scalar.activation(gelu[0:rows, c, :], bank[0:rows, 0:TOK], ACT.Gelu,
                                                          bias=b1[0:rows, 1, c:c + 1]))

            walk(act, WEIGHTS["g"], front, back, go)

        @block.gpsimd
        def _(pool):
            pool.wait_ge(norm.power_ready, 1)
            with pool.Fori(0, BATCH) as turn:
                norm.gpsimd(pool, turn)

        @block.vector
        def _(dve):
            for ring in (fronts, linears, outs):
                ring.start(dve)
            dve.memset(w2[:, 2, :], 0.0)
            dve.memset(hidden[:, 2, :], 0.0).then_inc(started, 1)
            norm.start(dve)
            dve.wait_ge(norm.power_ready, 1)

            def go(steps, bt, bo, ft, fo):
                front, linear_in, out = Uses(fronts, ft, fo, 2), Uses(linears, bt, bo, 3), Uses(outs, bt, bo, 1)
                chain, back_chain = Chain(dve, front_chained, ft, 2), Chain(dve, back_chained, bt, 1)
                for half, kind, *at in steps:
                    if kind == "take":
                        now = y[:, bass.ds(ft * QT, QT), :]
                        dve.tensor_copy(upper[:, :, :], now[:, :, H:D]).then_inc(upper_ready, 1)
                        dve.tensor_copy(shifted[:, :, 0:H], now[:, :, 0:H])
                    elif kind == "shift":
                        bank = front.take(dve)
                        front.emptied(dve.tensor_copy(shifted[:, :, H:D], bank[:, 0:QT * H].rearrange("p (t d) -> p t d", d=H)))
                        front.settled(dve)
                    elif kind == "norm":
                        norm.vector(dve, chain, ft, lambda t: shifted[:, t, :], xhat, xhat_ready)
                    elif kind == "hT":
                        bank = front.take(dve)
                        front.emptied(dve.tensor_scalar(hT[fo][:, :], bank[:, 0:TOK], affine[:, 0:1], affine[:, 1:2],
                                                        ALU.mult, ALU.add))
                        front.settled(dve)
                        dve.sem_inc(hT_ready, 1)
                    elif kind == "linear":
                        c, = at
                        rows = parts[c][1]
                        bank = linear_in.take(dve)
                        dve.wait_ge(gs.free, bt * 3 + c + 1 + 2)
                        linear_in.emptied(dve.scalar_tensor_tensor(out=hidden[0:rows, c, :], in0=bank[0:rows, 0:TOK],
                                                                   scalar=b1[0:rows, 0, c:c + 1], in1=gelu[0:rows, c, :],
                                                                   op0=ALU.add, op1=ALU.mult))
                    elif kind == "out":
                        bank = out.take(dve)
                        out.emptied(dve.tensor_tensor(scratch[:, :, :], bank[:, 0:QT * D].rearrange("p (t d) -> p t d", d=D),
                                                      b2[:, :].unsqueeze(1).broadcast_to([P, QT, D]), ALU.add))
                        out.settled(dve)
                        now = y[:, bass.ds(bt * QT, QT), :]
                        back_chain.link(dve.tensor_tensor(now, now, scratch[:, :, :], ALU.add))

            walk(dve, WEIGHTS["g"], front, back, go)


def shape_constants():
    r = np.arange(P)
    q, k = r[:, None], r[None, :]
    banned = [k > q, (k > q) | (k < q - WINDOW), k < q + P - WINDOW]
    masks = np.zeros((P, 6, P), np.float32)
    for n, m in enumerate(banned):
        masks[:, 2 * n, :] = np.where(m, BIG, 0.0)
        masks[:, 2 * n + 1, :] = np.where(m.T, BIG, 0.0)
    minus_head = np.zeros((P, 16, P), np.float32)
    for part in range(3):
        for h in range(16):
            minus_head[part * 16 + h, h, :] = -1.0
    shift = np.zeros((P, 2, P), np.float32)
    shift[r[:-1], 0, r[1:]] = 1.0
    shift[P - 1, 1, 0] = 1.0
    half = np.arange(0, 64, 2, dtype=np.float32)
    angle = np.arange(TOK, dtype=np.float32)[:, None] * (1.0 / 10000.0 ** (half / 64))[None, :].astype(np.float32)
    factor = ((half + 25.6) / 89.6)[None, :] ** ((np.arange(TOK) - TOK // 2) / 32.0)[:, None]
    cos, sin = np.cos(angle), np.sin(angle)
    rotary = np.zeros((2, 2, TOK, 64), np.float32)
    for n, f in enumerate((factor, 1.0 / factor)):
        rotary[n, 0] = np.concatenate([cos * f, cos * f], axis=1)
        rotary[n, 1] = np.concatenate([-sin * f, sin * f], axis=1)
    rotary = rotary.reshape(2, 2, QT, P, 64).transpose(3, 0, 1, 2, 4)
    return {"c_rotary": rotary, "c_ident": np.eye(P, dtype=np.float32), "c_masks": masks, "c_minus_head": minus_head,
            "c_shift": shift}


def lay_out(z):
    t = {"x": z["L0_attn_x"]}
    for n in range(4):
        t[f"L{n}_cT"] = z[f"L{n}_c"].T
        t[f"L{n}_wmod"] = z[f"L{n}_wmod"]
    w = z["L0_attn_W_attn"]
    w_q = w[:512].reshape(4, 16, 8, D).transpose(1, 0, 2, 3).reshape(512, D)
    t["L0_w"] = np.concatenate([w_q, w[512:]], axis=0).T
    t["L0_wo"] = z["L0_attn_W_proj"].reshape(D, 4, 16, 8).transpose(2, 1, 3, 0).reshape(512, D)
    t["L3_w"] = z["L3_attn_w_qkv"]
    t["L3_wo"] = z["L3_attn_w_proj"]
    t["L3_attn_b_proj"] = z["L3_attn_b_proj"]
    t.update(lay_out_rest(z))
    t.update(shape_constants())
    return {k: np.ascontiguousarray(v) for k, v in t.items()}


def resident(s):
    return {
        "x": s.sb("x", [P, BATCH * QT, D]),
        "ident": s.sb("ident", [P, P]),
        "identb": s.sb("identb", [P, P], BF16),
        "masks": s.sb("masks", [P, 6, P], BF16),
        "minus_head": s.sb("minus_head", [P, 16, P], BF16),
        "shift": s.sb("shift", [P, 2, P]),
        "one_hot": s.sb("one_hot", [P, BATCH, P]),
        "gate_rows": s.sb("gate_rows", [P, LAYERS, 2 * D]),
        "mods": [s.sb(f"mod{n}", [P, 4, BATCH]) for n in range(LAYERS)],
        "gate": s.sb("gate", [P, 2, BATCH, D]),
    }


def lay_out_rest(z):
    t = {}
    t["L1_w"] = z["L1_attn_Wqkv_w"].T
    t["L1_wo"] = z["L1_attn_Wo_w"].T
    t["L1_qk_bias"] = z["L1_attn_Wqkv_b"][:2048].reshape(16, P).T
    t["L1_v_bias"] = z["L1_attn_Wqkv_b"][2048:]
    t["L1_ghost"] = z["L1_attn_ghost"]
    t["L1_wo_bias"] = z["L1_attn_Wo_b"]
    t["L2_w"] = np.concatenate([z["L2_attn_Wq"].T, z["L2_attn_Wk"].T, z["L2_attn_Wv"].T], axis=1)
    t["L2_wo"] = z["L2_attn_Wo"].T
    t["L2_qk_bias"] = np.stack([z["L2_attn_bq"], z["L2_attn_bk"]], axis=1)
    t["L2_v_bias"] = z["L2_attn_bv"]
    t["L2_wo_bias"] = z["L2_attn_bo"]
    for n in ("gate", "up", "down"):
        t[f"L1_ffn_w_{n}"] = z[f"L1_ffn_w_{n}"]
    t["L3_sel"] = z["L3_ffn_expert_sel"].T
    t["L3_keys"] = z["L3_ffn_keys"].transpose(1, 0, 2).reshape(D, 512)
    t["L3_values"] = z["L3_ffn_values"].reshape(512, D)
    t["L3_ffn_route_scale"] = z["L3_ffn_route_scale"]
    t["L0_router"] = z["L0_ffn_router_weight"].T
    t["L0_router_bias"] = z["L0_ffn_router_bias"]
    t["L0_gate_up"] = z["L0_ffn_gate_up_proj"]
    t["L0_gate_up_bias"] = z["L0_ffn_gate_up_bias"].reshape(8, 4, P).transpose(2, 0, 1)
    t["L0_down"] = z["L0_ffn_down_proj"].reshape(8 * 256, D)
    t["L0_down_bias"] = z["L0_ffn_down_bias"]
    t["L2_wqkv"] = z["L2_ffn_wqkv"]
    t["L2_ffn_wo"] = z["L2_ffn_wo"]
    t["L2_q_scale"] = z["L2_ffn_q_scale"]
    t["L2_k_scale"] = z["L2_ffn_k_scale"]
    t["L2_w1"] = z["L2_ffn_w1"]
    t["L2_w2"] = z["L2_ffn_w2"]
    b1 = np.zeros((2, 2, 3 * P), np.float32)
    b1[:, :, 0:341] = z["L2_ffn_b1"].reshape(2, 2, 341)
    t["L2_b1"] = b1.reshape(2, 2, 3, P).transpose(0, 3, 1, 2)
    t["L2_b2"] = z["L2_ffn_b2"]
    t["L2_affine"] = np.stack([z["L2_ffn_ln_g"], z["L2_ffn_ln_b"]], axis=2)
    return t


OUT_SHAPE = (BATCH, TOK, D)


def build(nc, dram, out):
    with ExitStack() as ctx:
        res = resident(Scope(nc, ctx, "res"))
        constants_phase(nc, dram, res)
        for layer, (attention, ffn) in enumerate(((layer0_attention, layer0_ffn), (layer1_attention, layer1_ffn),
                                                  (layer2_attention, layer2_ffn), (layer3_attention, layer3_ffn))):
            gates_phase(nc, layer, res)
            res["mod"] = res["mods"][layer]
            attention(nc, dram, res)
            ffn(nc, dram, res)
        store_phase(nc, res, out)


def kernel(**inputs):
    import concourse.bacc as bacc
    from concourse.bass_utils import run_bass_kernel_spmd

    nc = bacc.Bacc("TRN2", target_bir_lowering=False, num_devices=1)
    arrays = lay_out(inputs)
    dram = {n: nc.dram_tensor(f"in_{n}", a.shape, mybir.dt.from_np(a.dtype), kind="ExternalInput").ap()
            for n, a in arrays.items()}
    out = nc.dram_tensor("out", OUT_SHAPE, F32, kind="ExternalOutput").ap()
    build(nc, dram, out)
    r = run_bass_kernel_spmd(nc, [{f"in_{n}": a for n, a in arrays.items()}], core_ids=[0])
    return r.results[0]["out"]
```
